# Optimizing a Trainium2 kernel written in Bass

```python
import numpy as np
import jax
import jax.numpy as jnp

def _softmax(x, axis=-1):
    return jax.nn.softmax(x, axis=axis)

def _gelu(x):
    return jax.nn.gelu(x, approximate=True)

def _silu(x):
    return jax.nn.silu(x)

def _sigmoid(x):
    return jax.nn.sigmoid(x)

def _layernorm(x, axis=-1, eps=1e-05):
    m = jnp.mean(x, axis=axis, keepdims=True)
    v = jnp.var(x, axis=axis, keepdims=True)
    return (x - m) / jnp.sqrt(v + eps)

def _scatter_add(tgt, idx, src, axis=0):
    return tgt.at[idx].add(src)

def _segment_sum(src, seg, n):
    return jax.ops.segment_sum(src, seg, n)
kernel_name = 'mk_lm_tower_d4_tok_ids256_r4_882f06'

def setup_inputs(seed: int=0):
    np.random.seed(seed)
    _w = jnp.asarray

    def _rec_inputs():
        import jax
        import jax.numpy as jnp
        _rk = jax.random.key(seed)
        x = jax.random.randint(jax.random.fold_in(_rk, 1), (2, 1024), 0, 64, jnp.int32)
        fside_BS_continuous_positions = jax.random.uniform(jax.random.fold_in(_rk, 21), (2, 1024), jnp.float32, 0.0, 0.999927)
        return (x, fside_BS_continuous_positions)
    x, fside_BS_continuous_positions = _rec_inputs()

    def _L0_tok_setup():
        import jax, jax.numpy as jnp
        import numpy as np
        N_SCALES = 4

        def _conv1d(x, w, b, pad):
            y = jax.lax.conv_general_dilated(x, w, window_strides=(1,), padding=[(pad, pad)], dimension_numbers=('NCH', 'OIH', 'NCH'))
            return y + b[None, :, None]
        key = jax.random.key(seed)
        ks = jax.random.split(key, 12)
        B, S, P, D = (8, 512, 512, 64)
        byte_sequence = jax.random.randint(ks[0], (B, S), 0, 64, dtype=jnp.int64)
        continuous_positions = jax.random.uniform(ks[1], (B, P), dtype=jnp.float32)
        emb = jax.random.normal(ks[2], (64, D), dtype=jnp.float32)
        locality_shapes = jax.random.normal(ks[3], (64, 4), dtype=jnp.float32)
        w1 = jax.random.normal(ks[4], (128, 64, 7), dtype=jnp.float32) * 0.02
        b1 = jnp.zeros((128,), dtype=jnp.float32)
        w2 = jax.random.normal(ks[5], (64, 128, 5), dtype=jnp.float32) * 0.02
        b2 = jnp.zeros((64,), dtype=jnp.float32)
        w3 = jax.random.normal(ks[6], (1, 64, 3), dtype=jnp.float32) * 0.02
        b3 = jnp.zeros((1,), dtype=jnp.float32)
        multiscale_widths = jnp.array([0.01, 0.02, 0.05, 0.1], dtype=jnp.float32)
        scale_weights = jnp.ones((4,), dtype=jnp.float32)
        return {'byte_sequence': byte_sequence, 'continuous_positions': continuous_positions, 'emb': emb, 'locality_shapes': locality_shapes, 'w1': w1, 'b1': b1, 'w2': w2, 'b2': b2, 'w3': w3, 'b3': b3, 'multiscale_widths': multiscale_widths, 'scale_weights': scale_weights}
    _L0_tok_all = _L0_tok_setup()
    _L0_tok_in = {k: v for k, v in _L0_tok_all.items() if k in ('emb', 'locality_shapes', 'w1', 'b1', 'w2', 'b2', 'w3', 'b3', 'multiscale_widths', 'scale_weights')}
    del _L0_tok_all

    def _L0_attn_setup():
        import jax, jax.numpy as jnp
        import numpy as np
        B, L, D, H = (4, 4096, 64, 8)
        DK = D // H

        def _heads(t):
            b, l, d = t.shape
            return t.reshape(b, l, H, DK).transpose(0, 2, 1, 3)
        key = jax.random.key(seed)
        ks = jax.random.split(key, 9)
        s = 0.02
        return {'x': jax.random.normal(ks[0], (B, L, D), dtype=jnp.float32), 'Wq': jax.random.normal(ks[1], (D, D), dtype=jnp.float32) * s, 'bq': jnp.zeros((D,), dtype=jnp.float32), 'Wk': jax.random.normal(ks[2], (D, D), dtype=jnp.float32) * s, 'bk': jnp.zeros((D,), dtype=jnp.float32), 'Wv': jax.random.normal(ks[3], (D, D), dtype=jnp.float32) * s, 'bv': jnp.zeros((D,), dtype=jnp.float32), 'Wfc': jax.random.normal(ks[4], (D, D), dtype=jnp.float32) * s, 'bfc': jnp.zeros((D,), dtype=jnp.float32)}
    _L0_attn_all = _L0_attn_setup()
    _L0_attn_in = {k: v for k, v in _L0_attn_all.items() if k in ('Wq', 'bq', 'Wk', 'bk', 'Wv', 'bv', 'Wfc', 'bfc')}
    del _L0_attn_all

    def _L0_ffn_setup():
        import jax, jax.numpy as jnp
        import numpy as np
        INPUT_WIDTH = 64
        DEPTH = 7
        OUTPUT_WIDTH = 64
        N_NODES = 2 ** (DEPTH + 1) - 1
        key = jax.random.key(seed)
        k_x, k_w1, k_w2 = jax.random.split(key, 3)
        init1 = 1.0 / np.sqrt(INPUT_WIDTH)
        x = jax.random.normal(k_x, (2, 256, INPUT_WIDTH), dtype=jnp.float32)
        w1s = jax.random.uniform(k_w1, (N_NODES, INPUT_WIDTH), jnp.float32, -init1, init1)
        b1s = jnp.zeros((N_NODES,), jnp.float32)
        w2s = jax.random.uniform(k_w2, (N_NODES, INPUT_WIDTH, OUTPUT_WIDTH), jnp.float32, -init1, init1)
        b2s = jnp.zeros((N_NODES, OUTPUT_WIDTH), jnp.float32)
        return {'x': x, 'w1s': w1s, 'b1s': b1s, 'w2s': w2s, 'b2s': b2s}
    _L0_ffn_all = _L0_ffn_setup()
    _L0_ffn_in = {k: v for k, v in _L0_ffn_all.items() if k in ('w1s', 'b1s', 'w2s', 'b2s')}
    del _L0_ffn_all

    def _L1_attn_setup():
        import jax, jax.numpy as jnp
        import numpy as np
        GAMMA = 0.96875
        SCALE_BASE = 512.0

        def xpos_rope(x, downscale=False):
            B, S, D = x.shape
            half = D // 2
            inv_freq = 1.0 / 10000.0 ** (jnp.arange(0, D, 2, dtype=jnp.float32) / D)
            pos = jnp.arange(S, dtype=jnp.float32)
            ang = pos[:, None] * inv_freq[None, :]
            sin, cos = (jnp.sin(ang), jnp.cos(ang))
            base = (jnp.arange(0, D, 2, dtype=jnp.float32) + 0.4 * D) / (1.4 * D)
            scale = base[None, :] ** (pos[:, None] / SCALE_BASE)
            if downscale:
                scale = 1.0 / scale
            x1 = x[..., 0::2]
            x2 = x[..., 1::2]
            r1 = (x1 * cos - x2 * sin) * scale
            r2 = (x1 * sin + x2 * cos) * scale
            out = jnp.stack([r1, r2], axis=-1).reshape(B, S, D)
            return out

        def get_D(gamma, seq_len):
            n = jnp.arange(seq_len, dtype=jnp.float32)
            diff = n[:, None] - n[None, :]
            mask = diff >= 0
            D = jnp.where(mask, gamma ** jnp.where(mask, diff, 0.0), 0.0)
            return D

        def _reference_tuple_inner(x, W_Q, W_K, W_V):
            S = x.shape[1]
            D = get_D(GAMMA, S)
            Q = xpos_rope(x @ W_Q, downscale=False)
            K = xpos_rope(x @ W_K, downscale=True)
            V = x @ W_V
            ret = jnp.einsum('bnd,bmd->bnm', Q, K) * D[None, :, :]
            out = jnp.einsum('bnm,bmv->bnv', ret, V)
            return (out, ret)
        key = jax.random.key(seed)
        k1, k2, k3, k4 = jax.random.split(key, 4)
        B, S, d_model, d_k, d_v = (8, 1024, 64, 64, 64)
        x = jax.random.normal(k1, (B, S, d_model), dtype=jnp.float32)
        W_Q = jax.random.normal(k2, (d_model, d_k), dtype=jnp.float32) / d_model
        W_K = jax.random.normal(k3, (d_model, d_k), dtype=jnp.float32) / d_model
        W_V = jax.random.normal(k4, (d_model, d_v), dtype=jnp.float32) / d_model
        return {'x': x, 'W_Q': W_Q, 'W_K': W_K, 'W_V': W_V}
    _L1_attn_all = _L1_attn_setup()
    _L1_attn_in = {k: v for k, v in _L1_attn_all.items() if k in ('W_Q', 'W_K', 'W_V')}
    del _L1_attn_all

    def _L1_ffn_setup():
        import jax, jax.numpy as jnp
        import numpy as np
        DIM = 64
        HEADS = 8
        NUM_KEYS = 64
        NUM_KV = NUM_KEYS ** 2
        PK_TOPK = 16
        FINAL_TOPK = 16
        DIM_KEY = DIM // 2
        P = 2

        def _pk(x, Wq_pk, pk_keys):
            b, n, _ = x.shape
            q = (x @ Wq_pk).reshape(b, n, P, HEADS, DIM_KEY).transpose(2, 0, 1, 3, 4)
            sim = jnp.einsum('pbnhd,pkhd->pbnhk', q, pk_keys)
            scores, idx = jax.lax.top_k(sim, PK_TOPK)
            idx0 = idx[0]
            idx1 = idx[1] * NUM_KEYS
            index = (idx0[..., :, None] + idx1[..., None, :]).reshape(b, n, HEADS, PK_TOPK * PK_TOPK)
            score = (scores[0][..., :, None] + scores[1][..., None, :]).reshape(b, n, HEADS, PK_TOPK * PK_TOPK)
            final_scores, pk_idx = jax.lax.top_k(score, FINAL_TOPK)
            final_indices = jnp.take_along_axis(index, pk_idx, axis=-1)
            final_scores = jax.nn.softmax(final_scores, axis=-1)
            return (final_scores, final_indices)
        key = jax.random.key(seed)
        ks = jax.random.split(key, 7)
        b, n = (2, 256)
        std = 0.02
        x = jax.random.normal(ks[0], (b, n, DIM), dtype=jnp.float32)
        Wq_pk = jax.random.normal(ks[1], (DIM, P * HEADS * DIM_KEY), dtype=jnp.float32) * std
        pk_keys = jax.random.normal(ks[2], (P, NUM_KEYS, HEADS, DIM_KEY), dtype=jnp.float32) * std
        Wq = jax.random.normal(ks[3], (DIM, HEADS * DIM), dtype=jnp.float32) * std
        keys_table = jax.random.normal(ks[4], (NUM_KV * HEADS, DIM), dtype=jnp.float32) * std
        values_table = jax.random.normal(ks[5], (NUM_KV * HEADS, DIM), dtype=jnp.float32) * std
        Wo = jax.random.normal(ks[6], (DIM * HEADS, DIM), dtype=jnp.float32) * std
        return {'x': x, 'Wq_pk': Wq_pk, 'pk_keys': pk_keys, 'Wq': Wq, 'keys_table': keys_table, 'values_table': values_table, 'Wo': Wo}
    _L1_ffn_all = _L1_ffn_setup()
    _L1_ffn_in = {k: v for k, v in _L1_ffn_all.items() if k in ('Wq_pk', 'pk_keys', 'Wq', 'keys_table', 'values_table', 'Wo')}
    del _L1_ffn_all

    def _L2_attn_setup():
        import jax, jax.numpy as jnp
        import numpy as np
        import math
        STATE_DIM = 64
        R_MIN, R_MAX = (0.4, 0.9)
        PHASE_MAX = 2.0 * math.pi
        BATCH, SEQ = (8, 1024)

        def _binop(e_i, e_j):
            a_i, b_i = e_i
            a_j, b_j = e_j
            return (a_j * a_i, a_j * b_i + b_j)
        key = jax.random.key(seed)
        k_x, k_u1, k_u2, k_br, k_bi, k_cr, k_ci = jax.random.split(key, 7)
        D = STATE_DIM
        x = jax.random.normal(k_x, (BATCH, SEQ, D), dtype=jnp.float32)
        u1 = jax.random.uniform(k_u1, (D,), dtype=jnp.float32)
        nu_log = jnp.log(-0.5 * jnp.log(u1 * (R_MAX + R_MIN) * (R_MAX - R_MIN) + R_MIN ** 2))
        u2 = jax.random.uniform(k_u2, (D,), dtype=jnp.float32)
        theta_log = jnp.log(PHASE_MAX * u2)
        lam_mod = jnp.exp(-jnp.exp(nu_log))
        gamma_log = jnp.log(jnp.sqrt(1.0 - jnp.square(lam_mod)))
        s_b = 1.0 / math.sqrt(2 * D)
        s_c = 1.0 / math.sqrt(D)
        B_re = jax.random.normal(k_br, (D, D), dtype=jnp.float32) * s_b
        B_im = jax.random.normal(k_bi, (D, D), dtype=jnp.float32) * s_b
        C_re = jax.random.normal(k_cr, (D, D), dtype=jnp.float32) * s_c
        C_im = jax.random.normal(k_ci, (D, D), dtype=jnp.float32) * s_c
        return {'x': x, 'nu_log': nu_log, 'theta_log': theta_log, 'gamma_log': gamma_log, 'B_re': B_re, 'B_im': B_im, 'C_re': C_re, 'C_im': C_im}
    _L2_attn_all = _L2_attn_setup()
    _L2_attn_in = {k: v for k, v in _L2_attn_all.items() if k in ('nu_log', 'theta_log', 'gamma_log', 'B_re', 'B_im', 'C_re', 'C_im')}
    del _L2_attn_all

    def _L2_ffn_setup():
        import jax, jax.numpy as jnp
        import numpy as np
        B, N, D = (16, 1024, 64)
        NUM_EXPERTS, TOP_K, HEADS = (4, 2, 4)
        N_EDGES = 262144
        LN_EPS = 1e-05

        def _layernorm(x, g, b):
            mu = x.mean(-1, keepdims=True)
            var = ((x - mu) ** 2).mean(-1, keepdims=True)
            return (x - mu) * jax.lax.rsqrt(var + LN_EPS) * g + b

        def _forward(x, edge_index, W_gat, att_src, att_dst, b_gat, ln_gamma, ln_beta, W1, b1, W2, b2):
            Bc, Nc, Dc = x.shape
            M = Bc * Nc
            x_flat = x.reshape(M, Dc)
            h = (x_flat @ W_gat).reshape(M, HEADS, NUM_EXPERTS)
            loops = jnp.arange(M, dtype=edge_index.dtype)
            src = jnp.concatenate([edge_index[0], loops])
            dst = jnp.concatenate([edge_index[1], loops])
            a_src = (h * att_src).sum(-1)
            a_dst = (h * att_dst).sum(-1)
            e = jax.nn.leaky_relu(a_src[src] + a_dst[dst], negative_slope=0.2)
            e_max = jax.ops.segment_max(e, dst, num_segments=M)
            ee = jnp.exp(e - e_max[dst])
            denom = jax.ops.segment_sum(ee, dst, num_segments=M)
            alpha = ee / (denom[dst] + 1e-16)
            msg = h[src] * alpha[:, :, None]
            agg = jax.ops.segment_sum(msg, dst, num_segments=M).reshape(M, HEADS * NUM_EXPERTS) + b_gat
            scores = _layernorm(agg, ln_gamma, ln_beta).reshape(M, HEADS, NUM_EXPERTS).mean(1)
            scores = scores.reshape(Bc, Nc, NUM_EXPERTS)
            topk_s, topk_i = jax.lax.top_k(scores, TOP_K)
            w = jax.nn.softmax(topk_s, axis=-1)
            out = jnp.zeros_like(x)
            for ei in range(NUM_EXPERTS):
                g = jnp.where(topk_i == ei, w, 0.0).sum(-1)
                hh = jax.nn.gelu(x @ W1[ei] + b1[ei], approximate=False)
                out = out + g[..., None] * (hh @ W2[ei] + b2[ei])
            return out
        key = jax.random.key(seed)
        ks = jax.random.split(key, 8)
        s = 0.05
        return {'x': jax.random.normal(ks[0], (B, N, D), jnp.float32), 'W_gat': jax.random.normal(ks[1], (D, HEADS * NUM_EXPERTS), jnp.float32) * s, 'att_src': jax.random.normal(ks[2], (HEADS, NUM_EXPERTS), jnp.float32) * s, 'att_dst': jax.random.normal(ks[3], (HEADS, NUM_EXPERTS), jnp.float32) * s, 'b_gat': jnp.zeros((HEADS * NUM_EXPERTS,), jnp.float32), 'ln_gamma': jnp.ones((HEADS * NUM_EXPERTS,), jnp.float32), 'ln_beta': jnp.zeros((HEADS * NUM_EXPERTS,), jnp.float32), 'W1': jax.random.normal(ks[4], (NUM_EXPERTS, D, 2 * D), jnp.float32) * s, 'b1': jnp.zeros((NUM_EXPERTS, 2 * D), jnp.float32), 'W2': jax.random.normal(ks[5], (NUM_EXPERTS, 2 * D, D), jnp.float32) * s, 'b2': jnp.zeros((NUM_EXPERTS, D), jnp.float32), 'edge_index': jax.random.randint(ks[6], (2, N_EDGES), 0, B * N, jnp.int32)}
    _L2_ffn_all = _L2_ffn_setup()
    _L2_ffn_in = {k: v for k, v in _L2_ffn_all.items() if k in ('W_gat', 'att_src', 'att_dst', 'b_gat', 'ln_gamma', 'ln_beta', 'W1', 'b1', 'W2', 'b2', 'edge_index')}
    del _L2_ffn_all

    def _L3_attn_setup():
        import math
        import jax, jax.numpy as jnp
        import numpy as np
        B, T, C = (4, 512, 64)
        LEVELS = 3
        NEAR_WINDOW = 16
        THETA = 10000.0
        EPS_L2 = 1e-08
        EPS_VAR = 1e-06

        def haar_basis(T, levels):
            cols = []
            for j in range(levels):
                bc = 2 ** j
                bs = T // bc
                half = bs // 2
                for k in range(bc):
                    v = np.zeros(T, np.float32)
                    s = k * bs
                    v[s:s + half] = 1.0 / math.sqrt(half)
                    v[s + half:s + bs] = -1.0 / math.sqrt(half)
                    cols.append(v)
            return jnp.asarray(np.stack(cols, axis=1))

        def rope_tables(T, dim):
            half = dim // 2
            inv_freq = 1.0 / THETA ** (np.arange(half, dtype=np.float32) / half)
            ang = np.arange(T, dtype=np.float32)[:, None] * inv_freq[None, :]
            return (jnp.asarray(np.cos(ang)), jnp.asarray(np.sin(ang)))

        def apply_rope(x, cos, sin):
            half = x.shape[-1] // 2
            x1, x2 = (x[..., :half], x[..., half:])
            return jnp.concatenate([x1 * cos - x2 * sin, x1 * sin + x2 * cos], axis=-1)

        def l2_normalize(x, eps=EPS_L2):
            return x / (jnp.linalg.norm(x, axis=-1, keepdims=True) + eps)

        def variance_scaled_softmax(scores, eps=EPS_VAR):
            finite = jnp.isfinite(scores)
            m = finite.astype(scores.dtype)
            n = jnp.clip(jnp.sum(m, axis=-1, keepdims=True), 1.0, None)
            safe = jnp.where(finite, scores, 0.0)
            mean = jnp.sum(safe * m, axis=-1, keepdims=True) / n
            var = jnp.sum((safe - mean) ** 2 * m, axis=-1, keepdims=True) / n
            std = jnp.sqrt(jnp.clip(var, eps, None))
            scaled = jnp.where(finite, (safe - mean) / std, -jnp.inf)
            out = jax.nn.softmax(scaled, axis=-1)
            return jnp.where(n == 0, jnp.zeros_like(out), out)
        key = jax.random.key(seed)
        kx, kq, kv, ko = jax.random.split(key, 4)
        lim = math.sqrt(6.0 / (C + C))
        return {'x': jax.random.normal(kx, (B, T, C), dtype=jnp.float32), 'W_Q': jax.random.uniform(kq, (C, C), jnp.float32, -lim, lim), 'W_V': jax.random.normal(kv, (C, C), jnp.float32) * 0.02, 'W_O': jax.random.normal(ko, (C, C), jnp.float32) * 0.02}
    _L3_attn_all = _L3_attn_setup()
    _L3_attn_in = {k: v for k, v in _L3_attn_all.items() if k in ('W_Q', 'W_V', 'W_O')}
    del _L3_attn_all

    def _L3_ffn_setup():
        import jax, jax.numpy as jnp
        import numpy as np
        NUM_EXPERTS = 8
        TOP_K = 2
        B, S, D = (8, 2048, 64)

        def _moe(tokens, router_w, w1, b1, w2, b2):
            N = tokens.shape[0]
            E = router_w.shape[0]
            logits = tokens.astype(jnp.float32) @ router_w.astype(jnp.float32).T
            probs = jax.nn.softmax(logits, axis=-1)
            rw, re = jax.lax.top_k(probs, TOP_K)
            if TOP_K > 1:
                rw = rw / jnp.maximum(rw.sum(-1, keepdims=True), 1e-12)
            rw = rw.astype(tokens.dtype)
            combine = jnp.zeros((N, E), tokens.dtype).at[jnp.arange(N)[:, None], re].set(rw)
            out = tokens
            for e in range(E):
                h = jax.nn.gelu(tokens @ w1[e] + b1[e], approximate=False)
                y = h @ w2[e] + b2[e]
                out = out + combine[:, e:e + 1] * y
            return out
        key = jax.random.key(seed)
        ks = jax.random.split(key, 4)
        scale = 1.0 / np.sqrt(D).astype(np.float32)
        return {'input_embeddings': jax.random.normal(ks[0], (B, S, D), jnp.float32), 'router_w': jax.random.normal(ks[1], (NUM_EXPERTS, D), jnp.float32) * scale, 'w1': jax.random.normal(ks[2], (NUM_EXPERTS, D, D), jnp.float32) * scale, 'b1': jnp.zeros((NUM_EXPERTS, D), jnp.float32), 'w2': jax.random.normal(ks[3], (NUM_EXPERTS, D, D), jnp.float32) * scale, 'b2': jnp.zeros((NUM_EXPERTS, D), jnp.float32)}
    _L3_ffn_all = _L3_ffn_setup()
    _L3_ffn_in = {k: v for k, v in _L3_ffn_all.items() if k in ('router_w', 'w1', 'b1', 'w2', 'b2')}
    del _L3_ffn_all
    return {'x': x, 'fside_BS_continuous_positions': fside_BS_continuous_positions, 'L0_tok_emb': _L0_tok_in['emb'], 'L0_tok_locality_shapes': _L0_tok_in['locality_shapes'], 'L0_tok_w1': _L0_tok_in['w1'], 'L0_tok_b1': _L0_tok_in['b1'], 'L0_tok_w2': _L0_tok_in['w2'], 'L0_tok_b2': _L0_tok_in['b2'], 'L0_tok_w3': _L0_tok_in['w3'], 'L0_tok_b3': _L0_tok_in['b3'], 'L0_tok_multiscale_widths': _L0_tok_in['multiscale_widths'], 'L0_tok_scale_weights': _L0_tok_in['scale_weights'], 'L0_attn_Wq': _L0_attn_in['Wq'], 'L0_attn_bq': _L0_attn_in['bq'], 'L0_attn_Wk': _L0_attn_in['Wk'], 'L0_attn_bk': _L0_attn_in['bk'], 'L0_attn_Wv': _L0_attn_in['Wv'], 'L0_attn_bv': _L0_attn_in['bv'], 'L0_attn_Wfc': _L0_attn_in['Wfc'], 'L0_attn_bfc': _L0_attn_in['bfc'], 'L0_ffn_w1s': _L0_ffn_in['w1s'], 'L0_ffn_b1s': _L0_ffn_in['b1s'], 'L0_ffn_w2s': _L0_ffn_in['w2s'], 'L0_ffn_b2s': _L0_ffn_in['b2s'], 'L1_attn_W_Q': _L1_attn_in['W_Q'], 'L1_attn_W_K': _L1_attn_in['W_K'], 'L1_attn_W_V': _L1_attn_in['W_V'], 'L1_ffn_Wq_pk': _L1_ffn_in['Wq_pk'], 'L1_ffn_pk_keys': _L1_ffn_in['pk_keys'], 'L1_ffn_Wq': _L1_ffn_in['Wq'], 'L1_ffn_keys_table': _L1_ffn_in['keys_table'], 'L1_ffn_values_table': _L1_ffn_in['values_table'], 'L1_ffn_Wo': _L1_ffn_in['Wo'], 'L2_attn_nu_log': _L2_attn_in['nu_log'], 'L2_attn_theta_log': _L2_attn_in['theta_log'], 'L2_attn_gamma_log': _L2_attn_in['gamma_log'], 'L2_attn_B_re': _L2_attn_in['B_re'], 'L2_attn_B_im': _L2_attn_in['B_im'], 'L2_attn_C_re': _L2_attn_in['C_re'], 'L2_attn_C_im': _L2_attn_in['C_im'], 'L2_ffn_W_gat': _L2_ffn_in['W_gat'], 'L2_ffn_att_src': _L2_ffn_in['att_src'], 'L2_ffn_att_dst': _L2_ffn_in['att_dst'], 'L2_ffn_b_gat': _L2_ffn_in['b_gat'], 'L2_ffn_ln_gamma': _L2_ffn_in['ln_gamma'], 'L2_ffn_ln_beta': _L2_ffn_in['ln_beta'], 'L2_ffn_W1': _L2_ffn_in['W1'], 'L2_ffn_b1': _L2_ffn_in['b1'], 'L2_ffn_W2': _L2_ffn_in['W2'], 'L2_ffn_b2': _L2_ffn_in['b2'], 'L2_ffn_edge_index': _L2_ffn_in['edge_index'], 'L3_attn_W_Q': _L3_attn_in['W_Q'], 'L3_attn_W_V': _L3_attn_in['W_V'], 'L3_attn_W_O': _L3_attn_in['W_O'], 'L3_ffn_router_w': _L3_ffn_in['router_w'], 'L3_ffn_w1': _L3_ffn_in['w1'], 'L3_ffn_b1': _L3_ffn_in['b1'], 'L3_ffn_w2': _L3_ffn_in['w2'], 'L3_ffn_b2': _L3_ffn_in['b2']}

def reference(x, fside_BS_continuous_positions, L0_tok_emb, L0_tok_locality_shapes, L0_tok_w1, L0_tok_b1, L0_tok_w2, L0_tok_b2, L0_tok_w3, L0_tok_b3, L0_tok_multiscale_widths, L0_tok_scale_weights, L0_attn_Wq, L0_attn_bq, L0_attn_Wk, L0_attn_bk, L0_attn_Wv, L0_attn_bv, L0_attn_Wfc, L0_attn_bfc, L0_ffn_w1s, L0_ffn_b1s, L0_ffn_w2s, L0_ffn_b2s, L1_attn_W_Q, L1_attn_W_K, L1_attn_W_V, L1_ffn_Wq_pk, L1_ffn_pk_keys, L1_ffn_Wq, L1_ffn_keys_table, L1_ffn_values_table, L1_ffn_Wo, L2_attn_nu_log, L2_attn_theta_log, L2_attn_gamma_log, L2_attn_B_re, L2_attn_B_im, L2_attn_C_re, L2_attn_C_im, L2_ffn_W_gat, L2_ffn_att_src, L2_ffn_att_dst, L2_ffn_b_gat, L2_ffn_ln_gamma, L2_ffn_ln_beta, L2_ffn_W1, L2_ffn_b1, L2_ffn_W2, L2_ffn_b2, L2_ffn_edge_index, L3_attn_W_Q, L3_attn_W_V, L3_attn_W_O, L3_ffn_router_w, L3_ffn_w1, L3_ffn_b1, L3_ffn_w2, L3_ffn_b2):
    import jax
    import jax.numpy as jnp

    def _L0_tok_ref(byte_sequence, continuous_positions, emb, locality_shapes, w1, b1, w2, b2, w3, b3, multiscale_widths, scale_weights):
        import jax, jax.numpy as jnp
        import numpy as np
        N_SCALES = 4

        def _conv1d(x, w, b, pad):
            y = jax.lax.conv_general_dilated(x, w, window_strides=(1,), padding=[(pad, pad)], dimension_numbers=('NCH', 'OIH', 'NCH'))
            return y + b[None, :, None]
        B, S = byte_sequence.shape
        P = continuous_positions.shape[1]
        amps = emb[byte_sequence]
        onehot = jax.nn.one_hot(byte_sequence, 64, dtype=jnp.float32)
        onehot = jnp.transpose(onehot, (0, 2, 1))
        h = jax.nn.gelu(_conv1d(onehot, w1, b1, 3), approximate=False)
        h = jax.nn.gelu(_conv1d(h, w2, b2, 2), approximate=False)
        ctx = jax.nn.sigmoid(_conv1d(h, w3, b3, 1))[:, 0, :]
        amps = amps * ctx[:, :, None]
        lp = locality_shapes[byte_sequence]
        byte_pos = jnp.linspace(0.0, 1.0, S, dtype=jnp.float32)
        center = byte_pos[None, :] + lp[..., 0] * 0.05
        xd = continuous_positions[:, None, :] - center[..., None]
        amp_scale = jax.nn.sigmoid(lp[..., 2])
        phase = lp[..., 3] * jnp.pi
        abs_w = jnp.abs(lp[..., 1])
        TWO_PI = 2.0 * jnp.pi
        basis_total = jnp.zeros((B, S, P), dtype=jnp.float32)
        for s in range(N_SCALES):
            width = abs_w * multiscale_widths[s] + 1e-05
            z = xd / width[..., None]
            basis = jnp.exp(-0.5 * z * z) * jnp.cos(phase[..., None] + TWO_PI * z)
            basis_total = basis_total + basis * (amp_scale[..., None] * scale_weights[s] ** 2)
        semantic_field = jnp.einsum('bsp,bsd->bpd', basis_total, amps)
        return semantic_field

    def _L0_attn_ref(x, Wq, bq, Wk, bk, Wv, bv, Wfc, bfc):
        import jax, jax.numpy as jnp
        import numpy as np
        B, L, D, H = (4, 4096, 64, 8)
        DK = D // H

        def _heads(t):
            b, l, d = t.shape
            return t.reshape(b, l, H, DK).transpose(0, 2, 1, 3)
        q = _heads(x @ Wq.T + bq)
        k = _heads(x @ Wk.T + bk)
        v = _heads(x @ Wv.T + bv)
        seq_len = q.shape[-2]
        p_attn = jnp.einsum('bhnd,bhne->bhde', k, v) / seq_len
        out = jnp.einsum('bhnd,bhde->bhne', q, p_attn)
        out = out.transpose(0, 2, 1, 3).reshape(x.shape[0], seq_len, H * DK)
        return out @ Wfc.T + bfc

    def _L0_ffn_ref(x, w1s, b1s, w2s, b2s):
        import jax, jax.numpy as jnp
        import numpy as np
        INPUT_WIDTH = 64
        DEPTH = 7
        OUTPUT_WIDTH = 64
        N_NODES = 2 ** (DEPTH + 1) - 1
        B, S, D = x.shape
        flat_x = x.reshape(B * S, D)
        T = flat_x.shape[0]
        current = jnp.zeros((T,), dtype=jnp.int32)
        all_nodes = []
        all_logits = []
        for _ in range(DEPTH + 1):
            all_nodes.append(current)
            score = jnp.einsum('td,td->t', flat_x, w1s[current]) + b1s[current]
            all_logits.append(score)
            choice = ((jnp.sign(score) + 1.0) / 2.0).astype(jnp.int32)
            current = current * 2 + choice + 1
        logits = jnp.stack(all_logits, axis=1)
        path_weights = jax.nn.gelu(jnp.abs(logits), approximate=False)
        out = jnp.zeros((T, OUTPUT_WIDTH), dtype=x.dtype)
        for i in range(DEPTH + 1):
            nodes_i = all_nodes[i]
            t_i = jnp.einsum('td,tdo->to', flat_x, w2s[nodes_i]) + b2s[nodes_i]
            out = out + t_i * path_weights[:, i][:, None]
        return out.reshape(B, S, OUTPUT_WIDTH)

    def _L1_attn_ref(x, W_Q, W_K, W_V):
        import jax, jax.numpy as jnp
        import numpy as np
        GAMMA = 0.96875
        SCALE_BASE = 512.0

        def xpos_rope(x, downscale=False):
            B, S, D = x.shape
            half = D // 2
            inv_freq = 1.0 / 10000.0 ** (jnp.arange(0, D, 2, dtype=jnp.float32) / D)
            pos = jnp.arange(S, dtype=jnp.float32)
            ang = pos[:, None] * inv_freq[None, :]
            sin, cos = (jnp.sin(ang), jnp.cos(ang))
            base = (jnp.arange(0, D, 2, dtype=jnp.float32) + 0.4 * D) / (1.4 * D)
            scale = base[None, :] ** (pos[:, None] / SCALE_BASE)
            if downscale:
                scale = 1.0 / scale
            x1 = x[..., 0::2]
            x2 = x[..., 1::2]
            r1 = (x1 * cos - x2 * sin) * scale
            r2 = (x1 * sin + x2 * cos) * scale
            out = jnp.stack([r1, r2], axis=-1).reshape(B, S, D)
            return out

        def get_D(gamma, seq_len):
            n = jnp.arange(seq_len, dtype=jnp.float32)
            diff = n[:, None] - n[None, :]
            mask = diff >= 0
            D = jnp.where(mask, gamma ** jnp.where(mask, diff, 0.0), 0.0)
            return D

        def _reference_tuple_inner(x, W_Q, W_K, W_V):
            S = x.shape[1]
            D = get_D(GAMMA, S)
            Q = xpos_rope(x @ W_Q, downscale=False)
            K = xpos_rope(x @ W_K, downscale=True)
            V = x @ W_V
            ret = jnp.einsum('bnd,bmd->bnm', Q, K) * D[None, :, :]
            out = jnp.einsum('bnm,bmv->bnv', ret, V)
            return (out, ret)
        return _reference_tuple_inner(x, W_Q, W_K, W_V)[0]

    def _L1_ffn_ref(x, Wq_pk, pk_keys, Wq, keys_table, values_table, Wo):
        import jax, jax.numpy as jnp
        import numpy as np
        DIM = 64
        HEADS = 8
        NUM_KEYS = 64
        NUM_KV = NUM_KEYS ** 2
        PK_TOPK = 16
        FINAL_TOPK = 16
        DIM_KEY = DIM // 2
        P = 2

        def _pk(x, Wq_pk, pk_keys):
            b, n, _ = x.shape
            q = (x @ Wq_pk).reshape(b, n, P, HEADS, DIM_KEY).transpose(2, 0, 1, 3, 4)
            sim = jnp.einsum('pbnhd,pkhd->pbnhk', q, pk_keys)
            scores, idx = jax.lax.top_k(sim, PK_TOPK)
            idx0 = idx[0]
            idx1 = idx[1] * NUM_KEYS
            index = (idx0[..., :, None] + idx1[..., None, :]).reshape(b, n, HEADS, PK_TOPK * PK_TOPK)
            score = (scores[0][..., :, None] + scores[1][..., None, :]).reshape(b, n, HEADS, PK_TOPK * PK_TOPK)
            final_scores, pk_idx = jax.lax.top_k(score, FINAL_TOPK)
            final_indices = jnp.take_along_axis(index, pk_idx, axis=-1)
            final_scores = jax.nn.softmax(final_scores, axis=-1)
            return (final_scores, final_indices)
        b, n, d = x.shape
        q = (x @ Wq).reshape(b, n, HEADS, DIM) * DIM ** (-0.5)
        kv_scores, indices = _pk(x, Wq_pk, pk_keys)
        offsets = jnp.arange(HEADS, dtype=indices.dtype) * NUM_KV
        ind = indices + offsets[None, None, :, None]
        k = jnp.einsum('bnhk,bnhkd->bnhd', kv_scores, keys_table[ind])
        v = jnp.einsum('bnhk,bnhkd->bnhd', kv_scores, values_table[ind])
        sim = jnp.einsum('bihd,bjhd->bhij', q, k)
        neg = -jnp.finfo(sim.dtype).max
        causal = jnp.tril(jnp.ones((n, n), dtype=bool))
        sim = jnp.where(causal, sim, neg)
        attn = jax.nn.softmax(sim, axis=-1)
        out = jnp.einsum('bhij,bjhd->bhid', attn, v)
        out = out.transpose(0, 2, 1, 3).reshape(b, n, HEADS * DIM)
        return out @ Wo

    def _L2_attn_ref(x, nu_log, theta_log, gamma_log, B_re, B_im, C_re, C_im):
        import jax, jax.numpy as jnp
        import numpy as np
        import math
        STATE_DIM = 64
        R_MIN, R_MAX = (0.4, 0.9)
        PHASE_MAX = 2.0 * math.pi
        BATCH, SEQ = (8, 1024)

        def _binop(e_i, e_j):
            a_i, b_i = e_i
            a_j, b_j = e_j
            return (a_j * a_i, a_j * b_i + b_j)
        L_mod = jnp.exp(-jnp.exp(nu_log))
        theta = jnp.exp(theta_log)
        L_diag = (L_mod * jnp.cos(theta) + 1j * L_mod * jnp.sin(theta)).astype(jnp.complex64)
        B = (B_re + 1j * B_im).astype(jnpp.complex64) if False else (B_re + 1j * B_im).astype(jnp.complex64)
        C = (C_re + 1j * C_im).astype(jnp.complex64)
        B_norm = B * jnp.exp(gamma_log)[:, None]
        B_elems = x.astype(jnp.complex64) @ B_norm.T
        L_elems = jnp.broadcast_to(L_diag, B_elems.shape)
        _, inner_states = jax.lax.associative_scan(_binop, (L_elems, B_elems), axis=1)
        return (inner_states @ C.T).real

    def _L2_ffn_ref(x, W_gat, att_src, att_dst, b_gat, ln_gamma, ln_beta, W1, b1, W2, b2, edge_index):
        import jax, jax.numpy as jnp
        import numpy as np
        B, N, D = (16, 1024, 64)
        NUM_EXPERTS, TOP_K, HEADS = (4, 2, 4)
        N_EDGES = 262144
        LN_EPS = 1e-05

        def _layernorm(x, g, b):
            mu = x.mean(-1, keepdims=True)
            var = ((x - mu) ** 2).mean(-1, keepdims=True)
            return (x - mu) * jax.lax.rsqrt(var + LN_EPS) * g + b

        def _forward(x, edge_index, W_gat, att_src, att_dst, b_gat, ln_gamma, ln_beta, W1, b1, W2, b2):
            Bc, Nc, Dc = x.shape
            M = Bc * Nc
            x_flat = x.reshape(M, Dc)
            h = (x_flat @ W_gat).reshape(M, HEADS, NUM_EXPERTS)
            loops = jnp.arange(M, dtype=edge_index.dtype)
            src = jnp.concatenate([edge_index[0], loops])
            dst = jnp.concatenate([edge_index[1], loops])
            a_src = (h * att_src).sum(-1)
            a_dst = (h * att_dst).sum(-1)
            e = jax.nn.leaky_relu(a_src[src] + a_dst[dst], negative_slope=0.2)
            e_max = jax.ops.segment_max(e, dst, num_segments=M)
            ee = jnp.exp(e - e_max[dst])
            denom = jax.ops.segment_sum(ee, dst, num_segments=M)
            alpha = ee / (denom[dst] + 1e-16)
            msg = h[src] * alpha[:, :, None]
            agg = jax.ops.segment_sum(msg, dst, num_segments=M).reshape(M, HEADS * NUM_EXPERTS) + b_gat
            scores = _layernorm(agg, ln_gamma, ln_beta).reshape(M, HEADS, NUM_EXPERTS).mean(1)
            scores = scores.reshape(Bc, Nc, NUM_EXPERTS)
            topk_s, topk_i = jax.lax.top_k(scores, TOP_K)
            w = jax.nn.softmax(topk_s, axis=-1)
            out = jnp.zeros_like(x)
            for ei in range(NUM_EXPERTS):
                g = jnp.where(topk_i == ei, w, 0.0).sum(-1)
                hh = jax.nn.gelu(x @ W1[ei] + b1[ei], approximate=False)
                out = out + g[..., None] * (hh @ W2[ei] + b2[ei])
            return out
        return _forward(x, edge_index, W_gat, att_src, att_dst, b_gat, ln_gamma, ln_beta, W1, b1, W2, b2)

    def _L3_attn_ref(x, W_Q, W_V, W_O):
        import math
        import jax, jax.numpy as jnp
        import numpy as np
        B, T, C = (4, 512, 64)
        LEVELS = 3
        NEAR_WINDOW = 16
        THETA = 10000.0
        EPS_L2 = 1e-08
        EPS_VAR = 1e-06

        def haar_basis(T, levels):
            cols = []
            for j in range(levels):
                bc = 2 ** j
                bs = T // bc
                half = bs // 2
                for k in range(bc):
                    v = np.zeros(T, np.float32)
                    s = k * bs
                    v[s:s + half] = 1.0 / math.sqrt(half)
                    v[s + half:s + bs] = -1.0 / math.sqrt(half)
                    cols.append(v)
            return jnp.asarray(np.stack(cols, axis=1))

        def rope_tables(T, dim):
            half = dim // 2
            inv_freq = 1.0 / THETA ** (np.arange(half, dtype=np.float32) / half)
            ang = np.arange(T, dtype=np.float32)[:, None] * inv_freq[None, :]
            return (jnp.asarray(np.cos(ang)), jnp.asarray(np.sin(ang)))

        def apply_rope(x, cos, sin):
            half = x.shape[-1] // 2
            x1, x2 = (x[..., :half], x[..., half:])
            return jnp.concatenate([x1 * cos - x2 * sin, x1 * sin + x2 * cos], axis=-1)

        def l2_normalize(x, eps=EPS_L2):
            return x / (jnp.linalg.norm(x, axis=-1, keepdims=True) + eps)

        def variance_scaled_softmax(scores, eps=EPS_VAR):
            finite = jnp.isfinite(scores)
            m = finite.astype(scores.dtype)
            n = jnp.clip(jnp.sum(m, axis=-1, keepdims=True), 1.0, None)
            safe = jnp.where(finite, scores, 0.0)
            mean = jnp.sum(safe * m, axis=-1, keepdims=True) / n
            var = jnp.sum((safe - mean) ** 2 * m, axis=-1, keepdims=True) / n
            std = jnp.sqrt(jnp.clip(var, eps, None))
            scaled = jnp.where(finite, (safe - mean) / std, -jnp.inf)
            out = jax.nn.softmax(scaled, axis=-1)
            return jnp.where(n == 0, jnp.zeros_like(out), out)
        Bx, Tx, Cx = x.shape
        cos, sin = rope_tables(Tx, Cx)
        W_h = haar_basis(Tx, LEVELS)
        WK = jnp.linalg.pinv(W_Q)
        q = x @ W_Q
        k = x @ WK.T
        v = x @ W_V.T
        q = l2_normalize(apply_rope(q, cos, sin))
        k = l2_normalize(apply_rope(k, cos, sin))
        pos = jnp.arange(Tx)
        dist = pos[None, :] - pos[:, None]
        near_mask = (dist >= 0) & (dist <= NEAR_WINDOW)
        causal = dist <= 0
        scale = 1.0 / math.sqrt(Cx)
        attn_scores = jnp.einsum('btc,bsc->bts', q, k) * scale
        attn_near = jnp.where(near_mask, attn_scores, -jnp.inf)
        q_coef = jnp.einsum('tw,btc->bwc', W_h, q)
        k_coef = jnp.einsum('tw,btc->bwc', W_h, k)
        attn_coef = jnp.einsum('bwc,bvc->bwv', q_coef, k_coef) * scale
        attn_far = jnp.einsum('tw,bwv,sv->bts', W_h, attn_coef, W_h)
        attn = jnp.where(near_mask, attn_near, attn_far)
        attn = jnp.where(causal, attn, -jnp.inf)
        n_visible = jnp.clip(jnp.sum(jnp.isfinite(attn), axis=-1, keepdims=True).astype(attn.dtype), 1.0, None)
        attn = attn / jnp.sqrt(n_visible)
        attn = variance_scaled_softmax(attn)
        y = jnp.einsum('bts,bsc->btc', attn, v)
        return y @ W_O.T

    def _L3_ffn_ref(input_embeddings, router_w, w1, b1, w2, b2):
        import jax, jax.numpy as jnp
        import numpy as np
        NUM_EXPERTS = 8
        TOP_K = 2
        B, S, D = (8, 2048, 64)

        def _moe(tokens, router_w, w1, b1, w2, b2):
            N = tokens.shape[0]
            E = router_w.shape[0]
            logits = tokens.astype(jnp.float32) @ router_w.astype(jnp.float32).T
            probs = jax.nn.softmax(logits, axis=-1)
            rw, re = jax.lax.top_k(probs, TOP_K)
            if TOP_K > 1:
                rw = rw / jnp.maximum(rw.sum(-1, keepdims=True), 1e-12)
            rw = rw.astype(tokens.dtype)
            combine = jnp.zeros((N, E), tokens.dtype).at[jnp.arange(N)[:, None], re].set(rw)
            out = tokens
            for e in range(E):
                h = jax.nn.gelu(tokens @ w1[e] + b1[e], approximate=False)
                y = h @ w2[e] + b2[e]
                out = out + combine[:, e:e + 1] * y
            return out
        b, s, d = input_embeddings.shape
        tokens = input_embeddings.reshape(b * s, d)
        return _moe(tokens, router_w, w1, b1, w2, b2).reshape(b, s, d)
    h = _L0_tok_ref(x, fside_BS_continuous_positions, L0_tok_emb, L0_tok_locality_shapes, L0_tok_w1, L0_tok_b1, L0_tok_w2, L0_tok_b2, L0_tok_w3, L0_tok_b3, L0_tok_multiscale_widths, L0_tok_scale_weights)
    h = h + _L0_attn_ref(_layernorm(h, axis=-1), L0_attn_Wq, L0_attn_bq, L0_attn_Wk, L0_attn_bk, L0_attn_Wv, L0_attn_bv, L0_attn_Wfc, L0_attn_bfc)
    h = h + _L0_ffn_ref(_layernorm(h, axis=-1), L0_ffn_w1s, L0_ffn_b1s, L0_ffn_w2s, L0_ffn_b2s)
    h = h + _L1_attn_ref(_layernorm(h, axis=-1), L1_attn_W_Q, L1_attn_W_K, L1_attn_W_V)
    h = h + _L1_ffn_ref(_layernorm(h, axis=-1), L1_ffn_Wq_pk, L1_ffn_pk_keys, L1_ffn_Wq, L1_ffn_keys_table, L1_ffn_values_table, L1_ffn_Wo)
    h = h + _L2_attn_ref(_layernorm(h, axis=-1), L2_attn_nu_log, L2_attn_theta_log, L2_attn_gamma_log, L2_attn_B_re, L2_attn_B_im, L2_attn_C_re, L2_attn_C_im)
    h = h + _L2_ffn_ref(_layernorm(h, axis=-1), L2_ffn_W_gat, L2_ffn_att_src, L2_ffn_att_dst, L2_ffn_b_gat, L2_ffn_ln_gamma, L2_ffn_ln_beta, L2_ffn_W1, L2_ffn_b1, L2_ffn_W2, L2_ffn_b2, L2_ffn_edge_index)
    h = h + _L3_attn_ref(_layernorm(h, axis=-1), L3_attn_W_Q, L3_attn_W_V, L3_attn_W_O)
    h = h + _L3_ffn_ref(_layernorm(h, axis=-1), L3_ffn_router_w, L3_ffn_w1, L3_ffn_b1, L3_ffn_w2, L3_ffn_b2)
    return h

_drawn_inputs = setup_inputs


def setup_inputs(seed=0):
    import zlib

    import numpy as np

    out = dict(_drawn_inputs(seed))
    spreads = {'L0_tok_b1': (0.0, 0.8),
     'L0_tok_b2': (0.0, 0.8),
     'L0_tok_scale_weights': (1.0, 0.2),
     'L0_attn_bq': (0.0, 0.8),
     'L0_attn_bk': (0.0, 0.8),
     'L0_attn_bv': (0.0, 0.8),
     'L0_attn_bfc': (0.0, 0.1),
     'L0_ffn_b1s': (0.0, 0.1),
     'L0_ffn_b2s': (0.0, 0.267),
     'L2_ffn_b_gat': (0.0, 2.0),
     'L2_ffn_ln_gamma': (1.0, 0.6),
     'L2_ffn_ln_beta': (0.0, 2.0),
     'L2_ffn_b1': (0.0, 2.0),
     'L2_ffn_b2': (0.0, 2.0),
     'L3_ffn_b1': (0.0, 2.0),
     'L3_ffn_b2': (0.0, 2.0)}
    factors = {'L0_tok_w1': 3.428,
     'L0_tok_w2': 3.638,
     'L0_tok_w3': 4.324,
     'L0_attn_Wq': 8.0,
     'L0_attn_Wk': 8.0,
     'L0_attn_Wv': 6.907,
     'L0_attn_Wfc': 8.0,
     'L1_ffn_Wq_pk': 48.603,
     'L1_ffn_pk_keys': 53.814,
     'L1_ffn_Wq': 64.0,
     'L1_ffn_keys_table': 64.0,
     'L1_ffn_values_table': 53.522,
     'L1_ffn_Wo': 46.999,
     'L2_ffn_att_src': 200.0,
     'L2_ffn_att_dst': 200.0,
     'L3_attn_W_Q': 64.0,
     'L3_attn_W_V': 8.0,
     'L3_attn_W_O': 8.0,
     'L2_ffn_W_gat': 58.888,
     'L2_attn_nu_log': 3.104,
     'L2_attn_gamma_log': 4.219,
     'L2_ffn_W1': 8.0,
     'L2_ffn_W2': 4.809}
    for name, (base, spread) in spreads.items():
        noise = np.random.default_rng([zlib.crc32(name.encode()), seed]).standard_normal(out[name].shape)
        drawn = base * np.exp(spread * noise) if base else spread * noise
        out[name] = jnp.asarray(drawn.astype(out[name].dtype))
    for name, factor in factors.items():
        out[name] = (out[name] * factor).astype(out[name].dtype)
    return out
```

```python
from contextlib import ExitStack

import numpy as np

import concourse.bass as bass
from concourse import mybir

F32 = mybir.dt.float32
BF16 = mybir.dt.bfloat16
I32 = mybir.dt.int32
U32 = mybir.dt.uint32
ALU = mybir.AluOpType
ACT = mybir.ActivationFunctionType
AX = mybir.AxisListType

P = 128
B = 2
S = 1024
D = 64
T = B * S
NT = T // P
TB = S // P
LN_EPS = 1e-5


class Stage:

    def __init__(self, nc, name):
        self.nc, self.name, self.sems = nc, name, []
        self.ctx = ExitStack()

    def __enter__(self):
        self.ctx.__enter__()
        return self

    def __exit__(self, *exc):
        self.ctx.__exit__(*exc)
        if self.sems:
            self.nc.clear_and_free_semaphores(self.sems)
            self.nc.all_engine_barrier()

    def sb(self, name, shape, dt=F32):
        return self.ctx.enter_context(self.nc.sbuf_tensor(f"{self.name}_{name}", shape, dt))

    def ps(self, name, shape, dt=F32):
        return self.ctx.enter_context(self.nc.psum_tensor(f"{self.name}_{name}", shape, dt))

    def sem(self, name):
        self.sems.append(self.nc.alloc_semaphore(f"{self.name}_{name}"))
        return self.sems[-1]

    def block(self):
        return self.ctx.enter_context(self.nc.Block())


class Chain:

    def __init__(self, engine, semaphore):
        self.engine, self.semaphore, self.count = engine, semaphore, 0

    def __call__(self, instruction):
        self.count += 1
        instruction.then_inc(self.semaphore, 1)
        self.engine.wait_ge(self.semaphore, self.count)


def bc(ap, shape):
    return ap.broadcast_to(shape)


def normalise(nc, m, tag):
    h, xn, xT, ident, eps = m["h"], m["xn"], m["xT"], m["ident"], m["eps"]
    with Stage(nc, f"ln{tag}") as s:
        mean = s.sb("mean", [P, NT])
        var = s.sb("var", [P, NT])
        std = s.sb("std", [P, NT])
        rstd = s.sb("rstd", [P, NT])
        square = s.sb("square", [P, NT, D])
        turned = [s.ps(f"turned{k}", [P, 512]) for k in range(4)]
        dve = s.sem("dve_step")
        var_ready = s.sem("var_ready")
        std_ready = s.sem("std_ready")
        xn_ready = s.sem("xn_ready")
        turned_ready = s.sem("turned_ready")
        block = s.block()

        @block.vector
        def _(v):
            step = Chain(v, dve)
            step(v.tensor_reduce(mean[:, :], h[:, :, :], AX.X, ALU.add))
            step(v.tensor_scalar(mean[:, :], mean[:, :], 1.0 / D, None, ALU.mult))
            step(v.tensor_tensor(xn[:, :, :], h[:, :, :], bc(mean[:, :].unsqueeze(2), [P, NT, D]), ALU.subtract))
            step(v.tensor_tensor(square[:, :, :], xn[:, :, :], xn[:, :, :], ALU.mult))
            step(v.tensor_reduce(var[:, :], square[:, :, :], AX.X, ALU.add))
            v.tensor_scalar(var[:, :], var[:, :], 1.0 / D, None, ALU.mult).then_inc(var_ready, 1)
            v.wait_ge(std_ready, 1)
            step(v.reciprocal(rstd[:, :], std[:, :]))
            for half in range(2):
                t = slice(half * TB, half * TB + TB)
                v.tensor_tensor(xn[:, t, :], xn[:, t, :], bc(rstd[:, t].unsqueeze(2), [P, TB, D]),
                                ALU.mult).then_inc(xn_ready, 1)
            for k in range(0, 4, 2):
                v.wait_ge(turned_ready, k + 1)
                v.tensor_copy(xT[0:D, k * 512:k * 512 + 512], turned[k][0:D, :])

        @block.scalar
        def _(a):
            a.wait_ge(var_ready, 1)
            a.activation(std[:, :], var[:, :], ACT.Sqrt, bias=eps[:, 0:1]).then_inc(std_ready, 1)
            for k in range(1, 4, 2):
                a.wait_ge(turned_ready, k + 1)
                a.copy(xT[0:D, k * 512:k * 512 + 512], turned[k][0:D, :])

        @block.tensor
        def _(pe):
            for k in range(4):
                if k % 2 == 0:
                    pe.wait_ge(xn_ready, k // 2 + 1)
                for j in range(4):
                    last = pe.transpose(turned[k][0:D, j * P:j * P + P], xn[:, 4 * k + j, :], ident[:, :])
                last.then_inc(turned_ready, 1)


def linear_attention(nc, m, d):
    h, xT = m["h"], m["xT"]
    with Stage(nc, "la") as s:
        w_kv = s.sb("w_kv", [D + 1, 2 * D])
        w_q = s.sb("w_q", [D + 1, D])
        w_fc = s.sb("w_fc", [D, D])
        head_mask = s.sb("head_mask", [D, D])
        vk = s.sb("vk", [P, NT, 2 * D])
        qT = s.sb("qT", [D + 1, T])
        pT = s.sb("pT", [D, B, D])
        fold = s.sb("fold", [D + 1, B, D])
        ps_vk = [s.ps(f"ps_vk{k}", [P, 4, 2 * D]) for k in range(2)]
        ps_q = [s.ps(f"ps_q{k}", [P, 512]) for k in range(2)]
        ps_p = s.ps("ps_p", [P, B, D])
        ps_f = s.ps("ps_f", [P, B, D])
        ps_o = [s.ps(f"ps_o{k}", [P, TB, D]) for k in range(B)]
        loaded = s.sem("loaded")
        vk_made = s.sem("vk_made")
        vk_kept = s.sem("vk_kept")
        q_made = s.sem("q_made")
        q_kept = s.sem("q_kept")
        p_made = s.sem("p_made")
        p_kept = s.sem("p_kept")
        f_made = s.sem("f_made")
        f_kept = s.sem("f_kept")
        o_made = s.sem("o_made")
        ones_set = s.sem("ones_set")
        block = s.block()
        LOADS = 6 * 16

        @block.sync
        def _(sp):
            sp.dma_start(w_kv[:, :], d["la_w_vk"]).then_inc(loaded, 16)
            sp.dma_start(w_q[:, :], d["la_w_q"]).then_inc(loaded, 16)
            sp.dma_start(w_fc[:, :], d["la_w_fc"]).then_inc(loaded, 16)
            sp.dma_start(head_mask[:, :], d["head_mask"]).then_inc(loaded, 16)
            for b in range(B):
                sp.dma_start(fold[D:D + 1, b, :], d["la_b_fc"]).then_inc(loaded, 16)

        @block.tensor
        def _(pe):
            pe.wait_ge(loaded, LOADS)
            for k in range(4):
                if k >= 2:
                    pe.wait_ge(vk_kept, k - 1)
                for j in range(4):
                    t = 4 * k + j
                    last = pe.matmul(ps_vk[k % 2][:, j, :], xT[:, t * P:t * P + P], w_kv[:, :],
                                     start=True, stop=True)
                last.then_inc(vk_made, 1)
            for k in range(4):
                if k >= 2:
                    pe.wait_ge(q_kept, k - 1)
                pe.matmul(ps_q[k % 2][0:D, :], w_q[:, :], xT[:, k * 512:k * 512 + 512],
                          start=True, stop=True).then_inc(q_made, 1)
            pe.wait_ge(vk_kept, 4)
            for b in range(B):
                for j in range(TB):
                    t = b * TB + j
                    last = pe.matmul(ps_p[0:D, b, :], vk[:, t, 0:D], vk[:, t, D:2 * D],
                                     start=(j == 0), stop=(j == TB - 1))
                last.then_inc(p_made, 1)
            for b in range(B):
                pe.wait_ge(p_kept, b + 1)
                pe.matmul(ps_f[0:D, b, :], pT[:, b, :], w_fc[:, :], start=True, stop=True).then_inc(f_made, 1)
            pe.wait_ge(q_kept, 4)
            pe.wait_ge(ones_set, 1)
            for b in range(B):
                pe.wait_ge(f_kept, b + 1)
                for j in range(TB):
                    t = b * TB + j
                    last = pe.matmul(ps_o[b][:, j, :], qT[:, t * P:t * P + P], fold[:, b, :],
                                     start=True, stop=True)
                last.then_inc(o_made, 1)

        @block.vector
        def _(v):
            v.memset(qT[D:D + 1, :], 1.0).then_inc(ones_set, 1)
            for k in range(4):
                v.wait_ge(vk_made, k + 1)
                v.tensor_copy(vk[:, 4 * k:4 * k + 4, :], ps_vk[k % 2][:, :, :]).then_inc(vk_kept, 1)
            v.wait_ge(p_made, B)
            for b in range(B):
                v.tensor_tensor(pT[:, b, :], ps_p[0:D, b, :], head_mask[:, :], ALU.mult).then_inc(p_kept, 1)
            v.wait_ge(f_made, B)
            for b in range(B):
                v.tensor_copy(fold[0:D, b, :], ps_f[0:D, b, :]).then_inc(f_kept, 1)
            for b in range(B):
                v.wait_ge(o_made, b + 1)
                t = slice(b * TB, b * TB + TB)
                v.tensor_tensor(h[:, t, :], h[:, t, :], ps_o[b][:, :, :], ALU.add)

        @block.scalar
        def _(a):
            for k in range(4):
                a.wait_ge(q_made, k + 1)
                a.copy(qT[0:D, k * 512:k * 512 + 512], ps_q[k % 2][0:D, :]).then_inc(q_kept, 1)


RET_GAMMA = 0.96875
RET_SCALE_BASE = 512.0


def retention(nc, m, d):
    h, xT, ident = m["h"], m["xT"], m["ident"]
    HALF = D // 2
    with Stage(nc, "ret") as s:
        w = s.sb("w", [D, 3 * D])
        cos = s.sb("cos", [P, TB, 2, HALF])
        sin = s.sb("sin", [P, TB, 2, HALF])
        decay = s.sb("decay", [P, P])
        k_decay = s.sb("k_decay", [P, 1])
        q_decay = s.sb("q_decay", [D, P])
        qkv = s.sb("qkv", [P, NT, 3 * D])
        rot = s.sb("rot", [P, NT, 2 * D])
        tmp = s.sb("tmp", [P, TB, 2, HALF])
        tmp2 = s.sb("tmp2", [P, TB, 2, HALF])
        kd = s.sb("kd", [P, NT, D])
        qT = s.sb("qT", [D, T])
        qTd = s.sb("qTd", [D, T])
        kT = s.sb("kT", [D, T])
        probs = s.sb("probs", [P, NT, P])
        state = s.sb("state", [D, TB, B, D])
        ps = [s.ps(f"ps{k}", [P, 512]) for k in range(8)]
        loaded = s.sem("loaded")
        qkv_made = s.sem("qkv_made")
        qkv_kept = s.sem("qkv_kept")
        dve = s.sem("dve_step")
        rotated = s.sem("rotated")
        turned = s.sem("turned")
        q_kept = s.sem("q_kept")
        k_kept = s.sem("k_kept")
        qd_kept = s.sem("qd_kept")
        scores_made = s.sem("scores_made")
        probs_kept = s.sem("probs_kept")
        kd_kept = s.sem("kd_kept")
        kv_made = s.sem("kv_made")
        states_kept = s.sem("states_kept")
        out_made = s.sem("out_made")
        block = s.block()
        LOADS = 6 * 16

        def halves(t):
            return t[:, :].rearrange("p (a e c) -> p a e c", a=2, e=2)

        @block.sync
        def _(sp):
            sp.dma_start(w[:, :], d["ret_w"]).then_inc(loaded, 16)
            sp.dma_start(cos[:, :, :, :], d["ret_cos"].rearrange("(t p) a c -> p t a c", p=P)).then_inc(loaded, 16)
            sp.dma_start(sin[:, :, :, :], d["ret_sin"].rearrange("(t p) a c -> p t a c", p=P)).then_inc(loaded, 16)
            sp.dma_start(decay[:, :], d["ret_decay"]).then_inc(loaded, 16)
            sp.dma_start(k_decay[:, :], d["ret_k_decay"]).then_inc(loaded, 16)
            sp.dma_start(q_decay[:, :], d["ret_q_decay"].broadcast_to([D, P])).then_inc(loaded, 16)

        @block.tensor
        def _(pe):
            pe.wait_ge(loaded, LOADS)
            for t in range(NT):
                last = pe.matmul(ps[t // 2][:, (t % 2) * 192:(t % 2) * 192 + 192], xT[0:D, t * P:t * P + P],
                                 w[:, :], start=True, stop=True)
                if t % 2 == 1:
                    last.then_inc(qkv_made, 1)
            for b in range(B):
                pe.wait_ge(rotated, b + 1)
                pe.wait_ge(qkv_kept, NT // 2)
                for g in range(2):
                    for qk in range(2):
                        bank = ps[4 * b + 2 * g + qk]
                        for j in range(4):
                            t = b * TB + 4 * g + j
                            last = pe.transpose(bank[0:D, j * P:j * P + P], rot[:, t, qk * D:qk * D + D], ident[:, :])
                        last.then_inc(turned, 1)
            for g in range(4):
                pe.wait_ge(k_kept, g + 1)
                pe.wait_ge(q_kept, g + 1)
                pe.wait_ge(qd_kept, g + 1)
                for j in range(4):
                    t = 4 * g + j
                    last = pe.matmul(ps[2 * g][:, j * P:j * P + P], kT[:, t * P:t * P + P],
                                     qT[:, t * P:t * P + P], start=True, stop=True)
                last.then_inc(scores_made, 1)
            pe.wait_ge(kd_kept, 1)
            for b in range(B):
                for c in range(TB):
                    t = b * TB + c
                    last = pe.matmul(ps[2 * b + 1][0:D, c * D:c * D + D], kd[:, t, :], qkv[:, t, 2 * D:3 * D],
                                     start=True, stop=True)
            last.then_inc(kv_made, 1)
            pe.wait_ge(states_kept, 1)
            pe.wait_ge(probs_kept, 4)
            for b in range(B):
                for c in range(TB):
                    t = b * TB + c
                    o = ps[4 + 2 * b + 1][:, c * D:c * D + D]
                    last = pe.matmul(o, probs[:, t, :], qkv[:, t, 2 * D:3 * D], start=True, stop=(c == 0))
                    if c > 0:
                        last = pe.matmul(o, qTd[:, t * P:t * P + P], state[:, c, b, :], start=False, stop=True)
                last.then_inc(out_made, 1)

        @block.scalar
        def _(a):
            for k in range(NT // 2):
                a.wait_ge(qkv_made, k + 1)
                a.copy(qkv[:, 2 * k:2 * k + 2, :],
                       ps[k][:, 0:384].rearrange("p (t c) -> p t c", t=2)).then_inc(qkv_kept, 1)
            for g in range(4):
                a.wait_ge(turned, 2 * g + 1)
                a.copy(qT[:, g * 512:g * 512 + 512], ps[2 * g][0:D, :]).then_inc(q_kept, 1)

        @block.vector
        def _(v):
            step = Chain(v, dve)
            v.wait_ge(loaded, LOADS)
            for b in range(B):
                v.wait_ge(qkv_kept, TB // 2 * (b + 1))
                t = slice(b * TB, b * TB + TB)
                x = qkv[:, t, 0:2 * D].rearrange("p t (a e c) -> p t a e c", a=2, e=2)
                y = rot[:, t, :].rearrange("p t (a e c) -> p t a e c", a=2, e=2)
                x1, x2, y1, y2 = x[:, :, :, 0, :], x[:, :, :, 1, :], y[:, :, :, 0, :], y[:, :, :, 1, :]
                c4, s4, u, w4 = cos[:, :, :, :], sin[:, :, :, :], tmp[:, :, :, :], tmp2[:, :, :, :]
                step(v.tensor_tensor(y1, x1, c4, ALU.mult))
                step(v.tensor_tensor(u, x2, s4, ALU.mult))
                step(v.tensor_tensor(y1, y1, u, ALU.subtract))
                step(v.tensor_tensor(w4, x1, s4, ALU.mult))
                step(v.tensor_tensor(y2, x2, c4, ALU.mult))
                v.tensor_tensor(y2, y2, w4, ALU.add).then_inc(rotated, 1)
            v.wait_ge(rotated, B)
            v.tensor_scalar(kd[:, :, :], rot[:, :, D:2 * D], k_decay[:, 0:1], None, ALU.mult).then_inc(kd_kept, 1)
            for g in range(4):
                v.wait_ge(q_kept, g + 1)
                v.tensor_tensor(qTd[:, g * 512:g * 512 + 512].rearrange("p (j n) -> p j n", j=4),
                                qT[:, g * 512:g * 512 + 512].rearrange("p (j n) -> p j n", j=4),
                                bc(q_decay[:, :].unsqueeze(1), [D, 4, P]), ALU.mult).then_inc(qd_kept, 1)
                v.wait_ge(turned, 2 * g + 2)
                v.tensor_copy(kT[:, g * 512:g * 512 + 512], ps[2 * g + 1][0:D, :]).then_inc(k_kept, 1)
            for g in range(4):
                v.wait_ge(scores_made, g + 1)
                v.tensor_tensor(probs[:, 4 * g:4 * g + 4, :], ps[2 * g][:, :].rearrange("p (j n) -> p j n", j=4),
                                bc(decay[:, :].unsqueeze(1), [P, 4, P]), ALU.mult).then_inc(probs_kept, 1)
            v.wait_ge(kv_made, 1)
            for c in range(1, TB):
                for b in range(B):
                    kv = ps[2 * b + 1][0:D, (c - 1) * D:c * D]
                    if c == 1:
                        step(v.tensor_copy(state[:, c, b, :], kv))
                    else:
                        step(v.scalar_tensor_tensor(state[:, c, b, :], state[:, c - 1, b, :], RET_GAMMA ** P,
                                                    kv, ALU.mult, ALU.add))
            v.engine_nop().then_inc(states_kept, 1)
            for b in range(B):
                v.wait_ge(out_made, b + 1)
                t = slice(b * TB, b * TB + TB)
                v.tensor_tensor(h[:, t, :], h[:, t, :],
                                ps[4 + 2 * b + 1][:, :].rearrange("p (t c) -> p t c", t=TB), ALU.add)


def retention_tables():
    c = {}
    inv_freq = (1.0 / np.float32(10000.0) ** (np.arange(0, D, 2, dtype=np.float32) / np.float32(D))).astype(np.float32)
    pos = np.arange(S, dtype=np.float32)
    ang = pos[:, None] * inv_freq[None, :]
    base = ((np.arange(0, D, 2, dtype=np.float32) + np.float32(0.4 * D)) / np.float32(1.4 * D)).astype(np.float32)
    scale = base[None, :] ** (pos[:, None] / np.float32(RET_SCALE_BASE))
    sin, cos = np.sin(ang), np.cos(ang)
    c["ret_cos"] = np.stack([cos * scale, cos / scale], 1).astype(np.float32)
    c["ret_sin"] = np.stack([sin * scale, sin / scale], 1).astype(np.float32)
    n = np.arange(P, dtype=np.float64)
    diff = n[None, :] - n[:, None]
    c["ret_decay"] = np.where(diff >= 0, RET_GAMMA ** np.maximum(diff, 0), 0.0).astype(np.float32)
    c["ret_k_decay"] = (RET_GAMMA ** (P - n))[:, None].astype(np.float32)
    c["ret_q_decay"] = (RET_GAMMA ** n)[None, :].astype(np.float32)
    return c


MAGIC = 12582912.0
SPLIT = 1536.0
TWO_PI = 6.2831850


def recurrence(nc, m, d):
    h, xT = m["h"], m["xT"]
    with Stage(nc, "rec") as s:
        w_in = s.sb("w_in", [D, 2, P])
        w_out = s.sb("w_out", [P, 2, D])
        par = s.sb("par", [P, 3])
        signs = s.sb("signs", [P, 2])
        ramp = s.sb("ramp", [P, S])
        mod = s.sb("mod", [P, 1])
        gam = s.sb("gam", [P, 1])
        turn = s.sb("turn", [P, 4])
        mod_row = s.sb("mod_row", [P, S])
        ang = s.sb("ang", [P, S])
        rnd = s.sb("rnd", [P, S])
        lo = s.sb("lo", [P, S])
        cosT = s.sb("cosT", [P, S])
        sinT = s.sb("sinT", [P, S])
        bx = s.sb("bx", [P, B, S])
        bx2 = s.sb("bx2", [P, B, S])
        g = s.sb("g", [P, B, S])
        gc = s.sb("gc", [P, B, S])
        gs = s.sb("gs", [P, B, S])
        ps = [s.ps(f"ps{k}", [P, 512]) for k in range(8)]
        loaded = s.sem("loaded")
        acts = s.sem("act_step")
        dve = s.sem("dve_step")
        exps_ready = s.sem("exps_ready")
        angle_ready = s.sem("angle_ready")
        table_ready = s.sem("table_ready")
        bx_made = s.sem("bx_made")
        g_ready = s.sem("g_ready")
        out_made = s.sem("out_made")
        w_ready = s.sem("w_ready")
        block = s.block()
        LOADS = 5 * 16

        @block.sync
        def _(sp):
            sp.dma_start(par[:, :], d["rec_par"]).then_inc(loaded, 16)
            sp.dma_start(signs[:, :], d["rec_signs"]).then_inc(loaded, 16)
            sp.dma_start(ramp[:, :], d["rec_ramp"].broadcast_to([P, S])).then_inc(loaded, 16)
            sp.dma_start(w_in[:, :, :], d["rec_w_in"]).then_inc(loaded, 16)
            sp.dma_start(w_out[:, :, :], d["rec_w_out"]).then_inc(loaded, 16)

        @block.scalar
        def _(a):
            step = Chain(a, acts)
            a.wait_ge(loaded, LOADS)
            step(a.activation(mod[:, :], par[:, 0:1], ACT.Exp))
            step(a.activation(mod[:, :], mod[:, :], ACT.Exp, scale=-1.0))
            a.activation(turn[:, 0:1], par[:, 1:2], ACT.Exp).then_inc(exps_ready, 1)
            a.activation(gam[:, :], par[:, 2:3], ACT.Exp).then_inc(exps_ready, 1)
            a.wait_ge(angle_ready, 1)
            a.activation(sinT[:, :], ang[:, :], ACT.Sin, scale=TWO_PI).then_inc(table_ready, 1)
            a.wait_ge(angle_ready, 2)
            a.activation(cosT[:, :], lo[:, :], ACT.Sin, scale=TWO_PI).then_inc(table_ready, 1)

        @block.tensor
        def _(pe):
            pe.wait_ge(loaded, LOADS)
            for k in range(4):
                for form in range(2):
                    last = pe.matmul(ps[2 * k + form][:, :], w_in[:, form, :], xT[0:D, k * 512:k * 512 + 512],
                                     start=True, stop=True)
            last.then_inc(bx_made, 1)
            pe.wait_ge(w_ready, 2)
            for b in range(B):
                pe.wait_ge(g_ready, b + 1)
                for j in range(TB):
                    o = ps[b][:, j * D:j * D + D]
                    pe.matmul(o, gc[:, b, j * P:j * P + P], w_out[:, 0, :], start=True, stop=False)
                    last = pe.matmul(o, gs[:, b, j * P:j * P + P], w_out[:, 1, :], start=False, stop=True)
                last.then_inc(out_made, 1)

        @block.vector
        def _(v):
            step = Chain(v, dve)
            v.wait_ge(loaded, LOADS)
            v.tensor_scalar(w_out[:, 0, :], w_out[:, 0, :], signs[:, 0:1], None, ALU.mult).then_inc(w_ready, 1)
            v.tensor_scalar(w_out[:, 1, :], w_out[:, 1, :], signs[:, 1:2], None, ALU.mult).then_inc(w_ready, 1)
            v.wait_ge(exps_ready, 2)
            step(v.tensor_scalar(turn[:, 0:1], turn[:, 0:1], 1.0 / (2 * np.pi), None, ALU.mult))
            step(v.tensor_scalar(turn[:, 1:2], turn[:, 0:1], MAGIC, MAGIC, ALU.add, ALU.subtract))
            step(v.tensor_tensor(turn[:, 0:1], turn[:, 0:1], turn[:, 1:2], ALU.subtract))
            step(v.tensor_scalar(turn[:, 2:3], turn[:, 0:1], SPLIT, SPLIT, ALU.add, ALU.subtract))
            step(v.tensor_tensor(turn[:, 3:4], turn[:, 0:1], turn[:, 2:3], ALU.subtract))
            step(v.tensor_scalar(ang[:, :], ramp[:, :], turn[:, 2:3], None, ALU.mult))
            step(v.tensor_scalar(rnd[:, :], ang[:, :], MAGIC, MAGIC, ALU.add, ALU.subtract))
            step(v.tensor_tensor(ang[:, :], ang[:, :], rnd[:, :], ALU.subtract))
            step(v.tensor_scalar(lo[:, :], ramp[:, :], turn[:, 3:4], None, ALU.mult))
            step(v.tensor_tensor(lo[:, :], ang[:, :], lo[:, :], ALU.add))
            step(v.tensor_scalar(rnd[:, :], lo[:, :], MAGIC, MAGIC, ALU.add, ALU.subtract))
            v.tensor_tensor(ang[:, :], lo[:, :], rnd[:, :], ALU.subtract).then_inc(angle_ready, 1)
            v.wait_ge(angle_ready, 1)
            step(v.tensor_scalar(lo[:, :], ang[:, :], 0.25, None, ALU.add))
            step(v.tensor_scalar(rnd[:, :], lo[:, :], MAGIC, MAGIC, ALU.add, ALU.subtract))
            v.tensor_tensor(lo[:, :], lo[:, :], rnd[:, :], ALU.subtract).then_inc(angle_ready, 1)
            step(v.memset(mod_row[:, :], 1.0))
            step(v.tensor_scalar(mod_row[:, :], mod_row[:, :], mod[:, 0:1], None, ALU.mult))
            v.wait_ge(table_ready, 2)
            step(v.tensor_scalar(sinT[:, :], sinT[:, :], signs[:, 0:1], None, ALU.mult))
            v.wait_ge(bx_made, 1)
            for b in range(B):
                for k in range(2):
                    c = slice(k * 512, k * 512 + 512)
                    step(v.scalar_tensor_tensor(bx[:, b, c], ps[4 * b + 2 * k][:, :], gam[:, 0:1], cosT[:, c],
                                                ALU.mult, ALU.mult))
                    step(v.scalar_tensor_tensor(bx2[:, b, c], ps[4 * b + 2 * k + 1][:, :], gam[:, 0:1], sinT[:, c],
                                                ALU.mult, ALU.mult))
                step(v.tensor_tensor(bx[:, b, :], bx[:, b, :], bx2[:, b, :], ALU.add))
            for b in range(B):
                step(v.tensor_tensor_scan(g[:, b, :], mod_row[:, :], bx[:, b, :], 0.0, ALU.mult, ALU.add))
                step(v.tensor_tensor(gc[:, b, :], g[:, b, :], cosT[:, :], ALU.mult))
                v.tensor_tensor(gs[:, b, :], g[:, b, :], sinT[:, :], ALU.mult).then_inc(g_ready, 1)
            for b in range(B):
                v.wait_ge(out_made, b + 1)
                t = slice(b * TB, b * TB + TB)
                v.tensor_tensor(h[:, t, :], h[:, t, :], ps[b][:, :].rearrange("p (t c) -> p t c", t=TB), ALU.add)


def recurrence_tables():
    c = {"rec_ramp": np.arange(S, dtype=np.float32)[None]}
    sg = np.ones((P, 2), np.float32)
    sg[D:, 0] = -1.0
    sg[:, 1] = -1.0
    sg[D:, 1] = 1.0
    c["rec_signs"] = sg
    return c


VOCAB = 64
SCALES = 4
CONV = ((7, 3), (5, 2), (3, 1))
PAIRS = TB // 2


def embed(nc, m, d):
    h, ident = m["h"], m["ident"]
    PAD1, PAD2, PAD3 = (p for _, p in CONV)
    with Stage(nc, "emb") as s:
        amps = s.sb("amps", [P, NT, D])
        scale4 = s.sb("scale4", [P, NT, SCALES])
        center = s.sb("center", [P, NT])
        shift = s.sb("shift", [P, NT])
        inv = s.sb("inv", [P, NT, SCALES])
        pos = s.sb("pos", [P, B, S])
        pos_loaded = s.sem("pos_loaded")
        with Stage(nc, "conv") as c:
            ids = c.sb("ids", [P, B, S], I32)
            vocab = c.sb("vocab", [P, 1])
            W1 = S + 2 * PAD1 + 1
            hot = c.sb("hot", [P, B, W1])
            w1 = c.sb("w1", [P, 4, P])
            w2 = c.sb("w2", [P, CONV[1][0], D])
            w3 = c.sb("w3", [D, CONV[2][0]])
            b1 = c.sb("b1", [P, 1])
            b2 = c.sb("b2", [D, 1])
            b3 = c.sb("b3", [P, 1])
            table = c.sb("table", [VOCAB, D + 4])
            widths = c.sb("widths", [P, SCALES])
            weights = c.sb("weights", [P, SCALES])
            where = c.sb("where", [P, NT])
            h1 = c.sb("h1", [P, B, S + 2 * PAD2])
            h2 = c.sb("h2", [D, B, S + 2 * PAD3])
            emb = c.sb("emb", [P, NT, D + 4])
            gate = c.sb("gate", [P, NT])
            amp = c.sb("amp", [P, NT])
            absw = c.sb("absw", [P, NT])
            ps = [c.ps(f"ps{k}", [P, 512]) for k in range(8)]
            names = ["loaded", "hot_set", "hot_ready", "c1_made", "h1_kept", "c2_made", "h2_kept", "emb_made",
                     "emb_kept", "gate_made", "gate_kept", "amp_kept", "dve_step", "pads_set"]
            (loaded, hot_set, hot_ready, c1_made, h1_kept, c2_made, h2_kept, emb_made, emb_kept, gate_made,
             gate_kept, amp_kept, dve, pads_set) = [c.sem(n) for n in names]
            block = c.block()
            LOADS = 13 * 16

            @block.sync
            def _(sp):
                for half in range(2):
                    sp.dma_start(ids[half * D:half * D + D, :, :], d["ids"].unsqueeze(0).broadcast_to([D, B, S])
                                 ).then_inc(loaded, 16)
                for buf, name in ((w1, "emb_w1"), (w2, "emb_w2"), (w3, "emb_w3"), (b1, "emb_b1"), (b2, "emb_b2"),
                                  (table, "emb_table"), (vocab, "vocab2"), (where, "emb_where")):
                    sp.dma_start(buf[tuple([slice(None)] * len(buf.shape))], d[name]).then_inc(loaded, 16)
                for buf, name, n in ((b3, "emb_b3", 1), (widths, "emb_widths", SCALES),
                                     (weights, "emb_weights", SCALES)):
                    sp.dma_start(buf[:, :], d[name].broadcast_to([P, n])).then_inc(loaded, 16)
                sp.dma_start(pos[:, :, :], d["positions"].unsqueeze(0).broadcast_to([P, B, S])).then_inc(pos_loaded, 16)

            @block.gpsimd
            def _(g):
                for b in range(B):
                    g.memset(h1[:, b, 0:PAD2], 0.0)
                    g.memset(h1[:, b, PAD2 + S:], 0.0)
                    g.memset(h2[:, b, 0:PAD3], 0.0)
                    last = g.memset(h2[:, b, PAD3 + S:], 0.0)
                last.then_inc(pads_set, 1)

            @block.vector
            def _(v):
                step = Chain(v, dve)
                v.memset(hot[:, :, :], 0.0).then_inc(hot_set, 1)
                v.wait_ge(hot_set, 1)
                v.wait_ge(loaded, LOADS)
                v.tensor_scalar(hot[0:D, :, PAD1:PAD1 + S], ids[0:D, :, :], vocab[0:D, 0:1], None,
                                ALU.is_equal).then_inc(hot_ready, 1)
                v.tensor_scalar(hot[D:P, :, PAD1 - 1:PAD1 - 1 + S], ids[D:P, :, :], vocab[D:P, 0:1], None,
                                ALU.is_equal).then_inc(hot_ready, 1)
                for k in range(4):
                    v.wait_ge(emb_made, k + 1)
                    v.tensor_copy(emb[:, 4 * k:4 * k + 4, :],
                                  ps[k][:, 0:4 * (D + 4)].rearrange("p (t c) -> p t c", t=4)).then_inc(emb_kept, 1)
                v.wait_ge(emb_kept, 4)
                lp = [emb[:, :, D + k] for k in range(4)]
                step(v.scalar_tensor_tensor(center[:, :], lp[0], 0.05, where[:, :], ALU.mult, ALU.add))
                step(v.tensor_scalar(shift[:, :], lp[3], 0.5, 0.25, ALU.mult, ALU.add))
                step(v.scalar_tensor_tensor(absw[:, :], lp[1], -1.0, lp[1], ALU.mult, ALU.max))
                for k in range(SCALES):
                    step(v.tensor_scalar(inv[:, :, k], absw[:, :], widths[:, k:k + 1], None, ALU.mult))
                step(v.tensor_scalar(inv[:, :, :], inv[:, :, :], 1e-5, None, ALU.add))
                step(v.reciprocal(inv[:, :, :], inv[:, :, :]))
                step(v.tensor_tensor(weights[:, :], weights[:, :], weights[:, :], ALU.mult))
                v.wait_ge(amp_kept, 1)
                for k in range(SCALES):
                    step(v.tensor_scalar(scale4[:, :, k], amp[:, :], weights[:, k:k + 1], None, ALU.mult))
                v.wait_ge(gate_kept, 1)
                step(v.tensor_tensor(amps[:, :, :], emb[:, :, 0:D], bc(gate[:, :].unsqueeze(2), [P, NT, D]), ALU.mult))

            @block.tensor
            def _(pe):
                pe.wait_ge(hot_ready, 2)
                for t in range(NT):
                    b, j = t // TB, t % TB
                    mm = pe.matmul(ps[t // 4][:, (t % 4) * (D + 4):(t % 4 + 1) * (D + 4)],
                                   hot[0:D, b, PAD1 + j * P:PAD1 + j * P + P], table[:, :], start=True, stop=True)
                    if t % 4 == 3:
                        mm.then_inc(emb_made, 1)
                for k in range(4):
                    b, j = k // 2, (k % 2) * 512
                    for tap in range(4):
                        mm = pe.matmul(ps[4 + k][:, :], w1[:, tap, :], hot[:, b, j + 2 * tap:j + 2 * tap + 512],
                                       start=(tap == 0), stop=(tap == 3))
                    mm.then_inc(c1_made, 1)
                pe.wait_ge(emb_kept, 4)
                pe.wait_ge(pads_set, 1)
                for k in range(4):
                    b, j = k // 2, (k % 2) * 512
                    pe.wait_ge(h1_kept, 2 * (b + 1))
                    for tap in range(CONV[1][0]):
                        mm = pe.matmul(ps[k][0:D, :], w2[:, tap, :], h1[:, b, j + tap:j + tap + 512],
                                       start=(tap == 0), stop=(tap == CONV[1][0] - 1))
                    mm.then_inc(c2_made, 1)
                pe.wait_ge(h2_kept, 4)
                for t in range(NT):
                    b, j = t // TB, (t % TB) * P
                    for tap in range(CONV[2][0]):
                        mm = pe.matmul(ps[4][:, t:t + 1], h2[:, b, j + tap:j + tap + P], w3[:, tap:tap + 1],
                                       start=(tap == 0), stop=(tap == CONV[2][0] - 1))
                mm.then_inc(gate_made, 1)

            @block.scalar
            def _(a):
                for k in range(4):
                    b, j = k // 2, (k % 2) * 512
                    a.wait_ge(c1_made, k + 1)
                    a.activation(h1[:, b, PAD2 + j:PAD2 + j + 512], ps[4 + k][:, :], ACT.Gelu,
                                 bias=b1[:, 0:1]).then_inc(h1_kept, 1)
                for k in range(4):
                    b, j = k // 2, (k % 2) * 512
                    a.wait_ge(c2_made, k + 1)
                    a.activation(h2[:, b, PAD3 + j:PAD3 + j + 512], ps[k][0:D, :], ACT.Gelu,
                                 bias=b2[:, 0:1]).then_inc(h2_kept, 1)
                a.wait_ge(emb_kept, 4)
                a.activation(amp[:, :], emb[:, :, D + 2], ACT.Sigmoid).then_inc(amp_kept, 1)
                a.wait_ge(gate_made, 1)
                a.activation(gate[:, :], ps[4][:, 0:NT], ACT.Sigmoid, bias=b3[:, 0:1]).then_inc(gate_kept, 1)

        with Stage(nc, "field") as f:
            far = f.sb("far", [P, 2, 2, S])
            bell = f.sb("bell", [P, 2, 2, SCALES, S])
            wave = f.sb("wave", [P, 2, 2, SCALES, S])
            whole = f.sb("whole", [P, SCALES, S])
            amp4 = f.sb("amp4", [P, 2, 2, SCALES, D])
            fieldT = f.sb("fieldT", [D, T])
            ps = [f.ps(f"ps{k}", [P, 512]) for k in range(2)]
            turned = [f.ps(f"turned{k}", [P, 4, D]) for k in range(4)]
            names = ["far_ready", "wave_ready", "squares", "bells", "sines", "basis_ready", "pairs_done",
                     "amp_ready", "dve_step", "field_kept", "turned_ready", "whole_step", "whole_free"]
            (far_ready, wave_ready, squares, bells, sines, basis_ready, pairs_done, amp_ready, dve, field_kept,
             turned_ready, whole_step, whole_free) = [f.sem(n) for n in names]
            block = f.block()
            N = PAIRS

            @block.vector
            def _(v):
                v.wait_ge(pos_loaded, 16)
                v.engine_nop().then_inc(pairs_done, 2)
                v.engine_nop().then_inc(whole_free, 1)
                with v.Fori(0, B) as b:
                    def angles(p):
                        r = p % 2
                        v.wait_ge(pairs_done, b * N + (p + 1))
                        for u in range(2):
                            t = b * TB + (2 * p + u)
                            v.tensor_scalar(far[:, r, u, :], pos[:, bass.ds(b, 1), :].rearrange("p b s -> p (b s)"),
                                            center[:, bass.ds(t, 1)], None, ALU.subtract).then_inc(far_ready, 1)
                            for k in range(SCALES):
                                v.tensor_scalar(amp4[:, r, u, k, :], amps[:, bass.ds(t, 1), :].rearrange("p t c -> p (t c)"),
                                                scale4[:, bass.ds(t, 1), k], None, ALU.mult).then_inc(amp_ready, 1)
                            v.wait_ge(far_ready, b * (2 * N) + (2 * p + u + 1))
                            for k in range(SCALES):
                                w = v.tensor_scalar(wave[:, r, u, k, :], far[:, r, u, :], inv[:, bass.ds(t, 1), k],
                                                    shift[:, bass.ds(t, 1)], ALU.mult, ALU.add)
                            w.then_inc(whole_step, 1)
                            v.wait_ge(whole_step, b * (4 * N) + (4 * p + 2 * u + 1))
                            v.wait_ge(whole_free, b * (2 * N) + (2 * p + u + 1))
                            v.tensor_scalar(whole[:, :, :], wave[:, r, u, :, :], MAGIC, MAGIC, ALU.add,
                                            ALU.subtract).then_inc(whole_step, 1)
                            v.wait_ge(whole_step, b * (4 * N) + (4 * p + 2 * u + 2))
                            v.tensor_tensor(wave[:, r, u, :, :], wave[:, r, u, :, :], whole[:, :, :],
                                            ALU.subtract).then_inc(whole_free, 1)

                    def basis(p):
                        r = p % 2
                        for u in range(2):
                            v.wait_ge(sines, b * (2 * N) + (2 * p + u + 1))
                            v.tensor_tensor(bell[:, r, u, :, :], bell[:, r, u, :, :], wave[:, r, u, :, :],
                                            ALU.mult).then_inc(basis_ready, 1)

                    angles(0)
                    for p in range(1, N):
                        angles(p)
                        basis(p - 1)
                    basis(N - 1)
                for k in range(4):
                    v.wait_ge(turned_ready, k + 1)
                    v.tensor_copy(h[:, 4 * k:4 * k + 4, :], turned[k][:, :, :])

            @block.scalar
            def _(a):
                with a.Fori(0, B) as b:
                    for p in range(N):
                        r = p % 2
                        a.wait_ge(pairs_done, b * N + (p + 1))
                        for u in range(2):
                            t = b * TB + (2 * p + u)
                            a.wait_ge(far_ready, b * (2 * N) + (2 * p + u + 1))
                            for k in range(SCALES):
                                a.activation(bell[:, r, u, k, :], far[:, r, u, :], ACT.Square,
                                             scale=inv[:, bass.ds(t, 1), k]).then_inc(squares, 1)
                        for u in range(2):
                            a.wait_ge(squares, b * (8 * N) + (8 * p + 4 * u + 4))
                            a.activation(bell[:, r, u, :, :], bell[:, r, u, :, :], ACT.Exp,
                                         scale=-0.5).then_inc(bells, 1)
                        for u in range(2):
                            a.wait_ge(whole_free, b * (2 * N) + (2 * p + u + 2))
                            a.activation(wave[:, r, u, :, :], wave[:, r, u, :, :], ACT.Sin,
                                         scale=TWO_PI).then_inc(sines, 1)
                    a.wait_ge(pairs_done, b * N + (N + 2))
                    for k in range(2):
                        a.copy(fieldT[:, bass.ds(b * S + k * 512, 512)], ps[k][0:D, :]).then_inc(field_kept, 1)

            @block.tensor
            def _(pe):
                pe.wait_ge(pos_loaded, 16)
                with pe.Fori(0, B) as b:
                    pe.wait_ge(field_kept, b * 2)
                    for p in range(N):
                        r = p % 2
                        pe.wait_ge(amp_ready, b * (8 * N) + (8 * p + 8))
                        for u in range(2):
                            pe.wait_ge(basis_ready, b * (2 * N) + (2 * p + u + 1))
                            for k in range(SCALES):
                                for q in range(2):
                                    mm = pe.matmul(ps[q][0:D, :], amp4[:, r, u, k, :],
                                                   bell[:, r, u, k, q * 512:q * 512 + 512],
                                                   start=(p == u == k == 0), stop=(p == N - 1 and u == 1 and k == SCALES - 1))
                        mm.then_inc(pairs_done, 1)
                for k in range(4):
                    pe.wait_ge(field_kept, k + 1)
                    for j in range(4):
                        last = pe.transpose(turned[k][:, j, :], fieldT[:, (4 * k + j) * P:(4 * k + j + 1) * P],
                                            ident[0:D, 0:D])
                    last.then_inc(turned_ready, 1)


def embed_tables():
    c = {"vocab2": np.concatenate([np.arange(VOCAB)] * 2).astype(np.float32)[:, None]}
    pos = np.linspace(0.0, 1.0, S, dtype=np.float32).reshape(TB, P).T
    c["emb_where"] = np.concatenate([pos, pos], 1)
    return c


TREE_DEPTH = 7
NODES = 2 ** (TREE_DEPTH + 1)
NODES_PER_BANK = 512 // D
NODE_CHUNKS = NODES // NODES_PER_BANK
RING = 4


def tree_ffn(nc, m, d):
    h, xT = m["h"], m["xT"]
    with Stage(nc, "tree") as s:
        w1 = s.sb("w1", [D + 1, NODES])
        w2 = s.sb("w2", [D + 1, NODES * D])
        logits = s.sb("logits", [P, NT, NODES])
        right = s.sb("right", [P, NT, NODES])
        mask = s.sb("mask", [P, NT, NODES])
        x_now = s.sb("x_now", [D + 1, 2, P])
        prod = s.sb("prod", [P, RING, NODES_PER_BANK * D])
        acc = s.sb("acc", [P, 2, NODES_PER_BANK * D])
        ps = [s.ps(f"ps{k}", [P, 512]) for k in range(8)]
        loaded = s.sem("loaded")
        w2_loaded = s.sem("w2_loaded")
        logits_made = s.sem("logits_made")
        logits_kept = s.sem("logits_kept")
        dve = s.sem("dve_step")
        abs_kept = s.sem("abs_kept")
        gelu_kept = s.sem("gelu_kept")
        gates_ready = s.sem("gates_ready")
        x_kept = s.sem("x_kept")
        bank_made = s.sem("bank_made")
        products = s.sem("products")
        added = s.sem("added")
        folded = s.sem("folded")
        block = s.block()
        PER = NODE_CHUNKS

        @block.sync
        def _(sp):
            sp.dma_start(w1[:, :], d["tree_w1"]).then_inc(loaded, 16)
            for k in range(4):
                c = slice(k * NODES * D // 4, (k + 1) * NODES * D // 4)
                sp.dma_start(w2[:, c], d["tree_w2"][:, c]).then_inc(w2_loaded, 16)

        @block.tensor
        def _(pe):
            pe.wait_ge(loaded, 16)
            for t in range(NT):
                last = pe.matmul(ps[t // 2][:, (t % 2) * NODES:(t % 2) * NODES + NODES],
                                 xT[:, t * P:t * P + P], w1[:, :], start=True, stop=True)
                if t % 2 == 1:
                    last.then_inc(logits_made, 1)
            pe.wait_ge(logits_kept, NT // 2)
            pe.wait_ge(w2_loaded, 4 * 16)
            with pe.Fori(0, NT // 2) as i:
                for par in range(2):
                    pe.wait_ge(x_kept, i * 2 + (par + 1))
                    for c in range(PER):
                        pe.wait_ge(products, i * (2 * PER) + (par * PER + c + 1))
                        pe.matmul(ps[c % RING][:, :], x_now[:, par, :], w2[:, c * 512:c * 512 + 512],
                                  start=True, stop=True).then_inc(bank_made, 1)

        @block.scalar
        def _(a):
            for k in range(NT // 2):
                a.wait_ge(logits_made, k + 1)
                a.copy(logits[:, 2 * k:2 * k + 2, :],
                       ps[k][:, :].rearrange("p (t n) -> p t n", t=2)).then_inc(logits_kept, 1)
            a.wait_ge(gates_ready, 1)
            a.activation(logits[:, :, :], logits[:, :, :], ACT.Abs).then_inc(abs_kept, 1)
            a.wait_ge(abs_kept, 1)
            a.activation(logits[:, :, :], logits[:, :, :], ACT.Gelu).then_inc(gelu_kept, 1)
            a.copy(x_now[:, 0, :], xT[:, 0:P]).then_inc(x_kept, 1)
            with a.Fori(0, NT // 2 - 1) as i:
                a.wait_ge(products, i * (2 * PER) + RING)
                a.copy(x_now[:, 1, :], xT[:, bass.ds(i * (2 * P) + P, P)]).then_inc(x_kept, 1)
                a.wait_ge(products, i * (2 * PER) + (RING + PER))
                a.copy(x_now[:, 0, :], xT[:, bass.ds(i * (2 * P) + 2 * P, P)]).then_inc(x_kept, 1)
            a.wait_ge(products, (NT - 2) * PER + RING)
            a.copy(x_now[:, 1, :], xT[:, (NT - 1) * P:NT * P]).then_inc(x_kept, 1)

        @block.vector
        def _(v):
            step = Chain(v, dve)
            v.wait_ge(logits_kept, NT // 2)
            step(v.tensor_scalar(right[:, :, :], logits[:, :, :], 0.0, None, ALU.is_gt))
            step(v.memset(mask[:, :, NODES - 1:NODES], 0.0))
            v.memset(mask[:, :, 0:1], 1.0).then_inc(gates_ready, 1)
            v.wait_ge(gates_ready, 1)
            for level in range(TREE_DEPTH):
                n = 2 ** level
                own = slice(n - 1, 2 * n - 1)
                kids = mask[:, :, 2 * n - 1:4 * n - 1].rearrange("p t (k c) -> p t k c", c=2)
                step(v.tensor_tensor(kids[:, :, :, 1], mask[:, :, own], right[:, :, own], ALU.mult))
                step(v.tensor_tensor(kids[:, :, :, 0], mask[:, :, own], kids[:, :, :, 1], ALU.subtract))
            v.wait_ge(gelu_kept, 1)
            step(v.tensor_tensor(mask[:, :, :], mask[:, :, :], logits[:, :, :], ALU.mult))
            v.engine_nop().then_inc(products, RING)
            with v.Fori(0, NT // 2) as i:
                for par in range(2):
                    for c in range(PER):
                        q = par * PER + c
                        gate = mask[:, bass.ds(i * 2 + par, 1), c * NODES_PER_BANK:(c + 1) * NODES_PER_BANK]
                        gate = gate.rearrange("p t n -> p (t n)").unsqueeze(2).broadcast_to([P, NODES_PER_BANK, D])
                        v.wait_ge(bank_made, i * (2 * PER) + (q + 1))
                        v.wait_ge(added, i * (2 * PER) + (q + 1))
                        v.tensor_tensor(prod[:, c % RING, :].rearrange("p (n o) -> p n o", o=D),
                                        ps[c % RING][:, :].rearrange("p (n o) -> p n o", o=D), gate,
                                        ALU.mult).then_inc(products, 1)

        @block.gpsimd
        def _(g):
            g.engine_nop().then_inc(added, RING)
            with g.Fori(0, NT // 2) as i:
                for par in range(2):
                    for c in range(1, PER):
                        q = par * PER + c
                        g.wait_ge(products, i * (2 * PER) + (q + 1 + RING))
                        if c == 1:
                            g.tensor_tensor(acc[:, par, :], prod[:, 0, :], prod[:, 1, :],
                                            ALU.add).then_inc(added, 2)
                        else:
                            g.wait_ge(added, i * (2 * PER) + (q + RING))
                            g.tensor_tensor(acc[:, par, :], acc[:, par, :], prod[:, c % RING, :],
                                            ALU.add).then_inc(added, 1)
                    g.wait_ge(added, i * (2 * PER) + ((par + 1) * PER + RING))
                    for f, n in enumerate((256, 128, 64)):
                        g.tensor_tensor(acc[:, par, 0:n], acc[:, par, 0:n], acc[:, par, n:2 * n],
                                        ALU.add).then_inc(folded, 1)
                        g.wait_ge(folded, i * 6 + (par * 3 + f + 1))
                    now = h[:, bass.ds(i * 2 + par, 1), :].rearrange("p t c -> p (t c)")
                    g.tensor_tensor(now, now, acc[:, par, 0:D], ALU.add)


GROUPS = 4


def run_experts(nc, m, d, name, per_group, gates, add_x):
    h, xn, xT = m["h"], m["xn"], m["xT"]
    E = GROUPS * per_group
    HID = P // per_group
    with Stage(nc, name) as s:
        w1 = s.sb("w1", [D + 1, GROUPS, P])
        w2 = s.sb("w2", [P, GROUPS, D])
        b2 = s.sb("b2", [P, E, D])
        hid = s.sb("hid", [P, 2, GROUPS, 512])
        y = s.sb("y", [P, 2, E, D])
        yg = s.sb("yg", [P, 2, E, D])
        total = s.sb("total", [P, 2, D])
        ps_h = [s.ps(f"ps_h{k}", [P, 512]) for k in range(4)]
        ps_y = [[s.ps(f"ps_y{k}_{r}", [P, 512]) for r in range(per_group)] for k in range(2)]
        loaded = s.sem("loaded")
        hid_made = s.sem("hid_made")
        hid_kept = s.sem("hid_kept")
        y_made = s.sem("y_made")
        y_kept = s.sem("y_kept")
        dve = s.sem("dve_step")
        block = s.block()

        @block.sync
        def _(sp):
            sp.dma_start(w1[:, :, :], d[f"{name}_w1"]).then_inc(loaded, 16)
            sp.dma_start(w2[:, :, :], d[f"{name}_w2"]).then_inc(loaded, 16)
            sp.dma_start(b2[:, :, :], d[f"{name}_b2"].broadcast_to([P, E, D])).then_inc(loaded, 16)

        @block.tensor
        def _(pe):
            pe.wait_ge(loaded, 3 * 16)

            def hidden(k):
                for g in range(GROUPS):
                    if k >= 1:
                        pe.wait_ge(hid_kept, (k - 1) * GROUPS + g + 1)
                    pe.matmul(ps_h[g][:, :], w1[:, g, :], xT[:, k * 512:k * 512 + 512],
                              start=True, stop=True).then_inc(hid_made, 1)

            hidden(0)
            for k in range(4):
                if k < 3:
                    hidden(k + 1)
                pe.wait_ge(hid_kept, (k + 1) * GROUPS)
                for j in range(4):
                    t = 4 * k + j
                    if t >= 2:
                        pe.wait_ge(y_kept, t - 1)
                    for e in range(E):
                        g, r = e // per_group, (e % per_group) * HID
                        mm = pe.matmul(ps_y[t % 2][e % per_group][:, g * D:g * D + D],
                                       hid[r:r + HID, k % 2, g, j * P:j * P + P], w2[r:r + HID, g, :],
                                       start=True, stop=True)
                    mm.then_inc(y_made, 1)

        @block.scalar
        def _(a):
            for k in range(4):
                for g in range(GROUPS):
                    a.wait_ge(hid_made, k * GROUPS + g + 1)
                    if k >= 2:
                        a.wait_ge(y_made, 4 * (k - 1))
                    a.activation(hid[:, k % 2, g, :], ps_h[g][:, :], ACT.Gelu).then_inc(hid_kept, 1)

        @block.vector
        def _(v):
            step = Chain(v, dve)
            v.wait_ge(loaded, 3 * 16)
            for t in range(NT):
                r = t % 2
                v.wait_ge(y_made, t + 1)
                for q in range(per_group):
                    mine = y[:, r, :, :].rearrange("p (g q) o -> p g q o", q=per_group)[:, :, q, :]
                    add = v.tensor_tensor(mine, ps_y[r][q][:, 0:GROUPS * D].rearrange("p (g o) -> p g o", g=GROUPS),
                                          b2[:, :, :].rearrange("p (g q) o -> p g q o", q=per_group)[:, :, q, :],
                                          ALU.add)
                add.then_inc(y_kept, 1)
                v.wait_ge(y_kept, t + 1)
                step(v.tensor_tensor(yg[:, r, :, :], y[:, r, :, :], bc(gates[:, t, :].unsqueeze(2), [P, E, D]),
                                     ALU.mult))
                step(v.tensor_reduce(total[:, r, :], yg[:, r, :, :].rearrange("p e o -> p o e"), AX.X, ALU.add))
                step(v.tensor_tensor(h[:, t, :], h[:, t, :], total[:, r, :], ALU.add))
            if add_x:
                v.tensor_tensor(h[:, :, :], h[:, :, :], xn[:, :, :], ALU.add)


def experts_eight(nc, m, d):
    xT = m["xT"]
    E = 8
    with Stage(nc, "route8") as outer:
        gates = outer.sb("gates", [P, NT, E])
        with Stage(nc, "route") as s:
            w = s.sb("w", [D, E])
            order = s.sb("order", [P, E])
            probs = s.sb("probs", [P, NT, E])
            best = [s.sb(f"best{k}", [P, NT]) for k in range(2)]
            picks = [s.sb(f"pick{k}", [P, NT, E]) for k in range(2)]
            rest = s.sb("rest", [P, NT, E])
            eq = s.sb("eq", [P, NT, E])
            one = s.sb("one", [P, NT])
            ps = s.ps("ps", [P, NT, E])
            loaded = s.sem("loaded")
            made = s.sem("made")
            dve = s.sem("dve_step")
            centred = s.sem("centred")
            exps = s.sem("exps")
            block = s.block()

            @block.sync
            def _(sp):
                sp.dma_start(w[:, :], d["route8_w"]).then_inc(loaded, 16)
                sp.dma_start(order[:, :], d["order8"].broadcast_to([P, E])).then_inc(loaded, 16)

            @block.tensor
            def _(pe):
                pe.wait_ge(loaded, 32)
                for t in range(NT):
                    mm = pe.matmul(ps[:, t, :], xT[0:D, t * P:t * P + P], w[:, :], start=True, stop=True)
                mm.then_inc(made, 1)

            @block.scalar
            def _(a):
                a.wait_ge(centred, 1)
                a.activation(probs[:, :, :], probs[:, :, :], ACT.Exp).then_inc(exps, 1)

            @block.vector
            def _(v):
                step = Chain(v, dve)
                v.wait_ge(loaded, 32)
                v.wait_ge(made, 1)
                wide = [P, NT, E]
                step(v.tensor_reduce(one[:, :], ps[:, :, :], AX.X, ALU.max))
                v.tensor_tensor(probs[:, :, :], ps[:, :, :], bc(one[:, :].unsqueeze(2), wide),
                                ALU.subtract).then_inc(centred, 1)
                v.wait_ge(exps, 1)
                step(v.tensor_reduce(one[:, :], probs[:, :, :], AX.X, ALU.add))
                step(v.reciprocal(one[:, :], one[:, :]))
                step(v.tensor_tensor(probs[:, :, :], probs[:, :, :], bc(one[:, :].unsqueeze(2), wide), ALU.mult))
                two_best(v, step, probs, best, rest, eq, picks, order, E)
                step(v.tensor_tensor(one[:, :], best[0][:, :], best[1][:, :], ALU.add))
                step(v.tensor_scalar(one[:, :], one[:, :], 1e-12, None, ALU.max))
                step(v.reciprocal(one[:, :], one[:, :]))
                step(v.tensor_tensor(gates[:, :, :], picks[0][:, :, :], picks[1][:, :, :], ALU.add))
                step(v.tensor_tensor(gates[:, :, :], gates[:, :, :], probs[:, :, :], ALU.mult))
                step(v.tensor_tensor(gates[:, :, :], gates[:, :, :], bc(one[:, :].unsqueeze(2), wide), ALU.mult))
        run_experts(nc, m, d, "moe8", 2, gates, True)


def two_best(v, step, values, best, rest, eq, picks, order, n):
    wide = [P, NT, n]
    row = bc(order[:, 0:n].unsqueeze(1), wide)
    left = values
    for k in range(2):
        step(v.tensor_reduce(best[k][:, :], left[:, :, :], AX.X, ALU.max))
        step(v.tensor_tensor(eq[:, :, :], left[:, :, :], bc(best[k][:, :].unsqueeze(2), wide), ALU.is_equal))
        step(v.tensor_tensor(eq[:, :, :], eq[:, :, :], row, ALU.mult))
        step(v.tensor_reduce(rest[:, :, 0], eq[:, :, :], AX.X, ALU.max))
        step(v.tensor_tensor(picks[k][:, :, :], row, bc(rest[:, :, 0:1], wide), ALU.is_equal))
        if k == 0:
            left = picks[1]
            step(v.scalar_tensor_tensor(left[:, :, :], picks[0][:, :, :], -1e30, values[:, :, :],
                                        ALU.mult, ALU.add))


HAAR_LEVELS = 3
HAAR = 2 ** HAAR_LEVELS - 1
INV_ROUNDS = 38
NEG = -1e30


def pseudo_inverse(nc, m, d):
    inv_wT = m["inv_wT"]
    with Stage(nc, "pinv") as s:
        w = s.sb("w", [D, D])
        wT = s.sb("wT", [D, P])
        square = s.sb("square", [D, D])
        norm = s.sb("norm", [D, 2])
        ones = s.sb("ones", [D, D])
        two = s.sb("two", [D, D])
        x = s.sb("x", [D, D])
        xT = s.sb("xT", [D, P])
        r = s.sb("r", [D, P])
        ps_n = s.ps("ps_n", [P, 512])
        ps_r = s.ps("ps_r", [P, 512])
        ps_x = s.ps("ps_x", [P, 512])
        ps_y = s.ps("ps_y", [P, 512])
        loaded = s.sem("loaded")
        dve = s.sem("dve_step")
        norm_ready = s.sem("norm_ready")
        norm_made = s.sem("norm_made")
        x_ready = s.sem("x_ready")
        xT_ready = s.sem("xT_ready")
        r_made = s.sem("r_made")
        r_ready = s.sem("r_ready")
        x_made = s.sem("x_made")
        block = s.block()

        @block.sync
        def _(sp):
            sp.dma_start(w[:, :], d["near_w_q"]).then_inc(loaded, 16)
            sp.dma_start(wT[:, 0:D], d["near_w_qT"]).then_inc(loaded, 16)
            sp.dma_start(two[:, :], d["two_ident"]).then_inc(loaded, 16)

        @block.vector
        def _(v):
            step = Chain(v, dve)
            v.wait_ge(loaded, 3 * 16)
            step(v.memset(ones[:, :], 1.0))
            for wide in (wT, xT, r):
                step(v.memset(wide[:, D:P], 0.0))
            step(v.tensor_tensor(square[:, :], w[:, :], w[:, :], ALU.mult))
            v.tensor_reduce(norm[:, 0:1], square[:, :], AX.X, ALU.add).then_inc(norm_ready, 1)
            v.wait_ge(norm_made, 1)
            step(v.reciprocal(norm[:, 1:2], ps_n[0:D, 0:1]))
            v.tensor_scalar(x[:, :], wT[:, 0:D], norm[:, 1:2], None, ALU.mult).then_inc(x_ready, 1)
            v.tensor_scalar(xT[:, 0:D], w[:, :], norm[:, 1:2], None, ALU.mult).then_inc(xT_ready, 1)
            with v.Fori(0, INV_ROUNDS) as i:
                v.wait_ge(r_made, i + 1)
                v.tensor_tensor(r[:, 0:D], two[:, :], ps_r[0:D, 0:D], ALU.subtract).then_inc(r_ready, 1)
                v.wait_ge(x_made, i * 2 + 2)
                v.tensor_copy(x[:, :], ps_x[0:D, 0:D]).then_inc(x_ready, 1)
                v.tensor_copy(xT[:, 0:D], ps_y[0:D, 0:D]).then_inc(xT_ready, 1)
            v.wait_ge(xT_ready, INV_ROUNDS + 1)
            v.tensor_copy(inv_wT[:, :], xT[:, 0:D])

        @block.tensor
        def _(pe):
            pe.wait_ge(norm_ready, 1)
            pe.matmul(ps_n[0:D, 0:1], ones[:, :], norm[:, 0:1], start=True, stop=True).then_inc(norm_made, 1)
            with pe.Fori(0, INV_ROUNDS) as i:
                pe.wait_ge(x_ready, i + 1)
                pe.matmul(ps_r[:, 0:D], wT[:, :], x[:, :], start=True, stop=True).then_inc(r_made, 1)
                pe.wait_ge(xT_ready, i + 1)
                pe.wait_ge(r_ready, i + 1)
                pe.matmul(ps_x[:, 0:D], xT[:, :], r[:, 0:D], start=True, stop=True).then_inc(x_made, 1)
                pe.matmul(ps_y[:, 0:D], r[:, :], xT[:, 0:D], start=True, stop=True).then_inc(x_made, 1)


def wavelet_attention(nc, m, d):
    h, xT, ident, inv_wT = m["h"], m["xT"], m["ident"], m["inv_wT"]
    HALF = D // 2
    with Stage(nc, "wav") as s:
        w = s.sb("w", [D, 3 * D])
        w_v = s.sb("w_v", [D, D])
        w_oT = s.sb("w_oT", [D, D])
        cos = s.sb("cos", [P, TB, 2, HALF])
        sin = s.sb("sin", [P, TB, 2, HALF])
        haar = s.sb("haar", [P, TB, HAAR])
        haar_blockT = s.sb("haar_blockT", [HAAR, TB])
        count = s.sb("count", [P, TB, TB])
        hide = s.sb("hide", [P, TB, TB])
        before = s.sb("before", [P, TB, TB])
        seen = s.sb("seen", [P, TB, 2])
        earlier = s.sb("earlier", [P, P])
        one_block = s.sb("one_block", [P, TB, TB])
        qkv = s.sb("qkv", [P, NT, 3 * D])
        rot = s.sb("rot", [P, NT, 2 * D])
        tmp = s.sb("tmp", [P, TB, 2, HALF])
        tmp2 = s.sb("tmp2", [P, TB, 2, HALF])
        square = s.sb("square", [P, NT, 2 * D])
        norm = s.sb("norm", [P, NT, 2])
        inv_norm = s.sb("inv_norm", [P, NT, 2])
        coef = s.sb("coef", [HAAR, B, 2 * D])
        qf = s.sb("qf", [D, B, TB])
        kf = s.sb("kf", [D, B, TB])
        qf_wide = s.sb("qf_wide", [D, B, TB, P])
        blocksum = s.sb("blocksum", [TB, B, D])
        z = s.sb("z", [P, NT, TB])
        e = s.sb("e", [P, NT, TB])
        zsq = s.sb("zsq", [P, NT, TB])
        own = s.sb("own", [P, NT])
        e_own = s.sb("e_own", [P, NT])
        stat = s.sb("stat", [P, NT])
        aux = s.sb("aux", [P, NT])
        var = s.sb("var", [P, NT])
        std = s.sb("std", [P, NT])
        den = s.sb("den", [P, NT])
        eT = s.sb("eT", [TB, NT, P])
        y = s.sb("y", [P, NT, D])
        y2 = s.sb("y2", [P, NT, D])
        ps = [s.ps(f"ps{k}", [P, 512]) for k in range(8)]
        names = ["loaded", "fold_made", "w_ready", "qkv_made", "qkv_kept", "norm_sq", "norm_root", "rot_ready",
                 "coef_made", "coef_kept", "f_made", "f_kept", "score_made", "var_ready", "std_ready", "z_ready",
                 "e_ready", "far_ready", "eT_made", "eT_kept", "sum_kept", "pre_made", "far_made", "blocksum_kept"]
        (loaded, fold_made, w_ready, qkv_made, qkv_kept, norm_sq, norm_root, rot_ready, coef_made, coef_kept,
         f_made, f_kept, score_made, var_ready, std_ready, z_ready, e_ready, far_ready, eT_made, eT_kept,
         sum_kept, pre_made, far_made, blocksum_kept) = [s.sem(n) for n in names]
        dve = s.sem("dve_step")
        block = s.block()
        LOADS = 12 * 16

        @block.sync
        def _(sp):
            sp.dma_start(w[:, 0:D], d["near_w_q"]).then_inc(loaded, 16)
            sp.dma_start(w_v[:, :], d["near_w_v"]).then_inc(loaded, 16)
            sp.dma_start(w_oT[:, :], d["near_w_oT"]).then_inc(loaded, 16)
            sp.dma_start(cos[:, :, :, :], d["wav_cos"].rearrange("(t p) a c -> p t a c", p=P)).then_inc(loaded, 16)
            sp.dma_start(sin[:, :, :, :], d["wav_sin"].rearrange("(t p) a c -> p t a c", p=P)).then_inc(loaded, 16)
            sp.dma_start(haar[:, :, :], d["wav_haar"].rearrange("(t p) w -> p t w", p=P)).then_inc(loaded, 16)
            sp.dma_start(haar_blockT[:, :], d["wav_haar_blockT"]).then_inc(loaded, 16)
            sp.dma_start(count[:, :, :], d["wav_count"]).then_inc(loaded, 16)
            sp.dma_start(hide[:, :, :], d["wav_hide"]).then_inc(loaded, 16)
            sp.dma_start(seen[:, :, :], d["wav_seen"]).then_inc(loaded, 16)
            sp.dma_start(earlier[:, :], d["wav_earlier"]).then_inc(loaded, 16)
            sp.dma_start(before[:, :, :], d["wav_before"]).then_inc(loaded, 16)

        @block.gpsimd
        def _(g):
            g.memset(one_block[:, :, :], 0.0).then_inc(sum_kept, 1)
            g.wait_ge(sum_kept, 1)
            for j in range(TB):
                last = g.memset(one_block[:, j, j:j + 1], 1.0)
            last.then_inc(sum_kept, 1)

        @block.tensor
        def _(pe):
            pe.wait_ge(loaded, LOADS)
            pe.matmul(ps[0][0:D, 0:D], w_v[:, :], w_oT[:, :], start=True, stop=True).then_inc(fold_made, 1)
            pe.wait_ge(w_ready, 2)
            for t in range(NT):
                last = pe.matmul(ps[t // 2][:, (t % 2) * 192:(t % 2) * 192 + 192], xT[0:D, t * P:t * P + P],
                                 w[:, :], start=True, stop=True)
                if t % 2 == 1:
                    last.then_inc(qkv_made, 1)
            pe.wait_ge(qkv_kept, NT // 2)
            pe.wait_ge(sum_kept, 2)
            for b in range(B):
                for j in range(TB):
                    t = b * TB + j
                    last = pe.matmul(ps[4 + b][:, j * D:j * D + D], earlier[:, :], qkv[:, t, 2 * D:3 * D],
                                     start=True, stop=True)
            last.then_inc(pre_made, 1)
            for b in range(B):
                for j in range(TB):
                    t = b * TB + j
                    last = pe.matmul(ps[6][0:TB, b * D:b * D + D], one_block[:, j, :], qkv[:, t, 2 * D:3 * D],
                                     start=(j == 0), stop=(j == TB - 1))
            last.then_inc(pre_made, 1)
            pe.wait_ge(rot_ready, 1)
            for b in range(B):
                for j in range(TB):
                    t = b * TB + j
                    last = pe.matmul(ps[b][0:HAAR, 0:2 * D], haar[:, j, :], rot[:, t, :],
                                     start=(j == 0), stop=(j == TB - 1))
            last.then_inc(coef_made, 1)
            pe.wait_ge(coef_kept, 1)
            for b in range(B):
                for qk in range(2):
                    last = pe.matmul(ps[2][0:D, (2 * b + qk) * TB:(2 * b + qk + 1) * TB],
                                     coef[:, b, qk * D:qk * D + D], haar_blockT[:, :], start=True, stop=True)
            last.then_inc(f_made, 1)
            pe.wait_ge(f_kept, 1)
            for b in range(B):
                for i in range(TB):
                    t = b * TB + i
                    last = pe.matmul(ps[3][:, t * TB:t * TB + TB], qf_wide[:, b, i, :], kf[:, b, :],
                                     start=True, stop=True)
            last.then_inc(score_made, 1)
            pe.wait_ge(far_ready, 1)
            for k in range(4):
                for j in range(4):
                    t = 4 * k + j
                    last = pe.transpose(ps[k][0:TB, j * P:j * P + P], z[:, t, :], ident[:, :])
                last.then_inc(eT_made, 1)
            pe.wait_ge(eT_kept, 4)
            pe.wait_ge(blocksum_kept, 1)
            for b in range(B):
                for j in range(TB):
                    t = b * TB + j
                    last = pe.matmul(ps[b][:, j * D:j * D + D], eT[:, t, :], blocksum[:, b, :],
                                     start=True, stop=True)
            last.then_inc(far_made, 1)

        @block.scalar
        def _(a):
            for k in range(NT // 2):
                a.wait_ge(qkv_made, k + 1)
                a.copy(qkv[:, 2 * k:2 * k + 2, :],
                       ps[k][:, 0:384].rearrange("p (t c) -> p t c", t=2)).then_inc(qkv_kept, 1)
            a.wait_ge(norm_sq, 1)
            a.activation(norm[:, :, :], norm[:, :, :], ACT.Sqrt).then_inc(norm_root, 1)
            a.wait_ge(var_ready, 1)
            a.activation(std[:, :], var[:, :], ACT.Sqrt).then_inc(std_ready, 1)
            a.wait_ge(z_ready, 1)
            a.activation(e[:, :, :], z[:, :, :], ACT.Exp).then_inc(e_ready, 1)
            a.activation(e_own[:, :], own[:, :], ACT.Exp).then_inc(e_ready, 1)
            for k in range(4):
                a.wait_ge(eT_made, k + 1)
                a.copy(eT[:, 4 * k:4 * k + 4, :],
                       ps[k][0:TB, :].rearrange("p (t c) -> p t c", t=4)).then_inc(eT_kept, 1)

        @block.vector
        def _(v):
            step = Chain(v, dve)
            v.wait_ge(fold_made, 1)
            v.tensor_copy(w[:, 2 * D:3 * D], ps[0][0:D, 0:D]).then_inc(w_ready, 1)
            v.tensor_copy(w[:, D:2 * D], inv_wT[:, :]).then_inc(w_ready, 1)
            for b in range(B):
                v.wait_ge(qkv_kept, TB // 2 * (b + 1))
                t = slice(b * TB, b * TB + TB)
                x = qkv[:, t, 0:2 * D].rearrange("p t (a e c) -> p t a e c", a=2, e=2)
                r = rot[:, t, :].rearrange("p t (a e c) -> p t a e c", a=2, e=2)
                x1, x2, r1, r2 = x[:, :, :, 0, :], x[:, :, :, 1, :], r[:, :, :, 0, :], r[:, :, :, 1, :]
                c4, s4, u, w4 = cos[:, :, :, :], sin[:, :, :, :], tmp[:, :, :, :], tmp2[:, :, :, :]
                step(v.tensor_tensor(r1, x1, c4, ALU.mult))
                step(v.tensor_tensor(u, x2, s4, ALU.mult))
                step(v.tensor_tensor(r1, r1, u, ALU.subtract))
                step(v.tensor_tensor(w4, x1, s4, ALU.mult))
                step(v.tensor_tensor(r2, x2, c4, ALU.mult))
                step(v.tensor_tensor(r2, r2, w4, ALU.add))
            step(v.tensor_tensor(square[:, :, :], rot[:, :, :], rot[:, :, :], ALU.mult))
            v.tensor_reduce(norm[:, :, :], square[:, :, :].rearrange("p t (a c) -> p t a c", a=2), AX.X,
                            ALU.add).then_inc(norm_sq, 1)
            v.wait_ge(norm_root, 1)
            step(v.tensor_scalar(norm[:, :, :], norm[:, :, :], 1e-8, None, ALU.add))
            step(v.reciprocal(inv_norm[:, :, :], norm[:, :, :]))
            v.tensor_tensor(rot[:, :, :].rearrange("p t (a c) -> p t a c", a=2),
                            rot[:, :, :].rearrange("p t (a c) -> p t a c", a=2),
                            bc(inv_norm[:, :, :].unsqueeze(3), [P, NT, 2, D]), ALU.mult).then_inc(rot_ready, 1)
            v.wait_ge(rot_ready, 1)
            step(v.tensor_tensor(square[:, :, 0:D], rot[:, :, 0:D], rot[:, :, D:2 * D], ALU.mult))
            step(v.tensor_reduce(own[:, :], square[:, :, 0:D], AX.X, ALU.add))
            v.wait_ge(coef_made, 1)
            for b in range(B):
                last = v.tensor_copy(coef[:, b, :], ps[b][0:HAAR, 0:2 * D])
            last.then_inc(coef_kept, 1)
            v.wait_ge(f_made, 1)
            both = ps[2][0:D, 0:2 * B * TB].rearrange("p (b a i) -> p b a i", b=B, a=2)
            step(v.tensor_copy(qf[:, :, :], both[:, :, 0, :]))
            step(v.tensor_copy(kf[:, :, :], both[:, :, 1, :]))
            v.tensor_copy(qf_wide[:, :, :, :].rearrange("p b i n -> p (b i) n"),
                          bc(qf[:, :, :].rearrange("p b i -> p (b i)").unsqueeze(2),
                             [D, B * TB, P])).then_inc(f_kept, 1)
            v.wait_ge(score_made, 1)

            def per_batch(ap):
                return ap.rearrange("p (b t) j -> p b (t j)", b=B)

            def twice(table):
                return bc(table.rearrange("p t j -> p (t j)").unsqueeze(1), [P, B, TB * TB])

            def rows(ap):
                return ap.rearrange("p (b t) -> p b t", b=B)

            def seen_by(k):
                return bc(seen[:, :, k].unsqueeze(1), [P, B, TB])

            def wide(ap):
                return bc(ap[:, :].unsqueeze(2), [P, NT, TB])

            step(v.tensor_copy(zsq[:, :, :], ps[3][:, 0:NT * TB].rearrange("p (t j) -> p t j", t=NT)))
            step(v.tensor_tensor(rows(own[:, :]), rows(own[:, :]), seen_by(0), ALU.mult))
            for b in range(B):
                t = slice(b * TB, b * TB + TB)
                step(v.tensor_tensor(z[:, t, :], zsq[:, t, :], bc(seen[:, :, 0:1], [P, TB, TB]), ALU.mult))
            step(v.tensor_tensor(per_batch(zsq[:, :, :]), per_batch(z[:, :, :]), twice(count[:, :, :]), ALU.mult))
            step(v.tensor_reduce(stat[:, :], zsq[:, :, :], AX.X, ALU.add))
            step(v.tensor_tensor(stat[:, :], stat[:, :], own[:, :], ALU.add))
            step(v.tensor_tensor(rows(stat[:, :]), rows(stat[:, :]), seen_by(1), ALU.mult))
            step(v.tensor_tensor(z[:, :, :], z[:, :, :], wide(stat), ALU.subtract))
            step(v.tensor_tensor(own[:, :], own[:, :], stat[:, :], ALU.subtract))
            step(v.tensor_tensor(zsq[:, :, :], z[:, :, :], z[:, :, :], ALU.mult))
            step(v.tensor_tensor(per_batch(zsq[:, :, :]), per_batch(zsq[:, :, :]), twice(count[:, :, :]), ALU.mult))
            step(v.tensor_reduce(stat[:, :], zsq[:, :, :], AX.X, ALU.add))
            step(v.tensor_tensor(aux[:, :], own[:, :], own[:, :], ALU.mult))
            step(v.tensor_tensor(stat[:, :], stat[:, :], aux[:, :], ALU.add))
            step(v.tensor_tensor(rows(var[:, :]), rows(stat[:, :]), seen_by(1), ALU.mult))
            v.wait_ge(dve, step.count)
            v.tensor_scalar(var[:, :], var[:, :], 1e-6, None, ALU.max).then_inc(var_ready, 1)
            v.wait_ge(std_ready, 1)
            step(v.reciprocal(stat[:, :], std[:, :]))
            step(v.tensor_tensor(z[:, :, :], z[:, :, :], wide(stat), ALU.mult))
            step(v.tensor_tensor(own[:, :], own[:, :], stat[:, :], ALU.mult))
            step(v.tensor_tensor(per_batch(z[:, :, :]), per_batch(z[:, :, :]), twice(hide[:, :, :]), ALU.add))
            step(v.tensor_reduce(stat[:, :], z[:, :, :], AX.X, ALU.max))
            step(v.tensor_tensor(stat[:, :], stat[:, :], own[:, :], ALU.max))
            step(v.tensor_tensor(own[:, :], own[:, :], stat[:, :], ALU.subtract))
            v.tensor_tensor(z[:, :, :], z[:, :, :], wide(stat), ALU.subtract).then_inc(z_ready, 1)
            v.wait_ge(e_ready, 2)
            step(v.tensor_tensor(per_batch(zsq[:, :, :]), per_batch(e[:, :, :]), twice(count[:, :, :]), ALU.mult))
            step(v.tensor_reduce(den[:, :], zsq[:, :, :], AX.X, ALU.add))
            v.tensor_tensor(per_batch(z[:, :, :]), per_batch(e[:, :, :]), twice(before[:, :, :]),
                            ALU.mult).then_inc(far_ready, 1)
            step(v.tensor_tensor(den[:, :], den[:, :], e_own[:, :], ALU.add))
            step(v.reciprocal(den[:, :], den[:, :]))
            v.wait_ge(pre_made, 2)
            v.tensor_copy(blocksum[:, :, :], ps[6][0:TB, 0:B * D].rearrange("p (b o) -> p b o", b=B)).then_inc(blocksum_kept, 1)
            for b in range(B):
                diag = e[:, b * TB:b * TB + TB, :].rearrange("p t j -> p (t j)")[:, 0:TB * TB:TB + 1]
                t = slice(b * TB, b * TB + TB)
                step(v.tensor_tensor(y[:, t, :], ps[4 + b][:, :].rearrange("p (t o) -> p t o", t=TB),
                                     bc(diag.unsqueeze(2), [P, TB, D]), ALU.mult))
            step(v.tensor_tensor(y2[:, :, :], qkv[:, :, 2 * D:3 * D], bc(e_own[:, :].unsqueeze(2), [P, NT, D]), ALU.mult))
            step(v.tensor_tensor(y[:, :, :], y[:, :, :], y2[:, :, :], ALU.add))
            v.wait_ge(far_made, 1)
            for b in range(B):
                t = slice(b * TB, b * TB + TB)
                step(v.tensor_tensor(y[:, t, :], y[:, t, :], ps[b][:, :].rearrange("p (t o) -> p t o", t=TB), ALU.add))
            step(v.tensor_tensor(y[:, :, :], y[:, :, :], bc(den[:, :].unsqueeze(2), [P, NT, D]), ALU.mult))
            v.tensor_tensor(h[:, :, :], h[:, :, :], y[:, :, :], ALU.add)


def wavelet_tables():
    c = {"two_ident": 2 * np.eye(D, dtype=np.float32)}
    half = D // 2
    inv_freq = (1.0 / 10000.0 ** (np.arange(half, dtype=np.float32) / half)).astype(np.float32)
    ang = np.arange(S, dtype=np.float32)[:, None] * inv_freq[None, :]
    c["wav_cos"] = np.stack([np.cos(ang)] * 2, 1).astype(np.float32)
    c["wav_sin"] = np.stack([np.sin(ang)] * 2, 1).astype(np.float32)
    cols = []
    for level in range(HAAR_LEVELS):
        size = S // 2 ** level
        for k in range(2 ** level):
            v = np.zeros(S, np.float32)
            v[k * size:k * size + size // 2] = 1.0 / np.sqrt(size // 2)
            v[k * size + size // 2:(k + 1) * size] = -1.0 / np.sqrt(size // 2)
            cols.append(v)
    c["wav_haar"] = np.stack(cols, 1)
    c["wav_haar_blockT"] = c["wav_haar"][::P].T
    p, i, j = np.arange(P)[:, None, None], np.arange(TB)[None, :, None], np.arange(TB)[None, None, :]
    count = np.where(j < i, P, np.where(j == i, p, 0))
    c["wav_count"] = count.astype(np.float32)
    c["wav_hide"] = np.where(count > 0, 0.0, NEG).astype(np.float32)
    c["wav_before"] = np.broadcast_to(j < i, (P, TB, TB)).astype(np.float32)
    n = (np.arange(TB)[None, :] * P + np.arange(P)[:, None] + 1).astype(np.float64)
    c["wav_seen"] = np.stack([D ** -0.5 / np.sqrt(n), 1.0 / n], 2).astype(np.float32)
    c["wav_earlier"] = (np.arange(P)[:, None] < np.arange(P)[None, :]).astype(np.float32)
    return c


F16 = mybir.dt.float16
EDGES = 262144
EC = EDGES // P
HG, GE = 4, 4
LO, HI = 32, T // 32
HC = 128
SLOTS = 4
LAST = T - 1
KEY_TILE = P * T


def graph_ffn(nc, m, d):
    with Stage(nc, "graph") as g:
        own = {"key": g.sb("key", [P, EC]), "tid": g.sb("tid", [P, EC]), "hist": g.sb("hist", [P, NT]),
               "rounds": g.sb("rounds", [1, NT + 1], I32), "gates": g.sb("gates", [P, NT, GE]),
               "agg": g.sb("agg", [P, NT, HG, GE + 1])}
        edge_keys(nc, own, d)
        edge_rounds(nc, own, d)
        graph_attention(nc, m, own, d)
        graph_route(nc, own, d)
        run_experts(nc, m, d, "moe4", 1, own["gates"], False)


def edge_keys(nc, own, d):
    key, tid, hist = own["key"], own["tid"], own["hist"]
    with Stage(nc, "keys") as s:
        src = s.sb("src", [P, EC], I32)
        dst = s.sb("dst", [P, EC], I32)
        digit = s.sb("digit", [P, EC], I32)
        srcf = s.sb("srcf", [P, EC])
        dstf = s.sb("dstf", [P, EC])
        near = s.sb("near", [P, EC])
        low = s.sb("low", [P, EC], F16)
        high = s.sb("high", [P, EC], F16)
        hot_lo = s.sb("hot_lo", [P, 2, LO, HC], F16)
        hot_hi = s.sb("hot_hi", [P, 2, HI, HC], F16)
        zero = s.sb("zero", [P, HI], F16)
        ps = s.ps("ps", [LO, 512])
        loaded = s.sem("loaded")
        dve = s.sem("dve_step")
        hot_ready = s.sem("hot_ready")
        hot_used = s.sem("hot_used")
        counted = s.sem("counted")
        zero_set = s.sem("zero_set")
        block = s.block()
        STEPS = EC // HC // 2

        @block.sync
        def _(sp):
            sp.dma_start(src[:, :], d["edges"][0]).then_inc(loaded, 16)
            sp.dma_start(dst[:, :], d["edges"][1]).then_inc(loaded, 16)

        @block.vector
        def _(v):
            step = Chain(v, dve)
            v.memset(zero[:, :], 0.0).then_inc(zero_set, 1)
            v.engine_nop().then_inc(hot_used, 2)
            v.wait_ge(loaded, 32)
            step(v.tensor_copy(srcf[:, :], src[:, :]))
            step(v.tensor_copy(dstf[:, :], dst[:, :]))
            step(v.tensor_scalar(near[:, :], srcf[:, :], float(LAST), None, ALU.is_lt))
            step(v.tensor_scalar(digit[:, :], dst[:, :], LO - 1, None, ALU.bitwise_and))
            step(v.tensor_copy(low[:, :], digit[:, :]))
            step(v.tensor_scalar(digit[:, :], dst[:, :], 5, None, ALU.logical_shift_right))
            step(v.tensor_copy(tid[:, :], digit[:, :]))
            step(v.tensor_scalar(key[:, :], near[:, :], -1024.0, None, ALU.mult))
            step(v.tensor_tensor(high[:, :], tid[:, :], key[:, :], ALU.add))
            step(v.scalar_tensor_tensor(near[:, :], dstf[:, :], float(T), near[:, :], ALU.is_lt, ALU.mult))
            step(v.scalar_tensor_tensor(key[:, :], dstf[:, :], float(T), srcf[:, :], ALU.mult, ALU.add))
            step(v.scalar_tensor_tensor(key[:, :], key[:, :], 1.0, near[:, :], ALU.add, ALU.mult))
            step(v.tensor_scalar(digit[:, :], dst[:, :], 7, None, ALU.logical_shift_right))
            step(v.tensor_copy(tid[:, :], digit[:, :]))
            step(v.scalar_tensor_tensor(tid[:, :], tid[:, :], 1.0, near[:, :], ALU.add, ALU.mult))
            step(v.tensor_scalar(tid[:, :], tid[:, :], -1.0, None, ALU.add))
            with v.Fori(0, STEPS) as i:
                for r in range(2):
                    v.wait_ge(hot_used, i * 2 + (r + 1))
                    cols = bass.ds(i * (2 * HC) + r * HC, HC)
                    for k in range(LO):
                        v.tensor_scalar(hot_lo[:, r, k, :], low[:, cols], float(k), None, ALU.is_equal)
                    for k in range(HI):
                        last = v.tensor_scalar(hot_hi[:, r, k, :], high[:, cols], float(k), None, ALU.is_equal)
                    last.then_inc(hot_ready, 1)
            v.wait_ge(counted, 1)
            for q in range(P // LO):
                v.tensor_copy(hist[q * LO:(q + 1) * LO, :], ps[:, q:HI:P // LO])

        @block.tensor
        def _(pe):
            pe.wait_ge(zero_set, 1)
            pe.matmul(ps[:, 0:HI], zero[:, 0:LO], zero[:, :], start=True, stop=False, skip_group_check=True)
            with pe.Fori(0, STEPS) as i:
                for r in range(2):
                    pe.wait_ge(hot_ready, i * 2 + (r + 1))
                    pe.wait_ge(zero_set, 1)
                    for c in range(HC):
                        mm = pe.matmul(ps[:, 0:HI], hot_lo[:, r, :, c], hot_hi[:, r, :, c],
                                       start=False, stop=False, skip_group_check=True)
                    mm.then_inc(hot_used, 1)
            pe.matmul(ps[:, 0:HI], zero[:, 0:LO], zero[:, :], start=False, stop=True,
                      skip_group_check=True).then_inc(counted, 1)


def edge_rounds(nc, own, d):
    tid, rounds = own["tid"], own["rounds"]
    with Stage(nc, "rounds") as s:
        hit = s.sb("hit", [P, 2, EC])
        count = s.sb("count", [P, NT])
        most = s.sb("most", [P, NT])
        whole = s.sb("whole", [1, NT], I32)
        row = s.sb("row", [1, NT])
        ones = s.sb("ones", [1, NT])
        upto = s.sb("upto", [1, NT + 1])
        dve = s.sem("dve_step")
        counted = s.sem("counted")
        reduced = s.sem("reduced")
        block = s.block()

        @block.vector
        def _(v):
            step = Chain(v, dve)
            for t in range(NT):
                if t >= 2:
                    v.wait_ge(counted, t - 1)
                step(v.tensor_scalar(hit[:, t % 2, :], tid[:, :], float(t), None, ALU.is_equal))
                v.tensor_reduce(count[:, t:t + 1], hit[:, t % 2, :], AX.X, ALU.add).then_inc(counted, 1)
            v.wait_ge(reduced, 1)
            step(v.tensor_scalar(row[:, :], most[0:1, :], 0.125, 3.5 / 8, ALU.mult, ALU.add))
            step(v.tensor_copy(whole[:, :], row[:, :]))
            step(v.tensor_copy(row[:, :], whole[:, :]))
            step(v.tensor_scalar(row[:, :], row[:, :], 1.0, None, ALU.max))
            step(v.memset(ones[:, :], 1.0))
            step(v.memset(upto[:, 0:1], 0.0))
            step(v.tensor_tensor_scan(upto[:, 1:NT + 1], ones[:, :], row[:, :], 0.0, ALU.mult, ALU.add))
            v.tensor_copy(rounds[:, :], upto[:, :])

        @block.gpsimd
        def _(g):
            g.wait_ge(counted, NT)
            g.partition_all_reduce(most[:, :], count[:, :], P, bass.bass_isa.ReduceOp.max).then_inc(reduced, 1)


def graph_attention(nc, m, own, d):
    xT, ident = m["xT"], m["ident"]
    key, tid, hist, rounds, agg = (own[k] for k in ("key", "tid", "hist", "rounds", "agg"))
    with Stage(nc, "gat") as s:
        w = s.sb("w", [D, HG * GE])
        att = s.sb("att", [D, 2, HG * GE])
        w_att = s.sb("w_att", [D, 2, HG])
        prod = s.sb("prod", [D, 2, HG * GE])
        w_src = s.sb("w_src", [D, HG, P])
        feat = s.sb("feat", [P, NT, HG, GE + 1])
        a_dst = s.sb("a_dst", [P, NT, HG])
        a_src = s.sb("a_src", [P, HG, T])
        iota = s.sb("iota", [P, T], F16)
        tiles = s.sb("tiles", [P, NT])
        bases = s.sb("bases", [P, NT])
        loops = s.sb("loops", [P, 2 * T - P], F16)
        identh = s.sb("identh", [P, P], F16)
        work = s.sb("work", [P, EC])
        top = s.sb("top", [P, 8])
        local = s.sb("local", [P, 8])
        place = s.sb("place", [P, 2, 8], I32)
        placef = s.sb("placef", [P, 2, 8])
        hot_d = s.sb("hot_d", [P, SLOTS, P], F16)
        hot_s = s.sb("hot_s", [P, SLOTS, T], F16)
        cnt = s.sb("cnt", [P, 2, T])
        hide = s.sb("hide", [P, T])
        seen = s.sb("seen", [P, HG, T])
        e1 = s.sb("e1", [P, 2, T])
        e2 = s.sb("e2", [P, 2, T])
        turned = s.sb("turned", [P, 2, 4, P])
        mx = s.sb("mx", [P, HG])
        mx2 = s.sb("mx2", [P, HG])
        bias = s.sb("bias", [P, 2, 2, HG])
        spare = s.sb("spare", [P, 64])
        C = [s.ps(f"C{k}", [P, 512]) for k in range(4)]
        ps_t = [s.ps(f"ps_t{k}", [P, 4, P]) for k in range(2)]
        ps_as = [s.ps(f"ps_a{k}", [P, 512]) for k in range(2)]
        ps_a = ps_as[0]
        names = ["loaded", "dve_step", "w_ready", "feat_made", "feat_kept", "src_made", "src_kept", "hots", "hots_used",
                 "near_done", "C_copied", "tile_step", "round_step", "e_ready", "w_max", "weighted",
                 "turns", "turns_kept", "head_done", "agg_kept", "bias_ready"]
        (loaded, dve, w_ready, feat_made, feat_kept, src_made, src_kept, hots, hots_used, near_done, C_copied,
         tile_step, round_step, e_ready, w_max, weighted, turns, turns_kept, head_done, agg_kept,
         bias_ready) = [s.sem(n) for n in names]
        block = s.block()
        LOADS = 7 * 16
        TILE_STEPS, ROUND_STEPS = 10, 6

        @block.sync
        def _(sp):
            sp.dma_start(w[:, :], d["gat_w"]).then_inc(loaded, 16)
            sp.dma_start(att[:, :, :], d["gat_att"].broadcast_to([D, 2, HG * GE])).then_inc(loaded, 16)
            sp.dma_start(iota[:, :], d["iota_nodes"].broadcast_to([P, T])).then_inc(loaded, 16)
            sp.dma_start(tiles[:, :], d["iota_tiles"].broadcast_to([P, NT])).then_inc(loaded, 16)
            sp.dma_start(bases[:, :], d["key_bases"].broadcast_to([P, NT])).then_inc(loaded, 16)
            sp.dma_start(loops[:, :], d["loops"]).then_inc(loaded, 16)
            sp.dma_start(identh[:, :], d["identh"]).then_inc(loaded, 16)

        @block.tensor
        def _(pe):
            pe.wait_ge(loaded, LOADS)
            pe.wait_ge(w_ready, 1)
            for t in range(NT):
                x = xT[0:D, t * P:t * P + P]
                pe.matmul(ps_a[:, t * 20:t * 20 + 16], x, w[:, :], start=True, stop=True)
                mm = pe.matmul(ps_a[:, t * 20 + 16:t * 20 + 20], x, w_att[:, 1, :], start=True, stop=True)
            mm.then_inc(feat_made, 1)
            for hd in range(HG):
                for k in range(4):
                    n = hd * 4 + k
                    if n >= 4:
                        pe.wait_ge(src_kept, n - 3)
                    pe.matmul(C[k][:, :], w_src[:, hd, :], xT[0:D, k * 512:k * 512 + 512],
                              start=True, stop=True).then_inc(src_made, 1)
            pe.wait_ge(src_kept, 16)
            pe.wait_ge(feat_kept, 1)

            def count(t):
                first = pe.value_load(rounds[0:1, bass.ds(t, 1)], min_val=0, max_val=EC * 2)
                end = pe.value_load(rounds[0:1, bass.ds(t + 1, 1)], min_val=1, max_val=EC * 2)
                pe.wait_ge(C_copied, t)
                for k in range(4):
                    pe.matmul(C[k][:, :], identh[:, :], loops[:, bass.ds(t * (-P) + (T - P + k * 512), 512)],
                              start=True, stop=False, skip_group_check=True)
                with pe.Fori(first, end) as r:
                    for e in range(8):
                        pe.wait_ge(hots, r * 8 + (e + 1))
                        for k in range(4):
                            mm = pe.matmul(C[k][:, :], hot_d[:, e % SLOTS, :],
                                           hot_s[:, e % SLOTS, k * 512:k * 512 + 512],
                                           start=False, stop=False, skip_group_check=True)
                        mm.then_inc(hots_used, 1)
                for k in range(4):
                    mm = pe.matmul(C[k][:, 0:1], hot_d[:, 0, :], loops[:, 0:1], start=False, stop=True,
                                   skip_group_check=True)
                mm.then_inc(near_done, 1)

            def sums(t, r):
                def turn(hd, q):
                    pe.wait_ge(turns_kept, t * 16 + (hd * 4 + q + 1))
                    for j in range(4):
                        c = (q * 4 + j) * P
                        mm = pe.transpose(ps_t[q % 2][:, j, :], e1[:, hd % 2, c:c + P], ident[:, :])
                    mm.then_inc(turns, 1)

                for hd in range(HG):
                    pe.wait_ge(weighted, t * HG + (hd + 1))
                    turn(hd, 0)
                    for q in range(4):
                        if q < 3:
                            turn(hd, q + 1)
                        if hd == 0 and q == 0:
                            pe.wait_ge(agg_kept, t + 1)
                        pe.wait_ge(turns_kept, t * 16 + (hd * 4 + q + 3))
                        for j in range(4):
                            u = q * 4 + j
                            mm = pe.matmul(ps_as[r][:, hd * 8:hd * 8 + GE + 1], turned[:, q % 2, j, :],
                                           feat[:, u, hd, :], start=(u == 0), stop=(u == NT - 1))
                    mm.then_inc(head_done, 1)

            count(0)
            with pe.Fori(0, NT // 2 - 1) as i:
                count(i * 2 + 1)
                sums(i * 2, 0)
                count(i * 2 + 2)
                sums(i * 2 + 1, 1)
            count(NT - 1)
            sums(NT - 2, 0)
            sums(NT - 1, 1)

        @block.scalar
        def _(a):
            for n in range(16):
                a.wait_ge(src_made, n + 1)
                a.copy(a_src[:, n // 4, n % 4 * 512:n % 4 * 512 + 512], C[n % 4][:, :]).then_inc(src_kept, 1)

            def weights(t, r):
                def exps(hd):
                    a.wait_ge(bias_ready, t + 1)
                    if not (isinstance(t, int) and t * HG + hd < 2):
                        a.wait_ge(head_done, t * HG + (hd - 1))
                    a.activation(e1[:, hd % 2, :], seen[:, hd, :], ACT.Exp, bias=bias[:, r, 0, hd:hd + 1])
                    a.activation(e2[:, hd % 2, :], seen[:, hd, :], ACT.Exp, bias=bias[:, r, 1, hd:hd + 1],
                                 scale=0.2).then_inc(e_ready, 1)

                exps(0)
                for hd in range(HG):
                    if hd + 1 < HG:
                        exps(hd + 1)
                    for q in range(4):
                        a.wait_ge(turns, t * 16 + (hd * 4 + q + 1))
                        a.copy(turned[:, q % 2, :, :], ps_t[q % 2][:, :, :]).then_inc(turns_kept, 1)

            weights(0, 0)
            with a.Fori(0, NT // 2 - 1) as i:
                weights(i * 2 + 1, 1)
                weights(i * 2 + 2, 0)
            weights(NT - 1, 1)

        @block.gpsimd
        def _(g):
            def weigh(t, r):
                for hd in range(HG):
                    g.wait_ge(w_max, t * HG + (hd + 1))
                    g.tensor_tensor(e1[:, hd % 2, :], e2[:, hd % 2, :], cnt[:, r, :], ALU.mult).then_inc(weighted, 1)

            with g.Fori(0, NT // 2) as i:
                weigh(i * 2, 0)
                weigh(i * 2 + 1, 1)

        @block.vector
        def _(v):
            step = Chain(v, dve)

            sites = [0]

            def carry():
                sites[0] += 1
                v.memset(spare[:, sites[0]:sites[0] + 1], 0.0)

            v.wait_ge(loaded, LOADS)
            for k in range(2):
                step(v.tensor_tensor(prod[:, k, :], w[:, :], att[:, k, :], ALU.mult))
            step(v.tensor_reduce(w_att[:, :, :], prod[:, :, :].rearrange("p k (h e) -> p k h e", h=HG), AX.X, ALU.add))
            v.tensor_copy(w_src[:, :, :], bc(w_att[:, 0, :].unsqueeze(2), [D, HG, P])).then_inc(w_ready, 1)
            v.memset(feat[:, :, :, GE:GE + 1], 1.0)
            v.wait_ge(feat_made, 1)
            both = ps_a[:, 0:NT * 20].rearrange("p (t c) -> p t c", t=NT)
            for hd in range(HG):
                v.tensor_copy(feat[:, :, hd, 0:GE], both[:, :, hd * GE:hd * GE + GE])
            v.tensor_copy(a_dst[:, :, :], both[:, :, 16:20]).then_inc(feat_kept, 1)
            v.wait_ge(feat_kept, 1)
            v.wait_ge(src_kept, 16)
            v.engine_nop().then_inc(hots_used, SLOTS)
            v.engine_nop().then_inc(turns_kept, 2)
            v.engine_nop().then_inc(round_step, 1)
            v.engine_nop().then_inc(agg_kept, 2)

            def largest(t, hd):
                v.wait_ge(e_ready, t * HG + (hd + 1))
                v.tensor_tensor(e2[:, hd % 2, :], e1[:, hd % 2, :], e2[:, hd % 2, :], ALU.max).then_inc(w_max, 1)

            def keep(t, r):
                v.wait_ge(head_done, t * HG + HG)
                v.tensor_copy(agg[:, bass.ds(t, 1), :, :].rearrange("p t h c -> p (t h) c"),
                              ps_as[r][:, 0:HG * 8].rearrange("p (h c) -> p h c", h=HG)[:, :, 0:GE + 1]
                              ).then_inc(agg_kept, 1)

            def tile(t, r, before, kept):
                first = v.value_load(rounds[0:1, bass.ds(t, 1)], min_val=0, max_val=EC * 2)
                end = v.value_load(rounds[0:1, bass.ds(t + 1, 1)], min_val=1, max_val=EC * 2)
                count = 0

                def after(ins):
                    nonlocal count
                    count += 1
                    ins.then_inc(tile_step, 1)
                    v.wait_ge(tile_step, t * TILE_STEPS + count)

                after(v.scalar_tensor_tensor(work[:, :], tid[:, :], tiles[:, bass.ds(t, 1)], key[:, :],
                                             ALU.is_equal, ALU.mult))
                carry()
                with v.Fori(first, end) as n:
                    steps = 0

                    def then(ins):
                        nonlocal steps
                        steps += 1
                        ins.then_inc(round_step, 1)
                        v.wait_ge(round_step, n * ROUND_STEPS + (steps + 1))

                    v.wait_ge(round_step, n * ROUND_STEPS + 1)
                    carry()
                    then(v.max(top[:, :], work[:, :]))
                    carry()
                    then(v.match_replace(work[:, :], top[:, :], work[:, :], 0.0))
                    then(v.tensor_scalar(local[:, :], top[:, :], bases[:, bass.ds(t, 1)], None, ALU.subtract))
                    then(v.tensor_copy(place[:, 0, :], local[:, :]))
                    v.tensor_scalar(place[:, 1, :], place[:, 0, :], T - 1, None, ALU.bitwise_and)
                    then(v.tensor_scalar(place[:, 0, :], place[:, 0, :], 11, None, ALU.arith_shift_right))
                    then(v.tensor_copy(placef[:, :, :], place[:, :, :]))
                    for e in range(8):
                        v.wait_ge(hots_used, n * 8 + (e + 1))
                        v.tensor_scalar(hot_d[:, e % SLOTS, :], iota[:, 0:P], placef[:, 0, e:e + 1], None, ALU.is_equal)
                        v.tensor_scalar(hot_s[:, e % SLOTS, :], iota[:, :], placef[:, 1, e:e + 1], None,
                                        ALU.is_equal).then_inc(hots, 1)
                if kept is not None:
                    keep(kept, r)
                if before is not None:
                    largest(before, 0)
                    v.wait_ge(weighted, t * HG - HG)
                v.wait_ge(near_done, t + 1)
                for k in range(4):
                    last = v.tensor_copy(cnt[:, r, k * 512:k * 512 + 512], C[k][:, :])
                last.then_inc(C_copied, 1)
                v.wait_ge(C_copied, t + 1)
                after(v.tensor_scalar(cnt[:, r, LAST:T], cnt[:, r, LAST:T], hist[:, bass.ds(t, 1)], None, ALU.add))
                after(v.tensor_scalar(hide[:, :], cnt[:, r, :], 0.0, NEG, ALU.is_equal, ALU.mult))
                for hd in range(HG):
                    if before is not None and hd > 0:
                        largest(before, hd)
                    carry()
                    after(v.tensor_tensor_reduce(out=seen[:, hd, :], in0=a_src[:, hd, :], in1=hide[:, :],
                                                 scale=1.0, scalar=NEG, op0=ALU.add, op1=ALU.max,
                                                 accum_out=mx[:, hd:hd + 1]))
                dst = a_dst[:, bass.ds(t, 1), :].rearrange("p t h -> p (t h)")
                after(v.tensor_tensor(mx[:, :], mx[:, :], dst, ALU.add))
                after(v.scalar_tensor_tensor(mx2[:, :], mx[:, :], 0.2, mx[:, :], ALU.mult, ALU.max))
                after(v.tensor_tensor(bias[:, r, 0, :], dst, mx2[:, :], ALU.subtract))
                v.scalar_tensor_tensor(bias[:, r, 1, :], dst, 0.2, mx2[:, :], ALU.mult, ALU.subtract
                                       ).then_inc(bias_ready, 1)
                assert count == TILE_STEPS

            tile(0, 0, None, None)
            tile(1, 1, 0, None)
            with v.Fori(0, NT // 2 - 1) as i:
                tile(i * 2 + 2, 0, i * 2 + 1, i * 2)
                tile(i * 2 + 3, 1, i * 2 + 2, i * 2 + 1)
            keep(NT - 2, 0)
            for hd in range(HG):
                largest(NT - 1, hd)
            keep(NT - 1, 1)


def graph_route(nc, own, d):
    agg, gates = own["agg"], own["gates"]
    F = HG * GE
    with Stage(nc, "route4") as s:
        par = s.sb("par", [P, 3, F])
        order = s.sb("order", [P, 8])
        x = s.sb("x", [P, NT, HG, GE])
        sq = s.sb("sq", [P, NT, HG, GE])
        rden = s.sb("rden", [P, NT, HG])
        mean = s.sb("mean", [P, NT])
        std = s.sb("std", [P, NT])
        scores = s.sb("scores", [P, NT, GE])
        best = [s.sb(f"best{k}", [P, NT]) for k in range(2)]
        picks = [s.sb(f"pick{k}", [P, NT, GE]) for k in range(2)]
        rest = s.sb("rest", [P, NT, GE])
        eq = s.sb("eq", [P, NT, GE])
        second = s.sb("second", [P, NT])
        loaded = s.sem("loaded")
        dve = s.sem("dve_step")
        var_ready = s.sem("var_ready")
        std_ready = s.sem("std_ready")
        gap_ready = s.sem("gap_ready")
        exp_ready = s.sem("exp_ready")
        eps = s.sb("eps", [P, 1])
        eps_set = s.sem("eps_set")
        block = s.block()

        @block.sync
        def _(sp):
            sp.dma_start(par[:, :, :], d["route4_par"].broadcast_to([P, 3, F])).then_inc(loaded, 16)
            sp.dma_start(order[:, 0:GE], d["order4"].broadcast_to([P, GE])).then_inc(loaded, 16)

        @block.scalar
        def _(a):
            a.wait_ge(var_ready, 1)
            a.wait_ge(eps_set, 1)
            a.activation(std[:, :], std[:, :], ACT.Sqrt, bias=eps[:, 0:1]).then_inc(std_ready, 1)
            a.wait_ge(gap_ready, 1)
            a.activation(second[:, :], second[:, :], ACT.Exp).then_inc(exp_ready, 1)

        @block.vector
        def _(v):
            step = Chain(v, dve)
            v.memset(eps[:, :], LN_EPS).then_inc(eps_set, 1)
            v.wait_ge(loaded, 32)
            flat, flat_sq = x[:, :, :, :].rearrange("p t h e -> p t (h e)"), sq[:, :, :, :].rearrange("p t h e -> p t (h e)")

            def row(k):
                return bc(par[:, k, :].unsqueeze(1), [P, NT, F])

            def col(ap, n):
                return bc(ap[:, :].unsqueeze(2), [P, NT, n])

            step(v.tensor_scalar(rden[:, :, :], agg[:, :, :, GE], 1e-16, None, ALU.add))
            step(v.reciprocal(rden[:, :, :], rden[:, :, :]))
            step(v.tensor_tensor(x[:, :, :, :], agg[:, :, :, 0:GE], bc(rden[:, :, :].unsqueeze(3), [P, NT, HG, GE]),
                                 ALU.mult))
            step(v.tensor_tensor(flat, flat, row(0), ALU.add))
            step(v.tensor_reduce(mean[:, :], flat, AX.X, ALU.add))
            step(v.tensor_scalar(mean[:, :], mean[:, :], 1.0 / F, None, ALU.mult))
            step(v.tensor_tensor(flat, flat, col(mean, F), ALU.subtract))
            step(v.tensor_tensor(flat_sq, flat, flat, ALU.mult))
            step(v.tensor_reduce(std[:, :], flat_sq, AX.X, ALU.add))
            v.tensor_scalar(std[:, :], std[:, :], 1.0 / F, None, ALU.mult).then_inc(var_ready, 1)
            v.wait_ge(std_ready, 1)
            step(v.reciprocal(std[:, :], std[:, :]))
            step(v.tensor_tensor(flat, flat, col(std, F), ALU.mult))
            step(v.tensor_tensor(flat, flat, row(1), ALU.mult))
            step(v.tensor_tensor(flat, flat, row(2), ALU.add))
            step(v.tensor_reduce(scores[:, :, :], x[:, :, :, :].rearrange("p t h e -> p t e h"), AX.X, ALU.add))
            step(v.tensor_scalar(scores[:, :, :], scores[:, :, :], 1.0 / HG, None, ALU.mult))
            two_best(v, step, scores, best, rest, eq, picks, order, GE)
            v.tensor_tensor(second[:, :], best[1][:, :], best[0][:, :], ALU.subtract).then_inc(gap_ready, 1)
            v.wait_ge(exp_ready, 1)
            step(v.tensor_scalar(mean[:, :], second[:, :], 1.0, None, ALU.add))
            step(v.reciprocal(mean[:, :], mean[:, :]))
            step(v.tensor_tensor(picks[1][:, :, :], picks[1][:, :, :], col(second, GE), ALU.mult))
            step(v.tensor_tensor(gates[:, :, :], picks[0][:, :, :], picks[1][:, :, :], ALU.add))
            v.tensor_tensor(gates[:, :, :], gates[:, :, :], col(mean, GE), ALU.mult)


def graph_tables():
    c = {"iota_nodes": np.arange(T, dtype=np.float16)[None], "identh": np.eye(P, dtype=np.float16)}
    c["iota_tiles"] = np.arange(NT, dtype=np.float32)[None]
    c["key_bases"] = (np.arange(NT) * KEY_TILE + 1).astype(np.float32)[None]
    loops = np.zeros((P, 2 * T - P), np.float16)
    loops[:, T - P:T] = np.eye(P)
    c["loops"] = loops
    c["order4"] = np.arange(GE, 0, -1, dtype=np.float32)[None]
    return c


class Steps:

    def __init__(self, engine, semaphore, base):
        self.engine, self.semaphore, self.base, self.count = engine, semaphore, base, 0

    def __call__(self, *instructions):
        self.count += 1
        instructions[-1].then_inc(self.semaphore, 1)
        self.engine.wait_ge(self.semaphore, self.base + self.count)


PK_HEADS = 8
PK_KEYS = 64
PK_DIM = D // 2
TOPK = 16
PAIRS_OF_HEADS = PK_HEADS // 2
CANDS = [(i, TOPK // (i + 1)) for i in range(TOPK)]
N_CAND = sum(n for _, n in CANDS)
GROUPS2 = 2 * PK_HEADS
G_RING = 4
LOWEST = -3e38


def product_keys(nc, m, d):
    with Stage(nc, "pkm") as s:
        own = {"k": s.sb("k", [P, PAIRS_OF_HEADS, NT, 2 * D]), "v": s.sb("v", [P, PAIRS_OF_HEADS, NT, 2, D])}
        with Stage(nc, "pkq") as first:
            own["qpT"] = first.sb("qpT", [P, 4, T])
            key_queries(nc, m, own["qpT"], d, 0)
            key_lookup(nc, own, d)
        own["qT"] = s.sb("qT", [P, PAIRS_OF_HEADS, T])
        key_queries(nc, m, own["qT"], d, 1)
        head_attention(nc, m, own, d)


def key_queries(nc, m, out, d, which):
    xT = m["xT"]
    with Stage(nc, f"keyq{which}") as s:
        w = s.sb("w", [D, 4, P])
        ps = [s.ps(f"ps{k}", [P, 512]) for k in range(4)]
        loaded = s.sem("loaded")
        made = s.sem("made")
        kept_even = s.sem("kept_even")
        kept_odd = s.sem("kept_odd")
        block = s.block()

        def place(n):
            return out[:, n // 4, n % 4 * 512:n % 4 * 512 + 512]

        @block.sync
        def _(sp):
            sp.dma_start(w[:, :, :], d["pk_wq"][:, 4 * which:4 * which + 4, :]).then_inc(loaded, 16)

        @block.tensor
        def _(pe):
            pe.wait_ge(loaded, 16)
            for n in range(16):
                if n >= 4:
                    pe.wait_ge(kept_even if n % 2 == 0 else kept_odd, n // 2 - 1)
                pe.matmul(ps[n % 4][:, :], w[:, n // 4, :], xT[0:D, n % 4 * 512:n % 4 * 512 + 512],
                          start=True, stop=True).then_inc(made, 1)

        @block.vector
        def _(v):
            for n in range(0, 16, 2):
                v.wait_ge(made, n + 1)
                v.tensor_copy(place(n), ps[n % 4][:, :]).then_inc(kept_even, 1)

        @block.scalar
        def _(a):
            for n in range(1, 16, 2):
                a.wait_ge(made, n + 1)
                a.copy(place(n), ps[n % 4][:, :]).then_inc(kept_odd, 1)


def key_lookup(nc, own, d):
    k_all, v_all, qpT = own["k"], own["v"], own["qpT"]
    with Stage(nc, "look") as s:
        keys = s.sb("keys", [P, 4, 4 * PK_KEYS])
        head_base = s.sb("head_base", [P, PK_HEADS, TOPK])
        iota = s.sb("iota", [P, N_CAND])
        q_now = s.sb("q_now", [P, 2, 4, P])
        sim = s.sb("sim", [P, 2, GROUPS2, PK_KEYS])
        top = s.sb("top", [P, GROUPS2, TOPK])
        at = s.sb("at", [P, GROUPS2, TOPK], U32)
        atf = s.sb("atf", [P, GROUPS2, TOPK])
        score = s.sb("score", [P, PK_HEADS, N_CAND])
        row = s.sb("row", [P, PK_HEADS, N_CAND])
        best = s.sb("best", [P, PK_HEADS, TOPK])
        pos = s.sb("pos", [P, PK_HEADS, TOPK], U32)
        posf = s.sb("posf", [P, PK_HEADS, TOPK])
        eq = s.sb("eq", [P, PK_HEADS, TOPK, N_CAND])
        picked = s.sb("picked", [P, PK_HEADS, TOPK])
        total = s.sb("total", [P, PK_HEADS])
        rows = s.sb("rows", [P, 2, PK_HEADS * TOPK], I32)
        weight = s.sb("weight", [P, 2, PK_HEADS, TOPK])
        got = [s.sb(f"got{k}", [P, TOPK, 2 * D]) for k in range(G_RING)]
        spare = s.sb("spare", [P, 128])
        pool_spare = s.sb("pool_spare", [P, 32])
        ps = [[s.ps(f"ps{k}{j}", [P, 512]) for j in range(2)] for k in range(2)]
        loaded = s.sem("loaded")
        q_staged = s.sem("q_staged")
        sim_made = s.sem("sim_made")
        sim_kept = s.sem("sim_kept")
        sim_used = s.sem("sim_used")
        best_ready = s.sem("best_ready")
        exp_ready = s.sem("exp_ready")
        rows_ready = s.sem("rows_ready")
        dve = s.sem("dve_step")
        combined = s.sem("combined")
        scaled = s.sem("scaled")
        carried = s.sem("carried")
        landed = [s.sem(f"landed{k}") for k in range(G_RING)]
        block = s.block()

        @block.sync
        def _(sp):
            sp.dma_start(keys[:, :, :], d["pk_keys"]).then_inc(loaded, 16)
            sp.dma_start(head_base[:, :, :], d["pk_base"].broadcast_to([P, PK_HEADS, TOPK])).then_inc(loaded, 16)
            sp.dma_start(iota[:, :], d["pk_iota"].broadcast_to([P, N_CAND])).then_inc(loaded, 16)

        @block.tensor
        def _(pe):
            pe.wait_ge(loaded, 48)
            with pe.Fori(0, NT // 2) as i:
                for r in range(2):
                    pe.wait_ge(q_staged, i * 2 + (r + 1))
                    for c in range(4):
                        mm = pe.matmul(ps[r][c // 2][:, c % 2 * 256:c % 2 * 256 + 256], q_now[:, r, c, :],
                                       keys[:, c, :], start=True, stop=True)
                    mm.then_inc(sim_made, 1)

        @block.scalar
        def _(a):
            with a.Fori(0, NT // 2) as i:
                for r in range(2):
                    a.wait_ge(sim_used, i * 2 + (r + 1))
                    a.copy(q_now[:, r, :, :], qpT[:, :, bass.ds(i * (2 * P) + r * P, P)]).then_inc(q_staged, 1)
                    a.wait_ge(sim_made, i * 2 + (r + 1))
                    for j in range(2):
                        last = a.copy(sim[:, r, j * PK_HEADS:(j + 1) * PK_HEADS, :],
                                      ps[r][j][:, :].rearrange("p (g k) -> p g k", g=PK_HEADS))
                    last.then_inc(sim_kept, 1)
                    a.wait_ge(best_ready, i * 2 + (r + 1))
                    a.activation(weight[:, r, :, :], weight[:, r, :, :], ACT.Exp).then_inc(exp_ready, 1)

        @block.gpsimd
        def _(g):
            g.memset(pool_spare[:, :], 0.0).then_inc(carried, 1)
            g.wait_ge(carried, 1)

            def carry(n):
                g.tensor_tensor(pool_spare[:, n + 1:n + 2], pool_spare[:, 0:1], pool_spare[:, 0:1],
                                ALU.add).then_inc(carried, 1)

            with g.Fori(0, NT // 2) as i:
                for r in range(2):
                    g.wait_ge(rows_ready, i * 2 + (r + 1))
                    for hd in range(PK_HEADS):
                        slot = hd % G_RING
                        g.wait_ge(carried, i * (2 * PK_HEADS) + (r * PK_HEADS + hd + 1))
                        g.wait_ge(combined, i * (2 * PK_HEADS) + (r * PK_HEADS + hd + 1))
                        carry(r * PK_HEADS + hd)
                        for k in range(TOPK):
                            n = hd * TOPK + k
                            g.indirect_dma_start(got[slot][:, k, :], None, d["pk_table"],
                                                 bass.IndirectOffsetOnAxis(ap=rows[:, r, n:n + 1].bitcast(U32), axis=0)
                                                 ).then_inc(landed[slot], 16)

        @block.vector
        def _(v):
            sites = [0]

            def carry():
                sites[0] += 1
                return v.memset(spare[:, sites[0]:sites[0] + 1], 0.0)

            def best_sixteen(step, values, out, index, n):
                carry()
                step(*[v.max(out[:, g, 0:8], values(g)) for g in range(n)])
                carry()
                step(*[v.max_index(index[:, g, 0:8], out[:, g, 0:8], values(g)) for g in range(n)])
                carry()
                step(*[v.match_replace(values(g), out[:, g, 0:8], values(g), LOWEST) for g in range(n)])
                carry()
                step(*[v.max(out[:, g, 8:16], values(g)) for g in range(n)])
                carry()
                step(*[v.max_index(index[:, g, 8:16], out[:, g, 8:16], values(g)) for g in range(n)])

            def look(t, r):
                step = Steps(v, dve, t * LOOK_STEPS)
                v.wait_ge(sim_kept, t + 1)
                best_sixteen(step, lambda g: sim[:, r, g, :], top, at, GROUPS2)
                step(v.tensor_copy(atf[:, :, :], at[:, :, :]))
                second = atf[:, PK_HEADS:, :]
                step(v.scalar_tensor_tensor(second, second, float(PK_KEYS), head_base[:, :, :], ALU.mult, ALU.add))
                done = []
                for src, dst in ((top, score), (atf, row)):
                    off = 0
                    for i, n in CANDS[:8]:
                        done.append(v.tensor_tensor(dst[:, :, off:off + n], src[:, PK_HEADS:, 0:n],
                                                    bc(src[:, 0:PK_HEADS, i:i + 1], [P, PK_HEADS, n]), ALU.add))
                        off += n
                    done.append(v.tensor_tensor(dst[:, :, off:off + 8], src[:, 0:PK_HEADS, 8:16],
                                                bc(src[:, PK_HEADS:, 0:1], [P, PK_HEADS, 8]), ALU.add))
                step(*done)
                best_sixteen(step, lambda g: score[:, g, :], best, pos, PK_HEADS)
                v.tensor_tensor(weight[:, r, :, :], best[:, :, :], bc(best[:, :, 0:1], [P, PK_HEADS, TOPK]),
                                ALU.subtract).then_inc(best_ready, 1)
                step(v.tensor_copy(posf[:, :, :], pos[:, :, :]))
                wide = [P, PK_HEADS, TOPK, N_CAND]
                step(v.tensor_tensor(eq[:, :, :, :].rearrange("p h k c -> p (h k) c"),
                                     bc(iota[:, :].unsqueeze(1), [P, PK_HEADS * TOPK, N_CAND]),
                                     bc(posf[:, :, :].rearrange("p h k -> p (h k)").unsqueeze(2),
                                        [P, PK_HEADS * TOPK, N_CAND]), ALU.is_equal))
                step(v.tensor_tensor(eq[:, :, :, :], eq[:, :, :, :], bc(row[:, :, :].unsqueeze(2), wide), ALU.mult))
                step(v.tensor_reduce(picked[:, :, :], eq[:, :, :, :], AX.X, ALU.add))
                v.tensor_copy(rows[:, r, :], picked[:, :, :].rearrange("p h k -> p (h k)")).then_inc(rows_ready, 1)
                v.wait_ge(exp_ready, t + 1)
                step(v.tensor_reduce(total[:, :], weight[:, r, :, :], AX.X, ALU.add))
                step(v.reciprocal(total[:, :], total[:, :]))
                step(v.tensor_tensor(weight[:, r, :, :], weight[:, r, :, :],
                                     bc(total[:, :].unsqueeze(2), [P, PK_HEADS, TOPK]), ALU.mult))
                carry().then_inc(sim_used, 1)
                assert step.count == LOOK_STEPS, step.count

            def combine(t, r):
                for hd in range(PK_HEADS):
                    slot = hd % G_RING
                    rowsg = got[slot]
                    v.wait_ge(landed[slot], t * (2 * 16 * TOPK) + (hd // G_RING + 1) * 16 * TOPK)
                    v.tensor_tensor(rowsg[:, :, :], rowsg[:, :, :],
                                    bc(weight[:, r, hd, :].unsqueeze(2), [P, TOPK, 2 * D]), ALU.mult).then_inc(scaled, 1)
                    v.wait_ge(scaled, t * PK_HEADS + (hd + 1))
                    half = slice(hd % 2 * D, hd % 2 * D + D)
                    v.tensor_reduce(k_all[:, hd // 2, bass.ds(t, 1), half].rearrange("p t c -> p (t c)"),
                                    rowsg[:, :, 0:D].rearrange("p k c -> p c k"), AX.X, ALU.add)
                    v.tensor_reduce(v_all[:, hd // 2, bass.ds(t, 1), hd % 2, :].rearrange("p t c -> p (t c)"),
                                    rowsg[:, :, D:2 * D].rearrange("p k c -> p c k"), AX.X, ALU.add).then_inc(combined, 1)

            v.engine_nop().then_inc(combined, G_RING)
            v.engine_nop().then_inc(sim_used, 2)
            v.wait_ge(loaded, 48)
            look(0, 0)
            with v.Fori(0, NT // 2 - 1) as i:
                look(i * 2 + 1, 1)
                combine(i * 2, 0)
                look(i * 2 + 2, 0)
                combine(i * 2 + 1, 1)
            look(NT - 1, 1)
            combine(NT - 2, 0)
            combine(NT - 1, 1)


LOOK_STEPS = 5 + 1 + 1 + 1 + 5 + 4 + 3


def head_attention(nc, m, own, d):
    h, ident = m["h"], m["ident"]
    k_all, v_all, qT = own["k"], own["v"], own["qT"]
    N = PAIRS_OF_HEADS * B
    ITEMS = [(a, i) for a in range(2) for i in range(TB)]
    PER = len(ITEMS)
    CH = [(i + 4) // 4 for _, i in ITEMS]
    PER_CH = sum(CH)
    with Stage(nc, "head") as outer:
        o = outer.sb("o", [P, PAIRS_OF_HEADS, NT, 2 * D])
        with Stage(nc, "hatt") as s:
            k_now = s.sb("k_now", [P, TB, 2 * D])
            q_now = s.sb("q_now", [P, S])
            kT = s.sb("kT", [P, S])
            mask = s.sb("mask", [P, P])
            probs = s.sb("probs", [P, 2, S])
            pT = s.sb("pT", [P, 2, 512])
            mx = s.sb("mx", [P, PER])
            bias = s.sb("bias", [P, PER])
            den = s.sb("den", [P, PER])
            rden = s.sb("rden", [P, PER])
            spare = s.sb("spare", [P, 2])
            sc = [[s.ps(f"sc{k}{j}", [P, 512]) for j in range(2)] for k in range(2)]
            ps_t = [s.ps(f"ps_t{k}", [P, 512]) for k in range(2)]
            ps_o = [s.ps(f"ps_o{k}", [P, 512]) for k in range(2)]
            names = ["loaded", "k_staged", "q_staged", "kT_made", "kT_kept", "qk_made", "masked", "max_step", "max_done",
                     "exp_done", "turned", "t_kept", "pv_made", "rden_step", "o_kept", "credit"]
            (loaded, k_staged, q_staged, kT_made, kT_kept, qk_made, masked, max_step, max_done, exp_done, turned,
             t_kept, pv_made, rden_step, o_kept, credit) = [s.sem(n) for n in names]
            block = s.block()

            def banks(r, n):
                return [(sc[r][j][:, 0:min(512, n - 512 * j)], 512 * j, min(512, n - 512 * j))
                        for j in range(2) if n > 512 * j]

            @block.sync
            def _(sp):
                sp.dma_start(mask[:, :], d["causal"]).then_inc(loaded, 16)

            @block.tensor
            def _(pe):
                with pe.Fori(0, N) as n:
                    pe.wait_ge(k_staged, n + 1)
                    pe.wait_ge(t_kept, n * PER_CH + 2)
                    for j in range(TB):
                        mm = pe.transpose(ps_t[j // 4][:, j % 4 * P:j % 4 * P + P], k_now[:, j, :], ident[:, :])
                    mm.then_inc(kT_made, 1)
                    pe.wait_ge(kT_kept, n * 2 + 2)
                    pe.wait_ge(q_staged, n + 1)

                    def scores(u):
                        a, i = ITEMS[u]
                        pe.wait_ge(exp_done, n * PER + (u + 1))
                        rows = slice(a * D, a * D + D)
                        for ap, at, size in banks(u % 2, (i + 1) * P):
                            mm = pe.matmul(ap, q_now[rows, i * P:i * P + P], kT[rows, at:at + size],
                                           start=True, stop=True)
                        mm.then_inc(qk_made, 1)

                    scores(0)
                    for u, (a, i) in enumerate(ITEMS):
                        if u + 1 < PER:
                            scores(u + 1)
                        c0 = sum(CH[:u])
                        pe.wait_ge(exp_done, n * PER + (u + 3))
                        for c in range(c0, c0 + CH[u]):
                            pe.wait_ge(t_kept, n * PER_CH + (c + 1))
                            for j in range(4 * (c - c0), min(i + 1, 4 * (c - c0) + 4)):
                                mm = pe.transpose(ps_t[c % 2][:, j % 4 * P:j % 4 * P + P],
                                                  probs[:, u % 2, j * P:j * P + P], ident[:, :])
                            mm.then_inc(turned, 1)
                        pe.wait_ge(o_kept, n * PER + (u + 1))
                        for c in range(c0, c0 + CH[u]):
                            pe.wait_ge(t_kept, n * PER_CH + (c + 3))
                            for j in range(4 * (c - c0), min(i + 1, 4 * (c - c0) + 4)):
                                mm = pe.matmul(ps_o[u % 2][:, 0:D], pT[:, c % 2, j % 4 * P:j % 4 * P + P],
                                               v_all[:, :, :, :, :].rearrange("p q t a c -> p (q t) a c")
                                               [:, bass.ds(n * TB + j, 1), a, :].rearrange("p t c -> p (t c)"),
                                               start=(j == 0), stop=(j == i))
                        mm.then_inc(pv_made, 1)

            @block.scalar
            def _(a):
                a.memzero(spare[:, 0:1]).then_inc(credit, 1)
                a.wait_ge(credit, 1)
                a.copy(spare[:, 1:2], spare[:, 0:1]).then_inc(exp_done, 2)
                a.wait_ge(exp_done, 2)
                a.copy(spare[:, 1:2], spare[:, 0:1]).then_inc(t_kept, 2)
                with a.Fori(0, N) as n:
                    a.copy(k_now[:, :, :], k_all[:, :, :, :].rearrange("p q t c -> p (q t) c")
                           [:, bass.ds(n * TB, TB), :]).then_inc(k_staged, 1)
                    a.copy(q_now[:, :], qT[:, :, :].rearrange("p q t -> p (q t)")[:, bass.ds(n * S, S)]
                           ).then_inc(q_staged, 1)

                    def exps(u):
                        hd, i = ITEMS[u]
                        a.wait_ge(max_done, n * PER + (u + 1))
                        size = (i + 1) * P
                        for ap, at, width in banks(u % 2, size):
                            last = a.activation(probs[:, u % 2, at:at + width], ap, ACT.Exp,
                                                bias=bias[:, u:u + 1], scale=D ** -0.5)
                        last.then_inc(exp_done, 1)

                    exps(0)
                    for u, (hd, i) in enumerate(ITEMS):
                        if u + 1 < PER:
                            exps(u + 1)
                        c0 = sum(CH[:u])
                        for c in range(c0, c0 + CH[u]):
                            a.wait_ge(turned, n * PER_CH + (c + 1))
                            size = min(i + 1 - 4 * (c - c0), 4) * P
                            a.copy(pT[:, c % 2, 0:size], ps_t[c % 2][:, 0:size]).then_inc(t_kept, 1)

            @block.vector
            def _(v):
                v.engine_nop().then_inc(o_kept, 2)
                v.wait_ge(loaded, 16)
                with v.Fori(0, N) as n:
                    v.wait_ge(kT_made, n + 1)
                    for j in range(2):
                        v.tensor_copy(kT[:, j * 512:j * 512 + 512], ps_t[j][:, :]).then_inc(kT_kept, 1)

                    def maxima(u):
                        hd, i = ITEMS[u]
                        v.wait_ge(qk_made, n * PER + (u + 1))
                        diag = sc[u % 2][i // 4][:, i % 4 * P:i % 4 * P + P]
                        v.tensor_tensor(diag, diag, mask[:, :], ALU.add).then_inc(masked, 1)
                        v.wait_ge(masked, n * PER + (u + 1))
                        parts = banks(u % 2, (i + 1) * P)
                        v.tensor_reduce(mx[:, u:u + 1], parts[0][0], AX.X, ALU.max).then_inc(max_step, 1)
                        if len(parts) == 2:
                            v.tensor_reduce(bias[:, u:u + 1], parts[1][0], AX.X, ALU.max).then_inc(max_step, 1)
                            done = sum(len(banks(0, (j + 1) * P)) for _, j in ITEMS[:u + 1]) + sum(
                                j >= 4 for _, j in ITEMS[:u])
                            v.wait_ge(max_step, n * MAX_STEPS + done)
                            v.tensor_tensor(mx[:, u:u + 1], mx[:, u:u + 1], bias[:, u:u + 1], ALU.max).then_inc(max_step, 1)
                            v.wait_ge(max_step, n * MAX_STEPS + (done + 1))
                        else:
                            done = sum(len(banks(0, (j + 1) * P)) for _, j in ITEMS[:u + 1]) + sum(
                                j >= 4 for _, j in ITEMS[:u])
                            v.wait_ge(max_step, n * MAX_STEPS + done)
                        v.tensor_scalar(bias[:, u:u + 1], mx[:, u:u + 1], -(D ** -0.5), None, ALU.mult).then_inc(max_done, 1)

                    def normalised(u):
                        hd, i = ITEMS[u]
                        v.wait_ge(exp_done, n * PER + (u + 3))
                        v.tensor_reduce(den[:, u:u + 1], probs[:, u % 2, 0:(i + 1) * P], AX.X, ALU.add).then_inc(rden_step, 1)
                        v.wait_ge(rden_step, n * (2 * PER) + (2 * u + 1))
                        v.reciprocal(rden[:, u:u + 1], den[:, u:u + 1]).then_inc(rden_step, 1)
                        v.wait_ge(rden_step, n * (2 * PER) + (2 * u + 2))
                        v.wait_ge(pv_made, n * PER + (u + 1))
                        flat = o[:, :, :, :].rearrange("p q t c -> p (q t) c")
                        v.tensor_scalar(flat[:, bass.ds(n * TB + i, 1), hd * D:hd * D + D].rearrange("p t c -> p (t c)"),
                                        ps_o[u % 2][:, 0:D], rden[:, u:u + 1], None, ALU.mult).then_inc(o_kept, 1)

                    MAX_STEPS = sum(len(banks(0, (j + 1) * P)) for _, j in ITEMS) + sum(j >= 4 for _, j in ITEMS)
                    maxima(0)
                    for u in range(PER):
                        if u + 1 < PER:
                            maxima(u + 1)
                        normalised(u)

        with Stage(nc, "wo") as s:
            w = s.sb("w", [P, PAIRS_OF_HEADS, D])
            oT = s.sb("oT", [P, 2, PAIRS_OF_HEADS, P])
            ps_t = [s.ps(f"ps_t{k}", [P, PAIRS_OF_HEADS, P]) for k in range(2)]
            ps_y = [s.ps(f"ps_y{k}", [P, TB, D]) for k in range(2)]
            loaded = s.sem("loaded")
            turned = s.sem("turned")
            kept = s.sem("kept")
            made = s.sem("made")
            block = s.block()

            @block.sync
            def _(sp):
                sp.dma_start(w[:, :, :], d["pk_wo"]).then_inc(loaded, 16)

            @block.tensor
            def _(pe):
                pe.wait_ge(loaded, 16)
                for t in range(NT + 1):
                    if t < NT:
                        if t >= 2:
                            pe.wait_ge(kept, t - 1)
                        for q in range(PAIRS_OF_HEADS):
                            mm = pe.transpose(ps_t[t % 2][:, q, :], o[:, q, t, :], ident[:, :])
                        mm.then_inc(turned, 1)
                    if t >= 1:
                        u = t - 1
                        pe.wait_ge(kept, u + 1)
                        for q in range(PAIRS_OF_HEADS):
                            mm = pe.matmul(ps_y[u // TB][:, u % TB, :], oT[:, u % 2, q, :], w[:, q, :],
                                           start=(q == 0), stop=(q == PAIRS_OF_HEADS - 1))
                        mm.then_inc(made, 1)

            @block.scalar
            def _(a):
                for t in range(NT):
                    a.wait_ge(turned, t + 1)
                    if t >= 2:
                        a.wait_ge(made, t - 1)
                    a.copy(oT[:, t % 2, :, :], ps_t[t % 2][:, :, :]).then_inc(kept, 1)

            @block.vector
            def _(v):
                for b in range(B):
                    v.wait_ge(made, (b + 1) * TB)
                    t = slice(b * TB, b * TB + TB)
                    v.tensor_tensor(h[:, t, :], h[:, t, :], ps_y[b][:, :, :], ALU.add)


def product_key_tables():
    c = {"pk_iota": np.arange(N_CAND, dtype=np.float32)[None]}
    base = np.arange(PK_HEADS, dtype=np.float32)[:, None] * PK_KEYS ** 2
    c["pk_base"] = np.broadcast_to(base, (PK_HEADS, TOPK))[None]
    c["causal"] = np.where(np.arange(P)[None, :] <= np.arange(P)[:, None], 0.0, NEG).astype(np.float32)
    return c

STAGES = [embed, linear_attention, tree_ffn, retention, product_keys, recurrence, graph_ffn, pseudo_inverse,
          wavelet_attention, experts_eight]


def tower(nc, d, out, stages):
    with ExitStack() as ctx:
        def sb(name, shape, dt=F32):
            return ctx.enter_context(nc.sbuf_tensor(name, shape, dt))
        m = {"h": sb("h", [P, NT, D]), "xn": sb("xn", [P, NT, D]), "xT": sb("xT", [D + 1, T]),
             "ident": sb("ident", [P, P]), "eps": sb("eps", [P, 1]), "inv_wT": sb("inv_wT", [D, D])}
        with Stage(nc, "begin") as s:
            loaded = s.sem("loaded")
            block = s.block()

            @block.sync
            def _(sp):
                sp.dma_start(m["ident"][:, :], d["ident"]).then_inc(loaded, 16)
                sp.wait_ge(loaded, 16)

            @block.vector
            def _(v):
                v.memset(m["xT"][D:D + 1, :], 1.0)
                v.memset(m["eps"][:, :], LN_EPS)
        for n, stage in enumerate(stages):
            if stage in (pseudo_inverse, embed):
                stage(nc, m, d)
                continue
            normalise(nc, m, n)
            stage(nc, m, d)
        with Stage(nc, "end") as s:
            stored = s.sem("stored")
            block = s.block()

            @block.sync
            def _(sp):
                sp.dma_start(out.rearrange("b (t p) d -> p (b t) d", p=P), m["h"][:, :, :]).then_inc(stored, 16)
                sp.wait_ge(stored, 16)


def constants():
    c = {"ident": np.eye(P, dtype=np.float32)}
    head = np.arange(D) // 8
    c["head_mask"] = ((head[:, None] == head[None, :]) / S).astype(np.float32)
    c.update(retention_tables())
    c.update(recurrence_tables())
    c.update(wavelet_tables())
    c.update(embed_tables())
    c.update(graph_tables())
    c.update(product_key_tables())
    c["order8"] = np.arange(8, 0, -1, dtype=np.float32)[None]
    return c


def layouts(i):
    cat = np.concatenate
    a = {}
    a["la_w_vk"] = cat([cat([i["L0_attn_Wv"].T, i["L0_attn_bv"][None]], 0),
                        cat([i["L0_attn_Wk"].T, i["L0_attn_bk"][None]], 0)], 1)
    a["la_w_q"] = cat([i["L0_attn_Wq"].T, i["L0_attn_bq"][None]], 0)
    a["la_w_fc"] = i["L0_attn_Wfc"].T
    a["la_b_fc"] = i["L0_attn_bfc"][None]
    even_odd = np.concatenate([np.arange(0, D, 2), np.arange(1, D, 2)])
    a["ret_w"] = cat([i["L1_attn_W_Q"][:, even_odd], i["L1_attn_W_K"][:, even_odd], i["L1_attn_W_V"]], 1)
    w1s = cat([i["L0_ffn_w1s"].T, i["L0_ffn_b1s"][None]], 0)
    a["tree_w1"] = cat([w1s, np.zeros((D + 1, 1), np.float32)], 1)
    w2s = cat([i["L0_ffn_w2s"].transpose(1, 0, 2).reshape(D, -1), i["L0_ffn_b2s"].reshape(1, -1)], 0)
    a["tree_w2"] = cat([w2s, np.zeros((D + 1, D), np.float32)], 1)
    par = np.stack([i["L2_attn_nu_log"], i["L2_attn_theta_log"], i["L2_attn_gamma_log"]], 1)
    a["rec_par"] = cat([par, par], 0)
    bre, bim, cre, cim = (i[f"L2_attn_{k}"].T for k in ("B_re", "B_im", "C_re", "C_im"))
    a["rec_w_in"] = np.stack([cat([bre, bim], 1), cat([bim, bre], 1)], 1)
    a["rec_w_out"] = np.stack([cat([cre, cim], 0), cat([cim, cre], 0)], 1)
    w1, b1, w2 = i["L3_ffn_w1"], i["L3_ffn_b1"], i["L3_ffn_w2"]
    a["moe8_w1"] = cat([w1.transpose(1, 0, 2).reshape(D, 4, P), b1.reshape(1, 4, P)], 0)
    a["moe8_w2"] = w2.reshape(4, P, D).transpose(1, 0, 2)
    a["moe8_b2"] = i["L3_ffn_b2"][None]
    a["route8_w"] = i["L3_ffn_router_w"].T
    a["near_w_q"], a["near_w_qT"] = i["L3_attn_W_Q"], i["L3_attn_W_Q"].T
    a["near_w_v"], a["near_w_oT"] = i["L3_attn_W_V"], i["L3_attn_W_O"].T
    a["ids"], a["positions"] = i["x"], i["fside_BS_continuous_positions"]
    taps = i["L0_tok_w1"].transpose(2, 1, 0)
    taps = cat([taps, np.zeros((1, VOCAB, P), np.float32)], 0)
    a["emb_w1"] = taps.reshape(4, P, P).transpose(1, 0, 2)
    a["emb_w2"] = i["L0_tok_w2"].transpose(1, 2, 0)
    a["emb_w3"] = i["L0_tok_w3"][0]
    a["emb_b1"], a["emb_b2"], a["emb_b3"] = (i[f"L0_tok_b{k}"][:, None] for k in (1, 2, 3))
    a["emb_table"] = cat([i["L0_tok_emb"], i["L0_tok_locality_shapes"]], 1)
    a["emb_widths"], a["emb_weights"] = i["L0_tok_multiscale_widths"][None], i["L0_tok_scale_weights"][None]
    a["edges"] = i["L2_ffn_edge_index"].reshape(2, P, EC)
    a["gat_w"] = i["L2_ffn_W_gat"]
    a["gat_att"] = np.stack([i["L2_ffn_att_src"].reshape(-1), i["L2_ffn_att_dst"].reshape(-1)])[None]
    a["route4_par"] = np.stack([i["L2_ffn_b_gat"], i["L2_ffn_ln_gamma"], i["L2_ffn_ln_beta"]])[None]
    w1, b1, w2 = i["L2_ffn_W1"], i["L2_ffn_b1"], i["L2_ffn_W2"]
    a["moe4_w1"] = cat([w1.transpose(1, 0, 2), b1[None]], 0)
    a["moe4_w2"], a["moe4_b2"] = w2.transpose(1, 0, 2), i["L2_ffn_b2"][None]
    a["pk_wq"] = cat([i["L1_ffn_Wq_pk"], i["L1_ffn_Wq"]], 1).reshape(D, 8, P)
    keys = i["L1_ffn_pk_keys"].transpose(0, 2, 3, 1).reshape(4, 4, PK_DIM, PK_KEYS)
    wide = np.zeros((4, 4, PK_DIM, 4, PK_KEYS), np.float32)
    for q in range(4):
        wide[:, q, :, q] = keys[:, q]
    a["pk_keys"] = wide.reshape(4, P, 4 * PK_KEYS).transpose(1, 0, 2)
    a["pk_table"] = cat([i["L1_ffn_keys_table"], i["L1_ffn_values_table"]], 1)
    a["pk_wo"] = i["L1_ffn_Wo"].reshape(4, P, D).transpose(1, 0, 2)
    return a


def kernel(**inputs):
    import concourse.bacc as bacc
    from concourse.bass_utils import run_bass_kernel_spmd as run

    inputs = {k: np.asarray(v) for k, v in inputs.items()}
    nc = bacc.Bacc("TRN2", target_bir_lowering=False, num_devices=1)
    arrays = {k: np.ascontiguousarray(v) for k, v in {**constants(), **layouts(inputs)}.items()}
    d = {k: nc.dram_tensor(f"in_{k}", v.shape, mybir.dt.from_np(v.dtype), kind="ExternalInput").ap()
         for k, v in arrays.items()}
    out = nc.dram_tensor("out_h", (B, S, D), F32, kind="ExternalOutput").ap()
    tower(nc, d, out, STAGES)
    r = run(nc, [{f"in_{k}": v for k, v in arrays.items()}], core_ids=[0])
    return np.asarray(r.results[0]["out_h"])
```

```python
from contextlib import ExitStack

import numpy as np

import concourse.bass as bass
from concourse import mybir

F32 = mybir.dt.float32
BF16 = mybir.dt.bfloat16
I32 = mybir.dt.int32
U32 = mybir.dt.uint32
ALU = mybir.AluOpType
ACT = mybir.ActivationFunctionType
AX = mybir.AxisListType

P = 128
B = 2
S = 1024
D = 64
T = B * S
NT = T // P
TB = S // P
LN_EPS = 1e-5


class Stage:

    def __init__(self, nc, name):
        self.nc, self.name, self.sems = nc, name, []
        self.ctx = ExitStack()

    def __enter__(self):
        self.ctx.__enter__()
        return self

    def __exit__(self, *exc):
        self.ctx.__exit__(*exc)
        if self.sems:
            self.nc.clear_and_free_semaphores(self.sems)
            self.nc.all_engine_barrier()

    def sb(self, name, shape, dt=F32):
        return self.ctx.enter_context(self.nc.sbuf_tensor(f"{self.name}_{name}", shape, dt))

    def ps(self, name, shape, dt=F32):
        return self.ctx.enter_context(self.nc.psum_tensor(f"{self.name}_{name}", shape, dt))

    def sem(self, name):
        self.sems.append(self.nc.alloc_semaphore(f"{self.name}_{name}"))
        return self.sems[-1]

    def block(self):
        return self.ctx.enter_context(self.nc.Block())


class Chain:

    def __init__(self, engine, semaphore):
        self.engine, self.semaphore, self.count = engine, semaphore, 0

    def __call__(self, instruction):
        self.count += 1
        instruction.then_inc(self.semaphore, 1)
        self.engine.wait_ge(self.semaphore, self.count)


def bc(ap, shape):
    return ap.broadcast_to(shape)


def normalise(nc, m, tag):
    h, xn, xT, ident, eps = m["h"], m["xn"], m["xT"], m["ident"], m["eps"]
    with Stage(nc, f"ln{tag}") as s:
        mean = s.sb("mean", [P, NT])
        var = s.sb("var", [P, NT])
        std = s.sb("std", [P, NT])
        rstd = s.sb("rstd", [P, NT])
        square = s.sb("square", [P, NT, D])
        turned = [s.ps(f"turned{k}", [P, 512]) for k in range(4)]
        dve = s.sem("dve_step")
        var_ready = s.sem("var_ready")
        std_ready = s.sem("std_ready")
        xn_ready = s.sem("xn_ready")
        turned_ready = s.sem("turned_ready")
        block = s.block()

        @block.vector
        def _(v):
            step = Chain(v, dve)
            step(v.tensor_reduce(mean[:, :], h[:, :, :], AX.X, ALU.add))
            step(v.tensor_scalar(mean[:, :], mean[:, :], 1.0 / D, None, ALU.mult))
            step(v.tensor_tensor(xn[:, :, :], h[:, :, :], bc(mean[:, :].unsqueeze(2), [P, NT, D]), ALU.subtract))
            step(v.tensor_tensor(square[:, :, :], xn[:, :, :], xn[:, :, :], ALU.mult))
            step(v.tensor_reduce(var[:, :], square[:, :, :], AX.X, ALU.add))
            v.tensor_scalar(var[:, :], var[:, :], 1.0 / D, None, ALU.mult).then_inc(var_ready, 1)
            v.wait_ge(std_ready, 1)
            step(v.reciprocal(rstd[:, :], std[:, :]))
            for half in range(2):
                t = slice(half * TB, half * TB + TB)
                v.tensor_tensor(xn[:, t, :], xn[:, t, :], bc(rstd[:, t].unsqueeze(2), [P, TB, D]),
                                ALU.mult).then_inc(xn_ready, 1)
            for k in range(0, 4, 2):
                v.wait_ge(turned_ready, k + 1)
                v.tensor_copy(xT[0:D, k * 512:k * 512 + 512], turned[k][0:D, :])

        @block.scalar
        def _(a):
            a.wait_ge(var_ready, 1)
            a.activation(std[:, :], var[:, :], ACT.Sqrt, bias=eps[:, 0:1]).then_inc(std_ready, 1)
            for k in range(1, 4, 2):
                a.wait_ge(turned_ready, k + 1)
                a.copy(xT[0:D, k * 512:k * 512 + 512], turned[k][0:D, :])

        @block.tensor
        def _(pe):
            for k in range(4):
                if k % 2 == 0:
                    pe.wait_ge(xn_ready, k // 2 + 1)
                for j in range(4):
                    last = pe.transpose(turned[k][0:D, j * P:j * P + P], xn[:, 4 * k + j, :], ident[:, :])
                last.then_inc(turned_ready, 1)


def linear_attention(nc, m, d):
    h, xT = m["h"], m["xT"]
    with Stage(nc, "la") as s:
        w_kv = s.sb("w_kv", [D + 1, 2 * D])
        w_q = s.sb("w_q", [D + 1, D])
        w_fc = s.sb("w_fc", [D, D])
        head_mask = s.sb("head_mask", [D, D])
        vk = s.sb("vk", [P, NT, 2 * D])
        qT = s.sb("qT", [D + 1, T])
        pT = s.sb("pT", [D, B, D])
        fold = s.sb("fold", [D + 1, B, D])
        ps_vk = [s.ps(f"ps_vk{k}", [P, 4, 2 * D]) for k in range(2)]
        ps_q = [s.ps(f"ps_q{k}", [P, 512]) for k in range(2)]
        ps_p = s.ps("ps_p", [P, B, D])
        ps_f = s.ps("ps_f", [P, B, D])
        ps_o = [s.ps(f"ps_o{k}", [P, TB, D]) for k in range(B)]
        loaded = s.sem("loaded")
        vk_made = s.sem("vk_made")
        vk_kept = s.sem("vk_kept")
        q_made = s.sem("q_made")
        q_kept = s.sem("q_kept")
        p_made = s.sem("p_made")
        p_kept = s.sem("p_kept")
        f_made = s.sem("f_made")
        f_kept = s.sem("f_kept")
        o_made = s.sem("o_made")
        ones_set = s.sem("ones_set")
        block = s.block()
        LOADS = 6 * 16

        @block.sync
        def _(sp):
            sp.dma_start(w_kv[:, :], d["la_w_vk"]).then_inc(loaded, 16)
            sp.dma_start(w_q[:, :], d["la_w_q"]).then_inc(loaded, 16)
            sp.dma_start(w_fc[:, :], d["la_w_fc"]).then_inc(loaded, 16)
            sp.dma_start(head_mask[:, :], d["head_mask"]).then_inc(loaded, 16)
            for b in range(B):
                sp.dma_start(fold[D:D + 1, b, :], d["la_b_fc"]).then_inc(loaded, 16)

        @block.tensor
        def _(pe):
            pe.wait_ge(loaded, LOADS)
            for k in range(4):
                if k >= 2:
                    pe.wait_ge(vk_kept, k - 1)
                for j in range(4):
                    t = 4 * k + j
                    last = pe.matmul(ps_vk[k % 2][:, j, :], xT[:, t * P:t * P + P], w_kv[:, :],
                                     start=True, stop=True)
                last.then_inc(vk_made, 1)
            for k in range(4):
                if k >= 2:
                    pe.wait_ge(q_kept, k - 1)
                pe.matmul(ps_q[k % 2][0:D, :], w_q[:, :], xT[:, k * 512:k * 512 + 512],
                          start=True, stop=True).then_inc(q_made, 1)
            pe.wait_ge(vk_kept, 4)
            for b in range(B):
                for j in range(TB):
                    t = b * TB + j
                    last = pe.matmul(ps_p[0:D, b, :], vk[:, t, 0:D], vk[:, t, D:2 * D],
                                     start=(j == 0), stop=(j == TB - 1))
                last.then_inc(p_made, 1)
            for b in range(B):
                pe.wait_ge(p_kept, b + 1)
                pe.matmul(ps_f[0:D, b, :], pT[:, b, :], w_fc[:, :], start=True, stop=True).then_inc(f_made, 1)
            pe.wait_ge(q_kept, 4)
            pe.wait_ge(ones_set, 1)
            for b in range(B):
                pe.wait_ge(f_kept, b + 1)
                for j in range(TB):
                    t = b * TB + j
                    last = pe.matmul(ps_o[b][:, j, :], qT[:, t * P:t * P + P], fold[:, b, :],
                                     start=True, stop=True)
                last.then_inc(o_made, 1)

        @block.vector
        def _(v):
            v.memset(qT[D:D + 1, :], 1.0).then_inc(ones_set, 1)
            for k in range(4):
                v.wait_ge(vk_made, k + 1)
                v.tensor_copy(vk[:, 4 * k:4 * k + 4, :], ps_vk[k % 2][:, :, :]).then_inc(vk_kept, 1)
            v.wait_ge(p_made, B)
            for b in range(B):
                v.tensor_tensor(pT[:, b, :], ps_p[0:D, b, :], head_mask[:, :], ALU.mult).then_inc(p_kept, 1)
            v.wait_ge(f_made, B)
            for b in range(B):
                v.tensor_copy(fold[0:D, b, :], ps_f[0:D, b, :]).then_inc(f_kept, 1)
            for b in range(B):
                v.wait_ge(o_made, b + 1)
                t = slice(b * TB, b * TB + TB)
                v.tensor_tensor(h[:, t, :], h[:, t, :], ps_o[b][:, :, :], ALU.add)

        @block.scalar
        def _(a):
            for k in range(4):
                a.wait_ge(q_made, k + 1)
                a.copy(qT[0:D, k * 512:k * 512 + 512], ps_q[k % 2][0:D, :]).then_inc(q_kept, 1)


RET_GAMMA = 0.96875
RET_SCALE_BASE = 512.0


def retention(nc, m, d):
    h, xT, ident = m["h"], m["xT"], m["ident"]
    HALF = D // 2
    with Stage(nc, "ret") as s:
        w = s.sb("w", [D, 3 * D])
        cos = s.sb("cos", [P, TB, 2, HALF])
        sin = s.sb("sin", [P, TB, 2, HALF])
        decay = s.sb("decay", [P, P])
        k_decay = s.sb("k_decay", [P, 1])
        q_decay = s.sb("q_decay", [D, P])
        qkv = s.sb("qkv", [P, NT, 3 * D])
        rot = s.sb("rot", [P, NT, 2 * D])
        tmp = s.sb("tmp", [P, TB, 2, HALF])
        tmp2 = s.sb("tmp2", [P, TB, 2, HALF])
        kd = s.sb("kd", [P, NT, D])
        qT = s.sb("qT", [D, T])
        qTd = s.sb("qTd", [D, T])
        kT = s.sb("kT", [D, T])
        probs = s.sb("probs", [P, NT, P])
        state = s.sb("state", [D, TB, B, D])
        ps = [s.ps(f"ps{k}", [P, 512]) for k in range(8)]
        loaded = s.sem("loaded")
        qkv_made = s.sem("qkv_made")
        qkv_kept = s.sem("qkv_kept")
        dve = s.sem("dve_step")
        rotated = s.sem("rotated")
        turned = s.sem("turned")
        q_kept = s.sem("q_kept")
        k_kept = s.sem("k_kept")
        qd_kept = s.sem("qd_kept")
        scores_made = s.sem("scores_made")
        probs_kept = s.sem("probs_kept")
        kd_kept = s.sem("kd_kept")
        kv_made = s.sem("kv_made")
        states_kept = s.sem("states_kept")
        out_made = s.sem("out_made")
        block = s.block()
        LOADS = 6 * 16

        def halves(t):
            return t[:, :].rearrange("p (a e c) -> p a e c", a=2, e=2)

        @block.sync
        def _(sp):
            sp.dma_start(w[:, :], d["ret_w"]).then_inc(loaded, 16)
            sp.dma_start(cos[:, :, :, :], d["ret_cos"].rearrange("(t p) a c -> p t a c", p=P)).then_inc(loaded, 16)
            sp.dma_start(sin[:, :, :, :], d["ret_sin"].rearrange("(t p) a c -> p t a c", p=P)).then_inc(loaded, 16)
            sp.dma_start(decay[:, :], d["ret_decay"]).then_inc(loaded, 16)
            sp.dma_start(k_decay[:, :], d["ret_k_decay"]).then_inc(loaded, 16)
            sp.dma_start(q_decay[:, :], d["ret_q_decay"].broadcast_to([D, P])).then_inc(loaded, 16)

        @block.tensor
        def _(pe):
            pe.wait_ge(loaded, LOADS)
            for t in range(NT):
                last = pe.matmul(ps[t // 2][:, (t % 2) * 192:(t % 2) * 192 + 192], xT[0:D, t * P:t * P + P],
                                 w[:, :], start=True, stop=True)
                if t % 2 == 1:
                    last.then_inc(qkv_made, 1)
            for b in range(B):
                pe.wait_ge(rotated, b + 1)
                pe.wait_ge(qkv_kept, NT // 2)
                for g in range(2):
                    for qk in range(2):
                        bank = ps[4 * b + 2 * g + qk]
                        for j in range(4):
                            t = b * TB + 4 * g + j
                            last = pe.transpose(bank[0:D, j * P:j * P + P], rot[:, t, qk * D:qk * D + D], ident[:, :])
                        last.then_inc(turned, 1)
            for g in range(4):
                pe.wait_ge(k_kept, g + 1)
                pe.wait_ge(q_kept, g + 1)
                pe.wait_ge(qd_kept, g + 1)
                for j in range(4):
                    t = 4 * g + j
                    last = pe.matmul(ps[2 * g][:, j * P:j * P + P], kT[:, t * P:t * P + P],
                                     qT[:, t * P:t * P + P], start=True, stop=True)
                last.then_inc(scores_made, 1)
            pe.wait_ge(kd_kept, 1)
            for b in range(B):
                for c in range(TB):
                    t = b * TB + c
                    last = pe.matmul(ps[2 * b + 1][0:D, c * D:c * D + D], kd[:, t, :], qkv[:, t, 2 * D:3 * D],
                                     start=True, stop=True)
            last.then_inc(kv_made, 1)
            pe.wait_ge(states_kept, 1)
            pe.wait_ge(probs_kept, 4)
            for b in range(B):
                for c in range(TB):
                    t = b * TB + c
                    o = ps[4 + 2 * b + 1][:, c * D:c * D + D]
                    last = pe.matmul(o, probs[:, t, :], qkv[:, t, 2 * D:3 * D], start=True, stop=(c == 0))
                    if c > 0:
                        last = pe.matmul(o, qTd[:, t * P:t * P + P], state[:, c, b, :], start=False, stop=True)
                last.then_inc(out_made, 1)

        @block.scalar
        def _(a):
            for k in range(NT // 2):
                a.wait_ge(qkv_made, k + 1)
                a.copy(qkv[:, 2 * k:2 * k + 2, :],
                       ps[k][:, 0:384].rearrange("p (t c) -> p t c", t=2)).then_inc(qkv_kept, 1)
            for g in range(4):
                a.wait_ge(turned, 2 * g + 1)
                a.copy(qT[:, g * 512:g * 512 + 512], ps[2 * g][0:D, :]).then_inc(q_kept, 1)

        @block.vector
        def _(v):
            step = Chain(v, dve)
            v.wait_ge(loaded, LOADS)
            for b in range(B):
                v.wait_ge(qkv_kept, TB // 2 * (b + 1))
                t = slice(b * TB, b * TB + TB)
                x = qkv[:, t, 0:2 * D].rearrange("p t (a e c) -> p t a e c", a=2, e=2)
                y = rot[:, t, :].rearrange("p t (a e c) -> p t a e c", a=2, e=2)
                x1, x2, y1, y2 = x[:, :, :, 0, :], x[:, :, :, 1, :], y[:, :, :, 0, :], y[:, :, :, 1, :]
                c4, s4, u, w4 = cos[:, :, :, :], sin[:, :, :, :], tmp[:, :, :, :], tmp2[:, :, :, :]
                step(v.tensor_tensor(y1, x1, c4, ALU.mult))
                step(v.tensor_tensor(u, x2, s4, ALU.mult))
                step(v.tensor_tensor(y1, y1, u, ALU.subtract))
                step(v.tensor_tensor(w4, x1, s4, ALU.mult))
                step(v.tensor_tensor(y2, x2, c4, ALU.mult))
                v.tensor_tensor(y2, y2, w4, ALU.add).then_inc(rotated, 1)
            v.wait_ge(rotated, B)
            v.tensor_scalar(kd[:, :, :], rot[:, :, D:2 * D], k_decay[:, 0:1], None, ALU.mult).then_inc(kd_kept, 1)
            for g in range(4):
                v.wait_ge(q_kept, g + 1)
                v.tensor_tensor(qTd[:, g * 512:g * 512 + 512].rearrange("p (j n) -> p j n", j=4),
                                qT[:, g * 512:g * 512 + 512].rearrange("p (j n) -> p j n", j=4),
                                bc(q_decay[:, :].unsqueeze(1), [D, 4, P]), ALU.mult).then_inc(qd_kept, 1)
                v.wait_ge(turned, 2 * g + 2)
                v.tensor_copy(kT[:, g * 512:g * 512 + 512], ps[2 * g + 1][0:D, :]).then_inc(k_kept, 1)
            for g in range(4):
                v.wait_ge(scores_made, g + 1)
                v.tensor_tensor(probs[:, 4 * g:4 * g + 4, :], ps[2 * g][:, :].rearrange("p (j n) -> p j n", j=4),
                                bc(decay[:, :].unsqueeze(1), [P, 4, P]), ALU.mult).then_inc(probs_kept, 1)
            v.wait_ge(kv_made, 1)
            for c in range(1, TB):
                for b in range(B):
                    kv = ps[2 * b + 1][0:D, (c - 1) * D:c * D]
                    if c == 1:
                        step(v.tensor_copy(state[:, c, b, :], kv))
                    else:
                        step(v.scalar_tensor_tensor(state[:, c, b, :], state[:, c - 1, b, :], RET_GAMMA ** P,
                                                    kv, ALU.mult, ALU.add))
            v.engine_nop().then_inc(states_kept, 1)
            for b in range(B):
                v.wait_ge(out_made, b + 1)
                t = slice(b * TB, b * TB + TB)
                v.tensor_tensor(h[:, t, :], h[:, t, :],
                                ps[4 + 2 * b + 1][:, :].rearrange("p (t c) -> p t c", t=TB), ALU.add)


def retention_tables():
    c = {}
    inv_freq = (1.0 / np.float32(10000.0) ** (np.arange(0, D, 2, dtype=np.float32) / np.float32(D))).astype(np.float32)
    pos = np.arange(S, dtype=np.float32)
    ang = pos[:, None] * inv_freq[None, :]
    base = ((np.arange(0, D, 2, dtype=np.float32) + np.float32(0.4 * D)) / np.float32(1.4 * D)).astype(np.float32)
    scale = base[None, :] ** (pos[:, None] / np.float32(RET_SCALE_BASE))
    sin, cos = np.sin(ang), np.cos(ang)
    c["ret_cos"] = np.stack([cos * scale, cos / scale], 1).astype(np.float32)
    c["ret_sin"] = np.stack([sin * scale, sin / scale], 1).astype(np.float32)
    n = np.arange(P, dtype=np.float64)
    diff = n[None, :] - n[:, None]
    c["ret_decay"] = np.where(diff >= 0, RET_GAMMA ** np.maximum(diff, 0), 0.0).astype(np.float32)
    c["ret_k_decay"] = (RET_GAMMA ** (P - n))[:, None].astype(np.float32)
    c["ret_q_decay"] = (RET_GAMMA ** n)[None, :].astype(np.float32)
    return c


MAGIC = 12582912.0
SPLIT = 1536.0
TWO_PI = 6.2831850


def recurrence(nc, m, d):
    h, xT = m["h"], m["xT"]
    with Stage(nc, "rec") as s:
        w_in = s.sb("w_in", [D, 2, P])
        w_out = s.sb("w_out", [P, 2, D])
        par = s.sb("par", [P, 3])
        signs = s.sb("signs", [P, 2])
        ramp = s.sb("ramp", [P, S])
        mod = s.sb("mod", [P, 1])
        gam = s.sb("gam", [P, 1])
        turn = s.sb("turn", [P, 4])
        mod_row = s.sb("mod_row", [P, S])
        ang = s.sb("ang", [P, S])
        rnd = s.sb("rnd", [P, S])
        lo = s.sb("lo", [P, S])
        cosT = s.sb("cosT", [P, S])
        sinT = s.sb("sinT", [P, S])
        bx = s.sb("bx", [P, B, S])
        bx2 = s.sb("bx2", [P, B, S])
        g = s.sb("g", [P, B, S])
        gc = s.sb("gc", [P, B, S])
        gs = s.sb("gs", [P, B, S])
        ps = [s.ps(f"ps{k}", [P, 512]) for k in range(8)]
        loaded = s.sem("loaded")
        acts = s.sem("act_step")
        dve = s.sem("dve_step")
        exps_ready = s.sem("exps_ready")
        angle_ready = s.sem("angle_ready")
        table_ready = s.sem("table_ready")
        bx_made = s.sem("bx_made")
        g_ready = s.sem("g_ready")
        out_made = s.sem("out_made")
        w_ready = s.sem("w_ready")
        block = s.block()
        LOADS = 5 * 16

        @block.sync
        def _(sp):
            sp.dma_start(par[:, :], d["rec_par"]).then_inc(loaded, 16)
            sp.dma_start(signs[:, :], d["rec_signs"]).then_inc(loaded, 16)
            sp.dma_start(ramp[:, :], d["rec_ramp"].broadcast_to([P, S])).then_inc(loaded, 16)
            sp.dma_start(w_in[:, :, :], d["rec_w_in"]).then_inc(loaded, 16)
            sp.dma_start(w_out[:, :, :], d["rec_w_out"]).then_inc(loaded, 16)

        @block.scalar
        def _(a):
            step = Chain(a, acts)
            a.wait_ge(loaded, LOADS)
            step(a.activation(mod[:, :], par[:, 0:1], ACT.Exp))
            step(a.activation(mod[:, :], mod[:, :], ACT.Exp, scale=-1.0))
            a.activation(turn[:, 0:1], par[:, 1:2], ACT.Exp).then_inc(exps_ready, 1)
            a.activation(gam[:, :], par[:, 2:3], ACT.Exp).then_inc(exps_ready, 1)
            a.wait_ge(angle_ready, 1)
            a.activation(sinT[:, :], ang[:, :], ACT.Sin, scale=TWO_PI).then_inc(table_ready, 1)
            a.wait_ge(angle_ready, 2)
            a.activation(cosT[:, :], lo[:, :], ACT.Sin, scale=TWO_PI).then_inc(table_ready, 1)

        @block.tensor
        def _(pe):
            pe.wait_ge(loaded, LOADS)
            for k in range(4):
                for form in range(2):
                    last = pe.matmul(ps[2 * k + form][:, :], w_in[:, form, :], xT[0:D, k * 512:k * 512 + 512],
                                     start=True, stop=True)
            last.then_inc(bx_made, 1)
            pe.wait_ge(w_ready, 2)
            for b in range(B):
                pe.wait_ge(g_ready, b + 1)
                for j in range(TB):
                    o = ps[b][:, j * D:j * D + D]
                    pe.matmul(o, gc[:, b, j * P:j * P + P], w_out[:, 0, :], start=True, stop=False)
                    last = pe.matmul(o, gs[:, b, j * P:j * P + P], w_out[:, 1, :], start=False, stop=True)
                last.then_inc(out_made, 1)

        @block.vector
        def _(v):
            step = Chain(v, dve)
            v.wait_ge(loaded, LOADS)
            v.tensor_scalar(w_out[:, 0, :], w_out[:, 0, :], signs[:, 0:1], None, ALU.mult).then_inc(w_ready, 1)
            v.tensor_scalar(w_out[:, 1, :], w_out[:, 1, :], signs[:, 1:2], None, ALU.mult).then_inc(w_ready, 1)
            v.wait_ge(exps_ready, 2)
            step(v.tensor_scalar(turn[:, 0:1], turn[:, 0:1], 1.0 / (2 * np.pi), None, ALU.mult))
            step(v.tensor_scalar(turn[:, 1:2], turn[:, 0:1], MAGIC, MAGIC, ALU.add, ALU.subtract))
            step(v.tensor_tensor(turn[:, 0:1], turn[:, 0:1], turn[:, 1:2], ALU.subtract))
            step(v.tensor_scalar(turn[:, 2:3], turn[:, 0:1], SPLIT, SPLIT, ALU.add, ALU.subtract))
            step(v.tensor_tensor(turn[:, 3:4], turn[:, 0:1], turn[:, 2:3], ALU.subtract))
            step(v.tensor_scalar(ang[:, :], ramp[:, :], turn[:, 2:3], None, ALU.mult))
            step(v.tensor_scalar(rnd[:, :], ang[:, :], MAGIC, MAGIC, ALU.add, ALU.subtract))
            step(v.tensor_tensor(ang[:, :], ang[:, :], rnd[:, :], ALU.subtract))
            step(v.tensor_scalar(lo[:, :], ramp[:, :], turn[:, 3:4], None, ALU.mult))
            step(v.tensor_tensor(lo[:, :], ang[:, :], lo[:, :], ALU.add))
            step(v.tensor_scalar(rnd[:, :], lo[:, :], MAGIC, MAGIC, ALU.add, ALU.subtract))
            v.tensor_tensor(ang[:, :], lo[:, :], rnd[:, :], ALU.subtract).then_inc(angle_ready, 1)
            v.wait_ge(angle_ready, 1)
            step(v.tensor_scalar(lo[:, :], ang[:, :], 0.25, None, ALU.add))
            step(v.tensor_scalar(rnd[:, :], lo[:, :], MAGIC, MAGIC, ALU.add, ALU.subtract))
            v.tensor_tensor(lo[:, :], lo[:, :], rnd[:, :], ALU.subtract).then_inc(angle_ready, 1)
            step(v.memset(mod_row[:, :], 1.0))
            step(v.tensor_scalar(mod_row[:, :], mod_row[:, :], mod[:, 0:1], None, ALU.mult))
            v.wait_ge(table_ready, 2)
            step(v.tensor_scalar(sinT[:, :], sinT[:, :], signs[:, 0:1], None, ALU.mult))
            v.wait_ge(bx_made, 1)
            for b in range(B):
                for k in range(2):
                    c = slice(k * 512, k * 512 + 512)
                    step(v.scalar_tensor_tensor(bx[:, b, c], ps[4 * b + 2 * k][:, :], gam[:, 0:1], cosT[:, c],
                                                ALU.mult, ALU.mult))
                    step(v.scalar_tensor_tensor(bx2[:, b, c], ps[4 * b + 2 * k + 1][:, :], gam[:, 0:1], sinT[:, c],
                                                ALU.mult, ALU.mult))
                step(v.tensor_tensor(bx[:, b, :], bx[:, b, :], bx2[:, b, :], ALU.add))
            for b in range(B):
                step(v.tensor_tensor_scan(g[:, b, :], mod_row[:, :], bx[:, b, :], 0.0, ALU.mult, ALU.add))
                step(v.tensor_tensor(gc[:, b, :], g[:, b, :], cosT[:, :], ALU.mult))
                v.tensor_tensor(gs[:, b, :], g[:, b, :], sinT[:, :], ALU.mult).then_inc(g_ready, 1)
            for b in range(B):
                v.wait_ge(out_made, b + 1)
                t = slice(b * TB, b * TB + TB)
                v.tensor_tensor(h[:, t, :], h[:, t, :], ps[b][:, :].rearrange("p (t c) -> p t c", t=TB), ALU.add)


def recurrence_tables():
    c = {"rec_ramp": np.arange(S, dtype=np.float32)[None]}
    sg = np.ones((P, 2), np.float32)
    sg[D:, 0] = -1.0
    sg[:, 1] = -1.0
    sg[D:, 1] = 1.0
    c["rec_signs"] = sg
    return c


VOCAB = 64
SCALES = 4
CONV = ((7, 3), (5, 2), (3, 1))
PAIRS = TB // 2


def embed(nc, m, d):
    h, ident = m["h"], m["ident"]
    PAD1, PAD2, PAD3 = (p for _, p in CONV)
    with Stage(nc, "emb") as s:
        amps = s.sb("amps", [P, NT, D])
        scale4 = s.sb("scale4", [P, NT, SCALES])
        center = s.sb("center", [P, NT])
        shift = s.sb("shift", [P, NT])
        inv = s.sb("inv", [P, NT, SCALES])
        pos = s.sb("pos", [P, B, S])
        pos_loaded = s.sem("pos_loaded")
        with Stage(nc, "conv") as c:
            ids = c.sb("ids", [P, B, S], I32)
            vocab = c.sb("vocab", [P, 1])
            W1 = S + 2 * PAD1 + 1
            hot = c.sb("hot", [P, B, W1])
            w1 = c.sb("w1", [P, 4, P])
            w2 = c.sb("w2", [P, CONV[1][0], D])
            w3 = c.sb("w3", [D, CONV[2][0]])
            b1 = c.sb("b1", [P, 1])
            b2 = c.sb("b2", [D, 1])
            b3 = c.sb("b3", [P, 1])
            table = c.sb("table", [VOCAB, D + 4])
            widths = c.sb("widths", [P, SCALES])
            weights = c.sb("weights", [P, SCALES])
            where = c.sb("where", [P, NT])
            h1 = c.sb("h1", [P, B, S + 2 * PAD2])
            h2 = c.sb("h2", [D, B, S + 2 * PAD3])
            emb = c.sb("emb", [P, NT, D + 4])
            gate = c.sb("gate", [P, NT])
            amp = c.sb("amp", [P, NT])
            absw = c.sb("absw", [P, NT])
            ps = [c.ps(f"ps{k}", [P, 512]) for k in range(8)]
            names = ["loaded", "hot_set", "hot_ready", "c1_made", "h1_kept", "c2_made", "h2_kept", "emb_made",
                     "emb_kept", "gate_made", "gate_kept", "amp_kept", "dve_step", "pads_set"]
            (loaded, hot_set, hot_ready, c1_made, h1_kept, c2_made, h2_kept, emb_made, emb_kept, gate_made,
             gate_kept, amp_kept, dve, pads_set) = [c.sem(n) for n in names]
            block = c.block()
            LOADS = 13 * 16

            @block.sync
            def _(sp):
                for half in range(2):
                    sp.dma_start(ids[half * D:half * D + D, :, :], d["ids"].unsqueeze(0).broadcast_to([D, B, S])
                                 ).then_inc(loaded, 16)
                for buf, name in ((w1, "emb_w1"), (w2, "emb_w2"), (w3, "emb_w3"), (b1, "emb_b1"), (b2, "emb_b2"),
                                  (table, "emb_table"), (vocab, "vocab2"), (where, "emb_where")):
                    sp.dma_start(buf[tuple([slice(None)] * len(buf.shape))], d[name]).then_inc(loaded, 16)
                for buf, name, n in ((b3, "emb_b3", 1), (widths, "emb_widths", SCALES),
                                     (weights, "emb_weights", SCALES)):
                    sp.dma_start(buf[:, :], d[name].broadcast_to([P, n])).then_inc(loaded, 16)
                sp.dma_start(pos[:, :, :], d["positions"].unsqueeze(0).broadcast_to([P, B, S])).then_inc(pos_loaded, 16)

            @block.gpsimd
            def _(g):
                for b in range(B):
                    g.memset(h1[:, b, 0:PAD2], 0.0)
                    g.memset(h1[:, b, PAD2 + S:], 0.0)
                    g.memset(h2[:, b, 0:PAD3], 0.0)
                    last = g.memset(h2[:, b, PAD3 + S:], 0.0)
                last.then_inc(pads_set, 1)

            @block.vector
            def _(v):
                step = Chain(v, dve)
                v.memset(hot[:, :, :], 0.0).then_inc(hot_set, 1)
                v.wait_ge(hot_set, 1)
                v.wait_ge(loaded, LOADS)
                v.tensor_scalar(hot[0:D, :, PAD1:PAD1 + S], ids[0:D, :, :], vocab[0:D, 0:1], None,
                                ALU.is_equal).then_inc(hot_ready, 1)
                v.tensor_scalar(hot[D:P, :, PAD1 - 1:PAD1 - 1 + S], ids[D:P, :, :], vocab[D:P, 0:1], None,
                                ALU.is_equal).then_inc(hot_ready, 1)
                for k in range(4):
                    v.wait_ge(emb_made, k + 1)
                    v.tensor_copy(emb[:, 4 * k:4 * k + 4, :],
                                  ps[k][:, 0:4 * (D + 4)].rearrange("p (t c) -> p t c", t=4)).then_inc(emb_kept, 1)
                v.wait_ge(emb_kept, 4)
                lp = [emb[:, :, D + k] for k in range(4)]
                step(v.scalar_tensor_tensor(center[:, :], lp[0], 0.05, where[:, :], ALU.mult, ALU.add))
                step(v.tensor_scalar(shift[:, :], lp[3], 0.5, 0.25, ALU.mult, ALU.add))
                step(v.scalar_tensor_tensor(absw[:, :], lp[1], -1.0, lp[1], ALU.mult, ALU.max))
                for k in range(SCALES):
                    step(v.tensor_scalar(inv[:, :, k], absw[:, :], widths[:, k:k + 1], None, ALU.mult))
                step(v.tensor_scalar(inv[:, :, :], inv[:, :, :], 1e-5, None, ALU.add))
                step(v.reciprocal(inv[:, :, :], inv[:, :, :]))
                step(v.tensor_tensor(weights[:, :], weights[:, :], weights[:, :], ALU.mult))
                v.wait_ge(amp_kept, 1)
                for k in range(SCALES):
                    step(v.tensor_scalar(scale4[:, :, k], amp[:, :], weights[:, k:k + 1], None, ALU.mult))
                v.wait_ge(gate_kept, 1)
                step(v.tensor_tensor(amps[:, :, :], emb[:, :, 0:D], bc(gate[:, :].unsqueeze(2), [P, NT, D]), ALU.mult))

            @block.tensor
            def _(pe):
                pe.wait_ge(hot_ready, 2)
                for t in range(NT):
                    b, j = t // TB, t % TB
                    mm = pe.matmul(ps[t // 4][:, (t % 4) * (D + 4):(t % 4 + 1) * (D + 4)],
                                   hot[0:D, b, PAD1 + j * P:PAD1 + j * P + P], table[:, :], start=True, stop=True)
                    if t % 4 == 3:
                        mm.then_inc(emb_made, 1)
                for k in range(4):
                    b, j = k // 2, (k % 2) * 512
                    for tap in range(4):
                        mm = pe.matmul(ps[4 + k][:, :], w1[:, tap, :], hot[:, b, j + 2 * tap:j + 2 * tap + 512],
                                       start=(tap == 0), stop=(tap == 3))
                    mm.then_inc(c1_made, 1)
                pe.wait_ge(emb_kept, 4)
                pe.wait_ge(pads_set, 1)
                for k in range(4):
                    b, j = k // 2, (k % 2) * 512
                    pe.wait_ge(h1_kept, 2 * (b + 1))
                    for tap in range(CONV[1][0]):
                        mm = pe.matmul(ps[k][0:D, :], w2[:, tap, :], h1[:, b, j + tap:j + tap + 512],
                                       start=(tap == 0), stop=(tap == CONV[1][0] - 1))
                    mm.then_inc(c2_made, 1)
                pe.wait_ge(h2_kept, 4)
                for t in range(NT):
                    b, j = t // TB, (t % TB) * P
                    for tap in range(CONV[2][0]):
                        mm = pe.matmul(ps[4][:, t:t + 1], h2[:, b, j + tap:j + tap + P], w3[:, tap:tap + 1],
                                       start=(tap == 0), stop=(tap == CONV[2][0] - 1))
                mm.then_inc(gate_made, 1)

            @block.scalar
            def _(a):
                for k in range(4):
                    b, j = k // 2, (k % 2) * 512
                    a.wait_ge(c1_made, k + 1)
                    a.activation(h1[:, b, PAD2 + j:PAD2 + j + 512], ps[4 + k][:, :], ACT.Gelu,
                                 bias=b1[:, 0:1]).then_inc(h1_kept, 1)
                for k in range(4):
                    b, j = k // 2, (k % 2) * 512
                    a.wait_ge(c2_made, k + 1)
                    a.activation(h2[:, b, PAD3 + j:PAD3 + j + 512], ps[k][0:D, :], ACT.Gelu,
                                 bias=b2[:, 0:1]).then_inc(h2_kept, 1)
                a.wait_ge(emb_kept, 4)
                a.activation(amp[:, :], emb[:, :, D + 2], ACT.Sigmoid).then_inc(amp_kept, 1)
                a.wait_ge(gate_made, 1)
                a.activation(gate[:, :], ps[4][:, 0:NT], ACT.Sigmoid, bias=b3[:, 0:1]).then_inc(gate_kept, 1)

        with Stage(nc, "field") as f:
            far = f.sb("far", [P, 2, 2, S])
            bell = f.sb("bell", [P, 2, 2, SCALES, S])
            wave = f.sb("wave", [P, 2, 2, SCALES, S])
            whole = f.sb("whole", [P, SCALES, S])
            amp4 = f.sb("amp4", [P, 2, 2, SCALES, D])
            fieldT = f.sb("fieldT", [D, T])
            ps = [f.ps(f"ps{k}", [P, 512]) for k in range(2)]
            turned = [f.ps(f"turned{k}", [P, 4, D]) for k in range(4)]
            names = ["far_ready", "wave_ready", "squares", "bells", "sines", "basis_ready", "pairs_done",
                     "amp_ready", "dve_step", "field_kept", "turned_ready", "whole_step", "whole_free"]
            (far_ready, wave_ready, squares, bells, sines, basis_ready, pairs_done, amp_ready, dve, field_kept,
             turned_ready, whole_step, whole_free) = [f.sem(n) for n in names]
            block = f.block()
            N = PAIRS

            @block.vector
            def _(v):
                v.wait_ge(pos_loaded, 16)
                v.engine_nop().then_inc(pairs_done, 2)
                v.engine_nop().then_inc(whole_free, 1)
                v.engine_nop().then_inc(field_kept, 1)
                with v.Fori(0, B) as b:
                    def angles(p):
                        r = p % 2
                        v.wait_ge(pairs_done, b * N + (p + 1))
                        for u in range(2):
                            t = b * TB + (2 * p + u)
                            v.tensor_scalar(far[:, r, u, :], pos[:, bass.ds(b, 1), :].rearrange("p b s -> p (b s)"),
                                            center[:, bass.ds(t, 1)], None, ALU.subtract).then_inc(far_ready, 1)
                            for k in range(SCALES):
                                v.tensor_scalar(amp4[:, r, u, k, :], amps[:, bass.ds(t, 1), :].rearrange("p t c -> p (t c)"),
                                                scale4[:, bass.ds(t, 1), k], None, ALU.mult).then_inc(amp_ready, 1)
                            v.wait_ge(far_ready, b * (2 * N) + (2 * p + u + 1))
                            for k in range(SCALES):
                                w = v.tensor_scalar(wave[:, r, u, k, :], far[:, r, u, :], inv[:, bass.ds(t, 1), k],
                                                    shift[:, bass.ds(t, 1)], ALU.mult, ALU.add)
                            w.then_inc(whole_step, 1)
                            v.wait_ge(whole_step, b * (4 * N) + (4 * p + 2 * u + 1))
                            v.wait_ge(whole_free, b * (2 * N) + (2 * p + u + 1))
                            v.tensor_scalar(whole[:, :, :], wave[:, r, u, :, :], MAGIC, MAGIC, ALU.add,
                                            ALU.subtract).then_inc(whole_step, 1)
                            v.wait_ge(whole_step, b * (4 * N) + (4 * p + 2 * u + 2))
                            v.tensor_tensor(wave[:, r, u, :, :], wave[:, r, u, :, :], whole[:, :, :],
                                            ALU.subtract).then_inc(whole_free, 1)

                    for p in range(N):
                        angles(p)
                for k in range(4):
                    v.wait_ge(turned_ready, k + 1)
                    v.tensor_copy(h[:, 4 * k:4 * k + 4, :], turned[k][:, :, :])

            @block.gpsimd
            def _(g):
                with g.Fori(0, B) as b:
                    for p in range(N):
                        for u in range(2):
                            g.wait_ge(sines, b * (2 * N) + (2 * p + u + 1))
                            g.tensor_tensor(bell[:, p % 2, u, :, :], bell[:, p % 2, u, :, :], wave[:, p % 2, u, :, :],
                                            ALU.mult).then_inc(basis_ready, 1)

            @block.scalar
            def _(a):
                with a.Fori(0, B) as b:
                    for p in range(N):
                        r = p % 2
                        a.wait_ge(pairs_done, b * N + (p + 1))
                        for u in range(2):
                            t = b * TB + (2 * p + u)
                            a.wait_ge(far_ready, b * (2 * N) + (2 * p + u + 1))
                            for k in range(SCALES):
                                a.activation(bell[:, r, u, k, :], far[:, r, u, :], ACT.Square,
                                             scale=inv[:, bass.ds(t, 1), k]).then_inc(squares, 1)
                        for u in range(2):
                            a.wait_ge(squares, b * (8 * N) + (8 * p + 4 * u + 4))
                            a.activation(bell[:, r, u, :, :], bell[:, r, u, :, :], ACT.Exp,
                                         scale=-0.5).then_inc(bells, 1)
                        for u in range(2):
                            a.wait_ge(whole_free, b * (2 * N) + (2 * p + u + 2))
                            a.activation(wave[:, r, u, :, :], wave[:, r, u, :, :], ACT.Sin,
                                         scale=TWO_PI).then_inc(sines, 1)
                    a.wait_ge(pairs_done, b * N + (N + 2))
                    for k in range(2):
                        a.copy(fieldT[:, bass.ds(b * S + k * 512, 512)], ps[k][0:D, :]).then_inc(field_kept, 1)

            @block.tensor
            def _(pe):
                pe.wait_ge(pos_loaded, 16)
                with pe.Fori(0, B) as b:
                    pe.wait_ge(field_kept, b * 2 + 1)
                    for p in range(N):
                        r = p % 2
                        pe.wait_ge(amp_ready, b * (8 * N) + (8 * p + 8))
                        for u in range(2):
                            pe.wait_ge(basis_ready, b * (2 * N) + (2 * p + u + 1))
                            for k in range(SCALES):
                                for q in range(2):
                                    mm = pe.matmul(ps[q][0:D, :], amp4[:, r, u, k, :],
                                                   bell[:, r, u, k, q * 512:q * 512 + 512],
                                                   start=(p == u == k == 0), stop=(p == N - 1 and u == 1 and k == SCALES - 1))
                        mm.then_inc(pairs_done, 1)
                for k in range(4):
                    pe.wait_ge(field_kept, k + 2)
                    for j in range(4):
                        last = pe.transpose(turned[k][:, j, :], fieldT[:, (4 * k + j) * P:(4 * k + j + 1) * P],
                                            ident[0:D, 0:D])
                    last.then_inc(turned_ready, 1)


def embed_tables():
    c = {"vocab2": np.concatenate([np.arange(VOCAB)] * 2).astype(np.float32)[:, None]}
    pos = np.linspace(0.0, 1.0, S, dtype=np.float32).reshape(TB, P).T
    c["emb_where"] = np.concatenate([pos, pos], 1)
    return c


TREE_DEPTH = 7
NODES = 2 ** (TREE_DEPTH + 1)
NODES_PER_BANK = 512 // D
NODE_CHUNKS = NODES // NODES_PER_BANK
BANKS = 8
POOL_RING = 6
SPLIT_COLS = 2048
SPLITS = NODES * D // SPLIT_COLS


def tree_ffn(nc, m, d):
    with Stage(nc, "tree") as s:
        own = {"gates": s.sb("gates", [P, NT, NODES]), "x": s.sb("x", [P, 2, T], BF16),
               "w": s.sb("w", [P, 3, NODES * D], BF16)}
        tree_gates(nc, m, own, d)
        tree_bias(nc, m, own, d)
        tree_outputs(nc, m, own)


def tree_gates(nc, m, own, d):
    xT, mask, x_parts, w_parts = m["xT"], own["gates"], own["x"], own["w"]
    with Stage(nc, "gate") as s:
        w1 = s.sb("w1", [D + 1, NODES])
        logits = s.sb("logits", [P, NT, NODES])
        right = s.sb("right", [P, NT, NODES])
        rest = s.sb("rest", [D, T])
        x2 = s.sb("x2", [D, T], BF16)
        raw = s.sb("raw", [P, 2, SPLIT_COLS])
        ps = [s.ps(f"ps{k}", [P, 512]) for k in range(8)]
        names = ["loaded", "logits_made", "logits_kept", "dve_step", "abs_kept", "gelu_kept", "gates_ready",
                 "x1_kept", "x2_kept", "x_rest", "part_kept", "part_left", "raw_used"]
        (loaded, logits_made, logits_kept, dve, abs_kept, gelu_kept, gates_ready, x1_kept, x2_kept, x_rest,
         part_kept, part_left, raw_used) = [s.sem(n) for n in names]
        w_loaded = [s.sem(f"w_loaded{k}") for k in range(2)]
        block = s.block()

        @block.sync
        def _(sp):
            sp.dma_start(w1[:, :], d["tree_w1"]).then_inc(loaded, 16)
            for k in range(SPLITS):
                c = slice(k * SPLIT_COLS, (k + 1) * SPLIT_COLS)
                if k >= 2:
                    sp.wait_ge(raw_used, k - 1)
                for half in range(2):
                    sp.dma_start(raw[half * D:half * D + D, k % 2, :], d["tree_w2"][:, c]).then_inc(w_loaded[k % 2], 16)

        @block.tensor
        def _(pe):
            pe.wait_ge(loaded, 16)
            for t in range(NT):
                last = pe.matmul(ps[t // 2][:, (t % 2) * NODES:(t % 2) * NODES + NODES],
                                 xT[:, t * P:t * P + P], w1[:, :], start=True, stop=True)
                if t % 2 == 1:
                    last.then_inc(logits_made, 1)

        @block.scalar
        def _(a):
            a.copy(x_parts[0:D, 0, :], xT[0:D, :]).then_inc(x1_kept, 1)
            for k in range(NT // 2):
                a.wait_ge(logits_made, k + 1)
                a.copy(logits[:, 2 * k:2 * k + 2, :],
                       ps[k][:, :].rearrange("p (t n) -> p t n", t=2)).then_inc(logits_kept, 1)
            a.wait_ge(x_rest, 1)
            a.copy(x2[:, :], rest[:, :]).then_inc(x2_kept, 1)
            a.copy(x_parts[D:P, 0, :], rest[:, :])
            a.wait_ge(gates_ready, 1)
            a.activation(logits[:, :, :], logits[:, :, :], ACT.Abs).then_inc(abs_kept, 1)
            a.wait_ge(abs_kept, 1)
            a.activation(logits[:, :, :], logits[:, :, :], ACT.Gelu).then_inc(gelu_kept, 1)
            a.wait_ge(x_rest, 2)
            a.copy(x_parts[D:P, 1, :], rest[:, :])
            for k in range(SPLITS):
                c = slice(k * SPLIT_COLS, (k + 1) * SPLIT_COLS)
                a.wait_ge(w_loaded[k % 2], (k // 2 + 1) * 32)
                a.copy(w_parts[:, 0, c], raw[:, k % 2, :]).then_inc(part_kept, 1)
                a.wait_ge(part_left, 2 * k + 1)
                a.copy(w_parts[:, 1, c], raw[:, k % 2, :]).then_inc(part_kept, 1)
                a.wait_ge(part_left, 2 * k + 2)
                a.copy(w_parts[0:D, 2, c], raw[0:D, k % 2, :]).then_inc(raw_used, 1)

        @block.gpsimd
        def _(g):
            g.wait_ge(x1_kept, 1)
            g.tensor_copy(x_parts[0:D, 1, :], x_parts[0:D, 0, :])
            for k in range(SPLITS):
                c = slice(k * SPLIT_COLS, (k + 1) * SPLIT_COLS)
                g.wait_ge(part_kept, 2 * k + 1)
                g.tensor_copy(w_parts[D:P, 2, c], w_parts[D:P, 0, c])

        @block.vector
        def _(v):
            step = Chain(v, dve)
            v.wait_ge(x1_kept, 1)
            v.tensor_tensor(rest[:, :], xT[0:D, :], x_parts[0:D, 0, :], ALU.subtract).then_inc(x_rest, 1)
            v.wait_ge(logits_kept, NT // 2)
            step(v.tensor_scalar(right[:, :, :], logits[:, :, :], 0.0, None, ALU.is_gt))
            step(v.memset(mask[:, :, NODES - 1:NODES], 0.0))
            v.memset(mask[:, :, 0:1], 1.0).then_inc(gates_ready, 1)
            v.wait_ge(gates_ready, 1)
            for level in range(TREE_DEPTH):
                n = 2 ** level
                here = slice(n - 1, 2 * n - 1)
                kids = mask[:, :, 2 * n - 1:4 * n - 1].rearrange("p t (k c) -> p t k c", c=2)
                step(v.tensor_tensor(kids[:, :, :, 1], mask[:, :, here], right[:, :, here], ALU.mult))
                step(v.tensor_tensor(kids[:, :, :, 0], mask[:, :, here], kids[:, :, :, 1], ALU.subtract))
            v.wait_ge(gelu_kept, 1)
            v.tensor_tensor(mask[:, :, :], mask[:, :, :], logits[:, :, :], ALU.mult)
            v.wait_ge(x2_kept, 1)
            v.tensor_tensor(rest[:, :], rest[:, :], x2[:, :], ALU.subtract).then_inc(x_rest, 1)
            for k in range(SPLITS):
                c = slice(k * SPLIT_COLS, (k + 1) * SPLIT_COLS)
                for part in range(2):
                    v.wait_ge(part_kept, 2 * k + part + 1)
                    v.tensor_tensor(raw[:, k % 2, :], raw[:, k % 2, :], w_parts[:, part, c],
                                    ALU.subtract).then_inc(part_left, 1)


def tree_bias(nc, m, own, d):
    h, ident, gates = m["h"], m["ident"], own["gates"]
    with Stage(nc, "treeb") as s:
        b2 = s.sb("b2", [P, 2, D])
        gT = s.sb("gT", [P, 2, 4, P])
        ps_t = [s.ps(f"ps_t{k}", [P, 4, P]) for k in range(2)]
        ps_y = [s.ps(f"ps_y{k}", [P, TB, D]) for k in range(2)]
        loaded = s.sem("loaded")
        turned = s.sem("turned")
        kept = s.sem("kept")
        made = s.sem("made")
        block = s.block()

        @block.sync
        def _(sp):
            sp.dma_start(b2[:, :, :], d["tree_b2"]).then_inc(loaded, 16)

        @block.tensor
        def _(pe):
            pe.wait_ge(loaded, 16)
            for k in range(NT // 2 + 1):
                if k < NT // 2:
                    if k >= 2:
                        pe.wait_ge(kept, k - 1)
                    for j in range(4):
                        mm = pe.transpose(ps_t[k % 2][:, j, :], gates[:, 2 * k + j // 2, j % 2 * P:j % 2 * P + P],
                                          ident[:, :])
                    mm.then_inc(turned, 1)
                if k > 0:
                    pe.wait_ge(kept, k)
                    for j in range(2):
                        t = 2 * (k - 1) + j
                        for half in range(2):
                            mm = pe.matmul(ps_y[t // TB][:, t % TB, :], gT[:, (k - 1) % 2, 2 * j + half, :],
                                           b2[:, half, :], start=(half == 0), stop=(half == 1))
                    mm.then_inc(made, 1)

        @block.scalar
        def _(a):
            for k in range(NT // 2):
                a.wait_ge(turned, k + 1)
                if k >= 2:
                    a.wait_ge(made, k - 1)
                a.copy(gT[:, k % 2, :, :], ps_t[k % 2][:, :, :]).then_inc(kept, 1)

        @block.vector
        def _(v):
            for b in range(B):
                v.wait_ge(made, (b + 1) * NT // 4)
                t = slice(b * TB, b * TB + TB)
                v.tensor_tensor(h[:, t, :], h[:, t, :], ps_y[b][:, :, :], ALU.add)


def tree_outputs(nc, m, own):
    h, gates, x_parts, w_parts = m["h"], own["gates"], own["x"], own["w"]
    WIDE = NODES_PER_BANK * D
    PER = NODE_CHUNKS
    VECTOR = [c for c in range(PER) if c % 4 == 3 or c >= PER - 4]
    POOL = [c for c in range(PER) if c not in VECTOR]
    OWN = len(VECTOR) - 1
    with Stage(nc, "treeo") as s:
        x_now = s.sb("x_now", [P, 2, 2, P], BF16)
        prod = s.sb("prod", [P, POOL_RING, WIDE])
        mine = s.sb("mine", [P, 2, WIDE])
        acc = s.sb("acc", [P, WIDE])
        acc_v = s.sb("acc_v", [P, WIDE])
        out = s.sb("out", [P, D])
        ps = [s.ps(f"ps{k}", [P, 512]) for k in range(BANKS)]
        names = ["x_kept", "bank_made", "weighed", "added", "mine_added", "fold_step"]
        x_kept, bank_made, weighed, added, mine_added, fold_step = [s.sem(n) for n in names]
        block = s.block()

        @block.tensor
        def _(pe):
            with pe.Fori(0, NT // 2) as i:
                for par in range(2):
                    pe.wait_ge(x_kept, i * 2 + (par + 1))
                    for c in range(PER):
                        pe.wait_ge(weighed, i * (2 * PER) + (par * PER + c + 1))
                        for k in range(3):
                            mm = pe.matmul(ps[c % BANKS][:, :], x_now[:, par, k // 2, :],
                                           w_parts[:, k, c * WIDE:(c + 1) * WIDE], start=(k == 0), stop=(k == 2))
                        mm.then_inc(bank_made, 1)

        @block.scalar
        def _(a):
            a.copy(x_now[:, 0, :, :], x_parts[:, :, 0:P]).then_inc(x_kept, 1)
            a.copy(x_now[:, 1, :, :], x_parts[:, :, P:2 * P]).then_inc(x_kept, 1)
            with a.Fori(0, NT // 2 - 1) as i:
                for par in range(2):
                    a.wait_ge(weighed, i * (2 * PER) + (BANKS + (par + 1) * PER))
                    a.copy(x_now[:, par, :, :], x_parts[:, :, bass.ds(i * (2 * P) + (par + 2) * P, P)]).then_inc(x_kept, 1)

        @block.vector
        def _(v):
            def nodes(ap):
                return ap.rearrange("p (n o) -> p n o", o=D)

            v.engine_nop().then_inc(weighed, BANKS)
            with v.Fori(0, NT // 2) as i:
                for par in range(2):
                    def add_own(n):
                        v.wait_ge(weighed, i * (2 * PER) + (BANKS + par * PER + VECTOR[n] + 1))
                        if n > 1:
                            v.wait_ge(mine_added, i * (2 * OWN) + (par * OWN + n - 1))
                        v.tensor_tensor(acc_v[:, :], acc_v[:, :], mine[:, n % 2, :], ALU.add).then_inc(mine_added, 1)

                    for c in range(PER):
                        gate = gates[:, bass.ds(i * 2 + par, 1), c * NODES_PER_BANK:(c + 1) * NODES_PER_BANK]
                        gate = gate.rearrange("p t n -> p (t n)").unsqueeze(2).broadcast_to([P, NODES_PER_BANK, D])
                        v.wait_ge(bank_made, i * (2 * PER) + (par * PER + c + 1))
                        if c in VECTOR:
                            n = VECTOR.index(c)
                            if n > 2:
                                v.wait_ge(mine_added, i * (2 * OWN) + (par * OWN + n - 2))
                            dst = acc_v[:, :] if n == 0 else mine[:, n % 2, :]
                        else:
                            q = par * len(POOL) + POOL.index(c)
                            v.wait_ge(added, i * (2 * len(POOL)) + (q + 1))
                            dst = prod[:, q % POOL_RING, :]
                        v.tensor_tensor(nodes(dst), nodes(ps[c % BANKS][:, :]), gate, ALU.mult).then_inc(weighed, 1)
                        own_before = [n for n in range(1, OWN + 1) if VECTOR[n] < c]
                        if own_before and (VECTOR[own_before[-1]] == c - 1):
                            add_own(own_before[-1])
                    add_own(OWN)
                    v.wait_ge(added, (i * 2 + (par + 1)) * len(POOL) + POOL_RING)
                    v.wait_ge(mine_added, (i * 2 + (par + 1)) * OWN)
                    v.tensor_tensor(acc_v[:, :], acc_v[:, :], acc[:, :], ALU.add).then_inc(fold_step, 1)
                    v.wait_ge(fold_step, i * 6 + (par * 3 + 1))
                    v.tensor_reduce(out[:, :], acc_v[:, :].rearrange("p (n o) -> p o n", o=D), AX.X,
                                    ALU.add).then_inc(fold_step, 1)
                    v.wait_ge(fold_step, i * 6 + (par * 3 + 2))
                    now = h[:, bass.ds(i * 2 + par, 1), :].rearrange("p t c -> p (t c)")
                    v.tensor_tensor(now, now, out[:, :], ALU.add).then_inc(fold_step, 1)
                    v.wait_ge(fold_step, i * 6 + (par * 3 + 3))

        @block.gpsimd
        def _(g):
            g.engine_nop().then_inc(added, POOL_RING)
            with g.Fori(0, NT // 2) as i:
                for par in range(2):
                    for n in range(1, len(POOL)):
                        q = par * len(POOL) + n
                        g.wait_ge(weighed, i * (2 * PER) + (BANKS + par * PER + POOL[n] + 1))
                        if n == 1:
                            g.tensor_tensor(acc[:, :], prod[:, (q - 1) % POOL_RING, :], prod[:, q % POOL_RING, :],
                                            ALU.add).then_inc(added, 2)
                        else:
                            g.wait_ge(added, i * (2 * len(POOL)) + (POOL_RING + q))
                            g.tensor_tensor(acc[:, :], acc[:, :], prod[:, q % POOL_RING, :],
                                            ALU.add).then_inc(added, 1)


GROUPS = 4


def run_experts(nc, m, d, name, per_group, gates, add_x):
    h, xn, xT = m["h"], m["xn"], m["xT"]
    E = GROUPS * per_group
    HID = P // per_group
    with Stage(nc, name) as s:
        w1 = s.sb("w1", [D + 1, GROUPS, P])
        w2 = s.sb("w2", [P, GROUPS, D])
        b2 = s.sb("b2", [P, E, D])
        hid = s.sb("hid", [P, 2, GROUPS, 512])
        y = s.sb("y", [P, 2, E, D])
        yg = s.sb("yg", [P, 2, E, D])
        total = s.sb("total", [P, 2, D])
        ps_h = [s.ps(f"ps_h{k}", [P, 512]) for k in range(4)]
        ps_y = [[s.ps(f"ps_y{k}_{r}", [P, 512]) for r in range(per_group)] for k in range(2)]
        loaded = s.sem("loaded")
        hid_made = s.sem("hid_made")
        hid_kept = s.sem("hid_kept")
        y_made = s.sem("y_made")
        y_kept = s.sem("y_kept")
        dve = s.sem("dve_step")
        block = s.block()

        @block.sync
        def _(sp):
            sp.dma_start(w1[:, :, :], d[f"{name}_w1"]).then_inc(loaded, 16)
            sp.dma_start(w2[:, :, :], d[f"{name}_w2"]).then_inc(loaded, 16)
            sp.dma_start(b2[:, :, :], d[f"{name}_b2"].broadcast_to([P, E, D])).then_inc(loaded, 16)

        @block.tensor
        def _(pe):
            pe.wait_ge(loaded, 3 * 16)

            def hidden(k):
                for g in range(GROUPS):
                    if k >= 1:
                        pe.wait_ge(hid_kept, (k - 1) * GROUPS + g + 1)
                    pe.matmul(ps_h[g][:, :], w1[:, g, :], xT[:, k * 512:k * 512 + 512],
                              start=True, stop=True).then_inc(hid_made, 1)

            hidden(0)
            for k in range(4):
                if k < 3:
                    hidden(k + 1)
                pe.wait_ge(hid_kept, (k + 1) * GROUPS)
                for j in range(4):
                    t = 4 * k + j
                    if t >= 2:
                        pe.wait_ge(y_kept, t - 1)
                    for e in range(E):
                        g, r = e // per_group, (e % per_group) * HID
                        mm = pe.matmul(ps_y[t % 2][e % per_group][:, g * D:g * D + D],
                                       hid[r:r + HID, k % 2, g, j * P:j * P + P], w2[r:r + HID, g, :],
                                       start=True, stop=True)
                    mm.then_inc(y_made, 1)

        @block.scalar
        def _(a):
            for k in range(4):
                for g in range(GROUPS):
                    a.wait_ge(hid_made, k * GROUPS + g + 1)
                    if k >= 2:
                        a.wait_ge(y_made, 4 * (k - 1))
                    a.activation(hid[:, k % 2, g, :], ps_h[g][:, :], ACT.Gelu).then_inc(hid_kept, 1)

        @block.vector
        def _(v):
            step = Chain(v, dve)
            v.wait_ge(loaded, 3 * 16)
            for t in range(NT):
                r = t % 2
                v.wait_ge(y_made, t + 1)
                for q in range(per_group):
                    mine = y[:, r, :, :].rearrange("p (g q) o -> p g q o", q=per_group)[:, :, q, :]
                    add = v.tensor_tensor(mine, ps_y[r][q][:, 0:GROUPS * D].rearrange("p (g o) -> p g o", g=GROUPS),
                                          b2[:, :, :].rearrange("p (g q) o -> p g q o", q=per_group)[:, :, q, :],
                                          ALU.add)
                add.then_inc(y_kept, 1)
                v.wait_ge(y_kept, t + 1)
                step(v.tensor_tensor(yg[:, r, :, :], y[:, r, :, :], bc(gates[:, t, :].unsqueeze(2), [P, E, D]),
                                     ALU.mult))
                step(v.tensor_reduce(total[:, r, :], yg[:, r, :, :].rearrange("p e o -> p o e"), AX.X, ALU.add))
                step(v.tensor_tensor(h[:, t, :], h[:, t, :], total[:, r, :], ALU.add))
            if add_x:
                v.tensor_tensor(h[:, :, :], h[:, :, :], xn[:, :, :], ALU.add)


def experts_eight(nc, m, d):
    xT = m["xT"]
    E = 8
    with Stage(nc, "route8") as outer:
        gates = outer.sb("gates", [P, NT, E])
        with Stage(nc, "route") as s:
            w = s.sb("w", [D, E])
            order = s.sb("order", [P, E])
            probs = s.sb("probs", [P, NT, E])
            best = [s.sb(f"best{k}", [P, NT]) for k in range(2)]
            picks = [s.sb(f"pick{k}", [P, NT, E]) for k in range(2)]
            rest = s.sb("rest", [P, NT, E])
            eq = s.sb("eq", [P, NT, E])
            one = s.sb("one", [P, NT])
            ps = s.ps("ps", [P, NT, E])
            loaded = s.sem("loaded")
            made = s.sem("made")
            dve = s.sem("dve_step")
            centred = s.sem("centred")
            exps = s.sem("exps")
            block = s.block()

            @block.sync
            def _(sp):
                sp.dma_start(w[:, :], d["route8_w"]).then_inc(loaded, 16)
                sp.dma_start(order[:, :], d["order8"].broadcast_to([P, E])).then_inc(loaded, 16)

            @block.tensor
            def _(pe):
                pe.wait_ge(loaded, 32)
                for t in range(NT):
                    mm = pe.matmul(ps[:, t, :], xT[0:D, t * P:t * P + P], w[:, :], start=True, stop=True)
                mm.then_inc(made, 1)

            @block.scalar
            def _(a):
                a.wait_ge(centred, 1)
                a.activation(probs[:, :, :], probs[:, :, :], ACT.Exp).then_inc(exps, 1)

            @block.vector
            def _(v):
                step = Chain(v, dve)
                v.wait_ge(loaded, 32)
                v.wait_ge(made, 1)
                wide = [P, NT, E]
                step(v.tensor_reduce(one[:, :], ps[:, :, :], AX.X, ALU.max))
                v.tensor_tensor(probs[:, :, :], ps[:, :, :], bc(one[:, :].unsqueeze(2), wide),
                                ALU.subtract).then_inc(centred, 1)
                v.wait_ge(exps, 1)
                step(v.tensor_reduce(one[:, :], probs[:, :, :], AX.X, ALU.add))
                step(v.reciprocal(one[:, :], one[:, :]))
                step(v.tensor_tensor(probs[:, :, :], probs[:, :, :], bc(one[:, :].unsqueeze(2), wide), ALU.mult))
                two_best(v, step, probs, best, rest, eq, picks, order, E)
                step(v.tensor_tensor(one[:, :], best[0][:, :], best[1][:, :], ALU.add))
                step(v.tensor_scalar(one[:, :], one[:, :], 1e-12, None, ALU.max))
                step(v.reciprocal(one[:, :], one[:, :]))
                step(v.tensor_tensor(gates[:, :, :], picks[0][:, :, :], picks[1][:, :, :], ALU.add))
                step(v.tensor_tensor(gates[:, :, :], gates[:, :, :], probs[:, :, :], ALU.mult))
                step(v.tensor_tensor(gates[:, :, :], gates[:, :, :], bc(one[:, :].unsqueeze(2), wide), ALU.mult))
        run_experts(nc, m, d, "moe8", 2, gates, True)


def two_best(v, step, values, best, rest, eq, picks, order, n):
    wide = [P, NT, n]
    row = bc(order[:, 0:n].unsqueeze(1), wide)
    left = values
    for k in range(2):
        step(v.tensor_reduce(best[k][:, :], left[:, :, :], AX.X, ALU.max))
        step(v.tensor_tensor(eq[:, :, :], left[:, :, :], bc(best[k][:, :].unsqueeze(2), wide), ALU.is_equal))
        step(v.tensor_tensor(eq[:, :, :], eq[:, :, :], row, ALU.mult))
        step(v.tensor_reduce(rest[:, :, 0], eq[:, :, :], AX.X, ALU.max))
        step(v.tensor_tensor(picks[k][:, :, :], row, bc(rest[:, :, 0:1], wide), ALU.is_equal))
        if k == 0:
            left = picks[1]
            step(v.scalar_tensor_tensor(left[:, :, :], picks[0][:, :, :], -1e30, values[:, :, :],
                                        ALU.mult, ALU.add))


HAAR_LEVELS = 3
HAAR = 2 ** HAAR_LEVELS - 1
INV_ROUNDS = 38
NEG = -1e30


def pseudo_inverse(nc, m, d):
    inv_wT = m["inv_wT"]
    with Stage(nc, "pinv") as s:
        w = s.sb("w", [D, D])
        wT = s.sb("wT", [D, P])
        square = s.sb("square", [D, D])
        norm = s.sb("norm", [D, 2])
        ones = s.sb("ones", [D, D])
        two = s.sb("two", [D, D])
        x = s.sb("x", [D, D])
        xT = s.sb("xT", [D, P])
        r = s.sb("r", [D, P])
        ps_n = s.ps("ps_n", [P, 512])
        ps_r = s.ps("ps_r", [P, 512])
        ps_x = s.ps("ps_x", [P, 512])
        ps_y = s.ps("ps_y", [P, 512])
        loaded = s.sem("loaded")
        dve = s.sem("dve_step")
        norm_ready = s.sem("norm_ready")
        norm_made = s.sem("norm_made")
        x_ready = s.sem("x_ready")
        xT_ready = s.sem("xT_ready")
        r_made = s.sem("r_made")
        r_ready = s.sem("r_ready")
        x_made = s.sem("x_made")
        block = s.block()

        @block.sync
        def _(sp):
            sp.dma_start(w[:, :], d["near_w_q"]).then_inc(loaded, 16)
            sp.dma_start(wT[:, 0:D], d["near_w_qT"]).then_inc(loaded, 16)
            sp.dma_start(two[:, :], d["two_ident"]).then_inc(loaded, 16)

        @block.vector
        def _(v):
            step = Chain(v, dve)
            v.wait_ge(loaded, 3 * 16)
            step(v.memset(ones[:, :], 1.0))
            for wide in (wT, xT, r):
                step(v.memset(wide[:, D:P], 0.0))
            step(v.tensor_tensor(square[:, :], w[:, :], w[:, :], ALU.mult))
            v.tensor_reduce(norm[:, 0:1], square[:, :], AX.X, ALU.add).then_inc(norm_ready, 1)
            v.wait_ge(norm_made, 1)
            step(v.reciprocal(norm[:, 1:2], ps_n[0:D, 0:1]))
            v.tensor_scalar(x[:, :], wT[:, 0:D], norm[:, 1:2], None, ALU.mult).then_inc(x_ready, 1)
            v.tensor_scalar(xT[:, 0:D], w[:, :], norm[:, 1:2], None, ALU.mult).then_inc(xT_ready, 1)
            with v.Fori(0, INV_ROUNDS) as i:
                v.wait_ge(r_made, i + 1)
                v.tensor_tensor(r[:, 0:D], two[:, :], ps_r[0:D, 0:D], ALU.subtract).then_inc(r_ready, 1)
                v.wait_ge(x_made, i * 2 + 2)
                v.tensor_copy(x[:, :], ps_x[0:D, 0:D]).then_inc(x_ready, 1)
                v.tensor_copy(xT[:, 0:D], ps_y[0:D, 0:D]).then_inc(xT_ready, 1)
            v.wait_ge(xT_ready, INV_ROUNDS + 1)
            v.tensor_copy(inv_wT[:, :], xT[:, 0:D])

        @block.tensor
        def _(pe):
            pe.wait_ge(norm_ready, 1)
            pe.matmul(ps_n[0:D, 0:1], ones[:, :], norm[:, 0:1], start=True, stop=True).then_inc(norm_made, 1)
            with pe.Fori(0, INV_ROUNDS) as i:
                pe.wait_ge(x_ready, i + 1)
                pe.matmul(ps_r[:, 0:D], wT[:, :], x[:, :], start=True, stop=True).then_inc(r_made, 1)
                pe.wait_ge(xT_ready, i + 1)
                pe.wait_ge(r_ready, i + 1)
                pe.matmul(ps_x[:, 0:D], xT[:, :], r[:, 0:D], start=True, stop=True).then_inc(x_made, 1)
                pe.matmul(ps_y[:, 0:D], r[:, :], xT[:, 0:D], start=True, stop=True).then_inc(x_made, 1)


def wavelet_attention(nc, m, d):
    h, xT, ident, inv_wT = m["h"], m["xT"], m["ident"], m["inv_wT"]
    HALF = D // 2
    with Stage(nc, "wav") as s:
        w = s.sb("w", [D, 3 * D])
        w_v = s.sb("w_v", [D, D])
        w_oT = s.sb("w_oT", [D, D])
        cos = s.sb("cos", [P, TB, 2, HALF])
        sin = s.sb("sin", [P, TB, 2, HALF])
        haar = s.sb("haar", [P, TB, HAAR])
        haar_blockT = s.sb("haar_blockT", [HAAR, TB])
        count = s.sb("count", [P, TB, TB])
        hide = s.sb("hide", [P, TB, TB])
        before = s.sb("before", [P, TB, TB])
        seen = s.sb("seen", [P, TB, 2])
        earlier = s.sb("earlier", [P, P])
        one_block = s.sb("one_block", [P, TB, TB])
        qkv = s.sb("qkv", [P, NT, 3 * D])
        rot = s.sb("rot", [P, NT, 2 * D])
        tmp = s.sb("tmp", [P, TB, 2, HALF])
        tmp2 = s.sb("tmp2", [P, TB, 2, HALF])
        square = s.sb("square", [P, NT, 2 * D])
        norm = s.sb("norm", [P, NT, 2])
        inv_norm = s.sb("inv_norm", [P, NT, 2])
        coef = s.sb("coef", [HAAR, B, 2 * D])
        qf = s.sb("qf", [D, B, TB])
        kf = s.sb("kf", [D, B, TB])
        qf_wide = s.sb("qf_wide", [D, B, TB, P])
        blocksum = s.sb("blocksum", [TB, B, D])
        z = s.sb("z", [P, NT, TB])
        e = s.sb("e", [P, NT, TB])
        zsq = s.sb("zsq", [P, NT, TB])
        own = s.sb("own", [P, NT])
        e_own = s.sb("e_own", [P, NT])
        stat = s.sb("stat", [P, NT])
        aux = s.sb("aux", [P, NT])
        var = s.sb("var", [P, NT])
        std = s.sb("std", [P, NT])
        den = s.sb("den", [P, NT])
        eT = s.sb("eT", [TB, NT, P])
        y = s.sb("y", [P, NT, D])
        y2 = s.sb("y2", [P, NT, D])
        ps = [s.ps(f"ps{k}", [P, 512]) for k in range(8)]
        names = ["loaded", "fold_made", "w_ready", "qkv_made", "qkv_kept", "norm_sq", "norm_root", "rot_ready",
                 "coef_made", "coef_kept", "f_made", "f_kept", "score_made", "var_ready", "std_ready", "z_ready",
                 "e_ready", "far_ready", "eT_made", "eT_kept", "sum_kept", "pre_made", "far_made", "blocksum_kept"]
        (loaded, fold_made, w_ready, qkv_made, qkv_kept, norm_sq, norm_root, rot_ready, coef_made, coef_kept,
         f_made, f_kept, score_made, var_ready, std_ready, z_ready, e_ready, far_ready, eT_made, eT_kept,
         sum_kept, pre_made, far_made, blocksum_kept) = [s.sem(n) for n in names]
        dve = s.sem("dve_step")
        block = s.block()
        LOADS = 12 * 16

        @block.sync
        def _(sp):
            sp.dma_start(w[:, 0:D], d["near_w_q"]).then_inc(loaded, 16)
            sp.dma_start(w_v[:, :], d["near_w_v"]).then_inc(loaded, 16)
            sp.dma_start(w_oT[:, :], d["near_w_oT"]).then_inc(loaded, 16)
            sp.dma_start(cos[:, :, :, :], d["wav_cos"].rearrange("(t p) a c -> p t a c", p=P)).then_inc(loaded, 16)
            sp.dma_start(sin[:, :, :, :], d["wav_sin"].rearrange("(t p) a c -> p t a c", p=P)).then_inc(loaded, 16)
            sp.dma_start(haar[:, :, :], d["wav_haar"].rearrange("(t p) w -> p t w", p=P)).then_inc(loaded, 16)
            sp.dma_start(haar_blockT[:, :], d["wav_haar_blockT"]).then_inc(loaded, 16)
            sp.dma_start(count[:, :, :], d["wav_count"]).then_inc(loaded, 16)
            sp.dma_start(hide[:, :, :], d["wav_hide"]).then_inc(loaded, 16)
            sp.dma_start(seen[:, :, :], d["wav_seen"]).then_inc(loaded, 16)
            sp.dma_start(earlier[:, :], d["wav_earlier"]).then_inc(loaded, 16)
            sp.dma_start(before[:, :, :], d["wav_before"]).then_inc(loaded, 16)

        @block.gpsimd
        def _(g):
            g.memset(one_block[:, :, :], 0.0).then_inc(sum_kept, 1)
            g.wait_ge(sum_kept, 1)
            for j in range(TB):
                last = g.memset(one_block[:, j, j:j + 1], 1.0)
            last.then_inc(sum_kept, 1)

        @block.tensor
        def _(pe):
            pe.wait_ge(loaded, LOADS)
            pe.matmul(ps[0][0:D, 0:D], w_v[:, :], w_oT[:, :], start=True, stop=True).then_inc(fold_made, 1)
            pe.wait_ge(w_ready, 2)
            for t in range(NT):
                last = pe.matmul(ps[t // 2][:, (t % 2) * 192:(t % 2) * 192 + 192], xT[0:D, t * P:t * P + P],
                                 w[:, :], start=True, stop=True)
                if t % 2 == 1:
                    last.then_inc(qkv_made, 1)
            pe.wait_ge(qkv_kept, NT // 2)
            pe.wait_ge(sum_kept, 2)
            for b in range(B):
                for j in range(TB):
                    t = b * TB + j
                    last = pe.matmul(ps[4 + b][:, j * D:j * D + D], earlier[:, :], qkv[:, t, 2 * D:3 * D],
                                     start=True, stop=True)
            last.then_inc(pre_made, 1)
            for b in range(B):
                for j in range(TB):
                    t = b * TB + j
                    last = pe.matmul(ps[6][0:TB, b * D:b * D + D], one_block[:, j, :], qkv[:, t, 2 * D:3 * D],
                                     start=(j == 0), stop=(j == TB - 1))
            last.then_inc(pre_made, 1)
            pe.wait_ge(rot_ready, 1)
            for b in range(B):
                for j in range(TB):
                    t = b * TB + j
                    last = pe.matmul(ps[b][0:HAAR, 0:2 * D], haar[:, j, :], rot[:, t, :],
                                     start=(j == 0), stop=(j == TB - 1))
            last.then_inc(coef_made, 1)
            pe.wait_ge(coef_kept, 1)
            for b in range(B):
                for qk in range(2):
                    last = pe.matmul(ps[2][0:D, (2 * b + qk) * TB:(2 * b + qk + 1) * TB],
                                     coef[:, b, qk * D:qk * D + D], haar_blockT[:, :], start=True, stop=True)
            last.then_inc(f_made, 1)
            pe.wait_ge(f_kept, 1)
            for b in range(B):
                for i in range(TB):
                    t = b * TB + i
                    last = pe.matmul(ps[3][:, t * TB:t * TB + TB], qf_wide[:, b, i, :], kf[:, b, :],
                                     start=True, stop=True)
            last.then_inc(score_made, 1)
            pe.wait_ge(far_ready, 1)
            for k in range(4):
                for j in range(4):
                    t = 4 * k + j
                    last = pe.transpose(ps[k][0:TB, j * P:j * P + P], z[:, t, :], ident[:, :])
                last.then_inc(eT_made, 1)
            pe.wait_ge(eT_kept, 4)
            pe.wait_ge(blocksum_kept, 1)
            for b in range(B):
                for j in range(TB):
                    t = b * TB + j
                    last = pe.matmul(ps[b][:, j * D:j * D + D], eT[:, t, :], blocksum[:, b, :],
                                     start=True, stop=True)
            last.then_inc(far_made, 1)

        @block.scalar
        def _(a):
            for k in range(NT // 2):
                a.wait_ge(qkv_made, k + 1)
                a.copy(qkv[:, 2 * k:2 * k + 2, :],
                       ps[k][:, 0:384].rearrange("p (t c) -> p t c", t=2)).then_inc(qkv_kept, 1)
            a.wait_ge(norm_sq, 1)
            a.activation(norm[:, :, :], norm[:, :, :], ACT.Sqrt).then_inc(norm_root, 1)
            a.wait_ge(var_ready, 1)
            a.activation(std[:, :], var[:, :], ACT.Sqrt).then_inc(std_ready, 1)
            a.wait_ge(z_ready, 1)
            a.activation(e[:, :, :], z[:, :, :], ACT.Exp).then_inc(e_ready, 1)
            a.activation(e_own[:, :], own[:, :], ACT.Exp).then_inc(e_ready, 1)
            for k in range(4):
                a.wait_ge(eT_made, k + 1)
                a.copy(eT[:, 4 * k:4 * k + 4, :],
                       ps[k][0:TB, :].rearrange("p (t c) -> p t c", t=4)).then_inc(eT_kept, 1)

        @block.vector
        def _(v):
            step = Chain(v, dve)
            v.wait_ge(fold_made, 1)
            v.tensor_copy(w[:, 2 * D:3 * D], ps[0][0:D, 0:D]).then_inc(w_ready, 1)
            v.tensor_copy(w[:, D:2 * D], inv_wT[:, :]).then_inc(w_ready, 1)
            for b in range(B):
                v.wait_ge(qkv_kept, TB // 2 * (b + 1))
                t = slice(b * TB, b * TB + TB)
                x = qkv[:, t, 0:2 * D].rearrange("p t (a e c) -> p t a e c", a=2, e=2)
                r = rot[:, t, :].rearrange("p t (a e c) -> p t a e c", a=2, e=2)
                x1, x2, r1, r2 = x[:, :, :, 0, :], x[:, :, :, 1, :], r[:, :, :, 0, :], r[:, :, :, 1, :]
                c4, s4, u, w4 = cos[:, :, :, :], sin[:, :, :, :], tmp[:, :, :, :], tmp2[:, :, :, :]
                step(v.tensor_tensor(r1, x1, c4, ALU.mult))
                step(v.tensor_tensor(u, x2, s4, ALU.mult))
                step(v.tensor_tensor(r1, r1, u, ALU.subtract))
                step(v.tensor_tensor(w4, x1, s4, ALU.mult))
                step(v.tensor_tensor(r2, x2, c4, ALU.mult))
                step(v.tensor_tensor(r2, r2, w4, ALU.add))
            step(v.tensor_tensor(square[:, :, :], rot[:, :, :], rot[:, :, :], ALU.mult))
            v.tensor_reduce(norm[:, :, :], square[:, :, :].rearrange("p t (a c) -> p t a c", a=2), AX.X,
                            ALU.add).then_inc(norm_sq, 1)
            v.wait_ge(norm_root, 1)
            step(v.tensor_scalar(norm[:, :, :], norm[:, :, :], 1e-8, None, ALU.add))
            step(v.reciprocal(inv_norm[:, :, :], norm[:, :, :]))
            v.tensor_tensor(rot[:, :, :].rearrange("p t (a c) -> p t a c", a=2),
                            rot[:, :, :].rearrange("p t (a c) -> p t a c", a=2),
                            bc(inv_norm[:, :, :].unsqueeze(3), [P, NT, 2, D]), ALU.mult).then_inc(rot_ready, 1)
            v.wait_ge(rot_ready, 1)
            step(v.tensor_tensor(square[:, :, 0:D], rot[:, :, 0:D], rot[:, :, D:2 * D], ALU.mult))
            step(v.tensor_reduce(own[:, :], square[:, :, 0:D], AX.X, ALU.add))
            v.wait_ge(coef_made, 1)
            for b in range(B):
                last = v.tensor_copy(coef[:, b, :], ps[b][0:HAAR, 0:2 * D])
            last.then_inc(coef_kept, 1)
            v.wait_ge(f_made, 1)
            both = ps[2][0:D, 0:2 * B * TB].rearrange("p (b a i) -> p b a i", b=B, a=2)
            step(v.tensor_copy(qf[:, :, :], both[:, :, 0, :]))
            step(v.tensor_copy(kf[:, :, :], both[:, :, 1, :]))
            v.tensor_copy(qf_wide[:, :, :, :].rearrange("p b i n -> p (b i) n"),
                          bc(qf[:, :, :].rearrange("p b i -> p (b i)").unsqueeze(2),
                             [D, B * TB, P])).then_inc(f_kept, 1)
            v.wait_ge(score_made, 1)

            def per_batch(ap):
                return ap.rearrange("p (b t) j -> p b (t j)", b=B)

            def twice(table):
                return bc(table.rearrange("p t j -> p (t j)").unsqueeze(1), [P, B, TB * TB])

            def rows(ap):
                return ap.rearrange("p (b t) -> p b t", b=B)

            def seen_by(k):
                return bc(seen[:, :, k].unsqueeze(1), [P, B, TB])

            def wide(ap):
                return bc(ap[:, :].unsqueeze(2), [P, NT, TB])

            step(v.tensor_copy(zsq[:, :, :], ps[3][:, 0:NT * TB].rearrange("p (t j) -> p t j", t=NT)))
            step(v.tensor_tensor(rows(own[:, :]), rows(own[:, :]), seen_by(0), ALU.mult))
            for b in range(B):
                t = slice(b * TB, b * TB + TB)
                step(v.tensor_tensor(z[:, t, :], zsq[:, t, :], bc(seen[:, :, 0:1], [P, TB, TB]), ALU.mult))
            step(v.tensor_tensor(per_batch(zsq[:, :, :]), per_batch(z[:, :, :]), twice(count[:, :, :]), ALU.mult))
            step(v.tensor_reduce(stat[:, :], zsq[:, :, :], AX.X, ALU.add))
            step(v.tensor_tensor(stat[:, :], stat[:, :], own[:, :], ALU.add))
            step(v.tensor_tensor(rows(stat[:, :]), rows(stat[:, :]), seen_by(1), ALU.mult))
            step(v.tensor_tensor(z[:, :, :], z[:, :, :], wide(stat), ALU.subtract))
            step(v.tensor_tensor(own[:, :], own[:, :], stat[:, :], ALU.subtract))
            step(v.tensor_tensor(zsq[:, :, :], z[:, :, :], z[:, :, :], ALU.mult))
            step(v.tensor_tensor(per_batch(zsq[:, :, :]), per_batch(zsq[:, :, :]), twice(count[:, :, :]), ALU.mult))
            step(v.tensor_reduce(stat[:, :], zsq[:, :, :], AX.X, ALU.add))
            step(v.tensor_tensor(aux[:, :], own[:, :], own[:, :], ALU.mult))
            step(v.tensor_tensor(stat[:, :], stat[:, :], aux[:, :], ALU.add))
            step(v.tensor_tensor(rows(var[:, :]), rows(stat[:, :]), seen_by(1), ALU.mult))
            v.wait_ge(dve, step.count)
            v.tensor_scalar(var[:, :], var[:, :], 1e-6, None, ALU.max).then_inc(var_ready, 1)
            v.wait_ge(std_ready, 1)
            step(v.reciprocal(stat[:, :], std[:, :]))
            step(v.tensor_tensor(z[:, :, :], z[:, :, :], wide(stat), ALU.mult))
            step(v.tensor_tensor(own[:, :], own[:, :], stat[:, :], ALU.mult))
            step(v.tensor_tensor(per_batch(z[:, :, :]), per_batch(z[:, :, :]), twice(hide[:, :, :]), ALU.add))
            step(v.tensor_reduce(stat[:, :], z[:, :, :], AX.X, ALU.max))
            step(v.tensor_tensor(stat[:, :], stat[:, :], own[:, :], ALU.max))
            step(v.tensor_tensor(own[:, :], own[:, :], stat[:, :], ALU.subtract))
            v.tensor_tensor(z[:, :, :], z[:, :, :], wide(stat), ALU.subtract).then_inc(z_ready, 1)
            v.wait_ge(e_ready, 2)
            step(v.tensor_tensor(per_batch(zsq[:, :, :]), per_batch(e[:, :, :]), twice(count[:, :, :]), ALU.mult))
            step(v.tensor_reduce(den[:, :], zsq[:, :, :], AX.X, ALU.add))
            v.tensor_tensor(per_batch(z[:, :, :]), per_batch(e[:, :, :]), twice(before[:, :, :]),
                            ALU.mult).then_inc(far_ready, 1)
            step(v.tensor_tensor(den[:, :], den[:, :], e_own[:, :], ALU.add))
            step(v.reciprocal(den[:, :], den[:, :]))
            v.wait_ge(pre_made, 2)
            v.tensor_copy(blocksum[:, :, :], ps[6][0:TB, 0:B * D].rearrange("p (b o) -> p b o", b=B)).then_inc(blocksum_kept, 1)
            for b in range(B):
                diag = e[:, b * TB:b * TB + TB, :].rearrange("p t j -> p (t j)")[:, 0:TB * TB:TB + 1]
                t = slice(b * TB, b * TB + TB)
                step(v.tensor_tensor(y[:, t, :], ps[4 + b][:, :].rearrange("p (t o) -> p t o", t=TB),
                                     bc(diag.unsqueeze(2), [P, TB, D]), ALU.mult))
            step(v.tensor_tensor(y2[:, :, :], qkv[:, :, 2 * D:3 * D], bc(e_own[:, :].unsqueeze(2), [P, NT, D]), ALU.mult))
            step(v.tensor_tensor(y[:, :, :], y[:, :, :], y2[:, :, :], ALU.add))
            v.wait_ge(far_made, 1)
            for b in range(B):
                t = slice(b * TB, b * TB + TB)
                step(v.tensor_tensor(y[:, t, :], y[:, t, :], ps[b][:, :].rearrange("p (t o) -> p t o", t=TB), ALU.add))
            step(v.tensor_tensor(y[:, :, :], y[:, :, :], bc(den[:, :].unsqueeze(2), [P, NT, D]), ALU.mult))
            v.tensor_tensor(h[:, :, :], h[:, :, :], y[:, :, :], ALU.add)


def wavelet_tables():
    c = {"two_ident": 2 * np.eye(D, dtype=np.float32)}
    half = D // 2
    inv_freq = (1.0 / 10000.0 ** (np.arange(half, dtype=np.float32) / half)).astype(np.float32)
    ang = np.arange(S, dtype=np.float32)[:, None] * inv_freq[None, :]
    c["wav_cos"] = np.stack([np.cos(ang)] * 2, 1).astype(np.float32)
    c["wav_sin"] = np.stack([np.sin(ang)] * 2, 1).astype(np.float32)
    cols = []
    for level in range(HAAR_LEVELS):
        size = S // 2 ** level
        for k in range(2 ** level):
            v = np.zeros(S, np.float32)
            v[k * size:k * size + size // 2] = 1.0 / np.sqrt(size // 2)
            v[k * size + size // 2:(k + 1) * size] = -1.0 / np.sqrt(size // 2)
            cols.append(v)
    c["wav_haar"] = np.stack(cols, 1)
    c["wav_haar_blockT"] = c["wav_haar"][::P].T
    p, i, j = np.arange(P)[:, None, None], np.arange(TB)[None, :, None], np.arange(TB)[None, None, :]
    count = np.where(j < i, P, np.where(j == i, p, 0))
    c["wav_count"] = count.astype(np.float32)
    c["wav_hide"] = np.where(count > 0, 0.0, NEG).astype(np.float32)
    c["wav_before"] = np.broadcast_to(j < i, (P, TB, TB)).astype(np.float32)
    n = (np.arange(TB)[None, :] * P + np.arange(P)[:, None] + 1).astype(np.float64)
    c["wav_seen"] = np.stack([D ** -0.5 / np.sqrt(n), 1.0 / n], 2).astype(np.float32)
    c["wav_earlier"] = (np.arange(P)[:, None] < np.arange(P)[None, :]).astype(np.float32)
    return c


F16 = mybir.dt.float16
EDGES = 262144
EC = EDGES // P
HG, GE = 4, 4
LO, HI = 32, T // 32
HC = 256
SLOTS = 4
LAST = T - 1
KEY_TILE = P * T


def graph_ffn(nc, m, d):
    with Stage(nc, "graph") as g:
        own = {"key": g.sb("key", [P, EC]), "tid": g.sb("tid", [P, EC]), "hist": g.sb("hist", [P, NT]),
               "rounds": g.sb("rounds", [1, NT + 1], I32), "gates": g.sb("gates", [P, NT, GE]),
               "agg": g.sb("agg", [P, NT, HG, GE + 1])}
        edge_keys(nc, own, d)
        edge_rounds(nc, own, d)
        graph_attention(nc, m, own, d)
        graph_route(nc, own, d)
        run_experts(nc, m, d, "moe4", 1, own["gates"], False)


def edge_keys(nc, own, d):
    key, tid, hist = own["key"], own["tid"], own["hist"]
    with Stage(nc, "keys") as s:
        src = s.sb("src", [P, EC], I32)
        dst = s.sb("dst", [P, EC], I32)
        digit = s.sb("digit", [P, EC], I32)
        srcf = s.sb("srcf", [P, EC])
        dstf = s.sb("dstf", [P, EC])
        near = s.sb("near", [P, EC])
        low = s.sb("low", [P, EC], F16)
        high = s.sb("high", [P, EC], F16)
        hot_lo = s.sb("hot_lo", [P, 2, LO, HC], F16)
        hot_hi = s.sb("hot_hi", [P, 2, HI, HC], F16)
        zero = s.sb("zero", [P, HI], F16)
        ps = s.ps("ps", [LO, 512])
        loaded = s.sem("loaded")
        dve = s.sem("dve_step")
        hot_ready = s.sem("hot_ready")
        hot_used = s.sem("hot_used")
        counted = s.sem("counted")
        zero_set = s.sem("zero_set")
        block = s.block()
        STEPS = EC // HC // 2

        @block.sync
        def _(sp):
            sp.dma_start(src[:, :], d["edges"][0]).then_inc(loaded, 16)
            sp.dma_start(dst[:, :], d["edges"][1]).then_inc(loaded, 16)

        @block.vector
        def _(v):
            step = Chain(v, dve)
            v.memset(zero[:, :], 0.0).then_inc(zero_set, 1)
            v.engine_nop().then_inc(hot_used, 2)
            v.wait_ge(loaded, 32)
            step(v.tensor_copy(srcf[:, :], src[:, :]))
            step(v.tensor_copy(dstf[:, :], dst[:, :]))
            step(v.tensor_scalar(near[:, :], srcf[:, :], float(LAST), None, ALU.is_lt))
            step(v.tensor_scalar(digit[:, :], dst[:, :], LO - 1, None, ALU.bitwise_and))
            step(v.tensor_copy(low[:, :], digit[:, :]))
            step(v.tensor_scalar(digit[:, :], dst[:, :], 5, None, ALU.logical_shift_right))
            step(v.tensor_copy(tid[:, :], digit[:, :]))
            step(v.tensor_scalar(key[:, :], near[:, :], -1024.0, None, ALU.mult))
            step(v.tensor_tensor(high[:, :], tid[:, :], key[:, :], ALU.add))
            step(v.scalar_tensor_tensor(near[:, :], dstf[:, :], float(T), near[:, :], ALU.is_lt, ALU.mult))
            step(v.scalar_tensor_tensor(key[:, :], dstf[:, :], float(T), srcf[:, :], ALU.mult, ALU.add))
            step(v.scalar_tensor_tensor(key[:, :], key[:, :], 1.0, near[:, :], ALU.add, ALU.mult))
            step(v.tensor_scalar(digit[:, :], dst[:, :], 7, None, ALU.logical_shift_right))
            step(v.tensor_copy(tid[:, :], digit[:, :]))
            step(v.scalar_tensor_tensor(tid[:, :], tid[:, :], 1.0, near[:, :], ALU.add, ALU.mult))
            step(v.tensor_scalar(tid[:, :], tid[:, :], -1.0, None, ALU.add))
            with v.Fori(0, STEPS) as i:
                for r in range(2):
                    v.wait_ge(hot_used, i * 2 + (r + 1))
                    cols = bass.ds(i * (2 * HC) + r * HC, HC)
                    for k in range(LO):
                        v.tensor_scalar(hot_lo[:, r, k, :], low[:, cols], float(k), None, ALU.is_equal)
                    for k in range(HI):
                        last = v.tensor_scalar(hot_hi[:, r, k, :], high[:, cols], float(k), None, ALU.is_equal)
                    last.then_inc(hot_ready, 1)
            v.wait_ge(counted, 1)
            for q in range(P // LO):
                v.tensor_copy(hist[q * LO:(q + 1) * LO, :], ps[:, q:HI:P // LO])

        @block.tensor
        def _(pe):
            pe.wait_ge(zero_set, 1)
            pe.matmul(ps[:, 0:HI], zero[:, 0:LO], zero[:, :], start=True, stop=False, skip_group_check=True)
            with pe.Fori(0, STEPS) as i:
                for r in range(2):
                    pe.wait_ge(hot_ready, i * 2 + (r + 1))
                    pe.wait_ge(zero_set, 1)
                    for c in range(HC):
                        mm = pe.matmul(ps[:, 0:HI], hot_lo[:, r, :, c], hot_hi[:, r, :, c],
                                       start=False, stop=False, skip_group_check=True)
                    mm.then_inc(hot_used, 1)
            pe.matmul(ps[:, 0:HI], zero[:, 0:LO], zero[:, :], start=False, stop=True,
                      skip_group_check=True).then_inc(counted, 1)


def edge_rounds(nc, own, d):
    tid, rounds = own["tid"], own["rounds"]
    with Stage(nc, "rounds") as s:
        hit = s.sb("hit", [P, 2, EC])
        count = s.sb("count", [P, NT])
        most = s.sb("most", [P, NT])
        whole = s.sb("whole", [1, NT], I32)
        row = s.sb("row", [1, NT])
        ones = s.sb("ones", [1, NT])
        upto = s.sb("upto", [1, NT + 1])
        dve = s.sem("dve_step")
        counted = s.sem("counted")
        reduced = s.sem("reduced")
        block = s.block()

        @block.vector
        def _(v):
            step = Chain(v, dve)
            for t in range(NT):
                if t >= 2:
                    v.wait_ge(counted, t - 1)
                step(v.tensor_scalar(hit[:, t % 2, :], tid[:, :], float(t), None, ALU.is_equal))
                v.tensor_reduce(count[:, t:t + 1], hit[:, t % 2, :], AX.X, ALU.add).then_inc(counted, 1)
            v.wait_ge(reduced, 1)
            step(v.tensor_scalar(row[:, :], most[0:1, :], 0.125, 3.5 / 8, ALU.mult, ALU.add))
            step(v.tensor_copy(whole[:, :], row[:, :]))
            step(v.tensor_copy(row[:, :], whole[:, :]))
            step(v.tensor_scalar(row[:, :], row[:, :], 1.0, None, ALU.max))
            step(v.memset(ones[:, :], 1.0))
            step(v.memset(upto[:, 0:1], 0.0))
            step(v.tensor_tensor_scan(upto[:, 1:NT + 1], ones[:, :], row[:, :], 0.0, ALU.mult, ALU.add))
            v.tensor_copy(rounds[:, :], upto[:, :])

        @block.gpsimd
        def _(g):
            g.wait_ge(counted, NT)
            g.partition_all_reduce(most[:, :], count[:, :], P, bass.bass_isa.ReduceOp.max).then_inc(reduced, 1)


def graph_attention(nc, m, own, d):
    xT, ident = m["xT"], m["ident"]
    key, tid, hist, rounds, agg = (own[k] for k in ("key", "tid", "hist", "rounds", "agg"))
    with Stage(nc, "gat") as s:
        w = s.sb("w", [D, HG * GE])
        att = s.sb("att", [D, 2, HG * GE])
        w_att = s.sb("w_att", [D, 2, HG])
        prod = s.sb("prod", [D, 2, HG * GE])
        w_src = s.sb("w_src", [D, HG, P])
        feat = s.sb("feat", [P, NT, HG, GE + 1])
        a_dst = s.sb("a_dst", [P, NT, HG])
        a_src = s.sb("a_src", [P, HG, T])
        iota = s.sb("iota", [P, T], F16)
        tiles = s.sb("tiles", [P, NT])
        bases = s.sb("bases", [P, NT])
        loops = s.sb("loops", [P, 2 * T - P], F16)
        identh = s.sb("identh", [P, P], F16)
        work = s.sb("work", [P, EC])
        top = s.sb("top", [P, 8])
        local = s.sb("local", [P, 8])
        place = s.sb("place", [P, 2, 8], I32)
        placef = s.sb("placef", [P, 2, 8])
        hot_d = s.sb("hot_d", [P, SLOTS, P], F16)
        hot_s = s.sb("hot_s", [P, SLOTS, T], F16)
        cnt = s.sb("cnt", [P, 2, T])
        hide = work
        seen = s.sb("seen", [P, HG, T])
        e1 = s.sb("e1", [P, HG, T])
        e2 = s.sb("e2", [P, 2, T])
        turned = s.sb("turned", [P, 2, 4, P])
        mx = s.sb("mx", [P, HG])
        mx2 = s.sb("mx2", [P, HG])
        bias = s.sb("bias", [P, 2, 2, HG])
        spare = s.sb("spare", [P, 30])
        C = [s.ps(f"C{k}", [P, 512]) for k in range(4)]
        ps_t = [s.ps(f"ps_t{k}", [P, 4, P]) for k in range(2)]
        ps_as = [s.ps(f"ps_a{k}", [P, 512]) for k in range(2)]
        ps_a = ps_as[0]
        names = ["loaded", "dve_step", "w_ready", "feat_made", "feat_kept", "src_made", "src_kept", "hots", "hots_used",
                 "near_done", "C_copied", "tile_step", "round_step", "e_ready", "w_max", "weighted",
                 "turns", "turns_kept", "head_done", "agg_kept", "bias_ready"]
        (loaded, dve, w_ready, feat_made, feat_kept, src_made, src_kept, hots, hots_used, near_done, C_copied,
         tile_step, round_step, e_ready, w_max, weighted, turns, turns_kept, head_done, agg_kept,
         bias_ready) = [s.sem(n) for n in names]
        block = s.block()
        LOADS = 7 * 16
        TILE_STEPS, ROUND_STEPS = 10, 6

        @block.sync
        def _(sp):
            sp.dma_start(w[:, :], d["gat_w"]).then_inc(loaded, 16)
            sp.dma_start(att[:, :, :], d["gat_att"].broadcast_to([D, 2, HG * GE])).then_inc(loaded, 16)
            sp.dma_start(iota[:, :], d["iota_nodes"].broadcast_to([P, T])).then_inc(loaded, 16)
            sp.dma_start(tiles[:, :], d["iota_tiles"].broadcast_to([P, NT])).then_inc(loaded, 16)
            sp.dma_start(bases[:, :], d["key_bases"].broadcast_to([P, NT])).then_inc(loaded, 16)
            sp.dma_start(loops[:, :], d["loops"]).then_inc(loaded, 16)
            sp.dma_start(identh[:, :], d["identh"]).then_inc(loaded, 16)

        @block.tensor
        def _(pe):
            pe.wait_ge(loaded, LOADS)
            pe.wait_ge(w_ready, 1)
            for t in range(NT):
                x = xT[0:D, t * P:t * P + P]
                pe.matmul(ps_a[:, t * 20:t * 20 + 16], x, w[:, :], start=True, stop=True)
                mm = pe.matmul(ps_a[:, t * 20 + 16:t * 20 + 20], x, w_att[:, 1, :], start=True, stop=True)
            mm.then_inc(feat_made, 1)
            for hd in range(HG):
                for k in range(4):
                    n = hd * 4 + k
                    if n >= 4:
                        pe.wait_ge(src_kept, n - 3)
                    pe.matmul(C[k][:, :], w_src[:, hd, :], xT[0:D, k * 512:k * 512 + 512],
                              start=True, stop=True).then_inc(src_made, 1)
            pe.wait_ge(src_kept, 16)
            pe.wait_ge(feat_kept, 1)

            def count(t):
                first = pe.value_load(rounds[0:1, bass.ds(t, 1)], min_val=0, max_val=EC * 2)
                end = pe.value_load(rounds[0:1, bass.ds(t + 1, 1)], min_val=1, max_val=EC * 2)
                pe.wait_ge(C_copied, t)
                for k in range(4):
                    pe.matmul(C[k][:, :], identh[:, :], loops[:, bass.ds(t * (-P) + (T - P + k * 512), 512)],
                              start=True, stop=False, skip_group_check=True)
                with pe.Fori(first, end) as r:
                    for e in range(8):
                        pe.wait_ge(hots, r * 8 + (e + 1))
                        for k in range(4):
                            mm = pe.matmul(C[k][:, :], hot_d[:, e % SLOTS, :],
                                           hot_s[:, e % SLOTS, k * 512:k * 512 + 512],
                                           start=False, stop=False, skip_group_check=True)
                        mm.then_inc(hots_used, 1)
                for k in range(4):
                    mm = pe.matmul(C[k][:, 0:1], hot_d[:, 0, :], loops[:, 0:1], start=False, stop=True,
                                   skip_group_check=True)
                mm.then_inc(near_done, 1)

            def sums(t, r):
                def turn(hd, q):
                    pe.wait_ge(turns_kept, t * 16 + (hd * 4 + q + 1))
                    for j in range(4):
                        c = (q * 4 + j) * P
                        mm = pe.transpose(ps_t[q % 2][:, j, :], e1[:, hd, c:c + P], ident[:, :])
                    mm.then_inc(turns, 1)

                for hd in range(HG):
                    pe.wait_ge(weighted, t * HG + (hd + 1))
                    turn(hd, 0)
                    for q in range(4):
                        if q < 3:
                            turn(hd, q + 1)
                        if hd == 0 and q == 0:
                            pe.wait_ge(agg_kept, t + 1)
                        pe.wait_ge(turns_kept, t * 16 + (hd * 4 + q + 3))
                        for j in range(4):
                            u = q * 4 + j
                            mm = pe.matmul(ps_as[r][:, hd * 8:hd * 8 + GE + 1], turned[:, q % 2, j, :],
                                           feat[:, u, hd, :], start=(u == 0), stop=(u == NT - 1))
                    mm.then_inc(head_done, 1)

            count(0)
            with pe.Fori(0, NT // 2 - 1) as i:
                count(i * 2 + 1)
                sums(i * 2, 0)
                count(i * 2 + 2)
                sums(i * 2 + 1, 1)
            count(NT - 1)
            sums(NT - 2, 0)
            sums(NT - 1, 1)

        @block.scalar
        def _(a):
            for n in range(16):
                a.wait_ge(src_made, n + 1)
                a.copy(a_src[:, n // 4, n % 4 * 512:n % 4 * 512 + 512], C[n % 4][:, :]).then_inc(src_kept, 1)


            def exps(t, r, hd):
                a.wait_ge(bias_ready, t + 1)
                if not isinstance(t, int) or t > 0:
                    a.wait_ge(head_done, t * HG + (hd + 1 - HG))
                if not isinstance(t, int) or t * HG + hd >= 2:
                    a.wait_ge(weighted, t * HG + (hd - 1))
                a.activation(e1[:, hd, :], seen[:, hd, :], ACT.Exp, bias=bias[:, r, 0, hd:hd + 1])
                a.activation(e2[:, hd % 2, :], seen[:, hd, :], ACT.Exp, bias=bias[:, r, 1, hd:hd + 1],
                             scale=0.2).then_inc(e_ready, 1)

            def weights(t, r, last=False):
                for hd in range(HG):
                    if hd < 2:
                        exps(t, r, hd + 2)
                    elif not last:
                        exps(t + 1, 1 - r, hd - 2)
                    for q in range(4):
                        a.wait_ge(turns, t * 16 + (hd * 4 + q + 1))
                        a.copy(turned[:, q % 2, :, :], ps_t[q % 2][:, :, :]).then_inc(turns_kept, 1)

            exps(0, 0, 0)
            exps(0, 0, 1)
            weights(0, 0)
            with a.Fori(0, NT // 2 - 1) as i:
                weights(i * 2 + 1, 1)
                weights(i * 2 + 2, 0)
            weights(NT - 1, 1, last=True)

        @block.gpsimd
        def _(g):
            def weigh(t, r):
                for hd in range(HG):
                    g.wait_ge(w_max, t * HG + (hd + 1))
                    g.tensor_tensor(e1[:, hd, :], e2[:, hd % 2, :], cnt[:, r, :], ALU.mult).then_inc(weighted, 1)

            with g.Fori(0, NT // 2) as i:
                weigh(i * 2, 0)
                weigh(i * 2 + 1, 1)

        @block.vector
        def _(v):
            step = Chain(v, dve)

            sites = [0]

            def carry():
                sites[0] += 1
                v.memset(spare[:, sites[0]:sites[0] + 1], 0.0)

            v.wait_ge(loaded, LOADS)
            for k in range(2):
                step(v.tensor_tensor(prod[:, k, :], w[:, :], att[:, k, :], ALU.mult))
            step(v.tensor_reduce(w_att[:, :, :], prod[:, :, :].rearrange("p k (h e) -> p k h e", h=HG), AX.X, ALU.add))
            v.tensor_copy(w_src[:, :, :], bc(w_att[:, 0, :].unsqueeze(2), [D, HG, P])).then_inc(w_ready, 1)
            v.memset(feat[:, :, :, GE:GE + 1], 1.0)
            v.wait_ge(feat_made, 1)
            both = ps_a[:, 0:NT * 20].rearrange("p (t c) -> p t c", t=NT)
            for hd in range(HG):
                v.tensor_copy(feat[:, :, hd, 0:GE], both[:, :, hd * GE:hd * GE + GE])
            v.tensor_copy(a_dst[:, :, :], both[:, :, 16:20]).then_inc(feat_kept, 1)
            v.wait_ge(feat_kept, 1)
            v.wait_ge(src_kept, 16)
            v.engine_nop().then_inc(hots_used, SLOTS)
            v.engine_nop().then_inc(turns_kept, 2)
            v.engine_nop().then_inc(round_step, 1)
            v.engine_nop().then_inc(agg_kept, 2)

            def largest(t, hd):
                v.wait_ge(e_ready, t * HG + (hd + 1))
                v.tensor_tensor(e2[:, hd % 2, :], e1[:, hd, :], e2[:, hd % 2, :], ALU.max).then_inc(w_max, 1)

            def keep(t, r):
                v.wait_ge(head_done, t * HG + HG)
                v.tensor_copy(agg[:, bass.ds(t, 1), :, :].rearrange("p t h c -> p (t h) c"),
                              ps_as[r][:, 0:HG * 8].rearrange("p (h c) -> p h c", h=HG)[:, :, 0:GE + 1]
                              ).then_inc(agg_kept, 1)

            def tile(t, r, before, kept):
                first = v.value_load(rounds[0:1, bass.ds(t, 1)], min_val=0, max_val=EC * 2)
                end = v.value_load(rounds[0:1, bass.ds(t + 1, 1)], min_val=1, max_val=EC * 2)
                count = 0

                def after(ins):
                    nonlocal count
                    count += 1
                    ins.then_inc(tile_step, 1)
                    v.wait_ge(tile_step, t * TILE_STEPS + count)

                after(v.scalar_tensor_tensor(work[:, :], tid[:, :], tiles[:, bass.ds(t, 1)], key[:, :],
                                             ALU.is_equal, ALU.mult))
                if before is not None:
                    largest(before, 0)
                carry()
                with v.Fori(first, end) as n:
                    steps = 0

                    def then(ins):
                        nonlocal steps
                        steps += 1
                        ins.then_inc(round_step, 1)
                        v.wait_ge(round_step, n * ROUND_STEPS + (steps + 1))

                    v.wait_ge(round_step, n * ROUND_STEPS + 1)
                    carry()
                    then(v.max(top[:, :], work[:, :]))
                    carry()
                    then(v.match_replace(work[:, :], top[:, :], work[:, :], 0.0))
                    then(v.tensor_scalar(local[:, :], top[:, :], bases[:, bass.ds(t, 1)], None, ALU.subtract))
                    then(v.tensor_copy(place[:, 0, :], local[:, :]))
                    v.tensor_scalar(place[:, 1, :], place[:, 0, :], T - 1, None, ALU.bitwise_and)
                    then(v.tensor_scalar(place[:, 0, :], place[:, 0, :], 11, None, ALU.arith_shift_right))
                    then(v.tensor_copy(placef[:, :, :], place[:, :, :]))
                    for e in range(8):
                        v.wait_ge(hots_used, n * 8 + (e + 1))
                        v.tensor_scalar(hot_d[:, e % SLOTS, :], iota[:, 0:P], placef[:, 0, e:e + 1], None, ALU.is_equal)
                        v.tensor_scalar(hot_s[:, e % SLOTS, :], iota[:, :], placef[:, 1, e:e + 1], None,
                                        ALU.is_equal).then_inc(hots, 1)
                if kept is not None:
                    keep(kept, r)
                if before is not None:
                    largest(before, 1)
                    v.wait_ge(weighted, t * HG - HG)
                v.wait_ge(near_done, t + 1)
                for k in range(4):
                    last = v.tensor_copy(cnt[:, r, k * 512:k * 512 + 512], C[k][:, :])
                last.then_inc(C_copied, 1)
                v.wait_ge(C_copied, t + 1)
                after(v.tensor_scalar(cnt[:, r, LAST:T], cnt[:, r, LAST:T], hist[:, bass.ds(t, 1)], None, ALU.add))
                after(v.tensor_scalar(hide[:, :], cnt[:, r, :], 0.0, NEG, ALU.is_equal, ALU.mult))
                if before is not None:
                    largest(before, 2)
                for hd in range(HG):
                    if before is not None and hd == 3:
                        largest(before, 3)
                    carry()
                    after(v.tensor_tensor_reduce(out=seen[:, hd, :], in0=a_src[:, hd, :], in1=hide[:, :],
                                                 scale=1.0, scalar=NEG, op0=ALU.add, op1=ALU.max,
                                                 accum_out=mx[:, hd:hd + 1]))
                dst = a_dst[:, bass.ds(t, 1), :].rearrange("p t h -> p (t h)")
                after(v.tensor_tensor(mx[:, :], mx[:, :], dst, ALU.add))
                after(v.scalar_tensor_tensor(mx2[:, :], mx[:, :], 0.2, mx[:, :], ALU.mult, ALU.max))
                after(v.tensor_tensor(bias[:, r, 0, :], dst, mx2[:, :], ALU.subtract))
                v.scalar_tensor_tensor(bias[:, r, 1, :], dst, 0.2, mx2[:, :], ALU.mult, ALU.subtract
                                       ).then_inc(bias_ready, 1)
                assert count == TILE_STEPS

            tile(0, 0, None, None)
            tile(1, 1, 0, None)
            with v.Fori(0, NT // 2 - 1) as i:
                tile(i * 2 + 2, 0, i * 2 + 1, i * 2)
                tile(i * 2 + 3, 1, i * 2 + 2, i * 2 + 1)
            keep(NT - 2, 0)
            for hd in range(HG):
                largest(NT - 1, hd)
            keep(NT - 1, 1)


def graph_route(nc, own, d):
    agg, gates = own["agg"], own["gates"]
    F = HG * GE
    with Stage(nc, "route4") as s:
        par = s.sb("par", [P, 3, F])
        order = s.sb("order", [P, 8])
        x = s.sb("x", [P, NT, HG, GE])
        sq = s.sb("sq", [P, NT, HG, GE])
        rden = s.sb("rden", [P, NT, HG])
        mean = s.sb("mean", [P, NT])
        std = s.sb("std", [P, NT])
        scores = s.sb("scores", [P, NT, GE])
        best = [s.sb(f"best{k}", [P, NT]) for k in range(2)]
        picks = [s.sb(f"pick{k}", [P, NT, GE]) for k in range(2)]
        rest = s.sb("rest", [P, NT, GE])
        eq = s.sb("eq", [P, NT, GE])
        second = s.sb("second", [P, NT])
        loaded = s.sem("loaded")
        dve = s.sem("dve_step")
        var_ready = s.sem("var_ready")
        std_ready = s.sem("std_ready")
        gap_ready = s.sem("gap_ready")
        exp_ready = s.sem("exp_ready")
        eps = s.sb("eps", [P, 1])
        eps_set = s.sem("eps_set")
        block = s.block()

        @block.sync
        def _(sp):
            sp.dma_start(par[:, :, :], d["route4_par"].broadcast_to([P, 3, F])).then_inc(loaded, 16)
            sp.dma_start(order[:, 0:GE], d["order4"].broadcast_to([P, GE])).then_inc(loaded, 16)

        @block.scalar
        def _(a):
            a.wait_ge(var_ready, 1)
            a.wait_ge(eps_set, 1)
            a.activation(std[:, :], std[:, :], ACT.Sqrt, bias=eps[:, 0:1]).then_inc(std_ready, 1)
            a.wait_ge(gap_ready, 1)
            a.activation(second[:, :], second[:, :], ACT.Exp).then_inc(exp_ready, 1)

        @block.vector
        def _(v):
            step = Chain(v, dve)
            v.memset(eps[:, :], LN_EPS).then_inc(eps_set, 1)
            v.wait_ge(loaded, 32)
            flat, flat_sq = x[:, :, :, :].rearrange("p t h e -> p t (h e)"), sq[:, :, :, :].rearrange("p t h e -> p t (h e)")

            def row(k):
                return bc(par[:, k, :].unsqueeze(1), [P, NT, F])

            def col(ap, n):
                return bc(ap[:, :].unsqueeze(2), [P, NT, n])

            step(v.tensor_scalar(rden[:, :, :], agg[:, :, :, GE], 1e-16, None, ALU.add))
            step(v.reciprocal(rden[:, :, :], rden[:, :, :]))
            step(v.tensor_tensor(x[:, :, :, :], agg[:, :, :, 0:GE], bc(rden[:, :, :].unsqueeze(3), [P, NT, HG, GE]),
                                 ALU.mult))
            step(v.tensor_tensor(flat, flat, row(0), ALU.add))
            step(v.tensor_reduce(mean[:, :], flat, AX.X, ALU.add))
            step(v.tensor_scalar(mean[:, :], mean[:, :], 1.0 / F, None, ALU.mult))
            step(v.tensor_tensor(flat, flat, col(mean, F), ALU.subtract))
            step(v.tensor_tensor(flat_sq, flat, flat, ALU.mult))
            step(v.tensor_reduce(std[:, :], flat_sq, AX.X, ALU.add))
            v.tensor_scalar(std[:, :], std[:, :], 1.0 / F, None, ALU.mult).then_inc(var_ready, 1)
            v.wait_ge(std_ready, 1)
            step(v.reciprocal(std[:, :], std[:, :]))
            step(v.tensor_tensor(flat, flat, col(std, F), ALU.mult))
            step(v.tensor_tensor(flat, flat, row(1), ALU.mult))
            step(v.tensor_tensor(flat, flat, row(2), ALU.add))
            step(v.tensor_reduce(scores[:, :, :], x[:, :, :, :].rearrange("p t h e -> p t e h"), AX.X, ALU.add))
            step(v.tensor_scalar(scores[:, :, :], scores[:, :, :], 1.0 / HG, None, ALU.mult))
            two_best(v, step, scores, best, rest, eq, picks, order, GE)
            v.tensor_tensor(second[:, :], best[1][:, :], best[0][:, :], ALU.subtract).then_inc(gap_ready, 1)
            v.wait_ge(exp_ready, 1)
            step(v.tensor_scalar(mean[:, :], second[:, :], 1.0, None, ALU.add))
            step(v.reciprocal(mean[:, :], mean[:, :]))
            step(v.tensor_tensor(picks[1][:, :, :], picks[1][:, :, :], col(second, GE), ALU.mult))
            step(v.tensor_tensor(gates[:, :, :], picks[0][:, :, :], picks[1][:, :, :], ALU.add))
            v.tensor_tensor(gates[:, :, :], gates[:, :, :], col(mean, GE), ALU.mult)


def graph_tables():
    c = {"iota_nodes": np.arange(T, dtype=np.float16)[None], "identh": np.eye(P, dtype=np.float16)}
    c["iota_tiles"] = np.arange(NT, dtype=np.float32)[None]
    c["key_bases"] = (np.arange(NT) * KEY_TILE + 1).astype(np.float32)[None]
    loops = np.zeros((P, 2 * T - P), np.float16)
    loops[:, T - P:T] = np.eye(P)
    c["loops"] = loops
    c["order4"] = np.arange(GE, 0, -1, dtype=np.float32)[None]
    return c


class Steps:

    def __init__(self, engine, semaphore, base):
        self.engine, self.semaphore, self.base, self.count = engine, semaphore, base, 0

    def __call__(self, *instructions):
        self.count += 1
        instructions[-1].then_inc(self.semaphore, 1)
        self.engine.wait_ge(self.semaphore, self.base + self.count)


PK_HEADS = 8
PK_KEYS = 64
PK_DIM = D // 2
TOPK = 16
PAIRS_OF_HEADS = PK_HEADS // 2
CANDS = [(i, TOPK // (i + 1)) for i in range(TOPK)]
N_CAND = sum(n for _, n in CANDS)
GROUPS2 = 2 * PK_HEADS
G_RING = 8
LOWEST = -3e38


def product_keys(nc, m, d):
    h, xT, ident = m["h"], m["xT"], m["ident"]
    with Stage(nc, "pkm") as s:
        w = s.sb("w", [D, 2, 4, P])
        wo = s.sb("wo", [P, PAIRS_OF_HEADS, D])
        keys = s.sb("keys", [P, 4, 4 * PK_KEYS])
        head_base = s.sb("head_base", [P, PK_HEADS, TOPK])
        iota = s.sb("iota", [P, N_CAND])
        later = s.sb("later", [P, 2 * S - P])
        mask = s.sb("mask", [P, S])
        qp_now = s.sb("qp_now", [P, 4, P])
        q_now = s.sb("q_now", [P, PAIRS_OF_HEADS, P])
        sim = s.sb("sim", [P, 2, GROUPS2, PK_KEYS])
        top = s.sb("top", [P, GROUPS2, TOPK])
        at = s.sb("at", [P, GROUPS2, TOPK], U32)
        atf = s.sb("atf", [P, GROUPS2, TOPK])
        score = s.sb("score", [P, PK_HEADS, N_CAND])
        row = s.sb("row", [P, PK_HEADS, N_CAND])
        best = s.sb("best", [P, PK_HEADS, TOPK])
        pos = s.sb("pos", [P, PK_HEADS, TOPK], U32)
        posf = s.sb("posf", [P, PK_HEADS, TOPK])
        eq = s.sb("eq", [P, PK_HEADS // 2, TOPK, N_CAND])
        picked = s.sb("picked", [P, PK_HEADS, TOPK])
        total = s.sb("total", [P, PK_HEADS])
        rows = s.sb("rows", [P, 2, PK_HEADS * TOPK], I32)
        weight = s.sb("weight", [P, 2, PK_HEADS, TOPK])
        got = [s.sb(f"got{k}", [P, TOPK, 2 * D]) for k in range(G_RING)]
        k_now = s.sb("k_now", [P, PAIRS_OF_HEADS, 2 * D])
        v_now = s.sb("v_now", [P, PK_HEADS, D])
        kT = s.sb("kT", [P, PAIRS_OF_HEADS, S])
        v_all = s.sb("v_all", [P, TB, PK_HEADS, D + 1])
        masked = s.sb("masked", [P, 2, S])
        probs = s.sb("probs", [P, 2, S])
        pT = s.sb("pT", [P, 2, 4, P])
        bias = s.sb("bias", [P, PK_HEADS])
        mx = s.sb("mx", [P, PK_HEADS, 2])
        rden = s.sb("rden", [P, PK_HEADS])
        o_now = s.sb("o_now", [P, PAIRS_OF_HEADS, 2 * D])
        oT = s.sb("oT", [P, PAIRS_OF_HEADS, P])
        spare = s.sb("spare", [P, 128])
        act_spare = s.sb("act_spare", [P, 2])
        pool_spare = s.sb("pool_spare", [P, 32])
        ps_q = s.ps("ps_q", [P, 4, P])
        ps_sim = [s.ps(f"ps_sim{k}", [P, 512]) for k in range(2)]
        ps_sc = [s.ps(f"ps_sc{k}", [P, 512]) for k in range(2)]
        ps_t = [s.ps(f"ps_t{k}", [P, 4, P]) for k in range(2)]
        ps_o = s.ps("ps_o", [P, 512])
        names = ["loaded", "cleared", "qp_made", "qp_kept", "sim_made", "sim_kept", "sim_used", "best_ready",
                 "exp_ready", "rows_ready", "dve_step", "combined", "scaled", "carried", "q_made", "q_kept",
                 "kv_staged", "qk_made", "max_step", "max_done", "exp_done", "turned", "t_kept", "pv_made",
                 "rden_ready", "o_kept", "y_made", "y_kept", "act_step"]
        (loaded, cleared, qp_made, qp_kept, sim_made, sim_kept, sim_used, best_ready, exp_ready, rows_ready, dve,
         combined, scaled, carried, q_made, q_kept, kv_staged, qk_made, max_step, max_done, exp_done, turned,
         t_kept, pv_made, rden_ready, o_kept, y_made, y_kept, act_step) = [s.sem(n) for n in names]
        landed = [s.sem(f"landed{k}") for k in range(G_RING)]
        block = s.block()
        TURNS = 2 * PK_HEADS + 2
        LOADS = 6 * 16

        @block.sync
        def _(sp):
            sp.dma_start(w[:, :, :, :], d["pk_wq"].rearrange("d (k c) p -> d k c p", k=2)).then_inc(loaded, 16)
            sp.dma_start(keys[:, :, :], d["pk_keys"]).then_inc(loaded, 16)
            sp.dma_start(head_base[:, :, :], d["pk_base"].broadcast_to([P, PK_HEADS, TOPK])).then_inc(loaded, 16)
            sp.dma_start(iota[:, :], d["pk_iota"].broadcast_to([P, N_CAND])).then_inc(loaded, 16)
            sp.dma_start(later[:, :], d["pk_later"]).then_inc(loaded, 16)
            sp.dma_start(wo[:, :, :], d["pk_wo"]).then_inc(loaded, 16)

        @block.tensor
        def _(pe):
            def tokens(t):
                return xT[0:D, bass.ds(t * P, P)]

            def similarities(t):
                if not isinstance(t, int) or t >= 2:
                    pe.wait_ge(q_kept, t - 1)
                for c in range(4):
                    mm = pe.matmul(ps_q[:, c, :], w[:, 0, c, :], tokens(t), start=True, stop=True)
                mm.then_inc(qp_made, 1)
                pe.wait_ge(qp_kept, t + 1)
                if not isinstance(t, int) or t >= 1:
                    pe.wait_ge(sim_kept, t)
                for c in range(4):
                    mm = pe.matmul(ps_sim[c // 2][:, c % 2 * 256:c % 2 * 256 + 256], qp_now[:, c, :],
                                   keys[:, c, :], start=True, stop=True)
                mm.then_inc(sim_made, 1)

            def turn_keys(t):
                pe.wait_ge(combined, t * PK_HEADS + (PK_HEADS + G_RING))
                pe.wait_ge(t_kept, t * TURNS + 2)
                for q in range(PAIRS_OF_HEADS):
                    mm = pe.transpose(ps_t[0][:, q, :], k_now[:, q, :], ident[:, :])
                mm.then_inc(turned, 1)

            def attend(t, looked_up):
                pe.wait_ge(qp_kept, looked_up)
                for c in range(4):
                    mm = pe.matmul(ps_q[:, c, :], w[:, 1, c, :], tokens(t), start=True, stop=True)
                mm.then_inc(q_made, 1)
                pe.wait_ge(q_kept, t + 2)
                pe.wait_ge(kv_staged, t + 1)

                def scores(hd):
                    rows = slice(hd % 2 * D, hd % 2 * D + D)
                    pe.wait_ge(max_done, t * PK_HEADS + (hd + 1))
                    for j in range(2):
                        mm = pe.matmul(ps_sc[j][:, :], q_now[rows, hd // 2, :],
                                       kT[rows, hd // 2, j * 512:j * 512 + 512], start=True, stop=True)
                    mm.then_inc(qk_made, 1)

                scores(0)
                for hd in range(PK_HEADS):
                    if hd + 1 < PK_HEADS:
                        scores(hd + 1)
                    pe.wait_ge(exp_done, t * PK_HEADS + (hd + 1))
                    for c in range(2):
                        n = 1 + 2 * hd + c
                        pe.wait_ge(t_kept, t * TURNS + max(n + 1, 3))
                        for j in range(4):
                            mm = pe.transpose(ps_t[c][:, j, :], probs[:, hd % 2, (4 * c + j) * P:(4 * c + j + 1) * P],
                                              ident[:, :])
                        mm.then_inc(turned, 1)
                    if hd == 0:
                        pe.wait_ge(y_kept, t + 1)
                    else:
                        pe.wait_ge(o_kept, t * PK_HEADS + hd)
                    for c in range(2):
                        pe.wait_ge(t_kept, t * TURNS + (1 + 2 * hd + c + 3))
                        for j in range(4):
                            mm = pe.matmul(ps_o[:, 0:D + 1], pT[:, c, j, :], v_all[:, 4 * c + j, hd, :],
                                           start=(c == j == 0), stop=(c == 1 and j == 3))
                    mm.then_inc(pv_made, 1)
                pe.wait_ge(o_kept, t * PK_HEADS + PK_HEADS)
                pe.wait_ge(t_kept, t * TURNS + (TURNS - 1 + 2))
                for q in range(PAIRS_OF_HEADS):
                    mm = pe.transpose(ps_t[1][:, q, :], o_now[:, q, :], ident[:, :])
                mm.then_inc(turned, 1)
                pe.wait_ge(t_kept, t * TURNS + (TURNS + 2))
                for q in range(PAIRS_OF_HEADS):
                    mm = pe.matmul(ps_o[:, 0:D], oT[:, q, :], wo[:, q, :], start=(q == 0), stop=(q == PAIRS_OF_HEADS - 1))
                mm.then_inc(y_made, 1)

            pe.wait_ge(loaded, LOADS)
            pe.wait_ge(cleared, 2)
            similarities(0)
            similarities(1)
            with pe.Fori(0, NT // 2 - 1) as i:
                for r in range(2):
                    turn_keys(i * 2 + r)
                    similarities(i * 2 + (r + 2))
                    attend(i * 2 + r, i * 2 + (r + 3))
            for t in range(NT - 2, NT):
                turn_keys(t)
                attend(t, NT)

        @block.scalar
        def _(a):
            def stage_keys(t):
                slot = t & (TB - 1)
                a.wait_ge(turned, t * TURNS + 1)
                a.copy(kT[:, :, bass.ds(slot * P, P)], ps_t[0][:, :, :]).then_inc(t_kept, 1)
                a.copy(mask[:, :], later[:, bass.ds(slot * (-P) + (S - P), S)])
                a.wait_ge(combined, t * PK_HEADS + (PK_HEADS + G_RING))
                a.copy(v_all[:, bass.ds(slot, 1), :, 0:D].rearrange("p t h c -> p (t h) c"),
                       v_now[:, :, :]).then_inc(kv_staged, 1)

            def stage_similarities(t, r):
                a.wait_ge(qp_made, t + 1)
                a.copy(qp_now[:, :, :], ps_q[:, :, :]).then_inc(qp_kept, 1)
                a.wait_ge(sim_used, t + 1)
                a.wait_ge(sim_made, t + 1)
                for j in range(2):
                    last = a.copy(sim[:, r, j * PK_HEADS:(j + 1) * PK_HEADS, :],
                                  ps_sim[j][:, :].rearrange("p (g k) -> p g k", g=PK_HEADS))
                last.then_inc(sim_kept, 1)

            def stage_queries(t):
                a.wait_ge(q_made, t + 1)
                a.copy(q_now[:, :, :], ps_q[:, :, :]).then_inc(q_kept, 1)

            def row_weights(t, r):
                a.wait_ge(best_ready, t + 1)
                a.activation(weight[:, r, :, :], weight[:, r, :, :], ACT.Exp).then_inc(exp_ready, 1)

            def attend(t):
                for hd in range(PK_HEADS):
                    a.wait_ge(max_done, t * PK_HEADS + (hd + 2))
                    a.activation(probs[:, hd % 2, :], masked[:, hd % 2, :], ACT.Exp, bias=bias[:, hd:hd + 1],
                                 scale=D ** -0.5).then_inc(exp_done, 1)
                    for c in range(2):
                        a.wait_ge(turned, t * TURNS + (2 * hd + c + 2))
                        a.copy(pT[:, c, :, :], ps_t[c][:, :, :]).then_inc(t_kept, 1)
                a.wait_ge(turned, t * TURNS + TURNS)
                a.copy(oT[:, :, :], ps_t[1][:, :, :]).then_inc(t_kept, 1)

            a.memzero(act_spare[:, 0:1]).then_inc(act_step, 1)
            a.wait_ge(act_step, 1)
            a.copy(act_spare[:, 1:2], act_spare[:, 0:1]).then_inc(t_kept, 2)
            a.wait_ge(t_kept, 2)
            a.copy(act_spare[:, 1:2], act_spare[:, 0:1]).then_inc(q_kept, 1)
            a.wait_ge(cleared, 2)
            stage_similarities(0, 0)
            row_weights(0, 0)
            stage_similarities(1, 1)
            row_weights(1, 1)
            with a.Fori(0, NT // 2 - 1) as i:
                for r in range(2):
                    stage_keys(i * 2 + r)
                    stage_similarities(i * 2 + (r + 2), r)
                    stage_queries(i * 2 + r)
                    row_weights(i * 2 + (r + 2), r)
                    attend(i * 2 + r)
            for t in range(NT - 2, NT):
                stage_keys(t)
                stage_queries(t)
                attend(t)

        @block.gpsimd
        def _(g):
            g.memset(pool_spare[:, :], 0.0).then_inc(carried, 1)
            g.wait_ge(carried, 1)

            def carry(n):
                g.tensor_tensor(pool_spare[:, n + 1:n + 2], pool_spare[:, 0:1], pool_spare[:, 0:1],
                                ALU.add).then_inc(carried, 1)

            with g.Fori(0, NT // 2) as i:
                for r in range(2):
                    g.wait_ge(rows_ready, i * 2 + (r + 1))
                    for hd in range(PK_HEADS):
                        slot = hd % G_RING
                        g.wait_ge(carried, i * (2 * PK_HEADS) + (r * PK_HEADS + hd + 1))
                        g.wait_ge(combined, i * (2 * PK_HEADS) + (r * PK_HEADS + hd + 1))
                        carry(r * PK_HEADS + hd)
                        for k in range(TOPK):
                            n = hd * TOPK + k
                            g.indirect_dma_start(got[slot][:, k, :], None, d["pk_table"],
                                                 bass.IndirectOffsetOnAxis(ap=rows[:, r, n:n + 1].bitcast(U32), axis=0)
                                                 ).then_inc(landed[slot], 16)

        @block.vector
        def _(v):
            sites = [0]

            def carry():
                sites[0] += 1
                return v.memset(spare[:, sites[0]:sites[0] + 1], 0.0)

            def best_sixteen(step, values, out, index, n):
                carry()
                step(*[v.max(out[:, g, 0:8], values(g)) for g in range(n)])
                carry()
                step(*[v.max_index(index[:, g, 0:8], out[:, g, 0:8], values(g)) for g in range(n)])
                carry()
                step(*[v.match_replace(values(g), out[:, g, 0:8], values(g), LOWEST) for g in range(n)])
                carry()
                step(*[v.max(out[:, g, 8:16], values(g)) for g in range(n)])
                carry()
                step(*[v.max_index(index[:, g, 8:16], out[:, g, 8:16], values(g)) for g in range(n)])

            def look(t, r):
                step = Steps(v, dve, t * LOOK_STEPS)
                v.wait_ge(sim_kept, t + 1)
                best_sixteen(step, lambda g: sim[:, r, g, :], top, at, GROUPS2)
                step(v.tensor_copy(atf[:, :, :], at[:, :, :]))
                second = atf[:, PK_HEADS:, :]
                step(v.scalar_tensor_tensor(second, second, float(PK_KEYS), head_base[:, :, :], ALU.mult, ALU.add))
                done = []
                for src, dst in ((top, score), (atf, row)):
                    off = 0
                    for i, n in CANDS[:8]:
                        done.append(v.tensor_tensor(dst[:, :, off:off + n], src[:, PK_HEADS:, 0:n],
                                                    bc(src[:, 0:PK_HEADS, i:i + 1], [P, PK_HEADS, n]), ALU.add))
                        off += n
                    done.append(v.tensor_tensor(dst[:, :, off:off + 8], src[:, 0:PK_HEADS, 8:16],
                                                bc(src[:, PK_HEADS:, 0:1], [P, PK_HEADS, 8]), ALU.add))
                step(*done)
                best_sixteen(step, lambda g: score[:, g, :], best, pos, PK_HEADS)
                v.tensor_tensor(weight[:, r, :, :], best[:, :, :], bc(best[:, :, 0:1], [P, PK_HEADS, TOPK]),
                                ALU.subtract).then_inc(best_ready, 1)
                step(v.tensor_copy(posf[:, :, :], pos[:, :, :]))
                n = PK_HEADS // 2
                for heads in (slice(0, n), slice(n, PK_HEADS)):
                    step(v.tensor_tensor(eq[:, :, :, :].rearrange("p h k c -> p (h k) c"),
                                         bc(iota[:, :].unsqueeze(1), [P, n * TOPK, N_CAND]),
                                         bc(posf[:, heads, :].rearrange("p h k -> p (h k)").unsqueeze(2),
                                            [P, n * TOPK, N_CAND]), ALU.is_equal))
                    step(v.tensor_tensor(eq[:, :, :, :], eq[:, :, :, :],
                                         bc(row[:, heads, :].unsqueeze(2), [P, n, TOPK, N_CAND]), ALU.mult))
                    step(v.tensor_reduce(picked[:, heads, :], eq[:, :, :, :], AX.X, ALU.add))
                v.tensor_copy(rows[:, r, :], picked[:, :, :].rearrange("p h k -> p (h k)")).then_inc(rows_ready, 1)
                v.wait_ge(exp_ready, t + 1)
                step(v.tensor_reduce(total[:, :], weight[:, r, :, :], AX.X, ALU.add))
                step(v.reciprocal(total[:, :], total[:, :]))
                step(v.tensor_tensor(weight[:, r, :, :], weight[:, r, :, :],
                                     bc(total[:, :].unsqueeze(2), [P, PK_HEADS, TOPK]), ALU.mult))
                carry().then_inc(sim_used, 1)
                assert step.count == LOOK_STEPS, step.count

            def combine(t, r, hd):
                uses = PK_HEADS // G_RING
                rowsg = got[hd % G_RING]
                v.wait_ge(landed[hd % G_RING], t * (uses * 16 * TOPK) + (hd // G_RING + 1) * 16 * TOPK)
                v.tensor_tensor(rowsg[:, :, :], rowsg[:, :, :],
                                bc(weight[:, r, hd, :].unsqueeze(2), [P, TOPK, 2 * D]), ALU.mult).then_inc(scaled, 1)
                v.wait_ge(scaled, t * PK_HEADS + (hd + 1))
                half = slice(hd % 2 * D, hd % 2 * D + D)
                v.tensor_reduce(k_now[:, hd // 2, half], rowsg[:, :, 0:D].rearrange("p k c -> p c k"), AX.X, ALU.add)
                v.tensor_reduce(v_now[:, hd, :], rowsg[:, :, D:2 * D].rearrange("p k c -> p c k"),
                                AX.X, ALU.add).then_inc(combined, 1)

            def maximum(t, hd):
                v.wait_ge(qk_made, t * PK_HEADS + (hd + 1))
                carry()
                for j in range(2):
                    v.tensor_tensor_reduce(out=masked[:, hd % 2, j * 512:j * 512 + 512], in0=ps_sc[j][:, :],
                                           in1=mask[:, j * 512:j * 512 + 512],
                                           scale=1.0, scalar=NEG, op0=ALU.add, op1=ALU.max,
                                           accum_out=mx[:, hd, j:j + 1]).then_inc(max_step, 1)
                v.wait_ge(max_step, t * (3 * PK_HEADS) + (3 * hd + 2))
                v.tensor_tensor(bias[:, hd:hd + 1], mx[:, hd, 0:1], mx[:, hd, 1:2], ALU.max).then_inc(max_step, 1)
                v.wait_ge(max_step, t * (3 * PK_HEADS) + (3 * hd + 3))
                v.tensor_scalar(bias[:, hd:hd + 1], bias[:, hd:hd + 1], -(D ** -0.5), None, ALU.mult).then_inc(max_done, 1)

            def output(t, hd):
                v.wait_ge(pv_made, t * PK_HEADS + (hd + 1))
                v.reciprocal(rden[:, hd:hd + 1], ps_o[:, D:D + 1]).then_inc(rden_ready, 1)
                v.wait_ge(rden_ready, t * PK_HEADS + (hd + 1))
                v.tensor_scalar(o_now[:, hd // 2, hd % 2 * D:hd % 2 * D + D], ps_o[:, 0:D], rden[:, hd:hd + 1], None,
                                ALU.mult).then_inc(o_kept, 1)

            def add_to_h(t):
                v.wait_ge(y_made, t + 1)
                now = h[:, bass.ds(t, 1), :].rearrange("p t c -> p (t c)")
                v.tensor_tensor(now, now, ps_o[:, 0:D], ALU.add).then_inc(y_kept, 1)

            v.memset(kT[:, :, :], 0.0).then_inc(cleared, 1)
            v.memset(v_all[:, :, :, 0:D], 0.0)
            v.memset(v_all[:, :, :, D:D + 1], 1.0).then_inc(cleared, 1)
            v.engine_nop().then_inc(combined, G_RING)
            v.engine_nop().then_inc(sim_used, 2)
            v.engine_nop().then_inc(max_done, 1)
            v.engine_nop().then_inc(y_kept, 1)
            v.wait_ge(loaded, LOADS)
            look(0, 0)
            look(1, 1)
            for hd in range(PK_HEADS):
                combine(0, 0, hd)
            with v.Fori(0, NT // 2 - 1) as i:
                for r in range(2):
                    t = i * 2 + r
                    look(i * 2 + (r + 2), r)
                    v.wait_ge(kv_staged, t + 1)
                    for hd in range(PK_HEADS):
                        combine(i * 2 + (r + 1), 1 - r, hd)
                        maximum(t, hd)
                        if hd > 0:
                            output(t, hd - 1)
                    output(t, PK_HEADS - 1)
                    add_to_h(t)
            for t in range(NT - 2, NT):
                v.wait_ge(kv_staged, t + 1)
                for hd in range(PK_HEADS):
                    if t < NT - 1:
                        combine(t + 1, 1, hd)
                    maximum(t, hd)
                    if hd > 0:
                        output(t, hd - 1)
                output(t, PK_HEADS - 1)
                add_to_h(t)


LOOK_STEPS = 5 + 1 + 1 + 1 + 5 + 1 + 6 + 3


def product_key_tables():
    c = {"pk_iota": np.arange(N_CAND, dtype=np.float32)[None]}
    base = np.arange(PK_HEADS, dtype=np.float32)[:, None] * PK_KEYS ** 2
    c["pk_base"] = np.broadcast_to(base, (PK_HEADS, TOPK))[None]
    c["pk_later"] = np.where(np.arange(2 * S - P)[None, :] <= np.arange(P)[:, None] + S - P, 0.0, NEG).astype(np.float32)
    return c

STAGES = [embed, linear_attention, tree_ffn, retention, product_keys, recurrence, graph_ffn, pseudo_inverse,
          wavelet_attention, experts_eight]


def tower(nc, d, out, stages):
    with ExitStack() as ctx:
        def sb(name, shape, dt=F32):
            return ctx.enter_context(nc.sbuf_tensor(name, shape, dt))
        m = {"h": sb("h", [P, NT, D]), "xn": sb("xn", [P, NT, D]), "xT": sb("xT", [D + 1, T]),
             "ident": sb("ident", [P, P]), "eps": sb("eps", [P, 1]), "inv_wT": sb("inv_wT", [D, D])}
        with Stage(nc, "begin") as s:
            loaded = s.sem("loaded")
            block = s.block()

            @block.sync
            def _(sp):
                sp.dma_start(m["ident"][:, :], d["ident"]).then_inc(loaded, 16)
                sp.wait_ge(loaded, 16)

            @block.vector
            def _(v):
                v.memset(m["xT"][D:D + 1, :], 1.0)
                v.memset(m["eps"][:, :], LN_EPS)
        for n, stage in enumerate(stages):
            if stage in (pseudo_inverse, embed):
                stage(nc, m, d)
                continue
            normalise(nc, m, n)
            stage(nc, m, d)
        with Stage(nc, "end") as s:
            stored = s.sem("stored")
            block = s.block()

            @block.sync
            def _(sp):
                sp.dma_start(out.rearrange("b (t p) d -> p (b t) d", p=P), m["h"][:, :, :]).then_inc(stored, 16)
                sp.wait_ge(stored, 16)


def constants():
    c = {"ident": np.eye(P, dtype=np.float32)}
    head = np.arange(D) // 8
    c["head_mask"] = ((head[:, None] == head[None, :]) / S).astype(np.float32)
    c.update(retention_tables())
    c.update(recurrence_tables())
    c.update(wavelet_tables())
    c.update(embed_tables())
    c.update(graph_tables())
    c.update(product_key_tables())
    c["order8"] = np.arange(8, 0, -1, dtype=np.float32)[None]
    return c


def layouts(i):
    cat = np.concatenate
    a = {}
    a["la_w_vk"] = cat([cat([i["L0_attn_Wv"].T, i["L0_attn_bv"][None]], 0),
                        cat([i["L0_attn_Wk"].T, i["L0_attn_bk"][None]], 0)], 1)
    a["la_w_q"] = cat([i["L0_attn_Wq"].T, i["L0_attn_bq"][None]], 0)
    a["la_w_fc"] = i["L0_attn_Wfc"].T
    a["la_b_fc"] = i["L0_attn_bfc"][None]
    even_odd = np.concatenate([np.arange(0, D, 2), np.arange(1, D, 2)])
    a["ret_w"] = cat([i["L1_attn_W_Q"][:, even_odd], i["L1_attn_W_K"][:, even_odd], i["L1_attn_W_V"]], 1)
    w1s = cat([i["L0_ffn_w1s"].T, i["L0_ffn_b1s"][None]], 0)
    a["tree_w1"] = cat([w1s, np.zeros((D + 1, 1), np.float32)], 1)
    a["tree_w2"] = cat([i["L0_ffn_w2s"].transpose(1, 0, 2).reshape(D, -1), np.zeros((D, D), np.float32)], 1)
    b2s = cat([i["L0_ffn_b2s"], np.zeros((1, D), np.float32)], 0)
    a["tree_b2"] = b2s.reshape(2, P, D).transpose(1, 0, 2)
    par = np.stack([i["L2_attn_nu_log"], i["L2_attn_theta_log"], i["L2_attn_gamma_log"]], 1)
    a["rec_par"] = cat([par, par], 0)
    bre, bim, cre, cim = (i[f"L2_attn_{k}"].T for k in ("B_re", "B_im", "C_re", "C_im"))
    a["rec_w_in"] = np.stack([cat([bre, bim], 1), cat([bim, bre], 1)], 1)
    a["rec_w_out"] = np.stack([cat([cre, cim], 0), cat([cim, cre], 0)], 1)
    w1, b1, w2 = i["L3_ffn_w1"], i["L3_ffn_b1"], i["L3_ffn_w2"]
    a["moe8_w1"] = cat([w1.transpose(1, 0, 2).reshape(D, 4, P), b1.reshape(1, 4, P)], 0)
    a["moe8_w2"] = w2.reshape(4, P, D).transpose(1, 0, 2)
    a["moe8_b2"] = i["L3_ffn_b2"][None]
    a["route8_w"] = i["L3_ffn_router_w"].T
    a["near_w_q"], a["near_w_qT"] = i["L3_attn_W_Q"], i["L3_attn_W_Q"].T
    a["near_w_v"], a["near_w_oT"] = i["L3_attn_W_V"], i["L3_attn_W_O"].T
    a["ids"], a["positions"] = i["x"], i["fside_BS_continuous_positions"]
    taps = i["L0_tok_w1"].transpose(2, 1, 0)
    taps = cat([taps, np.zeros((1, VOCAB, P), np.float32)], 0)
    a["emb_w1"] = taps.reshape(4, P, P).transpose(1, 0, 2)
    a["emb_w2"] = i["L0_tok_w2"].transpose(1, 2, 0)
    a["emb_w3"] = i["L0_tok_w3"][0]
    a["emb_b1"], a["emb_b2"], a["emb_b3"] = (i[f"L0_tok_b{k}"][:, None] for k in (1, 2, 3))
    a["emb_table"] = cat([i["L0_tok_emb"], i["L0_tok_locality_shapes"]], 1)
    a["emb_widths"], a["emb_weights"] = i["L0_tok_multiscale_widths"][None], i["L0_tok_scale_weights"][None]
    a["edges"] = i["L2_ffn_edge_index"].reshape(2, P, EC)
    a["gat_w"] = i["L2_ffn_W_gat"]
    a["gat_att"] = np.stack([i["L2_ffn_att_src"].reshape(-1), i["L2_ffn_att_dst"].reshape(-1)])[None]
    a["route4_par"] = np.stack([i["L2_ffn_b_gat"], i["L2_ffn_ln_gamma"], i["L2_ffn_ln_beta"]])[None]
    w1, b1, w2 = i["L2_ffn_W1"], i["L2_ffn_b1"], i["L2_ffn_W2"]
    a["moe4_w1"] = cat([w1.transpose(1, 0, 2), b1[None]], 0)
    a["moe4_w2"], a["moe4_b2"] = w2.transpose(1, 0, 2), i["L2_ffn_b2"][None]
    a["pk_wq"] = cat([i["L1_ffn_Wq_pk"], i["L1_ffn_Wq"]], 1).reshape(D, 8, P)
    keys = i["L1_ffn_pk_keys"].transpose(0, 2, 3, 1).reshape(4, 4, PK_DIM, PK_KEYS)
    wide = np.zeros((4, 4, PK_DIM, 4, PK_KEYS), np.float32)
    for q in range(4):
        wide[:, q, :, q] = keys[:, q]
    a["pk_keys"] = wide.reshape(4, P, 4 * PK_KEYS).transpose(1, 0, 2)
    a["pk_table"] = cat([i["L1_ffn_keys_table"], i["L1_ffn_values_table"]], 1)
    a["pk_wo"] = i["L1_ffn_Wo"].reshape(4, P, D).transpose(1, 0, 2)
    return a


def kernel(**inputs):
    import concourse.bacc as bacc
    from concourse.bass_utils import run_bass_kernel_spmd as run

    inputs = {k: np.asarray(v) for k, v in inputs.items()}
    nc = bacc.Bacc("TRN2", target_bir_lowering=False, num_devices=1)
    arrays = {k: np.ascontiguousarray(v) for k, v in {**constants(), **layouts(inputs)}.items()}
    d = {k: nc.dram_tensor(f"in_{k}", v.shape, mybir.dt.from_np(v.dtype), kind="ExternalInput").ap()
         for k, v in arrays.items()}
    out = nc.dram_tensor("out_h", (B, S, D), F32, kind="ExternalOutput").ap()
    tower(nc, d, out, STAGES)
    r = run(nc, [{f"in_{k}": v for k, v in arrays.items()}], core_ids=[0])
    return np.asarray(r.results[0]["out_h"])
```

```python
from contextlib import ExitStack

import numpy as np

import concourse.bass as bass
from concourse import mybir

F32 = mybir.dt.float32
BF16 = mybir.dt.bfloat16
I32 = mybir.dt.int32
U32 = mybir.dt.uint32
ALU = mybir.AluOpType
ACT = mybir.ActivationFunctionType
AX = mybir.AxisListType

P = 128
B = 2
S = 1024
D = 64
T = B * S
NT = T // P
TB = S // P
LN_EPS = 1e-5


class Stage:

    def __init__(self, nc, name):
        self.nc, self.name, self.sems = nc, name, []
        self.ctx = ExitStack()

    def __enter__(self):
        self.ctx.__enter__()
        return self

    def __exit__(self, *exc):
        self.ctx.__exit__(*exc)
        if self.sems:
            self.nc.clear_and_free_semaphores(self.sems)
            self.nc.all_engine_barrier()

    def sb(self, name, shape, dt=F32):
        return self.ctx.enter_context(self.nc.sbuf_tensor(f"{self.name}_{name}", shape, dt))

    def ps(self, name, shape, dt=F32):
        return self.ctx.enter_context(self.nc.psum_tensor(f"{self.name}_{name}", shape, dt))

    def sem(self, name):
        self.sems.append(self.nc.alloc_semaphore(f"{self.name}_{name}"))
        return self.sems[-1]

    def block(self):
        return self.ctx.enter_context(self.nc.Block())


class Chain:

    def __init__(self, engine, semaphore):
        self.engine, self.semaphore, self.count = engine, semaphore, 0

    def __call__(self, instruction):
        self.count += 1
        instruction.then_inc(self.semaphore, 1)
        self.engine.wait_ge(self.semaphore, self.count)


def bc(ap, shape):
    return ap.broadcast_to(shape)


def normalise(nc, m, tag, load=None):
    h, xn, xT, ident, eps = m["h"], m["xn"], m["xT"], m["ident"], m["eps"]
    with Stage(nc, f"ln{tag}") as s:
        mean = s.sb("mean", [P, NT])
        var = s.sb("var", [P, NT])
        std = s.sb("std", [P, NT])
        rstd = s.sb("rstd", [P, NT])
        banks = s.ps("banks", [P, 4, 512])
        turned = [banks[:, k, :] for k in range(4)]
        square = banks[:, 0:2, :].rearrange("p k (t d) -> p (k t) d", d=D)
        dve = s.sem("dve_step")
        var_ready = s.sem("var_ready")
        std_ready = s.sem("std_ready")
        xn_ready = s.sem("xn_ready")
        turned_ready = s.sem("turned_ready")
        block = s.block()

        @block.sync
        def _(sp):
            if load is not None:
                load(sp)

        @block.vector
        def _(v):
            step = Chain(v, dve)
            step(v.tensor_reduce(mean[:, :], h[:, :, :], AX.X, ALU.add))
            step(v.tensor_scalar(mean[:, :], mean[:, :], 1.0 / D, None, ALU.mult))
            step(v.tensor_tensor(xn[:, :, :], h[:, :, :], bc(mean[:, :].unsqueeze(2), [P, NT, D]), ALU.subtract))
            step(v.tensor_tensor(square, xn[:, :, :], xn[:, :, :], ALU.mult))
            step(v.tensor_reduce(var[:, :], square, AX.X, ALU.add))
            v.tensor_scalar(var[:, :], var[:, :], 1.0 / D, None, ALU.mult).then_inc(var_ready, 1)
            v.wait_ge(std_ready, 1)
            step(v.reciprocal(rstd[:, :], std[:, :]))
            for half in range(2):
                t = slice(half * TB, half * TB + TB)
                v.tensor_tensor(xn[:, t, :], xn[:, t, :], bc(rstd[:, t].unsqueeze(2), [P, TB, D]),
                                ALU.mult).then_inc(xn_ready, 1)
            for k in range(0, 4, 2):
                v.wait_ge(turned_ready, k + 1)
                v.tensor_copy(xT[0:D, k * 512:k * 512 + 512], turned[k][0:D])

        @block.scalar
        def _(a):
            a.wait_ge(var_ready, 1)
            a.activation(std[:, :], var[:, :], ACT.Sqrt, bias=eps[:, 0:1]).then_inc(std_ready, 1)
            for k in range(1, 4, 2):
                a.wait_ge(turned_ready, k + 1)
                a.copy(xT[0:D, k * 512:k * 512 + 512], turned[k][0:D])

        @block.tensor
        def _(pe):
            for k in range(4):
                if k % 2 == 0:
                    pe.wait_ge(xn_ready, k // 2 + 1)
                for j in range(4):
                    last = pe.transpose(banks[0:D, k, j * P:j * P + P], xn[:, 4 * k + j, :], ident[:, :])
                last.then_inc(turned_ready, 1)


def linear_attention(nc, m, d):
    h, xT = m["h"], m["xT"]
    with Stage(nc, "la") as s:
        w_kv = s.sb("w_kv", [D + 1, 2 * D])
        w_q = s.sb("w_q", [D + 1, D])
        w_fc = s.sb("w_fc", [D, D])
        head_mask = s.sb("head_mask", [D, D])
        vk = s.sb("vk", [P, NT, 2 * D])
        qT = s.sb("qT", [D + 1, T])
        pT = s.sb("pT", [D, B, D])
        fold = s.sb("fold", [D + 1, B, D])
        loaded = s.sem("loaded")

        def load(sp):
            sp.dma_start(w_kv[:, :], d["la_w_vk"]).then_inc(loaded, 16)
            sp.dma_start(w_q[:, :], d["la_w_q"]).then_inc(loaded, 16)
            sp.dma_start(w_fc[:, :], d["la_w_fc"]).then_inc(loaded, 16)
            sp.dma_start(head_mask[:, :], d["head_mask"]).then_inc(loaded, 16)
            for b in range(B):
                sp.dma_start(fold[D:D + 1, b, :], d["la_b_fc"]).then_inc(loaded, 16)

        normalise(nc, m, "la", load)
        ps_vk = [s.ps(f"ps_vk{k}", [P, 4, 2 * D]) for k in range(2)]
        ps_q = [s.ps(f"ps_q{k}", [P, 512]) for k in range(2)]
        ps_p = s.ps("ps_p", [P, B, D])
        ps_f = s.ps("ps_f", [P, B, D])
        ps_o = [s.ps(f"ps_o{k}", [P, TB, D]) for k in range(B)]
        vk_made = s.sem("vk_made")
        vk_kept = s.sem("vk_kept")
        q_made = s.sem("q_made")
        q_kept = s.sem("q_kept")
        p_made = s.sem("p_made")
        p_kept = s.sem("p_kept")
        f_made = s.sem("f_made")
        f_kept = s.sem("f_kept")
        o_made = s.sem("o_made")
        ones_set = s.sem("ones_set")
        block = s.block()
        LOADS = 6 * 16

        @block.tensor
        def _(pe):
            pe.wait_ge(loaded, LOADS)
            for k in range(4):
                if k >= 2:
                    pe.wait_ge(vk_kept, k - 1)
                for j in range(4):
                    t = 4 * k + j
                    last = pe.matmul(ps_vk[k % 2][:, j, :], xT[:, t * P:t * P + P], w_kv[:, :],
                                     start=True, stop=True)
                last.then_inc(vk_made, 1)
            for k in range(4):
                if k >= 2:
                    pe.wait_ge(q_kept, k - 1)
                pe.matmul(ps_q[k % 2][0:D, :], w_q[:, :], xT[:, k * 512:k * 512 + 512],
                          start=True, stop=True).then_inc(q_made, 1)
            pe.wait_ge(vk_kept, 4)
            for b in range(B):
                for j in range(TB):
                    t = b * TB + j
                    last = pe.matmul(ps_p[0:D, b, :], vk[:, t, 0:D], vk[:, t, D:2 * D],
                                     start=(j == 0), stop=(j == TB - 1))
                last.then_inc(p_made, 1)
            for b in range(B):
                pe.wait_ge(p_kept, b + 1)
                pe.matmul(ps_f[0:D, b, :], pT[:, b, :], w_fc[:, :], start=True, stop=True).then_inc(f_made, 1)
            pe.wait_ge(q_kept, 4)
            pe.wait_ge(ones_set, 1)
            for b in range(B):
                pe.wait_ge(f_kept, b + 1)
                for j in range(TB):
                    t = b * TB + j
                    last = pe.matmul(ps_o[b][:, j, :], qT[:, t * P:t * P + P], fold[:, b, :],
                                     start=True, stop=True)
                last.then_inc(o_made, 1)

        @block.vector
        def _(v):
            v.memset(qT[D:D + 1, :], 1.0).then_inc(ones_set, 1)
            for k in range(4):
                v.wait_ge(vk_made, k + 1)
                v.tensor_copy(vk[:, 4 * k:4 * k + 4, :], ps_vk[k % 2][:, :, :]).then_inc(vk_kept, 1)
            v.wait_ge(p_made, B)
            for b in range(B):
                v.tensor_tensor(pT[:, b, :], ps_p[0:D, b, :], head_mask[:, :], ALU.mult).then_inc(p_kept, 1)
            v.wait_ge(f_made, B)
            for b in range(B):
                v.tensor_copy(fold[0:D, b, :], ps_f[0:D, b, :]).then_inc(f_kept, 1)
            for b in range(B):
                v.wait_ge(o_made, b + 1)
                t = slice(b * TB, b * TB + TB)
                v.tensor_tensor(h[:, t, :], h[:, t, :], ps_o[b][:, :, :], ALU.add)

        @block.scalar
        def _(a):
            for k in range(4):
                a.wait_ge(q_made, k + 1)
                a.copy(qT[0:D, k * 512:k * 512 + 512], ps_q[k % 2][0:D, :]).then_inc(q_kept, 1)


RET_GAMMA = 0.96875
RET_SCALE_BASE = 512.0


def retention(nc, m, d):
    h, xT, ident = m["h"], m["xT"], m["ident"]
    HALF = D // 2
    with Stage(nc, "ret") as s:
        w = s.sb("w", [D, 3 * D])
        cos = s.sb("cos", [P, TB, 2, HALF])
        sin = s.sb("sin", [P, TB, 2, HALF])
        decay = s.sb("decay", [P, P])
        k_decay = s.sb("k_decay", [P, 1])
        q_decay = s.sb("q_decay", [D, P])
        qkv = s.sb("qkv", [P, NT, 3 * D])
        rot = s.sb("rot", [P, NT, 2 * D])
        tmp = s.sb("tmp", [P, TB, 2, HALF])
        tmp2 = s.sb("tmp2", [P, TB, 2, HALF])
        kd = s.sb("kd", [P, NT, D])
        qT = s.sb("qT", [D, T])
        qTd = s.sb("qTd", [D, T])
        kT = s.sb("kT", [D, T])
        probs = s.sb("probs", [P, NT, P])
        state = s.sb("state", [D, TB, B, D])
        loaded = s.sem("loaded")

        def load(sp):
            sp.dma_start(w[:, :], d["ret_w"]).then_inc(loaded, 16)
            sp.dma_start(cos[:, :, :, :], d["ret_cos"].rearrange("(t p) a c -> p t a c", p=P)).then_inc(loaded, 16)
            sp.dma_start(sin[:, :, :, :], d["ret_sin"].rearrange("(t p) a c -> p t a c", p=P)).then_inc(loaded, 16)
            sp.dma_start(decay[:, :], d["ret_decay"]).then_inc(loaded, 16)
            sp.dma_start(k_decay[:, :], d["ret_k_decay"]).then_inc(loaded, 16)
            sp.dma_start(q_decay[:, :], d["ret_q_decay"].broadcast_to([D, P])).then_inc(loaded, 16)

        normalise(nc, m, "ret", load)
        ps = [s.ps(f"ps{k}", [P, 512]) for k in range(8)]
        qkv_made = s.sem("qkv_made")
        qkv_kept = s.sem("qkv_kept")
        dve = s.sem("dve_step")
        rotated = s.sem("rotated")
        turned = s.sem("turned")
        q_kept = s.sem("q_kept")
        k_kept = s.sem("k_kept")
        qd_kept = s.sem("qd_kept")
        scores_made = s.sem("scores_made")
        probs_kept = s.sem("probs_kept")
        kd_kept = s.sem("kd_kept")
        kv_made = s.sem("kv_made")
        states_kept = s.sem("states_kept")
        out_made = s.sem("out_made")
        block = s.block()
        LOADS = 6 * 16

        def halves(t):
            return t[:, :].rearrange("p (a e c) -> p a e c", a=2, e=2)

        @block.tensor
        def _(pe):
            pe.wait_ge(loaded, LOADS)
            for t in range(NT):
                last = pe.matmul(ps[t // 2][:, (t % 2) * 192:(t % 2) * 192 + 192], xT[0:D, t * P:t * P + P],
                                 w[:, :], start=True, stop=True)
                if t % 2 == 1:
                    last.then_inc(qkv_made, 1)
            for b in range(B):
                pe.wait_ge(rotated, b + 1)
                pe.wait_ge(qkv_kept, NT // 2)
                for g in range(2):
                    for qk in range(2):
                        bank = ps[4 * b + 2 * g + qk]
                        for j in range(4):
                            t = b * TB + 4 * g + j
                            last = pe.transpose(bank[0:D, j * P:j * P + P], rot[:, t, qk * D:qk * D + D], ident[:, :])
                        last.then_inc(turned, 1)
            for g in range(4):
                pe.wait_ge(k_kept, g + 1)
                pe.wait_ge(q_kept, g + 1)
                pe.wait_ge(qd_kept, g + 1)
                for j in range(4):
                    t = 4 * g + j
                    last = pe.matmul(ps[2 * g][:, j * P:j * P + P], kT[:, t * P:t * P + P],
                                     qT[:, t * P:t * P + P], start=True, stop=True)
                last.then_inc(scores_made, 1)
            pe.wait_ge(kd_kept, 1)
            for b in range(B):
                for c in range(TB):
                    t = b * TB + c
                    last = pe.matmul(ps[2 * b + 1][0:D, c * D:c * D + D], kd[:, t, :], qkv[:, t, 2 * D:3 * D],
                                     start=True, stop=True)
            last.then_inc(kv_made, 1)
            pe.wait_ge(states_kept, 1)
            pe.wait_ge(probs_kept, 4)
            for b in range(B):
                for c in range(TB):
                    t = b * TB + c
                    o = ps[4 + 2 * b + 1][:, c * D:c * D + D]
                    last = pe.matmul(o, probs[:, t, :], qkv[:, t, 2 * D:3 * D], start=True, stop=(c == 0))
                    if c > 0:
                        last = pe.matmul(o, qTd[:, t * P:t * P + P], state[:, c, b, :], start=False, stop=True)
                last.then_inc(out_made, 1)

        @block.scalar
        def _(a):
            for k in range(NT // 2):
                a.wait_ge(qkv_made, k + 1)
                a.copy(qkv[:, 2 * k:2 * k + 2, :],
                       ps[k][:, 0:384].rearrange("p (t c) -> p t c", t=2)).then_inc(qkv_kept, 1)
            for g in range(4):
                a.wait_ge(turned, 2 * g + 1)
                a.copy(qT[:, g * 512:g * 512 + 512], ps[2 * g][0:D, :]).then_inc(q_kept, 1)

        @block.vector
        def _(v):
            step = Chain(v, dve)
            v.wait_ge(loaded, LOADS)
            for b in range(B):
                v.wait_ge(qkv_kept, TB // 2 * (b + 1))
                t = slice(b * TB, b * TB + TB)
                x = qkv[:, t, 0:2 * D].rearrange("p t (a e c) -> p t a e c", a=2, e=2)
                y = rot[:, t, :].rearrange("p t (a e c) -> p t a e c", a=2, e=2)
                x1, x2, y1, y2 = x[:, :, :, 0, :], x[:, :, :, 1, :], y[:, :, :, 0, :], y[:, :, :, 1, :]
                c4, s4, u, w4 = cos[:, :, :, :], sin[:, :, :, :], tmp[:, :, :, :], tmp2[:, :, :, :]
                step(v.tensor_tensor(y1, x1, c4, ALU.mult))
                step(v.tensor_tensor(u, x2, s4, ALU.mult))
                step(v.tensor_tensor(y1, y1, u, ALU.subtract))
                step(v.tensor_tensor(w4, x1, s4, ALU.mult))
                step(v.tensor_tensor(y2, x2, c4, ALU.mult))
                v.tensor_tensor(y2, y2, w4, ALU.add).then_inc(rotated, 1)
            v.wait_ge(rotated, B)
            v.tensor_scalar(kd[:, :, :], rot[:, :, D:2 * D], k_decay[:, 0:1], None, ALU.mult).then_inc(kd_kept, 1)
            for g in range(4):
                v.wait_ge(q_kept, g + 1)
                v.tensor_tensor(qTd[:, g * 512:g * 512 + 512].rearrange("p (j n) -> p j n", j=4),
                                qT[:, g * 512:g * 512 + 512].rearrange("p (j n) -> p j n", j=4),
                                bc(q_decay[:, :].unsqueeze(1), [D, 4, P]), ALU.mult).then_inc(qd_kept, 1)
                v.wait_ge(turned, 2 * g + 2)
                v.tensor_copy(kT[:, g * 512:g * 512 + 512], ps[2 * g + 1][0:D, :]).then_inc(k_kept, 1)
            for g in range(4):
                v.wait_ge(scores_made, g + 1)
                v.tensor_tensor(probs[:, 4 * g:4 * g + 4, :], ps[2 * g][:, :].rearrange("p (j n) -> p j n", j=4),
                                bc(decay[:, :].unsqueeze(1), [P, 4, P]), ALU.mult).then_inc(probs_kept, 1)
            v.wait_ge(kv_made, 1)
            for c in range(1, TB):
                for b in range(B):
                    kv = ps[2 * b + 1][0:D, (c - 1) * D:c * D]
                    if c == 1:
                        step(v.tensor_copy(state[:, c, b, :], kv))
                    else:
                        step(v.scalar_tensor_tensor(state[:, c, b, :], state[:, c - 1, b, :], RET_GAMMA ** P,
                                                    kv, ALU.mult, ALU.add))
            v.engine_nop().then_inc(states_kept, 1)
            for b in range(B):
                v.wait_ge(out_made, b + 1)
                t = slice(b * TB, b * TB + TB)
                v.tensor_tensor(h[:, t, :], h[:, t, :],
                                ps[4 + 2 * b + 1][:, :].rearrange("p (t c) -> p t c", t=TB), ALU.add)


def retention_tables():
    c = {}
    inv_freq = (1.0 / np.float32(10000.0) ** (np.arange(0, D, 2, dtype=np.float32) / np.float32(D))).astype(np.float32)
    pos = np.arange(S, dtype=np.float32)
    ang = pos[:, None] * inv_freq[None, :]
    base = ((np.arange(0, D, 2, dtype=np.float32) + np.float32(0.4 * D)) / np.float32(1.4 * D)).astype(np.float32)
    scale = base[None, :] ** (pos[:, None] / np.float32(RET_SCALE_BASE))
    sin, cos = np.sin(ang), np.cos(ang)
    c["ret_cos"] = np.stack([cos * scale, cos / scale], 1).astype(np.float32)
    c["ret_sin"] = np.stack([sin * scale, sin / scale], 1).astype(np.float32)
    n = np.arange(P, dtype=np.float64)
    diff = n[None, :] - n[:, None]
    c["ret_decay"] = np.where(diff >= 0, RET_GAMMA ** np.maximum(diff, 0), 0.0).astype(np.float32)
    c["ret_k_decay"] = (RET_GAMMA ** (P - n))[:, None].astype(np.float32)
    c["ret_q_decay"] = (RET_GAMMA ** n)[None, :].astype(np.float32)
    return c


MAGIC = 12582912.0
SPLIT = 1536.0
TWO_PI = 6.2831850


def recurrence(nc, m, d):
    h, xT = m["h"], m["xT"]
    with Stage(nc, "rec") as s:
        w_in = s.sb("w_in", [D, 2, P])
        w_out = s.sb("w_out", [P, 2, D])
        par = s.sb("par", [P, 3])
        signs = s.sb("signs", [P, 2])
        ramp = s.sb("ramp", [P, S])
        mod = s.sb("mod", [P, 1])
        gam = s.sb("gam", [P, 1])
        turn = s.sb("turn", [P, 4])
        mod_row = s.sb("mod_row", [P, S])
        ang = s.sb("ang", [P, S])
        rnd = s.sb("rnd", [P, S])
        lo = s.sb("lo", [P, S])
        cosT = s.sb("cosT", [P, S])
        sinT = s.sb("sinT", [P, S])
        bx = s.sb("bx", [P, B, S])
        bx2 = s.sb("bx2", [P, B, S])
        g = s.sb("g", [P, B, S])
        gc = s.sb("gc", [P, B, S])
        gs = s.sb("gs", [P, B, S])
        loaded = s.sem("loaded")

        def load(sp):
            sp.dma_start(par[:, :], d["rec_par"]).then_inc(loaded, 16)
            sp.dma_start(signs[:, :], d["rec_signs"]).then_inc(loaded, 16)
            sp.dma_start(ramp[:, :], d["rec_ramp"].broadcast_to([P, S])).then_inc(loaded, 16)
            sp.dma_start(w_in[:, :, :], d["rec_w_in"]).then_inc(loaded, 16)
            sp.dma_start(w_out[:, :, :], d["rec_w_out"]).then_inc(loaded, 16)

        normalise(nc, m, "rec", load)
        ps = [s.ps(f"ps{k}", [P, 512]) for k in range(8)]
        acts = s.sem("act_step")
        dve = s.sem("dve_step")
        exps_ready = s.sem("exps_ready")
        angle_ready = s.sem("angle_ready")
        table_ready = s.sem("table_ready")
        bx_made = s.sem("bx_made")
        g_ready = s.sem("g_ready")
        out_made = s.sem("out_made")
        w_ready = s.sem("w_ready")
        block = s.block()
        LOADS = 5 * 16

        @block.scalar
        def _(a):
            step = Chain(a, acts)
            a.wait_ge(loaded, LOADS)
            step(a.activation(mod[:, :], par[:, 0:1], ACT.Exp))
            step(a.activation(mod[:, :], mod[:, :], ACT.Exp, scale=-1.0))
            a.activation(turn[:, 0:1], par[:, 1:2], ACT.Exp).then_inc(exps_ready, 1)
            a.activation(gam[:, :], par[:, 2:3], ACT.Exp).then_inc(exps_ready, 1)
            a.wait_ge(angle_ready, 1)
            a.activation(sinT[:, :], ang[:, :], ACT.Sin, scale=TWO_PI).then_inc(table_ready, 1)
            a.wait_ge(angle_ready, 2)
            a.activation(cosT[:, :], lo[:, :], ACT.Sin, scale=TWO_PI).then_inc(table_ready, 1)

        @block.tensor
        def _(pe):
            pe.wait_ge(loaded, LOADS)
            for k in range(4):
                for form in range(2):
                    last = pe.matmul(ps[2 * k + form][:, :], w_in[:, form, :], xT[0:D, k * 512:k * 512 + 512],
                                     start=True, stop=True)
            last.then_inc(bx_made, 1)
            pe.wait_ge(w_ready, 2)
            for b in range(B):
                pe.wait_ge(g_ready, b + 1)
                for j in range(TB):
                    o = ps[b][:, j * D:j * D + D]
                    pe.matmul(o, gc[:, b, j * P:j * P + P], w_out[:, 0, :], start=True, stop=False)
                    last = pe.matmul(o, gs[:, b, j * P:j * P + P], w_out[:, 1, :], start=False, stop=True)
                last.then_inc(out_made, 1)

        @block.vector
        def _(v):
            step = Chain(v, dve)
            v.wait_ge(loaded, LOADS)
            v.tensor_scalar(w_out[:, 0, :], w_out[:, 0, :], signs[:, 0:1], None, ALU.mult).then_inc(w_ready, 1)
            v.tensor_scalar(w_out[:, 1, :], w_out[:, 1, :], signs[:, 1:2], None, ALU.mult).then_inc(w_ready, 1)
            v.wait_ge(exps_ready, 2)
            step(v.tensor_scalar(turn[:, 0:1], turn[:, 0:1], 1.0 / (2 * np.pi), None, ALU.mult))
            step(v.tensor_scalar(turn[:, 1:2], turn[:, 0:1], MAGIC, MAGIC, ALU.add, ALU.subtract))
            step(v.tensor_tensor(turn[:, 0:1], turn[:, 0:1], turn[:, 1:2], ALU.subtract))
            step(v.tensor_scalar(turn[:, 2:3], turn[:, 0:1], SPLIT, SPLIT, ALU.add, ALU.subtract))
            step(v.tensor_tensor(turn[:, 3:4], turn[:, 0:1], turn[:, 2:3], ALU.subtract))
            step(v.tensor_scalar(ang[:, :], ramp[:, :], turn[:, 2:3], None, ALU.mult))
            step(v.tensor_scalar(rnd[:, :], ang[:, :], MAGIC, MAGIC, ALU.add, ALU.subtract))
            step(v.tensor_tensor(ang[:, :], ang[:, :], rnd[:, :], ALU.subtract))
            step(v.tensor_scalar(lo[:, :], ramp[:, :], turn[:, 3:4], None, ALU.mult))
            step(v.tensor_tensor(lo[:, :], ang[:, :], lo[:, :], ALU.add))
            step(v.tensor_scalar(rnd[:, :], lo[:, :], MAGIC, MAGIC, ALU.add, ALU.subtract))
            v.tensor_tensor(ang[:, :], lo[:, :], rnd[:, :], ALU.subtract).then_inc(angle_ready, 1)
            v.wait_ge(angle_ready, 1)
            step(v.tensor_scalar(lo[:, :], ang[:, :], 0.25, None, ALU.add))
            step(v.tensor_scalar(rnd[:, :], lo[:, :], MAGIC, MAGIC, ALU.add, ALU.subtract))
            v.tensor_tensor(lo[:, :], lo[:, :], rnd[:, :], ALU.subtract).then_inc(angle_ready, 1)
            step(v.memset(mod_row[:, :], 1.0))
            step(v.tensor_scalar(mod_row[:, :], mod_row[:, :], mod[:, 0:1], None, ALU.mult))
            v.wait_ge(table_ready, 2)
            step(v.tensor_scalar(sinT[:, :], sinT[:, :], signs[:, 0:1], None, ALU.mult))
            v.wait_ge(bx_made, 1)
            for b in range(B):
                for k in range(2):
                    c = slice(k * 512, k * 512 + 512)
                    step(v.scalar_tensor_tensor(bx[:, b, c], ps[4 * b + 2 * k][:, :], gam[:, 0:1], cosT[:, c],
                                                ALU.mult, ALU.mult))
                    step(v.scalar_tensor_tensor(bx2[:, b, c], ps[4 * b + 2 * k + 1][:, :], gam[:, 0:1], sinT[:, c],
                                                ALU.mult, ALU.mult))
                step(v.tensor_tensor(bx[:, b, :], bx[:, b, :], bx2[:, b, :], ALU.add))
            for b in range(B):
                step(v.tensor_tensor_scan(g[:, b, :], mod_row[:, :], bx[:, b, :], 0.0, ALU.mult, ALU.add))
                step(v.tensor_tensor(gc[:, b, :], g[:, b, :], cosT[:, :], ALU.mult))
                v.tensor_tensor(gs[:, b, :], g[:, b, :], sinT[:, :], ALU.mult).then_inc(g_ready, 1)
            for b in range(B):
                v.wait_ge(out_made, b + 1)
                t = slice(b * TB, b * TB + TB)
                v.tensor_tensor(h[:, t, :], h[:, t, :], ps[b][:, :].rearrange("p (t c) -> p t c", t=TB), ALU.add)


def recurrence_tables():
    c = {"rec_ramp": np.arange(S, dtype=np.float32)[None]}
    sg = np.ones((P, 2), np.float32)
    sg[D:, 0] = -1.0
    sg[:, 1] = -1.0
    sg[D:, 1] = 1.0
    c["rec_signs"] = sg
    return c


VOCAB = 64
SCALES = 4
CONV = ((7, 3), (5, 2), (3, 1))
PAIRS = TB // 2


def embed(nc, m, d):
    h, ident = m["h"], m["ident"]
    PAD1, PAD2, PAD3 = (p for _, p in CONV)
    with Stage(nc, "emb") as s:
        amps = s.sb("amps", [P, NT, D])
        scale4 = s.sb("scale4", [P, NT, SCALES])
        center = s.sb("center", [P, NT])
        shift = s.sb("shift", [P, NT])
        inv = s.sb("inv", [P, NT, SCALES])
        pos = s.sb("pos", [P, B, S])
        pos_loaded = s.sem("pos_loaded")
        with Stage(nc, "conv") as c:
            ids = c.sb("ids", [P, B, S], I32)
            vocab = c.sb("vocab", [P, 1])
            W1 = S + 2 * PAD1 + 1
            hot = c.sb("hot", [P, B, W1], BF16)
            w1_left = c.sb("w1_left", [P, 4, P])
            w1 = c.sb("w1", [P, 3, 4, P], BF16)
            w2 = c.sb("w2", [P, CONV[1][0], D])
            w3 = c.sb("w3", [D, CONV[2][0]])
            b1 = c.sb("b1", [P, 1])
            b2 = c.sb("b2", [D, 1])
            b3 = c.sb("b3", [P, 1])
            table_left = c.sb("table_left", [VOCAB, D + 4])
            table = c.sb("table", [VOCAB, 3, D + 4], BF16)
            widths = c.sb("widths", [P, SCALES])
            weights = c.sb("weights", [P, SCALES])
            where = c.sb("where", [P, NT])
            h1 = c.sb("h1", [P, B, S + 2 * PAD2])
            h2 = c.sb("h2", [D, B, S + 2 * PAD3])
            emb = c.sb("emb", [P, NT, D + 4])
            gate = c.sb("gate", [P, NT])
            amp = c.sb("amp", [P, NT])
            absw = c.sb("absw", [P, NT])
            ps = [c.ps(f"ps{k}", [P, 512]) for k in range(8)]
            names = ["split_loaded", "loaded", "hot_set", "hot_ready", "c1_made", "h1_kept", "c2_made", "h2_kept", "emb_made",
                     "emb_kept", "gate_made", "gate_kept", "amp_kept", "dve_step", "pads_set"]
            (split_loaded, loaded, hot_set, hot_ready, c1_made, h1_kept, c2_made, h2_kept, emb_made, emb_kept, gate_made,
             gate_kept, amp_kept, dve, pads_set) = [c.sem(n) for n in names]
            block = c.block()
            LOADS = 11 * 16

            @block.sync
            def _(sp):
                sp.dma_start(w1_left[:, :, :], d["emb_w1"]).then_inc(split_loaded, 16)
                sp.dma_start(table_left[:, :], d["emb_table"]).then_inc(split_loaded, 16)
                for half in range(2):
                    sp.dma_start(ids[half * D:half * D + D, :, :], d["ids"].unsqueeze(0).broadcast_to([D, B, S])
                                 ).then_inc(loaded, 16)
                for buf, name in ((w2, "emb_w2"), (w3, "emb_w3"), (b1, "emb_b1"), (b2, "emb_b2"), (vocab, "vocab2"), (where, "emb_where")):
                    sp.dma_start(buf[tuple([slice(None)] * len(buf.shape))], d[name]).then_inc(loaded, 16)
                for buf, name, n in ((b3, "emb_b3", 1), (widths, "emb_widths", SCALES),
                                     (weights, "emb_weights", SCALES)):
                    sp.dma_start(buf[:, :], d[name].broadcast_to([P, n])).then_inc(loaded, 16)
                sp.dma_start(pos[:, :, :], d["positions"].unsqueeze(0).broadcast_to([P, B, S])).then_inc(pos_loaded, 16)

            @block.gpsimd
            def _(g):
                for b in range(B):
                    g.memset(h1[:, b, 0:PAD2], 0.0)
                    g.memset(h1[:, b, PAD2 + S:], 0.0)
                    g.memset(h2[:, b, 0:PAD3], 0.0)
                    last = g.memset(h2[:, b, PAD3 + S:], 0.0)
                last.then_inc(pads_set, 1)

            @block.vector
            def _(v):
                step = Chain(v, dve)
                v.memset(hot[:, :, :], 0.0).then_inc(hot_set, 1)
                v.wait_ge(hot_set, 1)
                v.wait_ge(split_loaded, 32)
                for part in range(3):
                    step(v.tensor_copy(w1[:, part, :, :], w1_left[:, :, :]))
                    step(v.tensor_copy(table[:, part, :], table_left[:, :]))
                    if part < 2:
                        step(v.tensor_tensor(w1_left[:, :, :], w1_left[:, :, :], w1[:, part, :, :], ALU.subtract))
                        step(v.tensor_tensor(table_left[:, :], table_left[:, :], table[:, part, :], ALU.subtract))
                v.wait_ge(loaded, LOADS)
                v.tensor_scalar(hot[0:D, :, PAD1:PAD1 + S], ids[0:D, :, :], vocab[0:D, 0:1], None,
                                ALU.is_equal).then_inc(hot_ready, 1)
                v.tensor_scalar(hot[D:P, :, PAD1 - 1:PAD1 - 1 + S], ids[D:P, :, :], vocab[D:P, 0:1], None,
                                ALU.is_equal).then_inc(hot_ready, 1)
                for k in range(4):
                    v.wait_ge(emb_made, k + 1)
                    v.tensor_copy(emb[:, 4 * k:4 * k + 4, :],
                                  ps[k][:, 0:4 * (D + 4)].rearrange("p (t c) -> p t c", t=4)).then_inc(emb_kept, 1)
                v.wait_ge(emb_kept, 4)
                lp = [emb[:, :, D + k] for k in range(4)]
                step(v.scalar_tensor_tensor(center[:, :], lp[0], 0.05, where[:, :], ALU.mult, ALU.add))
                step(v.tensor_scalar(shift[:, :], lp[3], 0.5, 0.25, ALU.mult, ALU.add))
                step(v.scalar_tensor_tensor(absw[:, :], lp[1], -1.0, lp[1], ALU.mult, ALU.max))
                for k in range(SCALES):
                    step(v.tensor_scalar(inv[:, :, k], absw[:, :], widths[:, k:k + 1], None, ALU.mult))
                step(v.tensor_scalar(inv[:, :, :], inv[:, :, :], 1e-5, None, ALU.add))
                step(v.reciprocal(inv[:, :, :], inv[:, :, :]))
                step(v.tensor_tensor(weights[:, :], weights[:, :], weights[:, :], ALU.mult))
                v.wait_ge(amp_kept, 1)
                for k in range(SCALES):
                    step(v.tensor_scalar(scale4[:, :, k], amp[:, :], weights[:, k:k + 1], None, ALU.mult))
                v.wait_ge(gate_kept, 1)
                step(v.tensor_tensor(amps[:, :, :], emb[:, :, 0:D], bc(gate[:, :].unsqueeze(2), [P, NT, D]), ALU.mult))

            @block.tensor
            def _(pe):
                pe.wait_ge(hot_ready, 2)
                for t in range(NT):
                    b, j = t // TB, t % TB
                    for part in range(3):
                        mm = pe.matmul(ps[t // 4][:, (t % 4) * (D + 4):(t % 4 + 1) * (D + 4)],
                                       hot[0:D, b, PAD1 + j * P:PAD1 + j * P + P], table[:, part, :],
                                       start=(part == 0), stop=(part == 2))
                    if t % 4 == 3:
                        mm.then_inc(emb_made, 1)
                for k in range(4):
                    b, j = k // 2, (k % 2) * 512
                    for tap in range(4):
                        for part in range(3):
                            mm = pe.matmul(ps[4 + k][:, :], w1[:, part, tap, :],
                                           hot[:, b, j + 2 * tap:j + 2 * tap + 512],
                                           start=(tap == part == 0), stop=(tap == 3 and part == 2))
                    mm.then_inc(c1_made, 1)
                pe.wait_ge(emb_kept, 4)
                pe.wait_ge(pads_set, 1)
                for k in range(4):
                    b, j = k // 2, (k % 2) * 512
                    pe.wait_ge(h1_kept, 2 * (b + 1))
                    for tap in range(CONV[1][0]):
                        mm = pe.matmul(ps[k][0:D, :], w2[:, tap, :], h1[:, b, j + tap:j + tap + 512],
                                       start=(tap == 0), stop=(tap == CONV[1][0] - 1))
                    mm.then_inc(c2_made, 1)
                pe.wait_ge(h2_kept, 4)
                for t in range(NT):
                    b, j = t // TB, (t % TB) * P
                    for tap in range(CONV[2][0]):
                        mm = pe.matmul(ps[4][:, t:t + 1], h2[:, b, j + tap:j + tap + P], w3[:, tap:tap + 1],
                                       start=(tap == 0), stop=(tap == CONV[2][0] - 1))
                mm.then_inc(gate_made, 1)

            @block.scalar
            def _(a):
                for k in range(4):
                    b, j = k // 2, (k % 2) * 512
                    a.wait_ge(c1_made, k + 1)
                    a.activation(h1[:, b, PAD2 + j:PAD2 + j + 512], ps[4 + k][:, :], ACT.Gelu,
                                 bias=b1[:, 0:1]).then_inc(h1_kept, 1)
                for k in range(4):
                    b, j = k // 2, (k % 2) * 512
                    a.wait_ge(c2_made, k + 1)
                    a.activation(h2[:, b, PAD3 + j:PAD3 + j + 512], ps[k][0:D, :], ACT.Gelu,
                                 bias=b2[:, 0:1]).then_inc(h2_kept, 1)
                a.wait_ge(emb_kept, 4)
                a.activation(amp[:, :], emb[:, :, D + 2], ACT.Sigmoid).then_inc(amp_kept, 1)
                a.wait_ge(gate_made, 1)
                a.activation(gate[:, :], ps[4][:, 0:NT], ACT.Sigmoid, bias=b3[:, 0:1]).then_inc(gate_kept, 1)

        with Stage(nc, "field") as f:
            far = f.sb("far", [P, 2, 2, S])
            bell = f.sb("bell", [P, 2, 2, SCALES, S])
            wave = f.sb("wave", [P, 2, 2, SCALES, S])
            whole = f.sb("whole", [P, SCALES, S])
            amp4 = f.sb("amp4", [P, 2, 2, SCALES, P])
            fieldT = f.sb("fieldT", [D, T])
            ps = f.ps("ps", [P, 2 * B, 512])
            turned = [f.ps(f"turned{k}", [P, 4, D]) for k in range(4)]
            names = ["far_ready", "squares", "bells", "sines", "basis_ready", "pairs_done",
                     "amp_ready", "field_kept", "turned_ready", "whole_step", "whole_free"]
            (far_ready, squares, bells, sines, basis_ready, pairs_done, amp_ready, field_kept,
             turned_ready, whole_step, whole_free) = [f.sem(n) for n in names]
            block = f.block()
            N = PAIRS

            @block.vector
            def _(v):
                v.memset(amp4[:, :, :, :, D:P], 0.0)
                v.wait_ge(pos_loaded, 16)
                v.engine_nop().then_inc(pairs_done, 2)
                v.engine_nop().then_inc(whole_free, 1)
                with v.Fori(0, B) as b:
                    def angles(p):
                        r = p % 2
                        v.wait_ge(pairs_done, b * N + (p + 1))
                        for u in range(2):
                            t = b * TB + (2 * p + u)
                            v.tensor_scalar(far[:, r, u, :], pos[:, bass.ds(b, 1), :].rearrange("p b s -> p (b s)"),
                                            center[:, bass.ds(t, 1)], None, ALU.subtract).then_inc(far_ready, 1)
                            for k in range(SCALES):
                                v.tensor_scalar(amp4[:, r, u, k, 0:D], amps[:, bass.ds(t, 1), :].rearrange("p t c -> p (t c)"),
                                                scale4[:, bass.ds(t, 1), k], None, ALU.mult).then_inc(amp_ready, 1)
                            v.wait_ge(far_ready, b * (2 * N) + (2 * p + u + 1))
                            for k in range(SCALES):
                                w = v.tensor_scalar(wave[:, r, u, k, :], far[:, r, u, :], inv[:, bass.ds(t, 1), k],
                                                    shift[:, bass.ds(t, 1)], ALU.mult, ALU.add)
                            w.then_inc(whole_step, 1)
                            v.wait_ge(whole_step, b * (4 * N) + (4 * p + 2 * u + 1))
                            v.wait_ge(whole_free, b * (2 * N) + (2 * p + u + 1))
                            v.tensor_scalar(whole[:, :, :], wave[:, r, u, :, :], MAGIC, MAGIC, ALU.add,
                                            ALU.subtract).then_inc(whole_step, 1)
                            v.wait_ge(whole_step, b * (4 * N) + (4 * p + 2 * u + 2))
                            v.tensor_tensor(wave[:, r, u, :, :], wave[:, r, u, :, :], whole[:, :, :],
                                            ALU.subtract).then_inc(whole_free, 1)

                    for p in range(N):
                        angles(p)
                for k in range(4):
                    v.wait_ge(turned_ready, k + 1)
                    v.tensor_copy(h[:, 4 * k:4 * k + 4, :], turned[k][:, :, :])

            @block.gpsimd
            def _(g):
                with g.Fori(0, B) as b:
                    for p in range(N):
                        for u in range(2):
                            g.wait_ge(sines, b * (2 * N) + (2 * p + u + 1))
                            g.tensor_tensor(bell[:, p % 2, u, :, :], bell[:, p % 2, u, :, :], wave[:, p % 2, u, :, :],
                                            ALU.mult).then_inc(basis_ready, 1)

            @block.scalar
            def _(a):
                with a.Fori(0, B) as b:
                    for p in range(N):
                        r = p % 2
                        a.wait_ge(pairs_done, b * N + (p + 1))
                        for u in range(2):
                            t = b * TB + (2 * p + u)
                            a.wait_ge(far_ready, b * (2 * N) + (2 * p + u + 1))
                            for k in range(SCALES):
                                a.activation(bell[:, r, u, k, :], far[:, r, u, :], ACT.Square,
                                             scale=inv[:, bass.ds(t, 1), k]).then_inc(squares, 1)
                        for u in range(2):
                            a.wait_ge(squares, b * (8 * N) + (8 * p + 4 * u + 4))
                            a.activation(bell[:, r, u, :, :], bell[:, r, u, :, :], ACT.Exp,
                                         scale=-0.5).then_inc(bells, 1)
                        for u in range(2):
                            a.wait_ge(whole_free, b * (2 * N) + (2 * p + u + 2))
                            a.activation(wave[:, r, u, :, :], wave[:, r, u, :, :], ACT.Sin,
                                         scale=TWO_PI).then_inc(sines, 1)
                for k in range(2 * B):
                    a.wait_ge(pairs_done, (k // 2 + 1) * N + 2)
                    a.copy(fieldT[:, k * 512:k * 512 + 512], ps[0:D, k, :]).then_inc(field_kept, 1)

            @block.tensor
            def _(pe):
                pe.wait_ge(pos_loaded, 16)
                with pe.Fori(0, B) as b:
                    for p in range(N):
                        r = p % 2
                        pe.wait_ge(amp_ready, b * (8 * N) + (8 * p + 8))
                        for u in range(2):
                            pe.wait_ge(basis_ready, b * (2 * N) + (2 * p + u + 1))
                            for k in range(SCALES):
                                for q in range(2):
                                    mm = pe.matmul(ps[:, bass.ds(b * 2 + q, 1), :].rearrange("p b n -> p (b n)"), amp4[:, r, u, k, :],
                                                   bell[:, r, u, k, q * 512:q * 512 + 512],
                                                   start=(p == u == k == 0), stop=(p == N - 1 and u == 1 and k == SCALES - 1))
                        mm.then_inc(pairs_done, 1)
                for k in range(4):
                    pe.wait_ge(field_kept, k + 1)
                    for j in range(4):
                        last = pe.transpose(turned[k][:, j, :], fieldT[:, (4 * k + j) * P:(4 * k + j + 1) * P],
                                            ident[0:D, 0:D])
                    last.then_inc(turned_ready, 1)


def embed_tables():
    c = {"vocab2": np.concatenate([np.arange(VOCAB)] * 2).astype(np.float32)[:, None]}
    pos = np.linspace(0.0, 1.0, S, dtype=np.float32).reshape(TB, P).T
    c["emb_where"] = np.concatenate([pos, pos], 1)
    return c


TREE_DEPTH = 7
NODES = 2 ** (TREE_DEPTH + 1)
NODES_PER_BANK = 512 // D
NODE_CHUNKS = NODES // NODES_PER_BANK
BANKS = 8
RAWS = 4
SPLIT_COLS = 2048
SPLITS = NODES * D // SPLIT_COLS


def tree_ffn(nc, m, d):
    with Stage(nc, "tree") as s:
        own = {"gates": s.sb("gates", [P, NT, NODES]), "x": s.sb("x", [P, 2, T], BF16),
               "w": s.sb("w", [P, 3, NODES * D], BF16)}
        tree_gates(nc, m, own, d)
        tree_outputs(nc, m, own)


def tree_gates(nc, m, own, d):
    h, ident, xT, mask, x_parts, w_parts = (
        m["h"], m["ident"], m["xT"], own["gates"], own["x"], own["w"])
    with Stage(nc, "gate") as s:
        w1 = s.sb("w1", [D + 1, NODES])
        logits = s.sb("logits", [P, NT, NODES])
        right = s.sb("right", [P, NT, NODES], BF16)
        rest = s.sb("rest", [D, T])
        x2 = s.sb("x2", [D, T], BF16)
        raw = s.sb("raw", [P, RAWS, SPLIT_COLS])
        b2 = s.sb("b2", [P, 2, D])
        gT = logits[:, 0:4, :].rearrange("p t n -> p (t n)").rearrange("p (k j n) -> p k j n", k=2, j=4)
        loaded = s.sem("loaded")
        w_loaded = [s.sem(f"w_loaded{k}") for k in range(RAWS)]

        def load(sp):
            sp.dma_start(w1[:, :], d["tree_w1"]).then_inc(loaded, 16)
            sp.dma_start(b2[:, :, :], d["tree_b2"]).then_inc(loaded, 16)
            for k in range(RAWS):
                for half in range(2):
                    sp.dma_start(raw[half * D:half * D + D, k, :],
                                 d["tree_w2"][:, k * SPLIT_COLS:(k + 1) * SPLIT_COLS]).then_inc(w_loaded[k], 16)

        normalise(nc, m, "tree", load)
        ps = [s.ps(f"ps{k}", [P, 512]) for k in range(8)]
        names = ["gates_kept", "turned", "turn_kept", "bias_made", "logits_made", "logits_kept", "dve_step", "abs_kept", "gelu_kept", "gates_ready",
                 "x1_kept", "x2_kept", "x_rest", "part_kept", "part_left", "raw_used"]
        (gates_kept, turned, turn_kept, bias_made, logits_made, logits_kept, dve, abs_kept, gelu_kept, gates_ready, x1_kept, x2_kept, x_rest,
         part_kept, part_left, raw_used) = [s.sem(n) for n in names]
        block = s.block()

        @block.sync
        def _(sp):
            for k in range(RAWS, SPLITS):
                c = slice(k * SPLIT_COLS, (k + 1) * SPLIT_COLS)
                sp.wait_ge(raw_used, k - RAWS + 1)
                for half in range(2):
                    sp.dma_start(raw[half * D:half * D + D, k % RAWS, :],
                                 d["tree_w2"][:, c]).then_inc(w_loaded[k % RAWS], 16)

        @block.tensor
        def _(pe):
            pe.wait_ge(loaded, 32)
            for t in range(NT):
                last = pe.matmul(ps[t // 2][:, (t % 2) * NODES:(t % 2) * NODES + NODES],
                                 xT[:, t * P:t * P + P], w1[:, :], start=True, stop=True)
                if t % 2 == 1:
                    last.then_inc(logits_made, 1)
            pe.wait_ge(gates_kept, 1)
            for k in range(NT // 2 + 1):
                if k < NT // 2:
                    if k >= 2:
                        pe.wait_ge(turn_kept, k - 1)
                    for j in range(4):
                        mm = pe.transpose(ps[k % 2][:, j * P:j * P + P], mask[:, 2 * k + j // 2, j % 2 * P:j % 2 * P + P],
                                          ident[:, :])
                    mm.then_inc(turned, 1)
                if k > 0:
                    pe.wait_ge(turn_kept, k)
                    for j in range(2):
                        t = 2 * (k - 1) + j
                        for half in range(2):
                            mm = pe.matmul(ps[2 + t // TB][:, t % TB * D:t % TB * D + D],
                                           gT[:, (k - 1) % 2, 2 * j + half, :], b2[:, half, :],
                                           start=(half == 0), stop=(half == 1))
                    mm.then_inc(bias_made, 1)

        @block.scalar
        def _(a):
            def keep_turn(k):
                if 0 <= k < NT // 2:
                    a.wait_ge(turned, k + 1)
                    if k >= 2:
                        a.wait_ge(bias_made, k - 1)
                    a.copy(gT[:, k % 2, :, :], ps[k % 2][:, :].rearrange("p (j n) -> p j n", j=4)).then_inc(turn_kept, 1)

            def split(pair):
                chunks = [(k, slice(k * SPLIT_COLS, (k + 1) * SPLIT_COLS)) for k in (2 * pair, 2 * pair + 1)]
                for k, c in chunks:
                    a.wait_ge(w_loaded[k % RAWS], (k // RAWS + 1) * 32)
                    a.copy(w_parts[:, 0, c], raw[:, k % RAWS, :]).then_inc(part_kept, 1)
                keep_turn(3 * pair - 3)
                for k, c in chunks:
                    a.wait_ge(part_left, 4 * pair + k % 2 + 1)
                    a.copy(w_parts[:, 1, c], raw[:, k % RAWS, :]).then_inc(part_kept, 1)
                keep_turn(3 * pair - 2)
                for k, c in chunks:
                    a.wait_ge(part_left, 4 * pair + k % 2 + 3)
                    a.copy(w_parts[0:D, 2, c], raw[0:D, k % RAWS, :]).then_inc(raw_used, 1)
                keep_turn(3 * pair - 1)

            a.copy(x_parts[0:D, 0, :], xT[0:D, :]).then_inc(x1_kept, 1)
            split(0)
            for k in range(NT // 2):
                a.wait_ge(logits_made, k + 1)
                a.copy(logits[:, 2 * k:2 * k + 2, :],
                       ps[k][:, :].rearrange("p (t n) -> p t n", t=2)).then_inc(logits_kept, 1)
            a.wait_ge(x_rest, 1)
            a.copy(x2[:, :], rest[:, :]).then_inc(x2_kept, 1)
            a.copy(x_parts[D:P, 0, :], rest[:, :])
            a.wait_ge(gates_ready, 1)
            a.activation(logits[:, :, :], logits[:, :, :], ACT.Abs).then_inc(abs_kept, 1)
            a.wait_ge(abs_kept, 1)
            a.activation(logits[:, :, :], logits[:, :, :], ACT.Gelu).then_inc(gelu_kept, 1)
            a.wait_ge(x_rest, 2)
            a.copy(x_parts[D:P, 1, :], rest[:, :])
            for pair in range(1, SPLITS // 2):
                split(pair)

        @block.vector
        def _(v):
            step = Chain(v, dve)

            def split(pair):
                for part in range(2):
                    for k in (2 * pair, 2 * pair + 1):
                        c = slice(k * SPLIT_COLS, (k + 1) * SPLIT_COLS)
                        v.wait_ge(part_kept, 4 * pair + 2 * part + k % 2 + 1)
                        v.tensor_tensor(raw[:, k % RAWS, :], raw[:, k % RAWS, :], w_parts[:, part, c],
                                        ALU.subtract).then_inc(part_left, 1)
                        if part == 0:
                            v.tensor_copy(w_parts[D:P, 2, c], w_parts[D:P, 0, c])

            v.wait_ge(x1_kept, 1)
            v.tensor_tensor(rest[:, :], xT[0:D, :], x_parts[0:D, 0, :], ALU.subtract).then_inc(x_rest, 1)
            v.tensor_copy(x_parts[0:D, 1, :], x_parts[0:D, 0, :])
            split(0)
            v.wait_ge(logits_kept, NT // 2)
            step(v.tensor_scalar(right[:, :, :], logits[:, :, :], 0.0, None, ALU.is_gt))
            step(v.memset(mask[:, :, NODES - 1:NODES], 0.0))
            v.memset(mask[:, :, 0:1], 1.0).then_inc(gates_ready, 1)
            v.wait_ge(gates_ready, 1)
            for level in range(TREE_DEPTH):
                n = 2 ** level
                here = slice(n - 1, 2 * n - 1)
                kids = mask[:, :, 2 * n - 1:4 * n - 1].rearrange("p t (k c) -> p t k c", c=2)
                step(v.tensor_tensor(kids[:, :, :, 1], mask[:, :, here], right[:, :, here], ALU.mult))
                step(v.tensor_tensor(kids[:, :, :, 0], mask[:, :, here], kids[:, :, :, 1], ALU.subtract))
            v.wait_ge(gelu_kept, 1)
            v.tensor_tensor(mask[:, :, :], mask[:, :, :], logits[:, :, :], ALU.mult).then_inc(gates_kept, 1)
            v.wait_ge(x2_kept, 1)
            v.tensor_tensor(rest[:, :], rest[:, :], x2[:, :], ALU.subtract).then_inc(x_rest, 1)
            for pair in range(1, SPLITS // 2):
                split(pair)
            for b in range(B):
                v.wait_ge(bias_made, (b + 1) * NT // 4)
                t = slice(b * TB, b * TB + TB)
                v.tensor_tensor(h[:, t, :], h[:, t, :], ps[2 + b][:, :].rearrange("p (t c) -> p t c", t=TB), ALU.add)


def tree_outputs(nc, m, own):
    h, gates, x_parts, w_parts = m["h"], own["gates"], own["x"], own["w"]
    WIDE = NODES_PER_BANK * D
    PER = NODE_CHUNKS
    BY_ACT = [c for c in range(PER) if c % 3 == 1 and c < PER - 3]
    BY_VECTOR = [c for c in range(PER) if c not in BY_ACT]
    VECTOR = [c for c in BY_VECTOR if c % 3 == 2 or c >= PER - 8]
    POOL = [c for c in range(PER) if c not in VECTOR]
    HANDED = [c for c in POOL if c in BY_VECTOR]
    OWN = len(VECTOR) - 1
    HANDED_RING, ACT_RING = 4, 5
    assert len(HANDED) % HANDED_RING == 0 and len(BY_ACT) % ACT_RING == 0

    def used(t, order, chunks, c, ring):
        n = chunks.index(c) - ring
        return (t if n < 0 else t + 1) * len(order) + (order.index(chunks[n]) + 1)

    with Stage(nc, "treeo") as s:
        x_now = s.sb("x_now", [P, 2, 2, P], BF16)
        handed = s.sb("handed", [P, HANDED_RING, WIDE])
        by_act = s.sb("by_act", [P, ACT_RING, WIDE])
        mine = s.sb("mine", [P, 2, WIDE])
        acc = s.sb("acc", [P, WIDE])
        acc_v = s.sb("acc_v", [P, WIDE])
        out = s.sb("out", [P, D])
        act_spare = s.sb("act_spare", [P, 2])
        ps = [s.ps(f"ps{k}", [P, 512]) for k in range(BANKS)]
        names = ["x_kept", "bank_made", "weighed", "act_weighed", "added", "mine_added", "fold_step", "act_step"]
        x_kept, bank_made, weighed, act_weighed, added, mine_added, fold_step, act_step = [s.sem(n) for n in names]
        block = s.block()
        ALL = list(range(PER))

        def is_weighed(engine, t, c):
            order, sem = (BY_ACT, act_weighed) if c in BY_ACT else (BY_VECTOR, weighed)
            engine.wait_ge(sem, (t + 1) * len(order) + (order.index(c) + 1))

        def product(c):
            if c in BY_ACT:
                return by_act[:, BY_ACT.index(c) % ACT_RING, :]
            return handed[:, HANDED.index(c) % HANDED_RING, :]

        @block.tensor
        def _(pe):
            with pe.Fori(0, NT // 2) as i:
                for par in range(2):
                    t = i * 2 + par
                    pe.wait_ge(x_kept, t + 1)
                    for c in range(PER):
                        before = ALL[c - BANKS]
                        order, sem = (BY_ACT, act_weighed) if before in BY_ACT else (BY_VECTOR, weighed)
                        pe.wait_ge(sem, used(t, order, ALL, c, BANKS))
                        for k in range(3):
                            mm = pe.matmul(ps[c % BANKS][:, :], x_now[:, par, k // 2, :],
                                           w_parts[:, k, c * WIDE:(c + 1) * WIDE], start=(k == 0), stop=(k == 2))
                        mm.then_inc(bank_made, 1)

        @block.scalar
        def _(a):
            a.memzero(act_spare[:, 0:1]).then_inc(act_step, 1)
            a.wait_ge(act_step, 1)
            a.copy(act_spare[:, 1:2], act_spare[:, 0:1]).then_inc(act_weighed, len(BY_ACT))
            a.copy(x_now[:, 0, :, :], x_parts[:, :, 0:P]).then_inc(x_kept, 1)
            a.copy(x_now[:, 1, :, :], x_parts[:, :, P:2 * P]).then_inc(x_kept, 1)

            def weigh(t):
                for c in BY_ACT:
                    n = BY_ACT.index(c)
                    a.wait_ge(bank_made, t * PER + (c + 1))
                    a.wait_ge(added, used(t, POOL, BY_ACT, c, ACT_RING))
                    for k in range(NODES_PER_BANK):
                        node = c * NODES_PER_BANK + k
                        gate = gates[:, bass.ds(t, 1), node:node + 1].rearrange("p t n -> p (t n)")
                        last = a.activation(by_act[:, n % ACT_RING, k * D:k * D + D],
                                            ps[c % BANKS][:, k * D:k * D + D], ACT.Copy, scale=gate)
                    last.then_inc(act_weighed, 1)

            with a.Fori(0, NT // 2 - 1) as i:
                for par in range(2):
                    weigh(i * 2 + par)
                    a.wait_ge(bank_made, (i * 2 + (par + 1)) * PER)
                    a.copy(x_now[:, par, :, :], x_parts[:, :, bass.ds(i * (2 * P) + (par + 2) * P, P)]
                           ).then_inc(x_kept, 1)
            weigh(NT - 2)
            weigh(NT - 1)

        @block.vector
        def _(v):
            def nodes(ap):
                return ap.rearrange("p (n o) -> p n o", o=D)

            v.engine_nop().then_inc(weighed, len(BY_VECTOR))
            with v.Fori(0, NT // 2) as i:
                for par in range(2):
                    t = i * 2 + par

                    def add_own(n):
                        is_weighed(v, t, VECTOR[n])
                        if n > 1:
                            v.wait_ge(mine_added, i * (2 * OWN) + (par * OWN + n - 1))
                        v.tensor_tensor(acc_v[:, :], acc_v[:, :], mine[:, n % 2, :], ALU.add).then_inc(mine_added, 1)

                    pending = []
                    for c in BY_VECTOR:
                        gate = gates[:, bass.ds(t, 1), c * NODES_PER_BANK:(c + 1) * NODES_PER_BANK]
                        gate = gate.rearrange("p t n -> p (t n)").unsqueeze(2).broadcast_to([P, NODES_PER_BANK, D])
                        v.wait_ge(bank_made, t * PER + (c + 1))
                        if c in VECTOR:
                            n = VECTOR.index(c)
                            if n > 2:
                                v.wait_ge(mine_added, i * (2 * OWN) + (par * OWN + n - 2))
                            dst = acc_v[:, :] if n == 0 else mine[:, n % 2, :]
                        else:
                            v.wait_ge(added, used(t, POOL, HANDED, c, HANDED_RING))
                            dst = product(c)
                        v.tensor_tensor(nodes(dst), nodes(ps[c % BANKS][:, :]), gate, ALU.mult).then_inc(weighed, 1)
                        while pending:
                            add_own(pending.pop())
                        if c in VECTOR and n > 0:
                            pending.append(n)
                    add_own(pending.pop())
                    v.wait_ge(added, (t + 2) * len(POOL))
                    v.wait_ge(mine_added, (i * 2 + (par + 1)) * OWN)
                    v.tensor_tensor(acc_v[:, :], acc_v[:, :], acc[:, :], ALU.add).then_inc(fold_step, 1)
                    v.wait_ge(fold_step, i * 6 + (par * 3 + 1))
                    v.tensor_reduce(out[:, :], acc_v[:, :].rearrange("p (n o) -> p o n", o=D), AX.X,
                                    ALU.add).then_inc(fold_step, 1)
                    v.wait_ge(fold_step, i * 6 + (par * 3 + 2))
                    now = h[:, bass.ds(t, 1), :].rearrange("p t c -> p (t c)")
                    v.tensor_tensor(now, now, out[:, :], ALU.add).then_inc(fold_step, 1)
                    v.wait_ge(fold_step, i * 6 + (par * 3 + 3))

        @block.gpsimd
        def _(g):
            g.engine_nop().then_inc(added, len(POOL))
            with g.Fori(0, NT // 2) as i:
                for par in range(2):
                    t = i * 2 + par
                    is_weighed(g, t, POOL[0])
                    is_weighed(g, t, POOL[1])
                    g.tensor_tensor(acc[:, :], product(POOL[0]), product(POOL[1]), ALU.add).then_inc(added, 2)
                    for n in range(2, len(POOL)):
                        is_weighed(g, t, POOL[n])
                        g.wait_ge(added, (t + 1) * len(POOL) + n)
                        g.tensor_tensor(acc[:, :], acc[:, :], product(POOL[n]), ALU.add).then_inc(added, 1)


GROUPS = 4


def run_experts(nc, m, d, name, per_group, gates, add_x):
    h, xn, xT = m["h"], m["xn"], m["xT"]
    E = GROUPS * per_group
    HID = P // per_group
    with Stage(nc, name) as s:
        w1 = s.sb("w1", [D + 1, GROUPS, P])
        w2 = s.sb("w2", [P, GROUPS, D])
        b2 = s.sb("b2", [P, E, D])
        hid = s.sb("hid", [P, 2, GROUPS, 512])
        y = s.sb("y", [P, 2, E, D])
        yg = s.sb("yg", [P, 2, E, D])
        total = s.sb("total", [P, 2, D])
        ps_h = [s.ps(f"ps_h{k}", [P, 512]) for k in range(4)]
        ps_y = [[s.ps(f"ps_y{k}_{r}", [P, 512]) for r in range(per_group)] for k in range(2)]
        loaded = s.sem("loaded")
        hid_made = s.sem("hid_made")
        hid_kept = s.sem("hid_kept")
        y_made = s.sem("y_made")
        y_kept = s.sem("y_kept")
        dve = s.sem("dve_step")
        block = s.block()

        @block.sync
        def _(sp):
            sp.dma_start(w1[:, :, :], d[f"{name}_w1"]).then_inc(loaded, 16)
            sp.dma_start(w2[:, :, :], d[f"{name}_w2"]).then_inc(loaded, 16)
            sp.dma_start(b2[:, :, :], d[f"{name}_b2"].broadcast_to([P, E, D])).then_inc(loaded, 16)

        @block.tensor
        def _(pe):
            pe.wait_ge(loaded, 3 * 16)

            def hidden(k):
                for g in range(GROUPS):
                    if k >= 1:
                        pe.wait_ge(hid_kept, (k - 1) * GROUPS + g + 1)
                    pe.matmul(ps_h[g][:, :], w1[:, g, :], xT[:, k * 512:k * 512 + 512],
                              start=True, stop=True).then_inc(hid_made, 1)

            hidden(0)
            for k in range(4):
                if k < 3:
                    hidden(k + 1)
                pe.wait_ge(hid_kept, (k + 1) * GROUPS)
                for j in range(4):
                    t = 4 * k + j
                    if t >= 2:
                        pe.wait_ge(y_kept, t - 1)
                    for e in range(E):
                        g, r = e // per_group, (e % per_group) * HID
                        mm = pe.matmul(ps_y[t % 2][e % per_group][:, g * D:g * D + D],
                                       hid[r:r + HID, k % 2, g, j * P:j * P + P], w2[r:r + HID, g, :],
                                       start=True, stop=True)
                    mm.then_inc(y_made, 1)

        @block.scalar
        def _(a):
            for k in range(4):
                for g in range(GROUPS):
                    a.wait_ge(hid_made, k * GROUPS + g + 1)
                    if k >= 2:
                        a.wait_ge(y_made, 4 * (k - 1))
                    a.activation(hid[:, k % 2, g, :], ps_h[g][:, :], ACT.Gelu).then_inc(hid_kept, 1)

        @block.vector
        def _(v):
            step = Chain(v, dve)
            v.wait_ge(loaded, 3 * 16)
            for t in range(NT):
                r = t % 2
                v.wait_ge(y_made, t + 1)
                for q in range(per_group):
                    mine = y[:, r, :, :].rearrange("p (g q) o -> p g q o", q=per_group)[:, :, q, :]
                    add = v.tensor_tensor(mine, ps_y[r][q][:, 0:GROUPS * D].rearrange("p (g o) -> p g o", g=GROUPS),
                                          b2[:, :, :].rearrange("p (g q) o -> p g q o", q=per_group)[:, :, q, :],
                                          ALU.add)
                add.then_inc(y_kept, 1)
                v.wait_ge(y_kept, t + 1)
                step(v.tensor_tensor(yg[:, r, :, :], y[:, r, :, :], bc(gates[:, t, :].unsqueeze(2), [P, E, D]),
                                     ALU.mult))
                step(v.tensor_reduce(total[:, r, :], yg[:, r, :, :].rearrange("p e o -> p o e"), AX.X, ALU.add))
                step(v.tensor_tensor(h[:, t, :], h[:, t, :], total[:, r, :], ALU.add))
            if add_x:
                v.tensor_tensor(h[:, :, :], h[:, :, :], xn[:, :, :], ALU.add)


def experts_eight(nc, m, d):
    xT = m["xT"]
    E = 8
    with Stage(nc, "route8") as outer:
        gates = outer.sb("gates", [P, NT, E])
        with Stage(nc, "route") as s:
            w = s.sb("w", [D, E])
            order = s.sb("order", [P, E])
            probs = s.sb("probs", [P, NT, E])
            best = [s.sb(f"best{k}", [P, NT]) for k in range(2)]
            picks = [s.sb(f"pick{k}", [P, NT, E]) for k in range(2)]
            rest = s.sb("rest", [P, NT, E])
            eq = s.sb("eq", [P, NT, E])
            one = s.sb("one", [P, NT])
            loaded = s.sem("loaded")

            def load(sp):
                sp.dma_start(w[:, :], d["route8_w"]).then_inc(loaded, 16)
                sp.dma_start(order[:, :], d["order8"].broadcast_to([P, E])).then_inc(loaded, 16)

            normalise(nc, m, "route8", load)
            ps = s.ps("ps", [P, NT, E])
            made = s.sem("made")
            dve = s.sem("dve_step")
            centred = s.sem("centred")
            exps = s.sem("exps")
            block = s.block()

            @block.tensor
            def _(pe):
                pe.wait_ge(loaded, 32)
                for t in range(NT):
                    mm = pe.matmul(ps[:, t, :], xT[0:D, t * P:t * P + P], w[:, :], start=True, stop=True)
                mm.then_inc(made, 1)

            @block.scalar
            def _(a):
                a.wait_ge(centred, 1)
                a.activation(probs[:, :, :], probs[:, :, :], ACT.Exp).then_inc(exps, 1)

            @block.vector
            def _(v):
                step = Chain(v, dve)
                v.wait_ge(loaded, 32)
                v.wait_ge(made, 1)
                wide = [P, NT, E]
                step(v.tensor_reduce(one[:, :], ps[:, :, :], AX.X, ALU.max))
                v.tensor_tensor(probs[:, :, :], ps[:, :, :], bc(one[:, :].unsqueeze(2), wide),
                                ALU.subtract).then_inc(centred, 1)
                v.wait_ge(exps, 1)
                step(v.tensor_reduce(one[:, :], probs[:, :, :], AX.X, ALU.add))
                step(v.reciprocal(one[:, :], one[:, :]))
                step(v.tensor_tensor(probs[:, :, :], probs[:, :, :], bc(one[:, :].unsqueeze(2), wide), ALU.mult))
                two_best(v, step, probs, best, rest, eq, picks, order, E)
                step(v.tensor_tensor(one[:, :], best[0][:, :], best[1][:, :], ALU.add))
                step(v.tensor_scalar(one[:, :], one[:, :], 1e-12, None, ALU.max))
                step(v.reciprocal(one[:, :], one[:, :]))
                step(v.tensor_tensor(gates[:, :, :], picks[0][:, :, :], picks[1][:, :, :], ALU.add))
                step(v.tensor_tensor(gates[:, :, :], gates[:, :, :], probs[:, :, :], ALU.mult))
                step(v.tensor_tensor(gates[:, :, :], gates[:, :, :], bc(one[:, :].unsqueeze(2), wide), ALU.mult))
        run_experts(nc, m, d, "moe8", 2, gates, True)


def two_best(v, step, values, best, rest, eq, picks, order, n):
    wide = [P, NT, n]
    row = bc(order[:, 0:n].unsqueeze(1), wide)
    left = values
    for k in range(2):
        step(v.tensor_reduce(best[k][:, :], left[:, :, :], AX.X, ALU.max))
        step(v.tensor_tensor(eq[:, :, :], left[:, :, :], bc(best[k][:, :].unsqueeze(2), wide), ALU.is_equal))
        step(v.tensor_tensor(eq[:, :, :], eq[:, :, :], row, ALU.mult))
        step(v.tensor_reduce(rest[:, :, 0], eq[:, :, :], AX.X, ALU.max))
        step(v.tensor_tensor(picks[k][:, :, :], row, bc(rest[:, :, 0:1], wide), ALU.is_equal))
        if k == 0:
            left = picks[1]
            step(v.scalar_tensor_tensor(left[:, :, :], picks[0][:, :, :], -1e30, values[:, :, :],
                                        ALU.mult, ALU.add))


HAAR_LEVELS = 3
HAAR = 2 ** HAAR_LEVELS - 1
NEG = -1e30


def wavelet_attention(nc, m, d):
    h, xT, ident, inv_wT = m["h"], m["xT"], m["ident"], m["inv_wT"]
    HALF = D // 2
    with Stage(nc, "wav") as s:
        w = s.sb("w", [D, 3 * D])
        w_v = s.sb("w_v", [D, D])
        w_oT = s.sb("w_oT", [D, D])
        cos = s.sb("cos", [P, TB, 2, HALF])
        sin = s.sb("sin", [P, TB, 2, HALF])
        haar = s.sb("haar", [P, TB, HAAR])
        haar_blockT = s.sb("haar_blockT", [HAAR, TB])
        count = s.sb("count", [P, TB, TB])
        hide = s.sb("hide", [P, TB, TB])
        before = s.sb("before", [P, TB, TB])
        seen = s.sb("seen", [P, TB, 2])
        earlier = s.sb("earlier", [P, P])
        one_block = s.sb("one_block", [P, TB, TB])
        qkv = s.sb("qkv", [P, NT, 3 * D])
        rot = s.sb("rot", [P, NT, 2 * D])
        tmp = s.sb("tmp", [P, TB, 2, HALF])
        tmp2 = s.sb("tmp2", [P, TB, 2, HALF])
        square = s.sb("square", [P, NT, 2 * D])
        norm = s.sb("norm", [P, NT, 2])
        inv_norm = s.sb("inv_norm", [P, NT, 2])
        coef = s.sb("coef", [HAAR, B, 2 * D])
        qf = s.sb("qf", [D, B, TB])
        kf = s.sb("kf", [D, B, TB])
        qf_wide = s.sb("qf_wide", [D, B, TB, P])
        blocksum = s.sb("blocksum", [TB, B, D])
        z = s.sb("z", [P, NT, TB])
        e = s.sb("e", [P, NT, TB])
        zsq = s.sb("zsq", [P, NT, TB])
        own = s.sb("own", [P, NT])
        e_own = s.sb("e_own", [P, NT])
        stat = s.sb("stat", [P, NT])
        aux = s.sb("aux", [P, NT])
        var = s.sb("var", [P, NT])
        std = s.sb("std", [P, NT])
        den = s.sb("den", [P, NT])
        eT = s.sb("eT", [TB, NT, P])
        y = s.sb("y", [P, NT, D])
        y2 = s.sb("y2", [P, NT, D])
        loaded = s.sem("loaded")

        def load(sp):
            sp.dma_start(w[:, 0:D], d["near_w_q"]).then_inc(loaded, 16)
            sp.dma_start(w_v[:, :], d["near_w_v"]).then_inc(loaded, 16)
            sp.dma_start(w_oT[:, :], d["near_w_oT"]).then_inc(loaded, 16)
            sp.dma_start(cos[:, :, :, :], d["wav_cos"].rearrange("(t p) a c -> p t a c", p=P)).then_inc(loaded, 16)
            sp.dma_start(sin[:, :, :, :], d["wav_sin"].rearrange("(t p) a c -> p t a c", p=P)).then_inc(loaded, 16)
            sp.dma_start(haar[:, :, :], d["wav_haar"].rearrange("(t p) w -> p t w", p=P)).then_inc(loaded, 16)
            sp.dma_start(haar_blockT[:, :], d["wav_haar_blockT"]).then_inc(loaded, 16)
            sp.dma_start(count[:, :, :], d["wav_count"]).then_inc(loaded, 16)
            sp.dma_start(hide[:, :, :], d["wav_hide"]).then_inc(loaded, 16)
            sp.dma_start(seen[:, :, :], d["wav_seen"]).then_inc(loaded, 16)
            sp.dma_start(earlier[:, :], d["wav_earlier"]).then_inc(loaded, 16)
            sp.dma_start(before[:, :, :], d["wav_before"]).then_inc(loaded, 16)

        normalise(nc, m, "wav", load)
        ps = [s.ps(f"ps{k}", [P, 512]) for k in range(8)]
        names = ["fold_made", "w_ready", "qkv_made", "qkv_kept", "norm_sq", "norm_root", "rot_ready",
                 "coef_made", "coef_kept", "f_made", "f_kept", "score_made", "var_ready", "std_ready", "z_ready",
                 "e_ready", "far_ready", "eT_made", "eT_kept", "sum_kept", "pre_made", "far_made", "blocksum_kept"]
        (fold_made, w_ready, qkv_made, qkv_kept, norm_sq, norm_root, rot_ready, coef_made, coef_kept,
         f_made, f_kept, score_made, var_ready, std_ready, z_ready, e_ready, far_ready, eT_made, eT_kept,
         sum_kept, pre_made, far_made, blocksum_kept) = [s.sem(n) for n in names]
        dve = s.sem("dve_step")
        block = s.block()
        LOADS = 12 * 16

        @block.gpsimd
        def _(g):
            g.memset(one_block[:, :, :], 0.0).then_inc(sum_kept, 1)
            g.wait_ge(sum_kept, 1)
            for j in range(TB):
                last = g.memset(one_block[:, j, j:j + 1], 1.0)
            last.then_inc(sum_kept, 1)

        @block.tensor
        def _(pe):
            pe.wait_ge(loaded, LOADS)
            pe.matmul(ps[0][0:D, 0:D], w_v[:, :], w_oT[:, :], start=True, stop=True).then_inc(fold_made, 1)
            pe.wait_ge(w_ready, 2)
            for t in range(NT):
                last = pe.matmul(ps[t // 2][:, (t % 2) * 192:(t % 2) * 192 + 192], xT[0:D, t * P:t * P + P],
                                 w[:, :], start=True, stop=True)
                if t % 2 == 1:
                    last.then_inc(qkv_made, 1)
            pe.wait_ge(qkv_kept, NT // 2)
            pe.wait_ge(sum_kept, 2)
            for b in range(B):
                for j in range(TB):
                    t = b * TB + j
                    last = pe.matmul(ps[4 + b][:, j * D:j * D + D], earlier[:, :], qkv[:, t, 2 * D:3 * D],
                                     start=True, stop=True)
            last.then_inc(pre_made, 1)
            for b in range(B):
                for j in range(TB):
                    t = b * TB + j
                    last = pe.matmul(ps[6][0:TB, b * D:b * D + D], one_block[:, j, :], qkv[:, t, 2 * D:3 * D],
                                     start=(j == 0), stop=(j == TB - 1))
            last.then_inc(pre_made, 1)
            pe.wait_ge(rot_ready, 1)
            for b in range(B):
                for j in range(TB):
                    t = b * TB + j
                    last = pe.matmul(ps[b][0:HAAR, 0:2 * D], haar[:, j, :], rot[:, t, :],
                                     start=(j == 0), stop=(j == TB - 1))
            last.then_inc(coef_made, 1)
            pe.wait_ge(coef_kept, 1)
            for b in range(B):
                for qk in range(2):
                    last = pe.matmul(ps[2][0:D, (2 * b + qk) * TB:(2 * b + qk + 1) * TB],
                                     coef[:, b, qk * D:qk * D + D], haar_blockT[:, :], start=True, stop=True)
            last.then_inc(f_made, 1)
            pe.wait_ge(f_kept, 1)
            for b in range(B):
                for i in range(TB):
                    t = b * TB + i
                    last = pe.matmul(ps[3][:, t * TB:t * TB + TB], qf_wide[:, b, i, :], kf[:, b, :],
                                     start=True, stop=True)
            last.then_inc(score_made, 1)
            pe.wait_ge(far_ready, 1)
            for k in range(4):
                for j in range(4):
                    t = 4 * k + j
                    last = pe.transpose(ps[k][0:TB, j * P:j * P + P], z[:, t, :], ident[:, :])
                last.then_inc(eT_made, 1)
            pe.wait_ge(eT_kept, 4)
            pe.wait_ge(blocksum_kept, 1)
            for b in range(B):
                for j in range(TB):
                    t = b * TB + j
                    last = pe.matmul(ps[b][:, j * D:j * D + D], eT[:, t, :], blocksum[:, b, :],
                                     start=True, stop=True)
            last.then_inc(far_made, 1)

        @block.scalar
        def _(a):
            for k in range(NT // 2):
                a.wait_ge(qkv_made, k + 1)
                a.copy(qkv[:, 2 * k:2 * k + 2, :],
                       ps[k][:, 0:384].rearrange("p (t c) -> p t c", t=2)).then_inc(qkv_kept, 1)
            a.wait_ge(norm_sq, 1)
            a.activation(norm[:, :, :], norm[:, :, :], ACT.Sqrt).then_inc(norm_root, 1)
            a.wait_ge(var_ready, 1)
            a.activation(std[:, :], var[:, :], ACT.Sqrt).then_inc(std_ready, 1)
            a.wait_ge(z_ready, 1)
            a.activation(e[:, :, :], z[:, :, :], ACT.Exp).then_inc(e_ready, 1)
            a.activation(e_own[:, :], own[:, :], ACT.Exp).then_inc(e_ready, 1)
            for k in range(4):
                a.wait_ge(eT_made, k + 1)
                a.copy(eT[:, 4 * k:4 * k + 4, :],
                       ps[k][0:TB, :].rearrange("p (t c) -> p t c", t=4)).then_inc(eT_kept, 1)

        @block.vector
        def _(v):
            step = Chain(v, dve)
            v.wait_ge(fold_made, 1)
            v.tensor_copy(w[:, 2 * D:3 * D], ps[0][0:D, 0:D]).then_inc(w_ready, 1)
            v.tensor_copy(w[:, D:2 * D], inv_wT[:, :]).then_inc(w_ready, 1)
            for b in range(B):
                v.wait_ge(qkv_kept, TB // 2 * (b + 1))
                t = slice(b * TB, b * TB + TB)
                x = qkv[:, t, 0:2 * D].rearrange("p t (a e c) -> p t a e c", a=2, e=2)
                r = rot[:, t, :].rearrange("p t (a e c) -> p t a e c", a=2, e=2)
                x1, x2, r1, r2 = x[:, :, :, 0, :], x[:, :, :, 1, :], r[:, :, :, 0, :], r[:, :, :, 1, :]
                c4, s4, u, w4 = cos[:, :, :, :], sin[:, :, :, :], tmp[:, :, :, :], tmp2[:, :, :, :]
                step(v.tensor_tensor(r1, x1, c4, ALU.mult))
                step(v.tensor_tensor(u, x2, s4, ALU.mult))
                step(v.tensor_tensor(r1, r1, u, ALU.subtract))
                step(v.tensor_tensor(w4, x1, s4, ALU.mult))
                step(v.tensor_tensor(r2, x2, c4, ALU.mult))
                step(v.tensor_tensor(r2, r2, w4, ALU.add))
            step(v.tensor_tensor(square[:, :, :], rot[:, :, :], rot[:, :, :], ALU.mult))
            v.tensor_reduce(norm[:, :, :], square[:, :, :].rearrange("p t (a c) -> p t a c", a=2), AX.X,
                            ALU.add).then_inc(norm_sq, 1)
            v.wait_ge(norm_root, 1)
            step(v.tensor_scalar(norm[:, :, :], norm[:, :, :], 1e-8, None, ALU.add))
            step(v.reciprocal(inv_norm[:, :, :], norm[:, :, :]))
            v.tensor_tensor(rot[:, :, :].rearrange("p t (a c) -> p t a c", a=2),
                            rot[:, :, :].rearrange("p t (a c) -> p t a c", a=2),
                            bc(inv_norm[:, :, :].unsqueeze(3), [P, NT, 2, D]), ALU.mult).then_inc(rot_ready, 1)
            v.wait_ge(rot_ready, 1)
            step(v.tensor_tensor(square[:, :, 0:D], rot[:, :, 0:D], rot[:, :, D:2 * D], ALU.mult))
            step(v.tensor_reduce(own[:, :], square[:, :, 0:D], AX.X, ALU.add))
            v.wait_ge(coef_made, 1)
            for b in range(B):
                last = v.tensor_copy(coef[:, b, :], ps[b][0:HAAR, 0:2 * D])
            last.then_inc(coef_kept, 1)
            v.wait_ge(f_made, 1)
            both = ps[2][0:D, 0:2 * B * TB].rearrange("p (b a i) -> p b a i", b=B, a=2)
            step(v.tensor_copy(qf[:, :, :], both[:, :, 0, :]))
            step(v.tensor_copy(kf[:, :, :], both[:, :, 1, :]))
            v.tensor_copy(qf_wide[:, :, :, :].rearrange("p b i n -> p (b i) n"),
                          bc(qf[:, :, :].rearrange("p b i -> p (b i)").unsqueeze(2),
                             [D, B * TB, P])).then_inc(f_kept, 1)
            v.wait_ge(score_made, 1)

            def per_batch(ap):
                return ap.rearrange("p (b t) j -> p b (t j)", b=B)

            def twice(table):
                return bc(table.rearrange("p t j -> p (t j)").unsqueeze(1), [P, B, TB * TB])

            def rows(ap):
                return ap.rearrange("p (b t) -> p b t", b=B)

            def seen_by(k):
                return bc(seen[:, :, k].unsqueeze(1), [P, B, TB])

            def wide(ap):
                return bc(ap[:, :].unsqueeze(2), [P, NT, TB])

            step(v.tensor_copy(zsq[:, :, :], ps[3][:, 0:NT * TB].rearrange("p (t j) -> p t j", t=NT)))
            step(v.tensor_tensor(rows(own[:, :]), rows(own[:, :]), seen_by(0), ALU.mult))
            for b in range(B):
                t = slice(b * TB, b * TB + TB)
                step(v.tensor_tensor(z[:, t, :], zsq[:, t, :], bc(seen[:, :, 0:1], [P, TB, TB]), ALU.mult))
            step(v.tensor_tensor(per_batch(zsq[:, :, :]), per_batch(z[:, :, :]), twice(count[:, :, :]), ALU.mult))
            step(v.tensor_reduce(stat[:, :], zsq[:, :, :], AX.X, ALU.add))
            step(v.tensor_tensor(stat[:, :], stat[:, :], own[:, :], ALU.add))
            step(v.tensor_tensor(rows(stat[:, :]), rows(stat[:, :]), seen_by(1), ALU.mult))
            step(v.tensor_tensor(z[:, :, :], z[:, :, :], wide(stat), ALU.subtract))
            step(v.tensor_tensor(own[:, :], own[:, :], stat[:, :], ALU.subtract))
            step(v.tensor_tensor(zsq[:, :, :], z[:, :, :], z[:, :, :], ALU.mult))
            step(v.tensor_tensor(per_batch(zsq[:, :, :]), per_batch(zsq[:, :, :]), twice(count[:, :, :]), ALU.mult))
            step(v.tensor_reduce(stat[:, :], zsq[:, :, :], AX.X, ALU.add))
            step(v.tensor_tensor(aux[:, :], own[:, :], own[:, :], ALU.mult))
            step(v.tensor_tensor(stat[:, :], stat[:, :], aux[:, :], ALU.add))
            step(v.tensor_tensor(rows(var[:, :]), rows(stat[:, :]), seen_by(1), ALU.mult))
            v.wait_ge(dve, step.count)
            v.tensor_scalar(var[:, :], var[:, :], 1e-6, None, ALU.max).then_inc(var_ready, 1)
            v.wait_ge(std_ready, 1)
            step(v.reciprocal(stat[:, :], std[:, :]))
            step(v.tensor_tensor(z[:, :, :], z[:, :, :], wide(stat), ALU.mult))
            step(v.tensor_tensor(own[:, :], own[:, :], stat[:, :], ALU.mult))
            step(v.tensor_tensor(per_batch(z[:, :, :]), per_batch(z[:, :, :]), twice(hide[:, :, :]), ALU.add))
            step(v.tensor_reduce(stat[:, :], z[:, :, :], AX.X, ALU.max))
            step(v.tensor_tensor(stat[:, :], stat[:, :], own[:, :], ALU.max))
            step(v.tensor_tensor(own[:, :], own[:, :], stat[:, :], ALU.subtract))
            v.tensor_tensor(z[:, :, :], z[:, :, :], wide(stat), ALU.subtract).then_inc(z_ready, 1)
            v.wait_ge(e_ready, 2)
            step(v.tensor_tensor(per_batch(zsq[:, :, :]), per_batch(e[:, :, :]), twice(count[:, :, :]), ALU.mult))
            step(v.tensor_reduce(den[:, :], zsq[:, :, :], AX.X, ALU.add))
            v.tensor_tensor(per_batch(z[:, :, :]), per_batch(e[:, :, :]), twice(before[:, :, :]),
                            ALU.mult).then_inc(far_ready, 1)
            step(v.tensor_tensor(den[:, :], den[:, :], e_own[:, :], ALU.add))
            step(v.reciprocal(den[:, :], den[:, :]))
            v.wait_ge(pre_made, 2)
            v.tensor_copy(blocksum[:, :, :], ps[6][0:TB, 0:B * D].rearrange("p (b o) -> p b o", b=B)).then_inc(blocksum_kept, 1)
            for b in range(B):
                diag = e[:, b * TB:b * TB + TB, :].rearrange("p t j -> p (t j)")[:, 0:TB * TB:TB + 1]
                t = slice(b * TB, b * TB + TB)
                step(v.tensor_tensor(y[:, t, :], ps[4 + b][:, :].rearrange("p (t o) -> p t o", t=TB),
                                     bc(diag.unsqueeze(2), [P, TB, D]), ALU.mult))
            step(v.tensor_tensor(y2[:, :, :], qkv[:, :, 2 * D:3 * D], bc(e_own[:, :].unsqueeze(2), [P, NT, D]), ALU.mult))
            step(v.tensor_tensor(y[:, :, :], y[:, :, :], y2[:, :, :], ALU.add))
            v.wait_ge(far_made, 1)
            for b in range(B):
                t = slice(b * TB, b * TB + TB)
                step(v.tensor_tensor(y[:, t, :], y[:, t, :], ps[b][:, :].rearrange("p (t o) -> p t o", t=TB), ALU.add))
            step(v.tensor_tensor(y[:, :, :], y[:, :, :], bc(den[:, :].unsqueeze(2), [P, NT, D]), ALU.mult))
            v.tensor_tensor(h[:, :, :], h[:, :, :], y[:, :, :], ALU.add)


def wavelet_tables():
    c = {"two_ident": 2 * np.eye(D, dtype=np.float32)}
    half = D // 2
    inv_freq = (1.0 / 10000.0 ** (np.arange(half, dtype=np.float32) / half)).astype(np.float32)
    ang = np.arange(S, dtype=np.float32)[:, None] * inv_freq[None, :]
    c["wav_cos"] = np.stack([np.cos(ang)] * 2, 1).astype(np.float32)
    c["wav_sin"] = np.stack([np.sin(ang)] * 2, 1).astype(np.float32)
    cols = []
    for level in range(HAAR_LEVELS):
        size = S // 2 ** level
        for k in range(2 ** level):
            v = np.zeros(S, np.float32)
            v[k * size:k * size + size // 2] = 1.0 / np.sqrt(size // 2)
            v[k * size + size // 2:(k + 1) * size] = -1.0 / np.sqrt(size // 2)
            cols.append(v)
    c["wav_haar"] = np.stack(cols, 1)
    c["wav_haar_blockT"] = c["wav_haar"][::P].T
    p, i, j = np.arange(P)[:, None, None], np.arange(TB)[None, :, None], np.arange(TB)[None, None, :]
    count = np.where(j < i, P, np.where(j == i, p, 0))
    c["wav_count"] = count.astype(np.float32)
    c["wav_hide"] = np.where(count > 0, 0.0, NEG).astype(np.float32)
    c["wav_before"] = np.broadcast_to(j < i, (P, TB, TB)).astype(np.float32)
    n = (np.arange(TB)[None, :] * P + np.arange(P)[:, None] + 1).astype(np.float64)
    c["wav_seen"] = np.stack([D ** -0.5 / np.sqrt(n), 1.0 / n], 2).astype(np.float32)
    c["wav_earlier"] = (np.arange(P)[:, None] < np.arange(P)[None, :]).astype(np.float32)
    return c


F16 = mybir.dt.float16
EDGES = 262144
EC = EDGES // P
HG, GE = 4, 4
LO, HI = 32, T // 32
HC = 256
SLOTS = 4
LAST = T - 1
KEY_TILE = P * T


def graph_ffn(nc, m, d):
    with Stage(nc, "graph") as g:
        own = {"key": g.sb("key", [P, EC]), "tid": g.sb("tid", [P, EC], BF16), "hist": g.sb("hist", [P, NT]),
               "rounds": g.sb("rounds", [1, NT + 1], I32), "gates": g.sb("gates", [P, NT, GE]),
               "agg": g.sb("agg", [P, NT, HG, GE + 1]),
               "feat": g.sb("feat", [P, NT, HG, GE + 1]),
               "a_dst": g.sb("a_dst", [P, NT, HG]),
               "a_src": g.sb("a_src", [P, HG, T])}
        edge_keys(nc, m, own, d)
        edge_rounds(nc, m, own)
        graph_attention(nc, m, own, d)
        graph_route(nc, own, d)
        run_experts(nc, m, d, "moe4", 1, own["gates"], False)


def edge_keys(nc, m, own, d):
    xT, key, tid, hist = m["xT"], own["key"], own["tid"], own["hist"]
    feat, a_dst, a_src = own["feat"], own["a_dst"], own["a_src"]
    with Stage(nc, "keys") as s:
        src = s.sb("src", [P, EC], I32)
        dst = s.sb("dst", [P, EC], I32)
        digit = src
        srcf = s.sb("srcf", [P, EC])
        dstf = s.sb("dstf", [P, EC])
        near = s.sb("near", [P, EC], BF16)
        low = s.sb("low", [P, EC], F16)
        high = s.sb("high", [P, EC], F16)
        hot_lo = s.sb("hot_lo", [P, 2, LO, HC], F16)
        hot_hi = s.sb("hot_hi", [P, 2, HI, HC], F16)
        zero = s.sb("zero", [P, HI], F16)
        w = s.sb("w", [D, HG * GE])
        att = s.sb("att", [D, 2, HG * GE])
        w_att = s.sb("w_att", [D, 2, HG])
        prod = s.sb("prod", [D, 2, HG * GE])
        w_src = s.sb("w_src", [D, HG, P])
        loaded = s.sem("loaded")
        w_loaded = s.sem("w_loaded")

        def load(sp):
            sp.dma_start(w[:, :], d["gat_w"]).then_inc(w_loaded, 16)
            sp.dma_start(att[:, :, :], d["gat_att"].broadcast_to([D, 2, HG * GE])).then_inc(w_loaded, 16)
            sp.dma_start(src[:, :], d["edges"][0]).then_inc(loaded, 16)
            sp.dma_start(dst[:, :], d["edges"][1]).then_inc(loaded, 16)

        normalise(nc, m, "graph", load)
        ps = s.ps("ps", [LO, 512])
        ps_src = [s.ps(f"ps_src{k}", [P, 512]) for k in range(4)]
        ps_a = s.ps("ps_a", [P, 512])
        w_ready = s.sem("w_ready")
        feat_made = s.sem("feat_made")
        src_made = s.sem("src_made")
        src_kept = s.sem("src_kept")
        dve = s.sem("dve_step")
        hot_ready = s.sem("hot_ready")
        hot_used = s.sem("hot_used")
        counted = s.sem("counted")
        zero_set = s.sem("zero_set")
        block = s.block()
        STEPS = EC // HC // 2

        @block.vector
        def _(v):
            step = Chain(v, dve)
            v.memset(zero[:, :], 0.0).then_inc(zero_set, 1)
            v.engine_nop().then_inc(hot_used, 2)
            v.wait_ge(w_loaded, 32)
            for k in range(2):
                step(v.tensor_tensor(prod[:, k, :], w[:, :], att[:, k, :], ALU.mult))
            step(v.tensor_reduce(w_att[:, :, :], prod[:, :, :].rearrange("p k (h e) -> p k h e", h=HG), AX.X, ALU.add))
            v.tensor_copy(w_src[:, :, :], bc(w_att[:, 0, :].unsqueeze(2), [D, HG, P])).then_inc(w_ready, 1)
            v.memset(feat[:, :, :, GE:GE + 1], 1.0)
            v.wait_ge(loaded, 32)
            step(v.tensor_copy(srcf[:, :], src[:, :]))
            step(v.tensor_copy(dstf[:, :], dst[:, :]))
            step(v.tensor_scalar(near[:, :], srcf[:, :], float(LAST), None, ALU.is_lt))
            step(v.tensor_scalar(digit[:, :], dst[:, :], LO - 1, None, ALU.bitwise_and))
            step(v.tensor_copy(low[:, :], digit[:, :]))
            step(v.tensor_scalar(digit[:, :], dst[:, :], 5, None, ALU.logical_shift_right))
            step(v.tensor_copy(key[:, :], digit[:, :]))
            step(v.scalar_tensor_tensor(high[:, :], near[:, :], -1024.0, key[:, :], ALU.mult, ALU.add))
            step(v.scalar_tensor_tensor(near[:, :], dstf[:, :], float(T), near[:, :], ALU.is_lt, ALU.mult))
            step(v.scalar_tensor_tensor(key[:, :], dstf[:, :], float(T), srcf[:, :], ALU.mult, ALU.add))
            step(v.scalar_tensor_tensor(key[:, :], key[:, :], 1.0, near[:, :], ALU.add, ALU.mult))
            step(v.tensor_scalar(digit[:, :], dst[:, :], 7, None, ALU.logical_shift_right))
            step(v.tensor_copy(srcf[:, :], digit[:, :]))
            step(v.scalar_tensor_tensor(srcf[:, :], srcf[:, :], 1.0, near[:, :], ALU.add, ALU.mult))
            step(v.tensor_scalar(tid[:, :], srcf[:, :], -1.0, None, ALU.add))
            v.wait_ge(feat_made, 1)
            both = ps_a[:, 0:NT * 20].rearrange("p (t c) -> p t c", t=NT)
            for hd in range(HG):
                v.tensor_copy(feat[:, :, hd, 0:GE], both[:, :, hd * GE:hd * GE + GE])
            v.tensor_copy(a_dst[:, :, :], both[:, :, 16:20])
            with v.Fori(0, STEPS) as i:
                for r in range(2):
                    v.wait_ge(hot_used, i * 2 + (r + 1))
                    cols = bass.ds(i * (2 * HC) + r * HC, HC)
                    for k in range(LO):
                        v.tensor_scalar(hot_lo[:, r, k, :], low[:, cols], float(k), None, ALU.is_equal)
                    for k in range(HI):
                        last = v.tensor_scalar(hot_hi[:, r, k, :], high[:, cols], float(k), None, ALU.is_equal)
                    last.then_inc(hot_ready, 1)
            v.wait_ge(counted, 1)
            for q in range(P // LO):
                v.tensor_copy(hist[q * LO:(q + 1) * LO, :], ps[:, q:HI:P // LO])

        @block.scalar
        def _(a):
            for n in range(16):
                a.wait_ge(src_made, n + 1)
                a.copy(a_src[:, n // 4, n % 4 * 512:n % 4 * 512 + 512], ps_src[n % 4][:, :]).then_inc(src_kept, 1)

        @block.tensor
        def _(pe):
            pe.wait_ge(w_ready, 1)
            for t in range(NT):
                x = xT[0:D, t * P:t * P + P]
                pe.matmul(ps_a[:, t * 20:t * 20 + 16], x, w[:, :], start=True, stop=True)
                mm = pe.matmul(ps_a[:, t * 20 + 16:t * 20 + 20], x, w_att[:, 1, :], start=True, stop=True)
            mm.then_inc(feat_made, 1)
            for n in range(16):
                if n >= 4:
                    pe.wait_ge(src_kept, n - 3)
                pe.matmul(ps_src[n % 4][:, :], w_src[:, n // 4, :], xT[0:D, n % 4 * 512:n % 4 * 512 + 512],
                          start=True, stop=True).then_inc(src_made, 1)
            pe.wait_ge(zero_set, 1)
            pe.matmul(ps[:, 0:HI], zero[:, 0:LO], zero[:, :], start=True, stop=False, skip_group_check=True)
            with pe.Fori(0, STEPS) as i:
                for r in range(2):
                    pe.wait_ge(hot_ready, i * 2 + (r + 1))
                    pe.wait_ge(zero_set, 1)
                    for c in range(HC):
                        mm = pe.matmul(ps[:, 0:HI], hot_lo[:, r, :, c], hot_hi[:, r, :, c],
                                       start=False, stop=False, skip_group_check=True)
                    mm.then_inc(hot_used, 1)
            pe.matmul(ps[:, 0:HI], zero[:, 0:LO], zero[:, :], start=False, stop=True,
                      skip_group_check=True).then_inc(counted, 1)


def edge_rounds(nc, m, own):
    ident, tid, rounds = m["ident"], own["tid"], own["rounds"]
    with Stage(nc, "rounds") as s:
        hit = s.sb("hit", [P, 2, EC], BF16)
        count = s.sb("count", [P, NT])
        most = s.sb("most", [NT, 1])
        whole = s.sb("whole", [1, NT], I32)
        row = s.sb("row", [1, NT])
        ones = s.sb("ones", [1, NT])
        upto = s.sb("upto", [1, NT + 1])
        ps_count = s.ps("ps_count", [P, P])
        ps_most = s.ps("ps_most", [P, NT])
        dve = s.sem("dve_step")
        counted = s.sem("counted")
        turned = s.sem("turned")
        most_ready = s.sem("most_ready")
        block = s.block()
        FOLDS = (EC // 2, EC // 4, EC // 8)

        @block.vector
        def _(v):
            step = Chain(v, dve)
            for t in range(NT):
                if t >= 2:
                    v.wait_ge(counted, t - 1)
                step(v.tensor_scalar(hit[:, t % 2, :], tid[:, :], float(t), None, ALU.is_equal))
                for n in FOLDS:
                    step(v.tensor_tensor(hit[:, t % 2, 0:n], hit[:, t % 2, 0:n], hit[:, t % 2, n:2 * n], ALU.add))
                v.tensor_reduce(count[:, t:t + 1], hit[:, t % 2, 0:FOLDS[-1]], AX.X, ALU.add).then_inc(counted, 1)
            v.wait_ge(turned, 1)
            v.tensor_reduce(most[:, :], ps_count[0:NT, :], AX.X, ALU.max).then_inc(most_ready, 1)
            v.wait_ge(turned, 2)
            step(v.tensor_scalar(row[:, :], ps_most[0:1, :], 0.125, 3.5 / 8, ALU.mult, ALU.add))
            step(v.tensor_copy(whole[:, :], row[:, :]))
            step(v.tensor_copy(row[:, :], whole[:, :]))
            step(v.tensor_scalar(row[:, :], row[:, :], 1.0, None, ALU.max))
            step(v.memset(ones[:, :], 1.0))
            step(v.memset(upto[:, 0:1], 0.0))
            step(v.tensor_tensor_scan(upto[:, 1:NT + 1], ones[:, :], row[:, :], 0.0, ALU.mult, ALU.add))
            v.tensor_copy(rounds[:, :], upto[:, :])

        @block.tensor
        def _(pe):
            pe.wait_ge(counted, NT)
            pe.transpose(ps_count[0:NT, :], count[:, :], ident[:, :]).then_inc(turned, 1)
            pe.wait_ge(most_ready, 1)
            pe.transpose(ps_most[0:1, :], most[:, :], ident[0:NT, 0:NT]).then_inc(turned, 1)


def graph_attention(nc, m, own, d):
    ident = m["ident"]
    key, tid, hist, rounds, agg = (own[k] for k in ("key", "tid", "hist", "rounds", "agg"))
    feat, a_dst, a_src = own["feat"], own["a_dst"], own["a_src"]
    with Stage(nc, "gat") as s:
        iota = s.sb("iota", [P, T], F16)
        tiles = s.sb("tiles", [P, NT])
        bases = s.sb("bases", [P, NT])
        loops = s.sb("loops", [P, 2 * T - P], F16)
        identh = s.sb("identh", [P, P], F16)
        work = s.sb("work", [P, EC])
        top = s.sb("top", [P, 8])
        local = s.sb("local", [P, 8])
        place = s.sb("place", [P, 2, 8], I32)
        placef = s.sb("placef", [P, 2, 8])
        hot_d = s.sb("hot_d", [P, SLOTS, P], F16)
        hot_s = s.sb("hot_s", [P, SLOTS, T], F16)
        cnt = s.sb("cnt", [P, 2, T])
        hide = work
        seen = s.sb("seen", [P, HG, T])
        e1 = s.sb("e1", [P, HG, T])
        e2 = s.sb("e2", [P, 2, T])
        turned = s.sb("turned", [P, 2, 4, P])
        mx = s.sb("mx", [P, HG])
        mx2 = s.sb("mx2", [P, HG])
        bias = s.sb("bias", [P, 2, 2, HG])
        spare = s.sb("spare", [P, 30])
        C = [s.ps(f"C{k}", [P, 512]) for k in range(4)]
        ps_t = [s.ps(f"ps_t{k}", [P, 4, P]) for k in range(2)]
        ps_as = [s.ps(f"ps_a{k}", [P, 512]) for k in range(2)]
        names = ["loaded", "hots", "hots_used",
                 "near_done", "C_copied", "tile_step", "round_step", "e_ready", "w_max", "weighted",
                 "turns", "turns_kept", "head_done", "agg_kept", "bias_ready"]
        (loaded, hots, hots_used, near_done, C_copied,
         tile_step, round_step, e_ready, w_max, weighted, turns, turns_kept, head_done, agg_kept,
         bias_ready) = [s.sem(n) for n in names]
        block = s.block()
        LOADS = 5 * 16
        TILE_STEPS, ROUND_STEPS = 10, 6

        @block.sync
        def _(sp):
            sp.dma_start(iota[:, :], d["iota_nodes"].broadcast_to([P, T])).then_inc(loaded, 16)
            sp.dma_start(tiles[:, :], d["iota_tiles"].broadcast_to([P, NT])).then_inc(loaded, 16)
            sp.dma_start(bases[:, :], d["key_bases"].broadcast_to([P, NT])).then_inc(loaded, 16)
            sp.dma_start(loops[:, :], d["loops"]).then_inc(loaded, 16)
            sp.dma_start(identh[:, :], d["identh"]).then_inc(loaded, 16)

        @block.tensor
        def _(pe):
            pe.wait_ge(loaded, LOADS)
            def count(t):
                first = pe.value_load(rounds[0:1, bass.ds(t, 1)], min_val=0, max_val=EC * 2)
                end = pe.value_load(rounds[0:1, bass.ds(t + 1, 1)], min_val=1, max_val=EC * 2)
                pe.wait_ge(C_copied, t)
                for k in range(4):
                    pe.matmul(C[k][:, :], identh[:, :], loops[:, bass.ds(t * (-P) + (T - P + k * 512), 512)],
                              start=True, stop=False, skip_group_check=True)
                with pe.Fori(first, end) as r:
                    for e in range(8):
                        pe.wait_ge(hots, r * 8 + (e + 1))
                        for k in range(4):
                            mm = pe.matmul(C[k][:, :], hot_d[:, e % SLOTS, :],
                                           hot_s[:, e % SLOTS, k * 512:k * 512 + 512],
                                           start=False, stop=False, skip_group_check=True)
                        mm.then_inc(hots_used, 1)
                for k in range(4):
                    mm = pe.matmul(C[k][:, 0:1], hot_d[:, 0, :], loops[:, 0:1], start=False, stop=True,
                                   skip_group_check=True)
                mm.then_inc(near_done, 1)

            def sums(t, r):
                def turn(hd, q):
                    pe.wait_ge(turns_kept, t * 16 + (hd * 4 + q + 1))
                    for j in range(4):
                        c = (q * 4 + j) * P
                        mm = pe.transpose(ps_t[q % 2][:, j, :], e1[:, hd, c:c + P], ident[:, :])
                    mm.then_inc(turns, 1)

                for hd in range(HG):
                    pe.wait_ge(weighted, t * HG + (hd + 1))
                    turn(hd, 0)
                    for q in range(4):
                        if q < 3:
                            turn(hd, q + 1)
                        if hd == 0 and q == 0:
                            pe.wait_ge(agg_kept, t + 1)
                        pe.wait_ge(turns_kept, t * 16 + (hd * 4 + q + 3))
                        for j in range(4):
                            u = q * 4 + j
                            mm = pe.matmul(ps_as[r][:, hd * 8:hd * 8 + GE + 1], turned[:, q % 2, j, :],
                                           feat[:, u, hd, :], start=(u == 0), stop=(u == NT - 1))
                    mm.then_inc(head_done, 1)

            count(0)
            with pe.Fori(0, NT // 2 - 1) as i:
                count(i * 2 + 1)
                sums(i * 2, 0)
                count(i * 2 + 2)
                sums(i * 2 + 1, 1)
            count(NT - 1)
            sums(NT - 2, 0)
            sums(NT - 1, 1)

        @block.scalar
        def _(a):

            def steep(t, r, hd):
                a.wait_ge(bias_ready, t + 1)
                if not isinstance(t, int) or t > 0:
                    a.wait_ge(head_done, t * HG + (hd + 1 - HG))
                a.activation(e1[:, hd, :], seen[:, hd, :], ACT.Exp, bias=bias[:, r, 0, hd:hd + 1])

            def flat(t, r, hd):
                if not isinstance(t, int) or t * HG + hd >= 2:
                    a.wait_ge(weighted, t * HG + (hd - 1))
                a.activation(e2[:, hd % 2, :], seen[:, hd, :], ACT.Exp, bias=bias[:, r, 1, hd:hd + 1],
                             scale=0.2).then_inc(e_ready, 1)

            def weights(t, r, last=False):
                for hd in range(HG):
                    ahead = (t, r, hd + 2) if hd < 2 else (t + 1, 1 - r, hd - 2)
                    for q in range(4):
                        if q in (1, 2) and not (last and hd >= 2):
                            (steep, flat)[q - 1](*ahead)
                        a.wait_ge(turns, t * 16 + (hd * 4 + q + 1))
                        a.copy(turned[:, q % 2, :, :], ps_t[q % 2][:, :, :]).then_inc(turns_kept, 1)

            for hd in range(2):
                steep(0, 0, hd)
                flat(0, 0, hd)
            weights(0, 0)
            with a.Fori(0, NT // 2 - 1) as i:
                weights(i * 2 + 1, 1)
                weights(i * 2 + 2, 0)
            weights(NT - 1, 1, last=True)

        @block.gpsimd
        def _(g):
            def weigh(t, r):
                for hd in range(HG):
                    g.wait_ge(w_max, t * HG + (hd + 1))
                    g.tensor_tensor(e1[:, hd, :], e2[:, hd % 2, :], cnt[:, r, :], ALU.mult).then_inc(weighted, 1)

            with g.Fori(0, NT // 2) as i:
                weigh(i * 2, 0)
                weigh(i * 2 + 1, 1)

        @block.vector
        def _(v):
            sites = [0]

            def carry():
                sites[0] += 1
                v.memset(spare[:, sites[0]:sites[0] + 1], 0.0)

            v.wait_ge(loaded, LOADS)
            v.engine_nop().then_inc(hots_used, SLOTS)
            v.engine_nop().then_inc(turns_kept, 2)
            v.engine_nop().then_inc(round_step, 1)
            v.engine_nop().then_inc(agg_kept, 2)

            def largest(t, hd):
                v.wait_ge(e_ready, t * HG + (hd + 1))
                v.tensor_tensor(e2[:, hd % 2, :], e1[:, hd, :], e2[:, hd % 2, :], ALU.max).then_inc(w_max, 1)

            def keep(t, r):
                v.wait_ge(head_done, t * HG + HG)
                v.tensor_copy(agg[:, bass.ds(t, 1), :, :].rearrange("p t h c -> p (t h) c"),
                              ps_as[r][:, 0:HG * 8].rearrange("p (h c) -> p h c", h=HG)[:, :, 0:GE + 1]
                              ).then_inc(agg_kept, 1)

            def tile(t, r, before, kept):
                first = v.value_load(rounds[0:1, bass.ds(t, 1)], min_val=0, max_val=EC * 2)
                end = v.value_load(rounds[0:1, bass.ds(t + 1, 1)], min_val=1, max_val=EC * 2)
                count = 0

                def after(ins):
                    nonlocal count
                    count += 1
                    ins.then_inc(tile_step, 1)
                    v.wait_ge(tile_step, t * TILE_STEPS + count)

                after(v.scalar_tensor_tensor(work[:, :], tid[:, :], tiles[:, bass.ds(t, 1)], key[:, :],
                                             ALU.is_equal, ALU.mult))
                if before is not None:
                    largest(before, 0)
                carry()
                with v.Fori(first, end) as n:
                    steps = 0

                    def then(ins):
                        nonlocal steps
                        steps += 1
                        ins.then_inc(round_step, 1)
                        v.wait_ge(round_step, n * ROUND_STEPS + (steps + 1))

                    v.wait_ge(round_step, n * ROUND_STEPS + 1)
                    carry()
                    then(v.max(top[:, :], work[:, :]))
                    carry()
                    then(v.match_replace(work[:, :], top[:, :], work[:, :], 0.0))
                    then(v.tensor_scalar(local[:, :], top[:, :], bases[:, bass.ds(t, 1)], None, ALU.subtract))
                    then(v.tensor_copy(place[:, 0, :], local[:, :]))
                    v.tensor_scalar(place[:, 1, :], place[:, 0, :], T - 1, None, ALU.bitwise_and)
                    then(v.tensor_scalar(place[:, 0, :], place[:, 0, :], 11, None, ALU.arith_shift_right))
                    then(v.tensor_copy(placef[:, :, :], place[:, :, :]))
                    for e in range(8):
                        v.wait_ge(hots_used, n * 8 + (e + 1))
                        v.tensor_scalar(hot_d[:, e % SLOTS, :], iota[:, 0:P], placef[:, 0, e:e + 1], None, ALU.is_equal)
                        v.tensor_scalar(hot_s[:, e % SLOTS, :], iota[:, :], placef[:, 1, e:e + 1], None,
                                        ALU.is_equal).then_inc(hots, 1)
                if kept is not None:
                    keep(kept, r)
                if before is not None:
                    largest(before, 1)
                    v.wait_ge(weighted, t * HG - HG)
                v.wait_ge(near_done, t + 1)
                for k in range(4):
                    last = v.tensor_copy(cnt[:, r, k * 512:k * 512 + 512], C[k][:, :])
                last.then_inc(C_copied, 1)
                v.wait_ge(C_copied, t + 1)
                after(v.tensor_scalar(cnt[:, r, LAST:T], cnt[:, r, LAST:T], hist[:, bass.ds(t, 1)], None, ALU.add))
                after(v.tensor_scalar(hide[:, :], cnt[:, r, :], 0.0, NEG, ALU.is_equal, ALU.mult))
                if before is not None:
                    largest(before, 2)
                for hd in range(HG):
                    if before is not None and hd == 3:
                        largest(before, 3)
                    carry()
                    after(v.tensor_tensor_reduce(out=seen[:, hd, :], in0=a_src[:, hd, :], in1=hide[:, :],
                                                 scale=1.0, scalar=NEG, op0=ALU.add, op1=ALU.max,
                                                 accum_out=mx[:, hd:hd + 1]))
                dst = a_dst[:, bass.ds(t, 1), :].rearrange("p t h -> p (t h)")
                after(v.tensor_tensor(mx[:, :], mx[:, :], dst, ALU.add))
                after(v.scalar_tensor_tensor(mx2[:, :], mx[:, :], 0.2, mx[:, :], ALU.mult, ALU.max))
                after(v.tensor_tensor(bias[:, r, 0, :], dst, mx2[:, :], ALU.subtract))
                v.scalar_tensor_tensor(bias[:, r, 1, :], dst, 0.2, mx2[:, :], ALU.mult, ALU.subtract
                                       ).then_inc(bias_ready, 1)
                assert count == TILE_STEPS

            tile(0, 0, None, None)
            tile(1, 1, 0, None)
            with v.Fori(0, NT // 2 - 1) as i:
                tile(i * 2 + 2, 0, i * 2 + 1, i * 2)
                tile(i * 2 + 3, 1, i * 2 + 2, i * 2 + 1)
            keep(NT - 2, 0)
            for hd in range(HG):
                largest(NT - 1, hd)
            keep(NT - 1, 1)


def graph_route(nc, own, d):
    agg, gates = own["agg"], own["gates"]
    F = HG * GE
    with Stage(nc, "route4") as s:
        par = s.sb("par", [P, 3, F])
        order = s.sb("order", [P, 8])
        x = s.sb("x", [P, NT, HG, GE])
        sq = s.sb("sq", [P, NT, HG, GE])
        rden = s.sb("rden", [P, NT, HG])
        mean = s.sb("mean", [P, NT])
        std = s.sb("std", [P, NT])
        scores = s.sb("scores", [P, NT, GE])
        best = [s.sb(f"best{k}", [P, NT]) for k in range(2)]
        picks = [s.sb(f"pick{k}", [P, NT, GE]) for k in range(2)]
        rest = s.sb("rest", [P, NT, GE])
        eq = s.sb("eq", [P, NT, GE])
        second = s.sb("second", [P, NT])
        loaded = s.sem("loaded")
        dve = s.sem("dve_step")
        var_ready = s.sem("var_ready")
        std_ready = s.sem("std_ready")
        gap_ready = s.sem("gap_ready")
        exp_ready = s.sem("exp_ready")
        eps = s.sb("eps", [P, 1])
        eps_set = s.sem("eps_set")
        block = s.block()

        @block.sync
        def _(sp):
            sp.dma_start(par[:, :, :], d["route4_par"].broadcast_to([P, 3, F])).then_inc(loaded, 16)
            sp.dma_start(order[:, 0:GE], d["order4"].broadcast_to([P, GE])).then_inc(loaded, 16)

        @block.scalar
        def _(a):
            a.wait_ge(var_ready, 1)
            a.wait_ge(eps_set, 1)
            a.activation(std[:, :], std[:, :], ACT.Sqrt, bias=eps[:, 0:1]).then_inc(std_ready, 1)
            a.wait_ge(gap_ready, 1)
            a.activation(second[:, :], second[:, :], ACT.Exp).then_inc(exp_ready, 1)

        @block.vector
        def _(v):
            step = Chain(v, dve)
            v.memset(eps[:, :], LN_EPS).then_inc(eps_set, 1)
            v.wait_ge(loaded, 32)
            flat, flat_sq = x[:, :, :, :].rearrange("p t h e -> p t (h e)"), sq[:, :, :, :].rearrange("p t h e -> p t (h e)")

            def row(k):
                return bc(par[:, k, :].unsqueeze(1), [P, NT, F])

            def col(ap, n):
                return bc(ap[:, :].unsqueeze(2), [P, NT, n])

            step(v.tensor_scalar(rden[:, :, :], agg[:, :, :, GE], 1e-16, None, ALU.add))
            step(v.reciprocal(rden[:, :, :], rden[:, :, :]))
            step(v.tensor_tensor(x[:, :, :, :], agg[:, :, :, 0:GE], bc(rden[:, :, :].unsqueeze(3), [P, NT, HG, GE]),
                                 ALU.mult))
            step(v.tensor_tensor(flat, flat, row(0), ALU.add))
            step(v.tensor_reduce(mean[:, :], flat, AX.X, ALU.add))
            step(v.tensor_scalar(mean[:, :], mean[:, :], 1.0 / F, None, ALU.mult))
            step(v.tensor_tensor(flat, flat, col(mean, F), ALU.subtract))
            step(v.tensor_tensor(flat_sq, flat, flat, ALU.mult))
            step(v.tensor_reduce(std[:, :], flat_sq, AX.X, ALU.add))
            v.tensor_scalar(std[:, :], std[:, :], 1.0 / F, None, ALU.mult).then_inc(var_ready, 1)
            v.wait_ge(std_ready, 1)
            step(v.reciprocal(std[:, :], std[:, :]))
            step(v.tensor_tensor(flat, flat, col(std, F), ALU.mult))
            step(v.tensor_tensor(flat, flat, row(1), ALU.mult))
            step(v.tensor_tensor(flat, flat, row(2), ALU.add))
            step(v.tensor_reduce(scores[:, :, :], x[:, :, :, :].rearrange("p t h e -> p t e h"), AX.X, ALU.add))
            step(v.tensor_scalar(scores[:, :, :], scores[:, :, :], 1.0 / HG, None, ALU.mult))
            two_best(v, step, scores, best, rest, eq, picks, order, GE)
            v.tensor_tensor(second[:, :], best[1][:, :], best[0][:, :], ALU.subtract).then_inc(gap_ready, 1)
            v.wait_ge(exp_ready, 1)
            step(v.tensor_scalar(mean[:, :], second[:, :], 1.0, None, ALU.add))
            step(v.reciprocal(mean[:, :], mean[:, :]))
            step(v.tensor_tensor(picks[1][:, :, :], picks[1][:, :, :], col(second, GE), ALU.mult))
            step(v.tensor_tensor(gates[:, :, :], picks[0][:, :, :], picks[1][:, :, :], ALU.add))
            v.tensor_tensor(gates[:, :, :], gates[:, :, :], col(mean, GE), ALU.mult)


def graph_tables():
    c = {"iota_nodes": np.arange(T, dtype=np.float16)[None], "identh": np.eye(P, dtype=np.float16)}
    c["iota_tiles"] = np.arange(NT, dtype=np.float32)[None]
    c["key_bases"] = (np.arange(NT) * KEY_TILE + 1).astype(np.float32)[None]
    loops = np.zeros((P, 2 * T - P), np.float16)
    loops[:, T - P:T] = np.eye(P)
    c["loops"] = loops
    c["order4"] = np.arange(GE, 0, -1, dtype=np.float32)[None]
    return c


class Steps:

    def __init__(self, engine, semaphore, base):
        self.engine, self.semaphore, self.base, self.count = engine, semaphore, base, 0

    def __call__(self, *instructions):
        self.count += 1
        instructions[-1].then_inc(self.semaphore, 1)
        self.engine.wait_ge(self.semaphore, self.base + self.count)


PK_HEADS = 8
PK_KEYS = 64
PK_DIM = D // 2
TOPK = 16
PAIRS_OF_HEADS = PK_HEADS // 2
CANDS = [(i, TOPK // (i + 1)) for i in range(TOPK)]
N_CAND = sum(n for _, n in CANDS)
GROUPS2 = 2 * PK_HEADS
G_RING = 8
LOWEST = -3e38
INV_TILE = 3


def product_keys(nc, m, d):
    h, xT, ident, inv_wT = m["h"], m["xT"], m["ident"], m["inv_wT"]
    with Stage(nc, "pkm") as s:
        near_w = s.sb("near_w", [D, D])
        near_wT = s.sb("near_wT", [D, P])
        two = s.sb("two", [D, D])
        square = s.sb("square", [D, D])
        norm = s.sb("norm", [D, 2])
        ones = s.sb("ones", [D, D])
        inv = s.sb("inv", [D, D])
        invT = s.sb("invT", [D, P])
        left = s.sb("left", [D, P])
        w = s.sb("w", [D, 2, 4, P])
        wo = s.sb("wo", [P, PAIRS_OF_HEADS, D])
        keys = s.sb("keys", [P, 4, 4 * PK_KEYS])
        head_base = s.sb("head_base", [P, PK_HEADS, TOPK])
        iota = s.sb("iota", [P, N_CAND])
        later = s.sb("later", [P, 2 * S - P])
        mask = s.sb("mask", [P, S])
        qp_now = s.sb("qp_now", [P, 4, P])
        q_now = s.sb("q_now", [P, PAIRS_OF_HEADS, P])
        sim = s.sb("sim", [P, 2, GROUPS2, PK_KEYS])
        top = s.sb("top", [P, GROUPS2, TOPK])
        at = s.sb("at", [P, GROUPS2, TOPK], U32)
        atf = s.sb("atf", [P, GROUPS2, TOPK])
        score = s.sb("score", [P, PK_HEADS, N_CAND])
        row = s.sb("row", [P, PK_HEADS, N_CAND])
        best = s.sb("best", [P, PK_HEADS, TOPK])
        pos = s.sb("pos", [P, PK_HEADS, TOPK], U32)
        posf = s.sb("posf", [P, PK_HEADS, TOPK])
        eq = s.sb("eq", [P, PK_HEADS // 2, TOPK, N_CAND])
        picked = s.sb("picked", [P, PK_HEADS, TOPK])
        total = s.sb("total", [P, PK_HEADS])
        rows = s.sb("rows", [P, 2, PK_HEADS * TOPK], I32)
        weight = s.sb("weight", [P, 2, PK_HEADS, TOPK])
        got = [s.sb(f"got{k}", [P, TOPK, 2 * D]) for k in range(G_RING)]
        k_now = s.sb("k_now", [P, PAIRS_OF_HEADS, 2 * D])
        v_now = s.sb("v_now", [P, PK_HEADS, D])
        kT = s.sb("kT", [P, PAIRS_OF_HEADS, S])
        v_all = s.sb("v_all", [P, TB, PK_HEADS, D + 1])
        masked = s.sb("masked", [P, 2, S])
        probs = s.sb("probs", [P, 2, S])
        pT = s.sb("pT", [P, 2, 4, P])
        bias = s.sb("bias", [P, PK_HEADS])
        mx = s.sb("mx", [P, PK_HEADS, 2])
        rden = s.sb("rden", [P, PK_HEADS])
        o_now = s.sb("o_now", [P, PAIRS_OF_HEADS, 2 * D])
        oT = s.sb("oT", [P, PAIRS_OF_HEADS, P])
        spare = s.sb("spare", [P, 128])
        act_spare = s.sb("act_spare", [P, 2])
        pool_spare = s.sb("pool_spare", [P, 32])
        loaded = s.sem("loaded")

        def load(sp):
            sp.dma_start(w[:, :, :, :], d["pk_wq"].rearrange("d (k c) p -> d k c p", k=2)).then_inc(loaded, 16)
            sp.dma_start(keys[:, :, :], d["pk_keys"]).then_inc(loaded, 16)
            sp.dma_start(head_base[:, :, :], d["pk_base"].broadcast_to([P, PK_HEADS, TOPK])).then_inc(loaded, 16)
            sp.dma_start(iota[:, :], d["pk_iota"].broadcast_to([P, N_CAND])).then_inc(loaded, 16)
            sp.dma_start(later[:, :], d["pk_later"]).then_inc(loaded, 16)
            sp.dma_start(wo[:, :, :], d["pk_wo"]).then_inc(loaded, 16)
            sp.dma_start(near_w[:, :], d["near_w_q"]).then_inc(loaded, 16)
            sp.dma_start(near_wT[:, 0:D], d["near_w_qT"]).then_inc(loaded, 16)
            sp.dma_start(two[:, :], d["two_ident"]).then_inc(loaded, 16)

        normalise(nc, m, "pkm", load)
        ps_q = s.ps("ps_q", [P, 4, P])
        ps_sim = [s.ps(f"ps_sim{k}", [P, 512]) for k in range(2)]
        ps_sc = [s.ps(f"ps_sc{k}", [P, 512]) for k in range(2)]
        ps_t = [s.ps(f"ps_t{k}", [P, 4, P]) for k in range(2)]
        ps_o = s.ps("ps_o", [P, 512])
        names = ["cleared", "qp_made", "qp_kept", "sim_made", "sim_kept", "sim_used", "best_ready",
                 "exp_ready", "rows_ready", "dve_step", "combined", "scaled", "carried", "q_made", "q_kept",
                 "kv_staged", "qk_made", "max_step", "max_done", "exp_done", "turned", "t_kept", "pv_made",
                 "rden_ready", "o_kept", "y_made", "y_kept", "act_step", "norm_step", "norm_ready", "norm_made",
                 "inv_ready", "left_made", "left_ready", "inv_made"]
        (cleared, qp_made, qp_kept, sim_made, sim_kept, sim_used, best_ready, exp_ready, rows_ready, dve,
         combined, scaled, carried, q_made, q_kept, kv_staged, qk_made, max_step, max_done, exp_done, turned,
         t_kept, pv_made, rden_ready, o_kept, y_made, y_kept, act_step, norm_step, norm_ready, norm_made,
         inv_ready, left_made, left_ready, inv_made) = [s.sem(n) for n in names]
        landed = [s.sem(f"landed{k}") for k in range(G_RING)]
        block = s.block()
        TURNS = 2 * PK_HEADS + 2
        LOADS = 9 * 16
        ps_left, ps_inv, ps_invT = (ps_o[:, c:c + D] for c in (2 * D, 3 * D, 4 * D))

        @block.tensor
        def _(pe):
            def tokens(t):
                return xT[0:D, bass.ds(t * P, P)]

            def similarities(t):
                if not isinstance(t, int) or t >= 2:
                    pe.wait_ge(q_kept, t - 1)
                for c in range(4):
                    mm = pe.matmul(ps_q[:, c, :], w[:, 0, c, :], tokens(t), start=True, stop=True)
                mm.then_inc(qp_made, 1)
                pe.wait_ge(qp_kept, t + 1)
                if not isinstance(t, int) or t >= 1:
                    pe.wait_ge(sim_kept, t)
                for c in range(4):
                    mm = pe.matmul(ps_sim[c // 2][:, c % 2 * 256:c % 2 * 256 + 256], qp_now[:, c, :],
                                   keys[:, c, :], start=True, stop=True)
                mm.then_inc(sim_made, 1)

            def turn_keys(t):
                pe.wait_ge(combined, t * PK_HEADS + (PK_HEADS + G_RING))
                pe.wait_ge(t_kept, t * TURNS + 2)
                for q in range(PAIRS_OF_HEADS):
                    mm = pe.transpose(ps_t[0][:, q, :], k_now[:, q, :], ident[:, :])
                mm.then_inc(turned, 1)

            def attend(t, looked_up):
                pe.wait_ge(qp_kept, looked_up)
                for c in range(4):
                    mm = pe.matmul(ps_q[:, c, :], w[:, 1, c, :], tokens(t), start=True, stop=True)
                mm.then_inc(q_made, 1)
                pe.wait_ge(q_kept, t + 2)
                pe.wait_ge(kv_staged, t + 1)

                def scores(hd):
                    rows = slice(hd % 2 * D, hd % 2 * D + D)
                    pe.wait_ge(max_done, t * PK_HEADS + (hd + 1))
                    for j in range(2):
                        mm = pe.matmul(ps_sc[j][:, :], q_now[rows, hd // 2, :],
                                       kT[rows, hd // 2, j * 512:j * 512 + 512], start=True, stop=True)
                    mm.then_inc(qk_made, 1)

                scores(0)
                for hd in range(PK_HEADS):
                    if hd + 1 < PK_HEADS:
                        scores(hd + 1)
                    pe.wait_ge(exp_done, t * PK_HEADS + (hd + 1))
                    for c in range(2):
                        n = 1 + 2 * hd + c
                        pe.wait_ge(t_kept, t * TURNS + max(n + 1, 3))
                        for j in range(4):
                            mm = pe.transpose(ps_t[c][:, j, :], probs[:, hd % 2, (4 * c + j) * P:(4 * c + j + 1) * P],
                                              ident[:, :])
                        mm.then_inc(turned, 1)
                    if hd == 0:
                        pe.wait_ge(y_kept, t + 1)
                        pe.wait_ge(inv_ready, min(t, NT - 2) * INV_TILE + 1 if isinstance(t, int) else t * INV_TILE + 1)
                    else:
                        pe.wait_ge(o_kept, t * PK_HEADS + hd)
                    for c in range(2):
                        pe.wait_ge(t_kept, t * TURNS + (1 + 2 * hd + c + 3))
                        for j in range(4):
                            mm = pe.matmul(ps_o[:, 0:D + 1], pT[:, c, j, :], v_all[:, 4 * c + j, hd, :],
                                           start=(c == j == 0), stop=(c == 1 and j == 3))
                    mm.then_inc(pv_made, 1)
                pe.wait_ge(o_kept, t * PK_HEADS + PK_HEADS)
                pe.wait_ge(t_kept, t * TURNS + (TURNS - 1 + 2))
                for q in range(PAIRS_OF_HEADS):
                    mm = pe.transpose(ps_t[1][:, q, :], o_now[:, q, :], ident[:, :])
                mm.then_inc(turned, 1)
                pe.wait_ge(t_kept, t * TURNS + (TURNS + 2))
                for q in range(PAIRS_OF_HEADS):
                    mm = pe.matmul(ps_o[:, 0:D], oT[:, q, :], wo[:, q, :], start=(q == 0), stop=(q == PAIRS_OF_HEADS - 1))
                mm.then_inc(y_made, 1)

            def invert(t):
                pe.wait_ge(y_kept, t + 2)
                for k in range(INV_TILE):
                    pe.wait_ge(inv_ready, t * INV_TILE + (k + 1))
                    pe.matmul(ps_left, near_wT[:, :], inv[:, :], start=True, stop=True).then_inc(left_made, 1)
                    pe.wait_ge(left_ready, t * INV_TILE + (k + 1))
                    pe.matmul(ps_inv, invT[:, :], left[:, 0:D], start=True, stop=True)
                    pe.matmul(ps_invT, left[:, :], invT[:, 0:D], start=True, stop=True).then_inc(inv_made, 1)

            pe.wait_ge(loaded, LOADS)
            similarities(0)
            similarities(1)
            pe.wait_ge(cleared, 2)
            pe.wait_ge(norm_ready, 1)
            pe.matmul(ps_o[0:D, 0:1], ones[:, :], norm[:, 0:1], start=True, stop=True).then_inc(norm_made, 1)
            with pe.Fori(0, NT // 2 - 1) as i:
                for r in range(2):
                    turn_keys(i * 2 + r)
                    similarities(i * 2 + (r + 2))
                    attend(i * 2 + r, i * 2 + (r + 3))
                    invert(i * 2 + r)
            for t in range(NT - 2, NT):
                turn_keys(t)
                attend(t, NT)

        @block.scalar
        def _(a):
            def stage_keys(t):
                slot = t & (TB - 1)
                a.wait_ge(turned, t * TURNS + 1)
                a.copy(kT[:, :, bass.ds(slot * P, P)], ps_t[0][:, :, :]).then_inc(t_kept, 1)
                a.copy(mask[:, :], later[:, bass.ds(slot * (-P) + (S - P), S)])
                a.wait_ge(combined, t * PK_HEADS + (PK_HEADS + G_RING))
                a.copy(v_all[:, bass.ds(slot, 1), :, 0:D].rearrange("p t h c -> p (t h) c"),
                       v_now[:, :, :]).then_inc(kv_staged, 1)

            def stage_similarities(t, r):
                a.wait_ge(qp_made, t + 1)
                a.copy(qp_now[:, :, :], ps_q[:, :, :]).then_inc(qp_kept, 1)
                a.wait_ge(sim_used, t + 1)
                a.wait_ge(sim_made, t + 1)
                for j in range(2):
                    last = a.copy(sim[:, r, j * PK_HEADS:(j + 1) * PK_HEADS, :],
                                  ps_sim[j][:, :].rearrange("p (g k) -> p g k", g=PK_HEADS))
                last.then_inc(sim_kept, 1)

            def stage_queries(t):
                a.wait_ge(q_made, t + 1)
                a.copy(q_now[:, :, :], ps_q[:, :, :]).then_inc(q_kept, 1)

            def row_weights(t, r):
                a.wait_ge(best_ready, t + 1)
                a.activation(weight[:, r, :, :], weight[:, r, :, :], ACT.Exp).then_inc(exp_ready, 1)

            def attend(t):
                for hd in range(PK_HEADS):
                    a.wait_ge(max_done, t * PK_HEADS + (hd + 2))
                    a.activation(probs[:, hd % 2, :], masked[:, hd % 2, :], ACT.Exp, bias=bias[:, hd:hd + 1],
                                 scale=D ** -0.5).then_inc(exp_done, 1)
                    for c in range(2):
                        a.wait_ge(turned, t * TURNS + (2 * hd + c + 2))
                        a.copy(pT[:, c, :, :], ps_t[c][:, :, :]).then_inc(t_kept, 1)
                a.wait_ge(turned, t * TURNS + TURNS)
                a.copy(oT[:, :, :], ps_t[1][:, :, :]).then_inc(t_kept, 1)

            a.memzero(act_spare[:, 0:1]).then_inc(act_step, 1)
            a.wait_ge(act_step, 1)
            a.copy(act_spare[:, 1:2], act_spare[:, 0:1]).then_inc(t_kept, 2)
            a.wait_ge(t_kept, 2)
            a.copy(act_spare[:, 1:2], act_spare[:, 0:1]).then_inc(q_kept, 1)
            stage_similarities(0, 0)
            row_weights(0, 0)
            stage_similarities(1, 1)
            row_weights(1, 1)
            a.wait_ge(cleared, 2)
            with a.Fori(0, NT // 2 - 1) as i:
                for r in range(2):
                    stage_keys(i * 2 + r)
                    stage_similarities(i * 2 + (r + 2), r)
                    stage_queries(i * 2 + r)
                    row_weights(i * 2 + (r + 2), r)
                    attend(i * 2 + r)
            for t in range(NT - 2, NT):
                stage_keys(t)
                stage_queries(t)
                attend(t)

        @block.gpsimd
        def _(g):
            g.memset(pool_spare[:, :], 0.0).then_inc(carried, 1)
            g.memset(kT[:, :, :], 0.0).then_inc(cleared, 1)
            g.memset(v_all[:, :, :, 0:D], 0.0)
            g.memset(v_all[:, :, :, D:D + 1], 1.0).then_inc(cleared, 1)
            g.wait_ge(carried, 1)

            def carry(n):
                g.tensor_tensor(pool_spare[:, n + 1:n + 2], pool_spare[:, 0:1], pool_spare[:, 0:1],
                                ALU.add).then_inc(carried, 1)

            with g.Fori(0, NT // 2) as i:
                for r in range(2):
                    g.wait_ge(rows_ready, i * 2 + (r + 1))
                    for hd in range(PK_HEADS):
                        slot = hd % G_RING
                        g.wait_ge(carried, i * (2 * PK_HEADS) + (r * PK_HEADS + hd + 1))
                        g.wait_ge(combined, i * (2 * PK_HEADS) + (r * PK_HEADS + hd + 1))
                        carry(r * PK_HEADS + hd)
                        for k in range(TOPK):
                            n = hd * TOPK + k
                            g.indirect_dma_start(got[slot][:, k, :], None, d["pk_table"],
                                                 bass.IndirectOffsetOnAxis(ap=rows[:, r, n:n + 1].bitcast(U32), axis=0)
                                                 ).then_inc(landed[slot], 16)

        @block.vector
        def _(v):
            sites = [0]

            def carry():
                sites[0] += 1
                return v.memset(spare[:, sites[0]:sites[0] + 1], 0.0)

            def best_sixteen(step, values, out, index, n):
                carry()
                step(*[v.max(out[:, g, 0:8], values(g)) for g in range(n)])
                carry()
                step(*[v.max_index(index[:, g, 0:8], out[:, g, 0:8], values(g)) for g in range(n)])
                carry()
                step(*[v.match_replace(values(g), out[:, g, 0:8], values(g), LOWEST) for g in range(n)])
                carry()
                step(*[v.max(out[:, g, 8:16], values(g)) for g in range(n)])
                carry()
                step(*[v.max_index(index[:, g, 8:16], out[:, g, 8:16], values(g)) for g in range(n)])

            def look(t, r):
                step = Steps(v, dve, t * LOOK_STEPS)
                v.wait_ge(sim_kept, t + 1)
                best_sixteen(step, lambda g: sim[:, r, g, :], top, at, GROUPS2)
                step(v.tensor_copy(atf[:, :, :], at[:, :, :]))
                second = atf[:, PK_HEADS:, :]
                step(v.scalar_tensor_tensor(second, second, float(PK_KEYS), head_base[:, :, :], ALU.mult, ALU.add))
                done = []
                for src, dst in ((top, score), (atf, row)):
                    off = 0
                    for i, n in CANDS[:8]:
                        done.append(v.tensor_tensor(dst[:, :, off:off + n], src[:, PK_HEADS:, 0:n],
                                                    bc(src[:, 0:PK_HEADS, i:i + 1], [P, PK_HEADS, n]), ALU.add))
                        off += n
                    done.append(v.tensor_tensor(dst[:, :, off:off + 8], src[:, 0:PK_HEADS, 8:16],
                                                bc(src[:, PK_HEADS:, 0:1], [P, PK_HEADS, 8]), ALU.add))
                step(*done)
                best_sixteen(step, lambda g: score[:, g, :], best, pos, PK_HEADS)
                v.tensor_tensor(weight[:, r, :, :], best[:, :, :], bc(best[:, :, 0:1], [P, PK_HEADS, TOPK]),
                                ALU.subtract).then_inc(best_ready, 1)
                step(v.tensor_copy(posf[:, :, :], pos[:, :, :]))
                n = PK_HEADS // 2
                for heads in (slice(0, n), slice(n, PK_HEADS)):
                    step(v.tensor_tensor(eq[:, :, :, :].rearrange("p h k c -> p (h k) c"),
                                         bc(iota[:, :].unsqueeze(1), [P, n * TOPK, N_CAND]),
                                         bc(posf[:, heads, :].rearrange("p h k -> p (h k)").unsqueeze(2),
                                            [P, n * TOPK, N_CAND]), ALU.is_equal))
                    step(v.tensor_tensor(eq[:, :, :, :], eq[:, :, :, :],
                                         bc(row[:, heads, :].unsqueeze(2), [P, n, TOPK, N_CAND]), ALU.mult))
                    step(v.tensor_reduce(picked[:, heads, :], eq[:, :, :, :], AX.X, ALU.add))
                v.tensor_copy(rows[:, r, :], picked[:, :, :].rearrange("p h k -> p (h k)")).then_inc(rows_ready, 1)
                v.wait_ge(exp_ready, t + 1)
                step(v.tensor_reduce(total[:, :], weight[:, r, :, :], AX.X, ALU.add))
                step(v.reciprocal(total[:, :], total[:, :]))
                step(v.tensor_tensor(weight[:, r, :, :], weight[:, r, :, :],
                                     bc(total[:, :].unsqueeze(2), [P, PK_HEADS, TOPK]), ALU.mult))
                carry().then_inc(sim_used, 1)
                assert step.count == LOOK_STEPS, step.count

            def combine(t, r, hd):
                uses = PK_HEADS // G_RING
                rowsg = got[hd % G_RING]
                v.wait_ge(landed[hd % G_RING], t * (uses * 16 * TOPK) + (hd // G_RING + 1) * 16 * TOPK)
                v.tensor_tensor(rowsg[:, :, :], rowsg[:, :, :],
                                bc(weight[:, r, hd, :].unsqueeze(2), [P, TOPK, 2 * D]), ALU.mult).then_inc(scaled, 1)
                v.wait_ge(scaled, t * PK_HEADS + (hd + 1))
                half = slice(hd % 2 * D, hd % 2 * D + D)
                v.tensor_reduce(k_now[:, hd // 2, half], rowsg[:, :, 0:D].rearrange("p k c -> p c k"), AX.X, ALU.add)
                v.tensor_reduce(v_now[:, hd, :], rowsg[:, :, D:2 * D].rearrange("p k c -> p c k"),
                                AX.X, ALU.add).then_inc(combined, 1)

            def maximum(t, hd):
                v.wait_ge(qk_made, t * PK_HEADS + (hd + 1))
                carry()
                for j in range(2):
                    v.tensor_tensor_reduce(out=masked[:, hd % 2, j * 512:j * 512 + 512], in0=ps_sc[j][:, :],
                                           in1=mask[:, j * 512:j * 512 + 512],
                                           scale=1.0, scalar=NEG, op0=ALU.add, op1=ALU.max,
                                           accum_out=mx[:, hd, j:j + 1]).then_inc(max_step, 1)
                v.wait_ge(max_step, t * (3 * PK_HEADS) + (3 * hd + 2))
                v.tensor_tensor(bias[:, hd:hd + 1], mx[:, hd, 0:1], mx[:, hd, 1:2], ALU.max).then_inc(max_step, 1)
                v.wait_ge(max_step, t * (3 * PK_HEADS) + (3 * hd + 3))
                v.tensor_scalar(bias[:, hd:hd + 1], bias[:, hd:hd + 1], -(D ** -0.5), None, ALU.mult).then_inc(max_done, 1)

            def output(t, hd):
                v.wait_ge(pv_made, t * PK_HEADS + (hd + 1))
                v.reciprocal(rden[:, hd:hd + 1], ps_o[:, D:D + 1]).then_inc(rden_ready, 1)
                v.wait_ge(rden_ready, t * PK_HEADS + (hd + 1))
                v.tensor_scalar(o_now[:, hd // 2, hd % 2 * D:hd % 2 * D + D], ps_o[:, 0:D], rden[:, hd:hd + 1], None,
                                ALU.mult).then_inc(o_kept, 1)

            def add_to_h(t):
                v.wait_ge(y_made, t + 1)
                now = h[:, bass.ds(t, 1), :].rearrange("p t c -> p (t c)")
                v.tensor_tensor(now, now, ps_o[:, 0:D], ALU.add).then_inc(y_kept, 1)

            def invert(t):
                for k in range(INV_TILE):
                    v.wait_ge(left_made, t * INV_TILE + (k + 1))
                    v.tensor_tensor(left[:, 0:D], two[:, :], ps_left[0:D], ALU.subtract).then_inc(left_ready, 1)
                    v.wait_ge(inv_made, t * INV_TILE + (k + 1))
                    v.tensor_copy(inv[:, :], ps_inv[0:D])
                    v.tensor_copy(invT[:, 0:D], ps_invT[0:D]).then_inc(inv_ready, 1)

            v.engine_nop().then_inc(combined, G_RING)
            v.engine_nop().then_inc(sim_used, 2)
            v.engine_nop().then_inc(max_done, 1)
            v.engine_nop().then_inc(y_kept, 1)
            v.wait_ge(loaded, LOADS)
            look(0, 0)
            step = Chain(v, norm_step)
            step(v.memset(ones[:, :], 1.0))
            for wide in (near_wT, invT, left):
                step(v.memset(wide[:, D:P], 0.0))
            step(v.tensor_tensor(square[:, :], near_w[:, :], near_w[:, :], ALU.mult))
            v.tensor_reduce(norm[:, 0:1], square[:, :], AX.X, ALU.add).then_inc(norm_ready, 1)
            look(1, 1)
            v.wait_ge(norm_made, 1)
            step(v.reciprocal(norm[:, 1:2], ps_o[0:D, 0:1]))
            v.tensor_scalar(inv[:, :], near_wT[:, 0:D], norm[:, 1:2], None, ALU.mult)
            v.tensor_scalar(invT[:, 0:D], near_w[:, :], norm[:, 1:2], None, ALU.mult).then_inc(inv_ready, 1)
            for hd in range(PK_HEADS):
                combine(0, 0, hd)
            with v.Fori(0, NT // 2 - 1) as i:
                for r in range(2):
                    t = i * 2 + r
                    look(i * 2 + (r + 2), r)
                    v.wait_ge(kv_staged, t + 1)
                    for hd in range(PK_HEADS):
                        combine(i * 2 + (r + 1), 1 - r, hd)
                        maximum(t, hd)
                        if hd > 0:
                            output(t, hd - 1)
                    output(t, PK_HEADS - 1)
                    add_to_h(t)
                    invert(t)
            for t in range(NT - 2, NT):
                v.wait_ge(kv_staged, t + 1)
                for hd in range(PK_HEADS):
                    if t < NT - 1:
                        combine(t + 1, 1, hd)
                    maximum(t, hd)
                    if hd > 0:
                        output(t, hd - 1)
                output(t, PK_HEADS - 1)
                add_to_h(t)
            v.wait_ge(inv_ready, (NT - 2) * INV_TILE + 1)
            v.tensor_copy(inv_wT[:, :], invT[:, 0:D])


LOOK_STEPS = 5 + 1 + 1 + 1 + 5 + 1 + 6 + 3


def product_key_tables():
    c = {"pk_iota": np.arange(N_CAND, dtype=np.float32)[None]}
    base = np.arange(PK_HEADS, dtype=np.float32)[:, None] * PK_KEYS ** 2
    c["pk_base"] = np.broadcast_to(base, (PK_HEADS, TOPK))[None]
    c["pk_later"] = np.where(np.arange(2 * S - P)[None, :] <= np.arange(P)[:, None] + S - P, 0.0, NEG).astype(np.float32)
    return c

STAGES = [embed, linear_attention, tree_ffn, retention, product_keys, recurrence, graph_ffn,
          wavelet_attention, experts_eight]


def tower(nc, d, out, stages):
    with ExitStack() as ctx:
        def sb(name, shape, dt=F32):
            return ctx.enter_context(nc.sbuf_tensor(name, shape, dt))
        m = {"h": sb("h", [P, NT, D]), "xn": sb("xn", [P, NT, D]), "xT": sb("xT", [D + 1, T]),
             "ident": sb("ident", [P, P]), "eps": sb("eps", [P, 1]), "inv_wT": sb("inv_wT", [D, D])}
        with Stage(nc, "begin") as s:
            loaded = s.sem("loaded")
            block = s.block()

            @block.sync
            def _(sp):
                sp.dma_start(m["ident"][:, :], d["ident"]).then_inc(loaded, 16)
                sp.wait_ge(loaded, 16)

            @block.vector
            def _(v):
                v.memset(m["xT"][D:D + 1, :], 1.0)
                v.memset(m["eps"][:, :], LN_EPS)
        for stage in stages:
            stage(nc, m, d)
        with Stage(nc, "end") as s:
            stored = s.sem("stored")
            block = s.block()

            @block.sync
            def _(sp):
                sp.dma_start(out.rearrange("b (t p) d -> p (b t) d", p=P), m["h"][:, :, :]).then_inc(stored, 16)
                sp.wait_ge(stored, 16)


def constants():
    c = {"ident": np.eye(P, dtype=np.float32)}
    head = np.arange(D) // 8
    c["head_mask"] = ((head[:, None] == head[None, :]) / S).astype(np.float32)
    c.update(retention_tables())
    c.update(recurrence_tables())
    c.update(wavelet_tables())
    c.update(embed_tables())
    c.update(graph_tables())
    c.update(product_key_tables())
    c["order8"] = np.arange(8, 0, -1, dtype=np.float32)[None]
    return c


def layouts(i):
    cat = np.concatenate
    a = {}
    a["la_w_vk"] = cat([cat([i["L0_attn_Wv"].T, i["L0_attn_bv"][None]], 0),
                        cat([i["L0_attn_Wk"].T, i["L0_attn_bk"][None]], 0)], 1)
    a["la_w_q"] = cat([i["L0_attn_Wq"].T, i["L0_attn_bq"][None]], 0)
    a["la_w_fc"] = i["L0_attn_Wfc"].T
    a["la_b_fc"] = i["L0_attn_bfc"][None]
    even_odd = np.concatenate([np.arange(0, D, 2), np.arange(1, D, 2)])
    a["ret_w"] = cat([i["L1_attn_W_Q"][:, even_odd], i["L1_attn_W_K"][:, even_odd], i["L1_attn_W_V"]], 1)
    w1s = cat([i["L0_ffn_w1s"].T, i["L0_ffn_b1s"][None]], 0)
    a["tree_w1"] = cat([w1s, np.zeros((D + 1, 1), np.float32)], 1)
    a["tree_w2"] = cat([i["L0_ffn_w2s"].transpose(1, 0, 2).reshape(D, -1), np.zeros((D, D), np.float32)], 1)
    b2s = cat([i["L0_ffn_b2s"], np.zeros((1, D), np.float32)], 0)
    a["tree_b2"] = b2s.reshape(2, P, D).transpose(1, 0, 2)
    par = np.stack([i["L2_attn_nu_log"], i["L2_attn_theta_log"], i["L2_attn_gamma_log"]], 1)
    a["rec_par"] = cat([par, par], 0)
    bre, bim, cre, cim = (i[f"L2_attn_{k}"].T for k in ("B_re", "B_im", "C_re", "C_im"))
    a["rec_w_in"] = np.stack([cat([bre, bim], 1), cat([bim, bre], 1)], 1)
    a["rec_w_out"] = np.stack([cat([cre, cim], 0), cat([cim, cre], 0)], 1)
    w1, b1, w2 = i["L3_ffn_w1"], i["L3_ffn_b1"], i["L3_ffn_w2"]
    a["moe8_w1"] = cat([w1.transpose(1, 0, 2).reshape(D, 4, P), b1.reshape(1, 4, P)], 0)
    a["moe8_w2"] = w2.reshape(4, P, D).transpose(1, 0, 2)
    a["moe8_b2"] = i["L3_ffn_b2"][None]
    a["route8_w"] = i["L3_ffn_router_w"].T
    a["near_w_q"], a["near_w_qT"] = i["L3_attn_W_Q"], i["L3_attn_W_Q"].T
    a["near_w_v"], a["near_w_oT"] = i["L3_attn_W_V"], i["L3_attn_W_O"].T
    a["ids"], a["positions"] = i["x"], i["fside_BS_continuous_positions"]
    taps = i["L0_tok_w1"].transpose(2, 1, 0)
    taps = cat([taps, np.zeros((1, VOCAB, P), np.float32)], 0)
    a["emb_w1"] = taps.reshape(4, P, P).transpose(1, 0, 2)
    a["emb_w2"] = i["L0_tok_w2"].transpose(1, 2, 0)
    a["emb_w3"] = i["L0_tok_w3"][0]
    a["emb_b1"], a["emb_b2"], a["emb_b3"] = (i[f"L0_tok_b{k}"][:, None] for k in (1, 2, 3))
    a["emb_table"] = cat([i["L0_tok_emb"], i["L0_tok_locality_shapes"]], 1)
    a["emb_widths"], a["emb_weights"] = i["L0_tok_multiscale_widths"][None], i["L0_tok_scale_weights"][None]
    a["edges"] = i["L2_ffn_edge_index"].reshape(2, P, EC)
    a["gat_w"] = i["L2_ffn_W_gat"]
    a["gat_att"] = np.stack([i["L2_ffn_att_src"].reshape(-1), i["L2_ffn_att_dst"].reshape(-1)])[None]
    a["route4_par"] = np.stack([i["L2_ffn_b_gat"], i["L2_ffn_ln_gamma"], i["L2_ffn_ln_beta"]])[None]
    w1, b1, w2 = i["L2_ffn_W1"], i["L2_ffn_b1"], i["L2_ffn_W2"]
    a["moe4_w1"] = cat([w1.transpose(1, 0, 2), b1[None]], 0)
    a["moe4_w2"], a["moe4_b2"] = w2.transpose(1, 0, 2), i["L2_ffn_b2"][None]
    a["pk_wq"] = cat([i["L1_ffn_Wq_pk"], i["L1_ffn_Wq"]], 1).reshape(D, 8, P)
    keys = i["L1_ffn_pk_keys"].transpose(0, 2, 3, 1).reshape(4, 4, PK_DIM, PK_KEYS)
    wide = np.zeros((4, 4, PK_DIM, 4, PK_KEYS), np.float32)
    for q in range(4):
        wide[:, q, :, q] = keys[:, q]
    a["pk_keys"] = wide.reshape(4, P, 4 * PK_KEYS).transpose(1, 0, 2)
    a["pk_table"] = cat([i["L1_ffn_keys_table"], i["L1_ffn_values_table"]], 1)
    a["pk_wo"] = i["L1_ffn_Wo"].reshape(4, P, D).transpose(1, 0, 2)
    return a


def kernel(**inputs):
    import concourse.bacc as bacc
    from concourse.bass_utils import run_bass_kernel_spmd as run

    inputs = {k: np.asarray(v) for k, v in inputs.items()}
    nc = bacc.Bacc("TRN2", target_bir_lowering=False, num_devices=1)
    arrays = {k: np.ascontiguousarray(v) for k, v in {**constants(), **layouts(inputs)}.items()}
    d = {k: nc.dram_tensor(f"in_{k}", v.shape, mybir.dt.from_np(v.dtype), kind="ExternalInput").ap()
         for k, v in arrays.items()}
    out = nc.dram_tensor("out_h", (B, S, D), F32, kind="ExternalOutput").ap()
    tower(nc, d, out, STAGES)
    r = run(nc, [{f"in_{k}": v for k, v in arrays.items()}], core_ids=[0])
    return np.asarray(r.results[0]["out_h"])
```
